# Optimizing a Trainium2 kernel written in Bass

```python
import numpy as np
import jax
import jax.numpy as jnp

def _softmax(x, axis=-1):
    return jax.nn.softmax(x, axis=axis)

def _gelu(x):
    return jax.nn.gelu(x, approximate=True)

def _silu(x):
    return jax.nn.silu(x)

def _sigmoid(x):
    return jax.nn.sigmoid(x)

def _layernorm(x, axis=-1, eps=1e-05):
    m = jnp.mean(x, axis=axis, keepdims=True)
    v = jnp.var(x, axis=axis, keepdims=True)
    return (x - m) / jnp.sqrt(v + eps)

def _scatter_add(tgt, idx, src, axis=0):
    return tgt.at[idx].add(src)

def _segment_sum(src, seg, n):
    return jax.ops.segment_sum(src, seg, n)
kernel_name = 'mk_decoder_preln_d2_seqx_r8_0219d4'

def setup_inputs(seed: int=0):
    np.random.seed(seed)
    _w = jnp.asarray

    def _rec_inputs():
        import jax
        import jax.numpy as jnp
        _rk = jax.random.key(seed)
        x = -0.0005207 + 1.001 * jax.random.normal(jax.random.fold_in(_rk, 1), (8, 256, 128), jnp.float32)
        _lenS = 256 - jax.random.randint(jax.random.fold_in(_rk, 7), (8,), 0, max(1, 256 // 4) + 1, jnp.int32)
        _lenS2 = 512 - jax.random.randint(jax.random.fold_in(_rk, 8), (8,), 0, max(1, 512 // 4) + 1, jnp.int32)
        _ctx_1024P = jax.random.normal(jax.random.fold_in(_rk, 11), (8, 16, 128), jnp.float32)
        _ctx_1024c = jax.random.dirichlet(jax.random.fold_in(_rk, 511), 0.3 * jnp.ones((16,), jnp.float32), (8, 512))
        _ctx_1024t = jnp.einsum('bsk,bkd->bsd', _ctx_1024c, _ctx_1024P)
        _ctx_1024t = _ctx_1024t * jax.lax.rsqrt(jnp.mean(jnp.square(_ctx_1024t)) + 1e-12) * 0.953939
        ctx_1024 = -1.52775e-05 + 0.999936 * (_ctx_1024t + 0.3 * jax.random.normal(jax.random.fold_in(_rk, 611), (8, 512, 128), jnp.float32))
        _validS = jnp.arange(256)[None, :] < _lenS[:, None]
        _validS2 = jnp.arange(512)[None, :] < _lenS2[:, None]
        _causal = jnp.tril(jnp.ones((256, 256), dtype=bool))
        mask_Bx1x1xS2_bk0 = jnp.logical_not(jnp.broadcast_to(_validS2[:, None, None, :], (8, 1, 1, 512)))
        return (x, ctx_1024, mask_Bx1x1xS2_bk0)
    x, ctx_1024, mask_Bx1x1xS2_bk0 = _rec_inputs()

    def _L0_attn_setup():
        import jax, jax.numpy as jnp
        import numpy as np
        DIM = 128
        HEADS = 16
        HD = DIM // HEADS
        HID = 4 * DIM
        TPF = 1374
        LR = 0.1
        NS_ITERS = 5
        TTT_STEPS = 2
        B, S = (2, 4)
        SN = S * TPF

        def _newton_schulz(G, iters=NS_ITERS):
            a, b, c = (3.4445, -4.775, 2.0315)
            X = G / (jnp.linalg.norm(G) + 1e-07)
            transposed = G.shape[0] > G.shape[1]
            if transposed:
                X = X.T
            for _ in range(iters):
                A = X @ X.T
                X = a * X + (b * A + c * (A @ A)) @ X
            return X.T if transposed else X

        def _muon_update(p, g):
            return p - LR * _newton_schulz(g)
        key = jax.random.key(seed)
        ks = jax.random.split(key, 8)
        inp = {'x': jax.random.normal(ks[0], (B, SN, DIM), jnp.float32), 'qkv_w': jax.random.normal(ks[1], (DIM, 3 * DIM), jnp.float32) * DIM ** (-0.5), 'qkv_b': jnp.zeros((3 * DIM,), jnp.float32), 'qn_scale': jnp.ones((HD,), jnp.float32), 'qn_bias': jnp.zeros((HD,), jnp.float32), 'kn_scale': jnp.ones((HD,), jnp.float32), 'kn_bias': jnp.zeros((HD,), jnp.float32), 'ttt_gate': jax.random.normal(ks[2], (DIM, HID), jnp.float32) * DIM ** (-0.5), 'ttt_val': jax.random.normal(ks[3], (DIM, HID), jnp.float32) * DIM ** (-0.5), 'ttt_proj': jax.random.normal(ks[4], (HID, DIM), jnp.float32) * HID ** (-0.5), 'proj_w': jax.random.normal(ks[5], (DIM, DIM), jnp.float32) * DIM ** (-0.5), 'proj_b': jnp.zeros((DIM,), jnp.float32)}
        return inp
    _L0_attn_all = _L0_attn_setup()
    _L0_attn_in = {k: v for k, v in _L0_attn_all.items() if k in ('qkv_w', 'qkv_b', 'qn_scale', 'qn_bias', 'kn_scale', 'kn_bias', 'ttt_gate', 'ttt_val', 'ttt_proj', 'proj_w', 'proj_b')}
    del _L0_attn_all

    def _L0_xattn_setup():
        import jax, jax.numpy as jnp
        import numpy as np
        DIM = 128
        HEADS = 16
        DHEAD = 64
        INNER = HEADS * DHEAD
        EPS = 1e-05

        def layer_norm(x, g, b):
            mu = jnp.mean(x, axis=-1, keepdims=True)
            var = jnp.mean(jnp.square(x - mu), axis=-1, keepdims=True)
            return (x - mu) * jax.lax.rsqrt(var + EPS) * g + b

        def apply_rope(x, cos, sin):
            d2 = x.shape[-1] // 2
            x1, x2 = (x[..., :d2], x[..., d2:])
            return jnp.concatenate([x1 * cos - x2 * sin, x2 * cos + x1 * sin], axis=-1)
        key = jax.random.key(seed)
        ks = jax.random.split(key, 10)
        B, N, S = (8, 32, 512)
        latents = jax.random.normal(ks[0], (B, N, DIM), dtype=jnp.float32)
        context = jax.random.normal(ks[1], (B, S, DIM), dtype=jnp.float32)
        cos = jax.random.uniform(ks[2], (S, DHEAD // 2), dtype=jnp.float32)
        sin = jax.random.uniform(ks[3], (S, DHEAD // 2), dtype=jnp.float32)
        init = lambda k, shp, fan_in: jax.random.normal(k, shp, dtype=jnp.float32) / np.sqrt(fan_in)
        return {'latents': latents, 'context': context, 'cos': cos, 'sin': sin, 'ln_lat_g': jnp.ones((DIM,), jnp.float32), 'ln_lat_b': jnp.zeros((DIM,), jnp.float32), 'ln_ctx_g': jnp.ones((DIM,), jnp.float32), 'ln_ctx_b': jnp.zeros((DIM,), jnp.float32), 'Wq': init(ks[4], (DIM, INNER), DIM), 'Wkv': init(ks[5], (DIM, 2 * INNER), DIM), 'Wo': init(ks[6], (INNER, DIM), INNER), 'bo': jnp.zeros((DIM,), jnp.float32)}
    _L0_xattn_all = _L0_xattn_setup()
    _L0_xattn_in = {k: v for k, v in _L0_xattn_all.items() if k in ('cos', 'sin', 'ln_lat_g', 'ln_lat_b', 'ln_ctx_g', 'ln_ctx_b', 'Wq', 'Wkv', 'Wo', 'bo')}
    del _L0_xattn_all

    def _L0_ffn_setup():
        import jax, jax.numpy as jnp
        import numpy as np
        S, B, D, H, E, K, F = (128, 4, 128, 16, 8, 2, 512)

        def _ln(x, g, b, eps=1e-05):
            mu = jnp.mean(x, axis=-1, keepdims=True)
            var = jnp.mean((x - mu) ** 2, axis=-1, keepdims=True)
            return (x - mu) * jax.lax.rsqrt(var + eps) * g + b
        key = jax.random.key(seed)
        ks = jax.random.split(key, 8)
        s = 0.02
        return {'src': jax.random.normal(ks[0], (S, B, D), jnp.float32), 'in_proj_w': jax.random.normal(ks[1], (3 * D, D), jnp.float32) * s, 'in_proj_b': jnp.zeros((3 * D,), jnp.float32), 'out_w': jax.random.normal(ks[2], (D, D), jnp.float32) * s, 'out_b': jnp.zeros((D,), jnp.float32), 'gate_w': jax.random.normal(ks[3], (E, D), jnp.float32) * s, 'gate_b': jnp.zeros((E,), jnp.float32), 'w1': jax.random.normal(ks[4], (E, F, D), jnp.float32) * s, 'b1': jnp.zeros((E, F), jnp.float32), 'w2': jax.random.normal(ks[5], (E, D, F), jnp.float32) * s, 'b2': jnp.zeros((E, D), jnp.float32), 'ln1_g': jnp.ones((D,), jnp.float32), 'ln1_b': jnp.zeros((D,), jnp.float32), 'ln2_g': jnp.ones((D,), jnp.float32), 'ln2_b': jnp.zeros((D,), jnp.float32)}
    _L0_ffn_all = _L0_ffn_setup()
    _L0_ffn_in = {k: v for k, v in _L0_ffn_all.items() if k in ('in_proj_w', 'in_proj_b', 'out_w', 'out_b', 'gate_w', 'gate_b', 'w1', 'b1', 'w2', 'b2', 'ln1_g', 'ln1_b', 'ln2_g', 'ln2_b')}
    del _L0_ffn_all

    def _L1_attn_setup():
        import jax, jax.numpy as jnp
        import numpy as np
        B, N, D, K = (2, 512, 128, 32)
        key = jax.random.key(seed)
        k1, k2, k3 = jax.random.split(key, 3)
        return {'x': jax.random.normal(k1, (B, N, D), dtype=jnp.float32), 'compare_left': jax.random.normal(k2, (D, K), dtype=jnp.float32) * 0.05, 'compare_right': jax.random.normal(k3, (D, K), dtype=jnp.float32) * 0.05, 'threshold': jnp.zeros((1,), dtype=jnp.float32), 'gate_bias': jnp.zeros((1,), dtype=jnp.float32)}
    _L1_attn_all = _L1_attn_setup()
    _L1_attn_in = {k: v for k, v in _L1_attn_all.items() if k in ('compare_left', 'compare_right', 'threshold', 'gate_bias')}
    del _L1_attn_all

    def _L1_xattn_setup():
        import jax, jax.numpy as jnp
        import numpy as np
        import math
        D_MODEL = 128
        N_HEADS = 16
        D_HEAD = D_MODEL // N_HEADS
        NUM_BUCKETS = 32
        MAX_DISTANCE = 128
        B, LQ, LK = (2, 256, 256)

        def _rel_pos_bucket(rel):
            n = jnp.clip(-rel, 0, None)
            max_exact = NUM_BUCKETS // 2
            is_small = n < max_exact
            val_if_large = max_exact + (jnp.log(n.astype(jnp.float32) / max_exact + 1e-09) / math.log(MAX_DISTANCE / max_exact) * (NUM_BUCKETS - max_exact)).astype(jnp.int32)
            val_if_large = jnp.minimum(val_if_large, NUM_BUCKETS - 1)
            return jnp.where(is_small, n, val_if_large)
        key = jax.random.key(seed)
        ks = jax.random.split(key, 9)
        scale = 1.0 / math.sqrt(D_MODEL)
        q = jax.random.normal(ks[0], (B, LQ, D_MODEL), dtype=jnp.float32)
        k = jax.random.normal(ks[1], (B, LK, D_MODEL), dtype=jnp.float32)
        v = jax.random.normal(ks[2], (B, LK, D_MODEL), dtype=jnp.float32)
        key_padding_mask = jax.random.randint(ks[3], (B, 1, 1, LK), 0, 2).astype(bool)
        Wq = jax.random.normal(ks[4], (D_MODEL, D_MODEL), dtype=jnp.float32) * scale
        Wk = jax.random.normal(ks[5], (D_MODEL, D_MODEL), dtype=jnp.float32) * scale
        Wv = jax.random.normal(ks[6], (D_MODEL, D_MODEL), dtype=jnp.float32) * scale
        Wo = jax.random.normal(ks[7], (D_MODEL, D_MODEL), dtype=jnp.float32) * scale
        rel_emb = jax.random.normal(ks[8], (NUM_BUCKETS, N_HEADS), dtype=jnp.float32) * 0.02
        return {'q': q, 'k': k, 'v': v, 'key_padding_mask': key_padding_mask, 'Wq': Wq, 'Wk': Wk, 'Wv': Wv, 'Wo': Wo, 'rel_emb': rel_emb}
    _L1_xattn_all = _L1_xattn_setup()
    _L1_xattn_in = {k: v for k, v in _L1_xattn_all.items() if k in ('Wq', 'Wk', 'Wv', 'Wo', 'rel_emb')}
    del _L1_xattn_all

    def _L1_ffn_setup():
        import jax, jax.numpy as jnp
        import numpy as np

        def fixed_quant(x, width, frac_width):
            scale = jnp.float32(2.0 ** frac_width)
            imax = jnp.float32(2 ** (width - 1) - 1)
            imin = jnp.float32(-2 ** (width - 1))
            return jnp.clip(jnp.round(x * scale), imin, imax) / scale
        IN_F, HID_F, OUT_F = (128, 512, 128)
        B, S = (4, 256)
        ACT_Q = (8, 4)
        W_Q = (8, 6)
        BIAS_Q = (8, 6)

        def quantized_linear(x, w, b):
            xq = fixed_quant(x, *ACT_Q)
            wq = fixed_quant(w, *W_Q)
            bq = fixed_quant(b, *BIAS_Q)
            return jnp.einsum('bsi,oi->bso', xq, wq) + bq

        def quantized_relu(x):
            return jax.nn.relu(fixed_quant(x, *ACT_Q))
        key = jax.random.key(seed)
        k_x, k_w1, k_b1, k_w2, k_b2 = jax.random.split(key, 5)
        x = jax.random.normal(k_x, (B, S, IN_F), dtype=jnp.float32)
        w1 = jax.random.normal(k_w1, (HID_F, IN_F), dtype=jnp.float32) / np.sqrt(IN_F)
        b1 = jax.random.normal(k_b1, (HID_F,), dtype=jnp.float32) / np.sqrt(IN_F)
        w2 = jax.random.normal(k_w2, (OUT_F, HID_F), dtype=jnp.float32) / np.sqrt(HID_F)
        b2 = jax.random.normal(k_b2, (OUT_F,), dtype=jnp.float32) / np.sqrt(HID_F)
        return {'x': x, 'w1': w1, 'b1': b1, 'w2': w2, 'b2': b2}
    _L1_ffn_all = _L1_ffn_setup()
    _L1_ffn_in = {k: v for k, v in _L1_ffn_all.items() if k in ('w1', 'b1', 'w2', 'b2')}
    del _L1_ffn_all
    return {'x': x, 'ctx_1024': ctx_1024, 'mask_Bx1x1xS2_bk0': mask_Bx1x1xS2_bk0, 'L0_attn_qkv_w': _L0_attn_in['qkv_w'], 'L0_attn_qkv_b': _L0_attn_in['qkv_b'], 'L0_attn_qn_scale': _L0_attn_in['qn_scale'], 'L0_attn_qn_bias': _L0_attn_in['qn_bias'], 'L0_attn_kn_scale': _L0_attn_in['kn_scale'], 'L0_attn_kn_bias': _L0_attn_in['kn_bias'], 'L0_attn_ttt_gate': _L0_attn_in['ttt_gate'], 'L0_attn_ttt_val': _L0_attn_in['ttt_val'], 'L0_attn_ttt_proj': _L0_attn_in['ttt_proj'], 'L0_attn_proj_w': _L0_attn_in['proj_w'], 'L0_attn_proj_b': _L0_attn_in['proj_b'], 'L0_xattn_cos': _L0_xattn_in['cos'], 'L0_xattn_sin': _L0_xattn_in['sin'], 'L0_xattn_ln_lat_g': _L0_xattn_in['ln_lat_g'], 'L0_xattn_ln_lat_b': _L0_xattn_in['ln_lat_b'], 'L0_xattn_ln_ctx_g': _L0_xattn_in['ln_ctx_g'], 'L0_xattn_ln_ctx_b': _L0_xattn_in['ln_ctx_b'], 'L0_xattn_Wq': _L0_xattn_in['Wq'], 'L0_xattn_Wkv': _L0_xattn_in['Wkv'], 'L0_xattn_Wo': _L0_xattn_in['Wo'], 'L0_xattn_bo': _L0_xattn_in['bo'], 'L0_ffn_in_proj_w': _L0_ffn_in['in_proj_w'], 'L0_ffn_in_proj_b': _L0_ffn_in['in_proj_b'], 'L0_ffn_out_w': _L0_ffn_in['out_w'], 'L0_ffn_out_b': _L0_ffn_in['out_b'], 'L0_ffn_gate_w': _L0_ffn_in['gate_w'], 'L0_ffn_gate_b': _L0_ffn_in['gate_b'], 'L0_ffn_w1': _L0_ffn_in['w1'], 'L0_ffn_b1': _L0_ffn_in['b1'], 'L0_ffn_w2': _L0_ffn_in['w2'], 'L0_ffn_b2': _L0_ffn_in['b2'], 'L0_ffn_ln1_g': _L0_ffn_in['ln1_g'], 'L0_ffn_ln1_b': _L0_ffn_in['ln1_b'], 'L0_ffn_ln2_g': _L0_ffn_in['ln2_g'], 'L0_ffn_ln2_b': _L0_ffn_in['ln2_b'], 'L1_attn_compare_left': _L1_attn_in['compare_left'], 'L1_attn_compare_right': _L1_attn_in['compare_right'], 'L1_attn_threshold': _L1_attn_in['threshold'], 'L1_attn_gate_bias': _L1_attn_in['gate_bias'], 'L1_xattn_Wq': _L1_xattn_in['Wq'], 'L1_xattn_Wk': _L1_xattn_in['Wk'], 'L1_xattn_Wv': _L1_xattn_in['Wv'], 'L1_xattn_Wo': _L1_xattn_in['Wo'], 'L1_xattn_rel_emb': _L1_xattn_in['rel_emb'], 'L1_ffn_w1': _L1_ffn_in['w1'], 'L1_ffn_b1': _L1_ffn_in['b1'], 'L1_ffn_w2': _L1_ffn_in['w2'], 'L1_ffn_b2': _L1_ffn_in['b2']}

def reference(x, ctx_1024, mask_Bx1x1xS2_bk0, L0_attn_qkv_w, L0_attn_qkv_b, L0_attn_qn_scale, L0_attn_qn_bias, L0_attn_kn_scale, L0_attn_kn_bias, L0_attn_ttt_gate, L0_attn_ttt_val, L0_attn_ttt_proj, L0_attn_proj_w, L0_attn_proj_b, L0_xattn_cos, L0_xattn_sin, L0_xattn_ln_lat_g, L0_xattn_ln_lat_b, L0_xattn_ln_ctx_g, L0_xattn_ln_ctx_b, L0_xattn_Wq, L0_xattn_Wkv, L0_xattn_Wo, L0_xattn_bo, L0_ffn_in_proj_w, L0_ffn_in_proj_b, L0_ffn_out_w, L0_ffn_out_b, L0_ffn_gate_w, L0_ffn_gate_b, L0_ffn_w1, L0_ffn_b1, L0_ffn_w2, L0_ffn_b2, L0_ffn_ln1_g, L0_ffn_ln1_b, L0_ffn_ln2_g, L0_ffn_ln2_b, L1_attn_compare_left, L1_attn_compare_right, L1_attn_threshold, L1_attn_gate_bias, L1_xattn_Wq, L1_xattn_Wk, L1_xattn_Wv, L1_xattn_Wo, L1_xattn_rel_emb, L1_ffn_w1, L1_ffn_b1, L1_ffn_w2, L1_ffn_b2):
    import jax
    import jax.numpy as jnp

    def _L0_attn_ref(x, qkv_w, qkv_b, qn_scale, qn_bias, kn_scale, kn_bias, ttt_gate, ttt_val, ttt_proj, proj_w, proj_b):
        import jax, jax.numpy as jnp
        import numpy as np
        DIM = 128
        HEADS = 16
        HD = DIM // HEADS
        HID = 4 * DIM
        TPF = 1374
        LR = 0.1
        NS_ITERS = 5
        TTT_STEPS = 2
        B, S = (2, 4)
        SN = S * TPF

        def _newton_schulz(G, iters=NS_ITERS):
            a, b, c = (3.4445, -4.775, 2.0315)
            X = G / (jnp.linalg.norm(G) + 1e-07)
            transposed = G.shape[0] > G.shape[1]
            if transposed:
                X = X.T
            for _ in range(iters):
                A = X @ X.T
                X = a * X + (b * A + c * (A @ A)) @ X
            return X.T if transposed else X

        def _muon_update(p, g):
            return p - LR * _newton_schulz(g)
        Bx, SNx, _ = x.shape
        qkv = x @ qkv_w + qkv_b
        q, k, v = jnp.split(qkv, 3, axis=-1)
        q = q.reshape(Bx, SNx, HEADS, HD)
        k = k.reshape(Bx, SNx, HEADS, HD)
        q = q / (jnp.linalg.norm(q, axis=-1, keepdims=True) + 1e-06) * qn_scale + qn_bias
        k = k / (jnp.linalg.norm(k, axis=-1, keepdims=True) + 1e-06) * kn_scale + kn_bias
        q_ttt = q.reshape(-1, DIM)
        k_ttt = k.reshape(-1, DIM)
        v_ttt = v.reshape(-1, DIM)
        theta = {'gate': ttt_gate, 'val': ttt_val, 'proj': ttt_proj}

        def loss_fn(p):
            h = jax.nn.swish(k_ttt @ p['gate']) * (k_ttt @ p['val'])
            pred = h @ p['proj']
            return jnp.mean((pred - v_ttt) ** 2)
        for _ in range(TTT_STEPS):
            grads = jax.grad(loss_fn)(theta)
            theta = {kk: _muon_update(theta[kk], grads[kk]) for kk in theta}
        h_q = jax.nn.swish(q_ttt @ theta['gate']) * (q_ttt @ theta['val'])
        o = h_q @ theta['proj'] @ proj_w + proj_b
        return o.reshape(Bx, SNx, DIM)

    def _L0_xattn_ref(latents, context, cos, sin, ln_lat_g, ln_lat_b, ln_ctx_g, ln_ctx_b, Wq, Wkv, Wo, bo):
        import jax, jax.numpy as jnp
        import numpy as np
        DIM = 128
        HEADS = 16
        DHEAD = 64
        INNER = HEADS * DHEAD
        EPS = 1e-05

        def layer_norm(x, g, b):
            mu = jnp.mean(x, axis=-1, keepdims=True)
            var = jnp.mean(jnp.square(x - mu), axis=-1, keepdims=True)
            return (x - mu) * jax.lax.rsqrt(var + EPS) * g + b

        def apply_rope(x, cos, sin):
            d2 = x.shape[-1] // 2
            x1, x2 = (x[..., :d2], x[..., d2:])
            return jnp.concatenate([x1 * cos - x2 * sin, x2 * cos + x1 * sin], axis=-1)
        b, n, _ = latents.shape
        s = context.shape[1]
        lat = layer_norm(latents, ln_lat_g, ln_lat_b)
        ctx = layer_norm(context, ln_ctx_g, ln_ctx_b)
        q = (lat @ Wq).reshape(b, n, HEADS, DHEAD).transpose(0, 2, 1, 3)
        kv = ctx @ Wkv
        k, v = jnp.split(kv, 2, axis=-1)
        k = k.reshape(b, s, HEADS, DHEAD).transpose(0, 2, 1, 3)
        v = v.reshape(b, s, HEADS, DHEAD).transpose(0, 2, 1, 3)
        k = apply_rope(k, cos[None, None], sin[None, None])
        scale = DHEAD ** (-0.5)
        attn = jnp.einsum('bhnd,bhsd->bhns', q, k) * scale
        attn = jnp.clip(attn, -11.0, 11.0)
        attn = jax.nn.softmax(attn, axis=-1)
        out = jnp.einsum('bhns,bhsd->bhnd', attn, v)
        out = out.transpose(0, 2, 1, 3).reshape(b, n, INNER)
        return out @ Wo + bo

    def _L0_ffn_ref(src, in_proj_w, in_proj_b, out_w, out_b, gate_w, gate_b, w1, b1, w2, b2, ln1_g, ln1_b, ln2_g, ln2_b):
        import jax, jax.numpy as jnp
        import numpy as np
        S, B, D, H, E, K, F = (128, 4, 128, 16, 8, 2, 512)

        def _ln(x, g, b, eps=1e-05):
            mu = jnp.mean(x, axis=-1, keepdims=True)
            var = jnp.mean((x - mu) ** 2, axis=-1, keepdims=True)
            return (x - mu) * jax.lax.rsqrt(var + eps) * g + b
        s_len, bsz, d = src.shape
        dh = d // H
        qkv = src @ in_proj_w.T + in_proj_b
        q, k, v = jnp.split(qkv, 3, axis=-1)
        q = q.reshape(s_len, bsz, H, dh)
        k = k.reshape(s_len, bsz, H, dh)
        v = v.reshape(s_len, bsz, H, dh)
        scale = dh ** (-0.5)
        scores = jnp.einsum('sbhd,tbhd->bhst', q, k) * scale
        attn = jax.nn.softmax(scores, axis=-1)
        ctx = jnp.einsum('bhst,tbhd->sbhd', attn, v).reshape(s_len, bsz, d)
        attn_out = ctx @ out_w.T + out_b
        x = _ln(src + attn_out, ln1_g, ln1_b)
        tok = x.reshape(-1, d)
        n_tok = tok.shape[0]
        logits = tok @ gate_w.T + gate_b
        probs = jax.nn.softmax(logits, axis=-1)
        topv, topi = jax.lax.top_k(probs, K)
        topv = topv / jnp.sum(topv, axis=-1, keepdims=True)
        combine = jnp.zeros_like(probs).at[jnp.arange(n_tok)[:, None], topi].set(topv)
        moe_out = jnp.zeros_like(tok)
        for e in range(E):
            h = jax.nn.relu(tok @ w1[e].T + b1[e]) @ w2[e].T + b2[e]
            moe_out = moe_out + combine[:, e:e + 1] * h
        moe_out = moe_out.reshape(s_len, bsz, d)
        return _ln(x + moe_out, ln2_g, ln2_b)

    def _L1_attn_ref(x, compare_left, compare_right, threshold, gate_bias):
        import jax, jax.numpy as jnp
        import numpy as np
        B, N, D, K = (2, 512, 128, 32)
        dim = x.shape[-1]
        left = x @ compare_left
        right = x @ compare_right
        comparison = jnp.einsum('bik,bjk->bij', left, right) / jnp.sqrt(jnp.float32(dim))
        mask = (comparison > threshold).astype(x.dtype)
        gated = jax.nn.softmax(comparison + gate_bias, axis=-1)
        return mask * gated @ x

    def _L1_xattn_ref(q, k, v, key_padding_mask, Wq, Wk, Wv, Wo, rel_emb):
        import jax, jax.numpy as jnp
        import numpy as np
        import math
        D_MODEL = 128
        N_HEADS = 16
        D_HEAD = D_MODEL // N_HEADS
        NUM_BUCKETS = 32
        MAX_DISTANCE = 128
        B, LQ, LK = (2, 256, 256)

        def _rel_pos_bucket(rel):
            n = jnp.clip(-rel, 0, None)
            max_exact = NUM_BUCKETS // 2
            is_small = n < max_exact
            val_if_large = max_exact + (jnp.log(n.astype(jnp.float32) / max_exact + 1e-09) / math.log(MAX_DISTANCE / max_exact) * (NUM_BUCKETS - max_exact)).astype(jnp.int32)
            val_if_large = jnp.minimum(val_if_large, NUM_BUCKETS - 1)
            return jnp.where(is_small, n, val_if_large)
        Bq, Lq, _ = q.shape
        Lk = k.shape[1]
        qh = (q @ Wq.T).reshape(Bq, Lq, N_HEADS, D_HEAD).transpose(0, 2, 1, 3)
        kh = (k @ Wk.T).reshape(Bq, Lk, N_HEADS, D_HEAD).transpose(0, 2, 1, 3)
        vh = (v @ Wv.T).reshape(Bq, Lk, N_HEADS, D_HEAD).transpose(0, 2, 1, 3)
        scores = jnp.einsum('bhqd,bhkd->bhqk', qh, kh) / math.sqrt(D_HEAD)
        rel = jnp.arange(Lk, dtype=jnp.int32)[None, :] - jnp.arange(Lq, dtype=jnp.int32)[:, None]
        buckets = _rel_pos_bucket(rel)
        bias = rel_emb[buckets]
        scores = scores + bias.transpose(2, 0, 1)[None]
        scores = jnp.where(key_padding_mask, scores, -1000000000.0)
        attn = jax.nn.softmax(scores, axis=-1)
        out = jnp.einsum('bhqk,bhkd->bhqd', attn, vh)
        out = out.transpose(0, 2, 1, 3).reshape(Bq, Lq, D_MODEL)
        return out @ Wo.T

    def _L1_ffn_ref(x, w1, b1, w2, b2):
        import jax, jax.numpy as jnp
        import numpy as np

        def fixed_quant(x, width, frac_width):
            scale = jnp.float32(2.0 ** frac_width)
            imax = jnp.float32(2 ** (width - 1) - 1)
            imin = jnp.float32(-2 ** (width - 1))
            return jnp.clip(jnp.round(x * scale), imin, imax) / scale
        IN_F, HID_F, OUT_F = (128, 512, 128)
        B, S = (4, 256)
        ACT_Q = (8, 4)
        W_Q = (8, 6)
        BIAS_Q = (8, 6)

        def quantized_linear(x, w, b):
            xq = fixed_quant(x, *ACT_Q)
            wq = fixed_quant(w, *W_Q)
            bq = fixed_quant(b, *BIAS_Q)
            return jnp.einsum('bsi,oi->bso', xq, wq) + bq

        def quantized_relu(x):
            return jax.nn.relu(fixed_quant(x, *ACT_Q))
        h = quantized_linear(x, w1, b1)
        h = quantized_relu(h)
        out = quantized_linear(h, w2, b2)
        return out
    x = x + _L0_attn_ref(_layernorm(x, axis=-1), L0_attn_qkv_w, L0_attn_qkv_b, L0_attn_qn_scale, L0_attn_qn_bias, L0_attn_kn_scale, L0_attn_kn_bias, L0_attn_ttt_gate, L0_attn_ttt_val, L0_attn_ttt_proj, L0_attn_proj_w, L0_attn_proj_b)
    x = x + _L0_xattn_ref(_layernorm(x, axis=-1), ctx_1024, L0_xattn_cos, L0_xattn_sin, L0_xattn_ln_lat_g, L0_xattn_ln_lat_b, L0_xattn_ln_ctx_g, L0_xattn_ln_ctx_b, L0_xattn_Wq, L0_xattn_Wkv, L0_xattn_Wo, L0_xattn_bo)
    x = x + _L0_ffn_ref(_layernorm(x, axis=-1), L0_ffn_in_proj_w, L0_ffn_in_proj_b, L0_ffn_out_w, L0_ffn_out_b, L0_ffn_gate_w, L0_ffn_gate_b, L0_ffn_w1, L0_ffn_b1, L0_ffn_w2, L0_ffn_b2, L0_ffn_ln1_g, L0_ffn_ln1_b, L0_ffn_ln2_g, L0_ffn_ln2_b)
    x = x + _L1_attn_ref(_layernorm(x, axis=-1), L1_attn_compare_left, L1_attn_compare_right, L1_attn_threshold, L1_attn_gate_bias)
    x = x + _L1_xattn_ref(_layernorm(x, axis=-1), ctx_1024, ctx_1024, mask_Bx1x1xS2_bk0, L1_xattn_Wq, L1_xattn_Wk, L1_xattn_Wv, L1_xattn_Wo, L1_xattn_rel_emb)
    x = x + _L1_ffn_ref(_layernorm(x, axis=-1), L1_ffn_w1, L1_ffn_b1, L1_ffn_w2, L1_ffn_b2)
    return x

_drawn_inputs = setup_inputs


def setup_inputs(seed=0):
    import zlib

    import numpy as np

    out = dict(_drawn_inputs(seed))
    spreads = {'L0_attn_qkv_b': (0.0, 0.493),
     'L0_attn_qn_scale': (1.0, 0.6),
     'L0_attn_qn_bias': (0.0, 0.341),
     'L0_attn_kn_scale': (1.0, 0.6),
     'L0_attn_kn_bias': (0.0, 0.573),
     'L0_attn_proj_b': (0.0, 0.1),
     'L0_xattn_ln_lat_g': (1.0, 0.6),
     'L0_xattn_ln_lat_b': (0.0, 0.452),
     'L0_xattn_ln_ctx_g': (1.0, 0.2),
     'L0_xattn_ln_ctx_b': (0.0, 0.1),
     'L0_xattn_bo': (0.0, 0.1),
     'L0_ffn_in_proj_b': (0.0, 0.445),
     'L0_ffn_out_b': (0.0, 0.1),
     'L0_ffn_gate_b': (0.0, 0.269),
     'L0_ffn_b1': (0.0, 0.614),
     'L0_ffn_b2': (0.0, 0.1),
     'L0_ffn_ln1_g': (1.0, 0.2),
     'L0_ffn_ln1_b': (0.0, 0.1),
     'L0_ffn_ln2_g': (1.0, 0.2),
     'L0_ffn_ln2_b': (0.0, 0.1)}
    factors = {'L0_xattn_cos': 3.85,
     'L0_xattn_sin': 3.82,
     'L0_ffn_in_proj_w': 4.916,
     'L0_ffn_out_w': 3.333,
     'L0_ffn_w1': 2.734,
     'L1_xattn_rel_emb': 8.0,
     'L1_ffn_b2': 3.028}
    for name, (base, spread) in spreads.items():
        noise = np.random.default_rng([zlib.crc32(name.encode()), seed]).standard_normal(out[name].shape)
        drawn = base * np.exp(spread * noise) if base else spread * noise
        out[name] = jnp.asarray(drawn.astype(out[name].dtype))
    for name, factor in factors.items():
        out[name] = (out[name] * factor).astype(out[name].dtype)
    return out
```

```python
import math
from contextlib import ExitStack

import numpy as np

import concourse.bass as bass
from concourse import mybir

F32 = mybir.dt.float32
BF16 = mybir.dt.bfloat16
U8 = mybir.dt.uint8
ALU = mybir.AluOpType
ACT = mybir.ActivationFunctionType
AX = mybir.AxisListType

LAST_STAGE = 6

P = 128
B, S = 8, 256
T = B * S
NT = T // P
BLK = 512
NB = T // BLK
SC = 512
HID = 512
NJ = HID // P
LN_EPS = 1e-5


class Steps:

    def __init__(self, sem, names, ahead=0):
        self.sem, self.names, self.ahead = sem, list(names), ahead
        assert len(set(self.names)) == len(self.names)
        self.next = 0

    def at(self, name, t=0):
        return (t + self.ahead) * len(self.names) + self.names.index(name) + 1

    def tick(self, name):
        assert self.names[self.next % len(self.names)] == name, (name, self.names[self.next % len(self.names)])
        self.next += 1
        return 1


def bcast(stat, n, width=P):
    return stat.unsqueeze(2).to_broadcast([P, n, width])


def rows(flat, n, width=P):
    return flat.rearrange("p (n d) -> p n d", n=n)


def banks(ps, a, b):
    return ps[:, a:b, :].rearrange("p a b -> p (a b)")


LN_VECTOR = ["sum", "mean", "centred", "square", "squares", "variance", "rstd", "normal"]


def layernorm_vector(dve, vec, root, src, dst, sq, st, n):
    at = vec.at
    dve.tensor_reduce(st[:, 0, :], src, AX.X, ALU.add).then_inc(vec.sem, vec.tick("sum"))
    dve.wait_ge(vec.sem, at("sum"))
    dve.tensor_scalar(st[:, 1, :], st[:, 0, :], 1.0 / P, None, ALU.mult).then_inc(vec.sem, vec.tick("mean"))
    dve.wait_ge(vec.sem, at("mean"))
    dve.tensor_tensor(dst, src, bcast(st[:, 1, :], n), ALU.subtract).then_inc(vec.sem, vec.tick("centred"))
    dve.wait_ge(vec.sem, at("centred"))
    dve.tensor_tensor(sq, dst, dst, ALU.mult).then_inc(vec.sem, vec.tick("square"))
    dve.wait_ge(vec.sem, at("square"))
    dve.tensor_reduce(st[:, 2, :], sq, AX.X, ALU.add).then_inc(vec.sem, vec.tick("squares"))
    dve.wait_ge(vec.sem, at("squares"))
    dve.tensor_scalar(st[:, 2, :], st[:, 2, :], 1.0 / P, LN_EPS, ALU.mult, ALU.add) \
       .then_inc(vec.sem, vec.tick("variance"))
    dve.wait_ge(root.sem, root.at("root"))
    dve.reciprocal(st[:, 3, :], st[:, 3, :]).then_inc(vec.sem, vec.tick("rstd"))
    dve.wait_ge(vec.sem, at("rstd"))
    dve.tensor_tensor(dst, dst, bcast(st[:, 3, :], n), ALU.mult).then_inc(vec.sem, vec.tick("normal"))


def layernorm_root(act, vec, root, st):
    act.wait_ge(vec.sem, vec.at("variance"))
    act.activation(st[:, 3, :], st[:, 2, :], ACT.Sqrt).then_inc(root.sem, root.tick("root"))


class Stage:

    def __init__(self, nc, name):
        self.nc, self.name, self.stack = nc, name, ExitStack()

    def __enter__(self):
        return self

    def __exit__(self, *failed):
        return self.stack.__exit__(*failed)

    def sb(self, name, shape, dt=F32):
        return self.stack.enter_context(self.nc.sbuf_tensor(f"{self.name}_{name}", shape, dt))

    def steps(self, name, names, ahead=0):
        return Steps(self.stack.enter_context(self.nc.semaphore(f"{self.name}_{name}")), names, ahead)

    def block(self):
        return self.stack.enter_context(self.nc.Block())



NS_A, NS_B, NS_C = 3.4445, -4.775, 2.0315
NS_ITERS = 5
TTT_STEPS = 2
LR = 0.1
NS_GUARD = 1e-7 * T * P / 2


def stage_fast_weights(nc, g, a):
    with Stage(nc, "fw") as st:
        w_qkv = st.sb("w_qkv", [P, 3 * P])
        b_qk = st.sb("b_qk", [P, 2])
        b_v = st.sb("b_v", [P, P])
        b_o = st.sb("b_o", [P, P])
        w_o = st.sb("w_o", [P, P])
        head8 = st.sb("head8", [8, 4])
        hd = st.sb("hd", [P, 4])
        gate = st.sb("gate", [P, HID])
        val = st.sb("val", [P, HID])
        proj = st.sb("proj", [P, NJ, P])
        projT = st.sb("projT", [P, HID])
        nrm = st.sb("nrm", [P, NT, P])
        nT = st.sb("nT", [P, T])
        sq = st.sb("sq", [P, T])
        stat = st.sb("stat", [P, 4, NT])
        qT = st.sb("qT", [P, T])
        kk = st.sb("kk", [P, NT, 2, P])
        v = st.sb("v", [P, NT, P])
        qn = st.sb("qn", [P, T])
        kn = st.sb("kn", [P, T])
        kT_cur = st.sb("kT_cur", [P, P])
        k_cur = st.sb("k_cur", [P, P])
        sg = st.sb("sg", [P, 2, HID])
        sw = st.sb("sw", [P, 2, HID])
        h = st.sb("h", [P, 2, HID])
        vs = st.sb("vs", [P, 2, HID])
        u = st.sb("u", [P, 2, HID])
        e = st.sb("e", [P, 2, HID])
        dV = st.sb("dV", [P, 2, HID])
        dG = st.sb("dG", [P, 2, HID])
        hT = st.sb("hT", [P, 2, HID])
        dp = st.sb("dp", [P, 2, P])
        dpT = st.sb("dpT", [P, 2, P])
        X = st.sb("X", [P, 3, HID])
        XT = st.sb("XT", [P, 3, HID])
        Am = st.sb("Am", [P, 3, P])
        bA = st.sb("bA", [P, 3, P])
        Bm = st.sb("Bm", [P, 3, P])
        aI = st.sb("aI", [P, P])
        fro = st.sb("fro", [P, 3])
        frn = st.sb("frn", [P, 3])
        wo2 = st.sb("wo2", [P, NJ, P])
        fh = st.sb("fh", [P, NJ, BLK])
        fs = st.sb("fs", [P, 2, BLK])
        ps, x = g.ps, g.x
        ident, bd8, rep8, ones = g.ident, g.bd8, g.rep8, g.ones

        load = st.steps("load", [f"{i}" for i in range(256)])
        pre_v = st.steps("pre_v", LN_VECTOR + ["hd", "zeroed", "aI", "nT1", "nT3", "kT_raw", "k_sq", "k_guard", "k_inv", "k_unit",
                                               "kT", "v", "q_guard", "q_inv", "q_unit", "qT", "x_bias", "projT"])
        root = st.steps("root", ["root"])
        pre_a = st.steps("pre_a", ["nT0", "nT2", "qT_raw", "q_sq", "k_norm", "q_norm", "k_tok"])
        pre_p = st.steps("pre_p", ["hd", "nT0", "nT1", "nT2", "nT3", "k", "q", "k_sq", "q_sq", "v", "k_tok", "projT"])
        names = lambda *xs: [f"{n}{s}" for s in range(2) for n in xs]
        ttt_p = st.steps("ttt_p", names("gv", "grads", "hT", "pred", "dpT", "dh"), ahead=1)
        ttt_a = st.steps("ttt_a", names("sg", "vs", "hT", "dpT"), ahead=1)
        ttt_v = st.steps("ttt_v", names("sw", "h", "u", "ds", "dp", "dV", "dG"), ahead=1)
        ttt_g = st.steps("ttt_g", names("kT_cur", "k_cur", "e"), ahead=1)
        open_p = st.steps("open_p", ["opened", "last", "fro", "XT"])
        open_a = st.steps("open_a", ["fro0", "fro1", "fro2", "root", "XT0", "XT1", "XT2"])
        open_v = st.steps("open_v", ["guard", "inv", "X0", "X1", "X2"])
        ns_p = st.steps("ns_p", [f"{n}{m}" for n in ("A", "A2", "X") for m in range(3)], ahead=1)
        ns_a = st.steps("ns_a", [f"{n}{m}" for n in ("A", "X") for m in range(3)], ahead=1)
        ns_v = st.steps("ns_v", [f"{n}{m}" for n in ("bA", "B", "XT") for m in range(3)], ahead=1)
        upd_v = st.steps("upd_v", ["gate", "val", "projT", "proj"], ahead=1)
        fin_p = st.steps("fin_p", ["wo2"])
        fin_v = st.steps("fin_v", ["wo2"])
        ask_p = st.steps("ask_p", ["gv0", "gv1", "gv2", "gv3", "o"], ahead=1)
        ask_a = st.steps("ask_a", ["s0", "s1", "s2", "s3"], ahead=1)
        ask_v = st.steps("ask_v", [f"{n}{j}" for j in range(4) for n in ("sw", "h")] + ["x"], ahead=1)
        zero = st.sb("zero", [P, P])
        made_g = st.steps("made_g", ["zero"])
        zero_v = st.steps("zero_v", ["dp"])
        zero_g = st.steps("zero_g", ["k"])

        block = st.block()

        @block.sync
        def _(sp):
            for dst, src in (
                (w_qkv[:], a["L0_attn_qkv_w"]), (b_qk[:, 0:1], a["L0_attn_qkv_b"][0:P].unsqueeze(1)),
                (b_qk[:, 1:2], a["L0_attn_qkv_b"][P:2 * P].unsqueeze(1)),
                (b_v[:], a["L0_attn_qkv_b"][2 * P:3 * P].partition_broadcast(P)),
                (head8[:, 0:1], a["L0_attn_qn_scale"].unsqueeze(1)), (head8[:, 1:2], a["L0_attn_qn_bias"].unsqueeze(1)),
                (head8[:, 2:3], a["L0_attn_kn_scale"].unsqueeze(1)), (head8[:, 3:4], a["L0_attn_kn_bias"].unsqueeze(1)),
                (gate[:], a["L0_attn_ttt_gate"]), (val[:], a["L0_attn_ttt_val"]),
                (proj[:], a["L0_attn_ttt_proj"].rearrange("(j p) d -> p j d", p=P)),
                (w_o[:], a["L0_attn_proj_w"]), (b_o[:], a["L0_attn_proj_b"].partition_broadcast(P)),
            ):
                sp.dma_start(dst, src).then_inc(load.sem, 16)

        N_LOADS = 13

        @block.gpsimd
        def _(pool):
            pool.memset(zero[:], 0.0).then_inc(made_g.sem, made_g.tick("zero"))
            pool.wait_ge(made_g.sem, made_g.at("zero"))
            pool.sem_inc(ttt_g.sem, ttt_g.at("e1", -1))
            pool.wait_ge(pre_v.sem, pre_v.at("kT"))
            pool.wait_ge(pre_a.sem, pre_a.at("k_tok"))
            with pool.Fori(0, TTT_STEPS) as step:
                pool.wait_ge(upd_v.sem, upd_v.at("proj", step - 1))
                pool.tensor_tensor(k_cur[:], zero[:], zero[:], ALU.add).then_inc(zero_g.sem, zero_g.tick("k"))
                with pool.Fori(0, NT // 2) as i:
                    t = step * (NT // 2) + i
                    for s in range(2):
                        pool.wait_ge(ttt_p.sem, ttt_p.at("gv1", t - 1) if s == 0 else ttt_p.at("gv0", t))
                        pool.tensor_copy(kT_cur[:].unsqueeze(1), kk[:, bass.ds(2 * i + s, 1), 0, :]) \
                            .then_inc(ttt_g.sem, ttt_g.tick(f"kT_cur{s}"))
                        pool.wait_ge(ttt_p.sem, ttt_p.at(f"grads{s}", t))
                        pool.tensor_copy(k_cur[:].unsqueeze(1), kk[:, bass.ds(2 * i + s, 1), 1, :]) \
                            .then_inc(ttt_g.sem, ttt_g.tick(f"k_cur{s}"))
                        pool.wait_ge(ttt_v.sem, ttt_v.at(f"ds{s}", t))
                        pool.wait_ge(ttt_a.sem, ttt_a.at(f"vs{s}", t))
                        pool.tensor_tensor(e[:, s, :], u[:, s, :], vs[:, s, :], ALU.mult) \
                            .then_inc(ttt_g.sem, ttt_g.tick(f"e{s}"))

        @block.scalar
        def _(act):
            layernorm_root(act, pre_v, root, stat)
            for b in (0, 2):
                act.wait_ge(pre_p.sem, pre_p.at(f"nT{b}"))
                act.activation(nT[:, bass.ts(b, BLK)], ps[:, b, :], ACT.Copy).then_inc(pre_a.sem, pre_a.tick(f"nT{b}"))
            act.wait_ge(pre_p.sem, pre_p.at("q"))
            act.wait_ge(load.sem, 16 * N_LOADS)
            act.activation(qT[:], banks(ps, 4, 8), ACT.Identity, bias=b_qk[:, 0:1]) \
               .then_inc(pre_a.sem, pre_a.tick("qT_raw"))
            act.wait_ge(pre_a.sem, pre_a.at("qT_raw"))
            act.wait_ge(pre_v.sem, pre_v.at("normal"))
            act.activation(sq[:], qT[:], ACT.Square).then_inc(pre_a.sem, pre_a.tick("q_sq"))
            act.wait_ge(pre_p.sem, pre_p.at("k_sq"))
            act.activation(kn[:], banks(ps, 0, 4), ACT.Sqrt) \
               .then_inc(pre_a.sem, pre_a.tick("k_norm"))
            act.wait_ge(pre_p.sem, pre_p.at("q_sq"))
            act.activation(qn[:], banks(ps, 4, 8), ACT.Sqrt) \
               .then_inc(pre_a.sem, pre_a.tick("q_norm"))
            act.wait_ge(pre_p.sem, pre_p.at("k_tok"))
            act.activation(kk[:, :, 1, :], rows(banks(ps, 4, 8), NT), ACT.Copy) \
               .then_inc(pre_a.sem, pre_a.tick("k_tok"))
            act.sem_inc(ttt_a.sem, ttt_a.at("dpT1", -1))
            act.sem_inc(ns_a.sem, ns_a.at("X2", -1))
            act.sem_inc(ask_a.sem, ask_a.at("s3", -1))
            with act.Fori(0, TTT_STEPS) as step:
                with act.Fori(0, NT // 2) as i:
                    t = step * (NT // 2) + i
                    for s in range(2):
                        act.wait_ge(ttt_p.sem, ttt_p.at(f"gv{s}", t))
                        act.wait_ge(ttt_v.sem, ttt_v.at(f"u{s}", t - 1))
                        act.activation(sg[:, s, :], ps[:, 0, :], ACT.Sigmoid).then_inc(ttt_a.sem, ttt_a.tick(f"sg{s}"))
                        act.wait_ge(ttt_g.sem, ttt_g.at(f"e{s}", t - 1))
                        act.activation(vs[:, s, :], ps[:, 1, :], ACT.Copy).then_inc(ttt_a.sem, ttt_a.tick(f"vs{s}"))
                        act.wait_ge(ttt_p.sem, ttt_p.at(f"hT{s}", t))
                        act.activation(hT[:, s, :], ps[:, 2, :], ACT.Copy).then_inc(ttt_a.sem, ttt_a.tick(f"hT{s}"))
                        act.wait_ge(ttt_p.sem, ttt_p.at(f"dpT{s}", t))
                        act.activation(dpT[:, s, :], ps[:, 3, 0:P], ACT.Copy).then_inc(ttt_a.sem, ttt_a.tick(f"dpT{s}"))
                act.wait_ge(open_p.sem, open_p.at("last", step))
                for m in range(3):
                    act.activation(XT[:, m, :], ps[:, 5 + m, :], ACT.Square, accum_out=fro[:, m:m + 1]) \
                       .then_inc(open_a.sem, open_a.tick(f"fro{m}"))
                act.wait_ge(open_p.sem, open_p.at("fro", step))
                act.activation(frn[:], ps[:, 0, 0:3], ACT.Sqrt).then_inc(open_a.sem, open_a.tick("root"))
                act.wait_ge(open_p.sem, open_p.at("XT", step))
                for m in range(3):
                    act.activation(XT[:, m, :], ps[:, 1 + m, :], ACT.Copy).then_inc(open_a.sem, open_a.tick(f"XT{m}"))
                with act.Fori(0, NS_ITERS) as it:
                    n = step * NS_ITERS + it
                    for m in range(3):
                        act.wait_ge(ns_p.sem, ns_p.at(f"A{m}", n))
                        act.activation(Am[:, m, :], ps[:, m, 0:P], ACT.Copy).then_inc(ns_a.sem, ns_a.tick(f"A{m}"))
                    for m in range(3):
                        act.wait_ge(ns_p.sem, ns_p.at(f"X{m}", n))
                        act.activation(X[:, m, :], ps[:, m, :], ACT.Copy).then_inc(ns_a.sem, ns_a.tick(f"X{m}"))
            with act.Fori(0, NB) as blk:
                for j in range(NJ):
                    act.wait_ge(ask_p.sem, ask_p.at(f"gv{j}", blk))
                    act.wait_ge(ask_v.sem, ask_v.at(f"sw{(j - 2) % 4}", blk - (j < 2)))
                    act.activation(fs[:, j % 2, :], ps[:, 2 * (j % 2), :], ACT.Sigmoid) \
                       .then_inc(ask_a.sem, ask_a.tick(f"s{j}"))

        @block.vector
        def _(dve):
            layernorm_vector(dve, pre_v, root, x[:], nrm[:], rows(sq[:], NT), stat[:], NT)
            dve.wait_ge(pre_p.sem, pre_p.at("hd"))
            dve.tensor_copy(hd[:], ps[:, 7, 0:4]).then_inc(pre_v.sem, pre_v.tick("hd"))
            for buffer in (h, dV, dG):
                zeroed = dve.memset(buffer[:, 1, :], 0.0)
            zeroed.then_inc(pre_v.sem, pre_v.tick("zeroed"))
            dve.tensor_scalar(aI[:], ident, NS_A, None, ALU.mult).then_inc(pre_v.sem, pre_v.tick("aI"))
            for b in (1, 3):
                dve.wait_ge(pre_p.sem, pre_p.at(f"nT{b}"))
                dve.tensor_copy(nT[:, bass.ts(b, BLK)], ps[:, b, :]).then_inc(pre_v.sem, pre_v.tick(f"nT{b}"))
            kT = kk[:, :, 0, :]
            kn3 = rows(kn[:], NT)
            k_ps = rows(banks(ps, 0, 4), NT)
            dve.wait_ge(pre_p.sem, pre_p.at("k"))
            dve.wait_ge(load.sem, 16 * N_LOADS)
            dve.tensor_scalar(kT, k_ps, b_qk[:, 1:2], None, ALU.add).then_inc(pre_v.sem, pre_v.tick("kT_raw"))
            dve.wait_ge(pre_v.sem, pre_v.at("kT_raw"))
            dve.tensor_tensor(kn3, kT, kT, ALU.mult).then_inc(pre_v.sem, pre_v.tick("k_sq"))
            dve.wait_ge(pre_a.sem, pre_a.at("k_norm"))
            dve.tensor_scalar(kn[:], kn[:], 1e-6, None, ALU.add).then_inc(pre_v.sem, pre_v.tick("k_guard"))
            dve.wait_ge(pre_v.sem, pre_v.at("k_guard"))
            dve.reciprocal(kn[:], kn[:]).then_inc(pre_v.sem, pre_v.tick("k_inv"))
            dve.wait_ge(pre_v.sem, pre_v.at("k_inv"))
            dve.tensor_tensor(kT, kT, kn3, ALU.mult).then_inc(pre_v.sem, pre_v.tick("k_unit"))
            dve.wait_ge(pre_v.sem, pre_v.at("k_unit"))
            dve.tensor_scalar(kT, kT, hd[:, 2:3], hd[:, 3:4], ALU.mult, ALU.add) \
               .then_inc(pre_v.sem, pre_v.tick("kT"))
            dve.wait_ge(pre_p.sem, pre_p.at("v"))
            dve.tensor_tensor(v[:], k_ps, b_v[:].unsqueeze(1).to_broadcast([P, NT, P]), ALU.add) \
               .then_inc(pre_v.sem, pre_v.tick("v"))
            dve.wait_ge(pre_a.sem, pre_a.at("q_norm"))
            dve.tensor_scalar(qn[:], qn[:], 1e-6, None, ALU.add).then_inc(pre_v.sem, pre_v.tick("q_guard"))
            dve.wait_ge(pre_v.sem, pre_v.at("q_guard"))
            dve.reciprocal(qn[:], qn[:]).then_inc(pre_v.sem, pre_v.tick("q_inv"))
            dve.wait_ge(pre_v.sem, pre_v.at("q_inv"))
            dve.tensor_tensor(qT[:], qT[:], qn[:], ALU.mult).then_inc(pre_v.sem, pre_v.tick("q_unit"))
            dve.wait_ge(pre_v.sem, pre_v.at("q_unit"))
            dve.tensor_scalar(qT[:], qT[:], hd[:, 0:1], hd[:, 1:2], ALU.mult, ALU.add) \
               .then_inc(pre_v.sem, pre_v.tick("qT"))
            dve.tensor_tensor(x[:], x[:], b_o[:].unsqueeze(1).to_broadcast([P, NT, P]), ALU.add) \
               .then_inc(pre_v.sem, pre_v.tick("x_bias"))
            dve.wait_ge(pre_p.sem, pre_p.at("projT"))
            dve.tensor_copy(projT[:], ps[:, 0, :]).then_inc(pre_v.sem, pre_v.tick("projT"))
            dve.sem_inc(ttt_v.sem, ttt_v.at("dG1", -1))
            dve.sem_inc(ns_v.sem, ns_v.at("XT2", -1))
            dve.sem_inc(upd_v.sem, upd_v.at("proj", -1))
            dve.sem_inc(ask_v.sem, ask_v.at("x", -1))
            with dve.Fori(0, TTT_STEPS) as step:
                dve.memset(dp[:, 1, :], 0.0).then_inc(zero_v.sem, zero_v.tick("dp"))
                with dve.Fori(0, NT // 2) as i:
                    t = step * (NT // 2) + i
                    for s in range(2):
                        dve.wait_ge(ttt_a.sem, ttt_a.at(f"sg{s}", t))
                        dve.tensor_tensor(sw[:, s, :], ps[:, 0, :], sg[:, s, :], ALU.mult) \
                           .then_inc(ttt_v.sem, ttt_v.tick(f"sw{s}"))
                        dve.wait_ge(ttt_v.sem, ttt_v.at(f"sw{s}", t))
                        dve.wait_ge(ttt_a.sem, ttt_a.at(f"vs{s}", t))
                        dve.wait_ge(ttt_p.sem, ttt_p.at("grads1", t - 1) if s == 0 else ttt_p.at("grads0", t))
                        dve.tensor_tensor(h[:, s, :], sw[:, s, :], vs[:, s, :], ALU.mult) \
                           .then_inc(ttt_v.sem, ttt_v.tick(f"h{s}"))
                        dve.scalar_tensor_tensor(u[:, s, :], sw[:, s, :], 1.0, sg[:, s, :], ALU.subtract, ALU.mult) \
                           .then_inc(ttt_v.sem, ttt_v.tick(f"u{s}"))
                        dve.wait_ge(ttt_v.sem, ttt_v.at(f"u{s}", t))
                        dve.tensor_tensor(u[:, s, :], sw[:, s, :], u[:, s, :], ALU.subtract) \
                           .then_inc(ttt_v.sem, ttt_v.tick(f"ds{s}"))
                        dve.wait_ge(ttt_p.sem, ttt_p.at(f"pred{s}", t))
                        dve.tensor_tensor(dp[:, bass.ds(s, 1), :], ps[:, 3:4, 0:P], v[:, bass.ds(2 * i + s, 1), :],
                                          ALU.subtract).then_inc(ttt_v.sem, ttt_v.tick(f"dp{s}"))
                        dve.wait_ge(ttt_p.sem, ttt_p.at(f"dh{s}", t))
                        dve.tensor_tensor(dV[:, s, :], ps[:, 4, :], sw[:, s, :], ALU.mult) \
                           .then_inc(ttt_v.sem, ttt_v.tick(f"dV{s}"))
                        dve.wait_ge(ttt_g.sem, ttt_g.at(f"e{s}", t))
                        dve.tensor_tensor(dG[:, s, :], ps[:, 4, :], e[:, s, :], ALU.mult) \
                           .then_inc(ttt_v.sem, ttt_v.tick(f"dG{s}"))
                dve.wait_ge(open_a.sem, open_a.at("root", step))
                dve.tensor_scalar(frn[:], frn[:], NS_GUARD, None, ALU.add).then_inc(open_v.sem, open_v.tick("guard"))
                dve.wait_ge(open_v.sem, open_v.at("guard", step))
                dve.reciprocal(frn[:], frn[:]).then_inc(open_v.sem, open_v.tick("inv"))
                dve.wait_ge(open_v.sem, open_v.at("inv", step))
                for m in range(3):
                    dve.tensor_scalar(X[:, m, :], ps[:, 5 + m, :], frn[:, m:m + 1], None, ALU.mult) \
                       .then_inc(open_v.sem, open_v.tick(f"X{m}"))
                with dve.Fori(0, NS_ITERS) as it:
                    n = step * NS_ITERS + it
                    for m in range(3):
                        dve.wait_ge(ns_a.sem, ns_a.at(f"A{m}", n))
                        dve.scalar_tensor_tensor(bA[:, m, :], Am[:, m, :], NS_B, aI[:], ALU.mult, ALU.add) \
                           .then_inc(ns_v.sem, ns_v.tick(f"bA{m}"))
                    for m in range(3):
                        dve.wait_ge(ns_p.sem, ns_p.at(f"A2{m}", n))
                        dve.wait_ge(ns_v.sem, ns_v.at(f"bA{m}", n))
                        dve.scalar_tensor_tensor(Bm[:, m, :], ps[:, 3 + m, 0:P], NS_C, bA[:, m, :], ALU.mult, ALU.add) \
                           .then_inc(ns_v.sem, ns_v.tick(f"B{m}"))
                    for m in range(3):
                        dve.wait_ge(ns_p.sem, ns_p.at(f"X{m}", n))
                        dve.tensor_copy(XT[:, m, :], ps[:, 3 + m, :]).then_inc(ns_v.sem, ns_v.tick(f"XT{m}"))
                dve.wait_ge(ns_a.sem, ns_a.at("X2", step * NS_ITERS + NS_ITERS - 1))
                dve.wait_ge(ns_v.sem, ns_v.at("XT2", step * NS_ITERS + NS_ITERS - 1))
                for name, theta, d in (("gate", gate[:], X[:, 0, :]), ("val", val[:], X[:, 1, :]),
                                       ("projT", projT[:], X[:, 2, :]), ("proj", proj[:].rearrange("p j d -> p (j d)"), XT[:, 2, :])):
                    dve.scalar_tensor_tensor(theta, d, -LR, theta, ALU.mult, ALU.add) \
                       .then_inc(upd_v.sem, upd_v.tick(name))
            dve.wait_ge(fin_p.sem, fin_p.at("wo2"))
            dve.tensor_copy(wo2[:].rearrange("p j d -> p (j d)"), ps[:, 0, :]).then_inc(fin_v.sem, fin_v.tick("wo2"))
            with dve.Fori(0, NB) as blk:
                for j in range(NJ):
                    b = 2 * (j % 2)
                    dve.wait_ge(ask_a.sem, ask_a.at(f"s{j}", blk))
                    if j == 0:
                        dve.wait_ge(ask_p.sem, ask_p.at("o", blk - 1))
                    dve.tensor_tensor(fh[:, j, :], ps[:, b, :], fs[:, j % 2, :], ALU.mult) \
                       .then_inc(ask_v.sem, ask_v.tick(f"sw{j}"))
                    dve.wait_ge(ask_v.sem, ask_v.at(f"sw{j}", blk))
                    dve.tensor_tensor(fh[:, j, :], ps[:, b + 1, :], fh[:, j, :], ALU.mult) \
                       .then_inc(ask_v.sem, ask_v.tick(f"h{j}"))
                dve.wait_ge(ask_p.sem, ask_p.at("o", blk))
                xb = x[:, bass.ds(4 * blk, 4), :]
                dve.tensor_tensor(xb, rows(ps[:, 4, :], 4), xb, ALU.add).then_inc(ask_v.sem, ask_v.tick("x"))

        @block.tensor
        def _(pe):
            pe.wait_ge(load.sem, 16 * N_LOADS)
            pe.matmul(ps[:, 7, 0:4], rep8, head8[:], start=True, stop=True).then_inc(pre_p.sem, pre_p.tick("hd"))
            pe.wait_ge(pre_v.sem, pre_v.at("normal"))
            for b in range(NB):
                for i in range(4):
                    mm = pe.transpose(ps[:, b, bass.ts(i, P)], nrm[:, 4 * b + i, :], ident)
                mm.then_inc(pre_p.sem, pre_p.tick(f"nT{b}"))
            pe.wait_ge(pre_a.sem, pre_a.at("nT2"))
            pe.wait_ge(pre_v.sem, pre_v.at("nT3"))
            for name, part, b0 in (("k", 1, 0), ("q", 0, 4)):
                for b in range(NB):
                    mm = pe.matmul(ps[:, b0 + b, :], w_qkv[:, bass.ts(part, P)], nT[:, bass.ts(b, BLK)], start=True, stop=True)
                mm.then_inc(pre_p.sem, pre_p.tick(name))
            pe.wait_ge(pre_v.sem, pre_v.at("k_sq"))
            for b in range(NB):
                mm = pe.matmul(ps[:, b, :], bd8, kn[:, bass.ts(b, BLK)], start=True, stop=True)
            mm.then_inc(pre_p.sem, pre_p.tick("k_sq"))
            pe.wait_ge(pre_a.sem, pre_a.at("q_sq"))
            for b in range(NB):
                mm = pe.matmul(ps[:, 4 + b, :], bd8, sq[:, bass.ts(b, BLK)], start=True, stop=True)
            mm.then_inc(pre_p.sem, pre_p.tick("q_sq"))
            pe.wait_ge(pre_a.sem, pre_a.at("k_norm"))
            for t in range(NT):
                mm = pe.matmul(ps[:, t // 4, bass.ts(t % 4, P)], nT[:, bass.ts(t, P)], w_qkv[:, 2 * P:3 * P],
                               start=True, stop=True)
            mm.then_inc(pre_p.sem, pre_p.tick("v"))
            pe.wait_ge(pre_v.sem, pre_v.at("kT"))
            pe.wait_ge(pre_a.sem, pre_a.at("q_norm"))
            for t in range(NT):
                mm = pe.transpose(ps[:, 4 + t // 4, bass.ts(t % 4, P)], kk[:, t, 0, :], ident)
            mm.then_inc(pre_p.sem, pre_p.tick("k_tok"))
            pe.wait_ge(pre_v.sem, pre_v.at("v"))
            for j in range(NJ):
                mm = pe.transpose(ps[:, 0, bass.ts(j, P)], proj[:, j, :], ident)
            mm.then_inc(pre_p.sem, pre_p.tick("projT"))
            pe.wait_ge(pre_a.sem, pre_a.at("k_tok"))
            pe.sem_inc(ttt_p.sem, ttt_p.at("dh1", -1))
            pe.sem_inc(ns_p.sem, ns_p.at("X2", -1))
            pe.sem_inc(ask_p.sem, ask_p.at("o", -1))
            pe.wait_ge(pre_v.sem, pre_v.at("projT"))

            def gradients(s, start=False, stop=False):
                pe.matmul(ps[:, 7, :], dp[:, s, :], h[:, s, :], start=start, stop=stop, skip_group_check=True)
                pe.matmul(ps[:, 6, :], k_cur[:], dV[:, s, :], start=start, stop=stop, skip_group_check=True)
                return pe.matmul(ps[:, 5, :], k_cur[:], dG[:, s, :], start=start, stop=stop, skip_group_check=True)

            with pe.Fori(0, TTT_STEPS) as step:
                pe.wait_ge(upd_v.sem, upd_v.at("proj", step - 1))
                pe.wait_ge(zero_v.sem, zero_v.at("dp", step))
                pe.wait_ge(zero_g.sem, zero_g.at("k", step))
                gradients(1, start=True).then_inc(open_p.sem, open_p.tick("opened"))
                with pe.Fori(0, NT // 2) as i:
                    t = step * (NT // 2) + i
                    for s in range(2):
                        before = lambda name: f"{name}{1 - s}"
                        t_before = t - 1 if s == 0 else t
                        pe.wait_ge(ttt_g.sem, ttt_g.at(f"kT_cur{s}", t))
                        pe.wait_ge(ttt_v.sem, ttt_v.at(before("sw"), t_before))
                        pe.matmul(ps[:, 0, :], kT_cur[:], gate[:], start=True, stop=True)
                        pe.wait_ge(ttt_a.sem, ttt_a.at(before("vs"), t_before))
                        pe.matmul(ps[:, 1, :], kT_cur[:], val[:], start=True, stop=True) \
                          .then_inc(ttt_p.sem, ttt_p.tick(f"gv{s}"))
                        pe.wait_ge(ttt_v.sem, ttt_v.at(before("dG"), t_before))
                        pe.wait_ge(ttt_g.sem, ttt_g.at(before("k_cur"), t_before))
                        gradients(1 - s).then_inc(ttt_p.sem, ttt_p.tick(f"grads{s}"))
                        pe.wait_ge(ttt_v.sem, ttt_v.at(f"h{s}", t))
                        pe.wait_ge(ttt_a.sem, ttt_a.at(before("hT"), t_before))
                        for j in range(NJ):
                            mm = pe.transpose(ps[:, 2, bass.ts(j, P)], h[:, s, bass.ts(j, P)], ident)
                        mm.then_inc(ttt_p.sem, ttt_p.tick(f"hT{s}"))
                        pe.wait_ge(ttt_a.sem, ttt_a.at(f"hT{s}", t))
                        pe.wait_ge(ttt_a.sem, ttt_a.at(before("dpT"), t_before))
                        for j in range(NJ):
                            mm = pe.matmul(ps[:, 3, 0:P], hT[:, s, bass.ts(j, P)], proj[:, j, :],
                                           start=(j == 0), stop=(j == NJ - 1))
                        mm.then_inc(ttt_p.sem, ttt_p.tick(f"pred{s}"))
                        pe.wait_ge(ttt_v.sem, ttt_v.at(f"dp{s}", t))
                        pe.transpose(ps[:, 3, 0:P], dp[:, s, :], ident).then_inc(ttt_p.sem, ttt_p.tick(f"dpT{s}"))
                        pe.wait_ge(ttt_a.sem, ttt_a.at(f"dpT{s}", t))
                        pe.wait_ge(ttt_v.sem, ttt_v.at(before("dG"), t_before))
                        pe.matmul(ps[:, 4, :], dpT[:, s, :], projT[:], start=True, stop=True) \
                          .then_inc(ttt_p.sem, ttt_p.tick(f"dh{s}"))
                last = step * (NT // 2) + NT // 2 - 1
                pe.wait_ge(ttt_v.sem, ttt_v.at("dG1", last))
                pe.wait_ge(ttt_g.sem, ttt_g.at("k_cur1", last))
                gradients(1, stop=True).then_inc(open_p.sem, open_p.tick("last"))
                pe.wait_ge(open_a.sem, open_a.at("fro2", step))
                pe.matmul(ps[:, 0, 0:3], ones, fro[:], start=True, stop=True).then_inc(open_p.sem, open_p.tick("fro"))
                pe.wait_ge(open_v.sem, open_v.at("X2", step))
                for m in range(3):
                    for j in range(NJ):
                        mm = pe.transpose(ps[:, 1 + m, bass.ts(j, P)], X[:, m, bass.ts(j, P)], ident)
                mm.then_inc(open_p.sem, open_p.tick("XT"))
                with pe.Fori(0, NS_ITERS) as it:
                    n = step * NS_ITERS + it
                    pe.wait_ge(open_a.sem, open_a.at("XT2", step))
                    for m in range(3):
                        pe.wait_ge(ns_v.sem, ns_v.at(f"XT{m}", n - 1))
                        pe.wait_ge(ns_a.sem, ns_a.at(f"X{m}", n - 1))
                        for j in range(NJ):
                            mm = pe.matmul(ps[:, m, 0:P], XT[:, m, bass.ts(j, P)], XT[:, m, bass.ts(j, P)],
                                           start=(j == 0), stop=(j == NJ - 1))
                        mm.then_inc(ns_p.sem, ns_p.tick(f"A{m}"))
                    for m in range(3):
                        pe.wait_ge(ns_a.sem, ns_a.at(f"A{m}", n))
                        pe.matmul(ps[:, 3 + m, 0:P], Am[:, m, :], Am[:, m, :], start=True, stop=True) \
                          .then_inc(ns_p.sem, ns_p.tick(f"A2{m}"))
                    for m in range(3):
                        pe.wait_ge(ns_v.sem, ns_v.at(f"B{m}", n))
                        pe.matmul(ps[:, m, :], Bm[:, m, :], X[:, m, :], start=True, stop=True)
                        for j in range(NJ):
                            mm = pe.matmul(ps[:, 3 + m, bass.ts(j, P)], X[:, m, bass.ts(j, P)], Bm[:, m, :],
                                           start=True, stop=True)
                        mm.then_inc(ns_p.sem, ns_p.tick(f"X{m}"))
            pe.wait_ge(upd_v.sem, upd_v.at("proj", TTT_STEPS - 1))
            for j in range(NJ):
                mm = pe.matmul(ps[:, 0, bass.ts(j, P)], projT[:, bass.ts(j, P)], w_o[:], start=True, stop=True)
            mm.then_inc(fin_p.sem, fin_p.tick("wo2"))
            pe.wait_ge(fin_v.sem, fin_v.at("wo2"))
            pe.wait_ge(pre_v.sem, pre_v.at("qT"))
            with pe.Fori(0, NB) as blk:
                for j in range(NJ):
                    b = 2 * (j % 2)
                    pe.wait_ge(ask_v.sem, ask_v.at(f"h{(j - 2) % 4}", blk - (j < 2)))
                    for w, bank in ((gate, b), (val, b + 1)):
                        mm = pe.matmul(ps[:, bank, :], w[:, bass.ts(j, P)], qT[:, bass.ds(blk * BLK, BLK)],
                                       start=True, stop=True)
                    mm.then_inc(ask_p.sem, ask_p.tick(f"gv{j}"))
                pe.wait_ge(ask_v.sem, ask_v.at("h3", blk))
                pe.wait_ge(ask_v.sem, ask_v.at("x", blk - 1))
                for i in range(4):
                    for j in range(NJ):
                        mm = pe.matmul(ps[:, 4, bass.ts(i, P)], fh[:, j, bass.ts(i, P)], wo2[:, j, :],
                                       start=(j == 0), stop=(j == NJ - 1))
                mm.then_inc(ask_p.sem, ask_p.tick("o"))



XH, XD = 16, 64
INNER = XH * XD
NC = INNER // P
NK = SC // P
NCT = B * NK
CLIP = 11.0


def stage_cross_attention(nc, g, a):
    with Stage(nc, "xa") as st:
        wq = st.sb("wq", [P, INNER])
        wkv = st.sb("wkv", [P, 2 * INNER])
        wk_sw = st.sb("wk_sw", [P, INNER])
        wo = st.sb("wo", [P, NC, P])
        col = st.sb("col", [P, 4])
        b_o = st.sb("b_o", [P, P])
        turn = st.sb("turn", [P, 2, NK, 4, XD // 2])
        turnT = st.sb("turnT", [P, 2, SC])
        nrm = st.sb("nrm", [P, NT, P])
        cn = st.sb("cn", [P, NCT, P])
        latT = st.sb("latT", [P, T])
        ctxT = st.sb("ctxT", [P, B * SC])
        stat = st.sb("stat", [P, 4, NT])
        stat2 = st.sb("stat2", [P, 4, NT])
        statc = st.sb("statc", [P, 4, NCT])
        ctx_cur = st.sb("ctx_cur", [P, SC])
        qh = st.sb("qh", [P, NC, S])
        kh = st.sb("kh", [P, NC, SC])
        kc = st.sb("kc", [P, 2, SC])
        ks = st.sb("ks", [P, 2, SC])
        va = st.sb("va", [P, NK, XH, XD + 1])
        pt = st.sb("pt", [P, 2, NK, S])
        rec = st.sb("rec", [P, 2, 2])
        oh = st.sb("oh", [P, 2, NC, P])
        ohT = st.sb("ohT", [P, 2, NC, P])
        ps, x, ctx = g.ps, g.x, g.ctx
        ident = g.ident
        sq = cn

        load = st.steps("load", ["all"])
        N_LOADS = 17
        ln1_v, ln1_a = st.steps("ln1_v", LN_VECTOR), st.steps("ln1_a", ["root"])
        ln2_v, ln2_a = st.steps("ln2_v", LN_VECTOR), st.steps("ln2_a", ["root"])
        lnc_v, lnc_a = st.steps("lnc_v", LN_VECTOR), st.steps("lnc_a", ["root"])
        pre_v = st.steps("pre_v", ["x_bias", "ones", "cos", "sin", "ctx"])
        pre_a = st.steps("pre_a", ["lat", "ctx"])
        pre_g = st.steps("pre_g", ["sw0", "sw1", "sign"])
        pre_p = st.steps("pre_p", ["turn", "lat", "ctx0", "ctx1"])
        heads = lambda *xs: [f"{n}{h}" for h in range(XH) for n in xs]
        at_p = st.steps("at_p", ["q"] + [f"k{c}" for c in range(NC)] + [f"v{n}" for n in range(NK)] + ["S0"]
                        + [n for h in range(XH) for n in ([f"S{h + 1}"] if h + 1 < XH else []) + [f"O{h}"]]
                        + ["oT0", "oT1", "out"], ahead=1)
        at_a = st.steps("at_a", ["q"] + [f"v{n}" for n in range(NK)] + heads("E") + ["oT0"], ahead=1)
        at_v = st.steps("at_v", [f"{n}{c}" for c in range(NC) for n in ("kc", "ks")]
                        + [n for h in range(XH) for n in ([f"C{h}"] + ([f"R{h - 1}", f"N{h - 1}"] if h else []))]
                        + [f"R{XH - 1}", f"N{XH - 1}", "oT1", "x"], ahead=1)
        at_g = st.steps("at_g", ["ctx_cur"] + [f"k{c}" for c in range(NC)], ahead=1)

        block = st.block()

        @block.sync
        def _(sp):
            for dst, src in (
                (wq[:], a["L0_xattn_Wq"]), (wkv[:], a["L0_xattn_Wkv"]),
                (wo[:], a["L0_xattn_Wo"].rearrange("(c p) d -> p c d", p=P)),
                (col[:, 0:1], a["L0_xattn_ln_lat_g"].unsqueeze(1)), (col[:, 1:2], a["L0_xattn_ln_lat_b"].unsqueeze(1)),
                (col[:, 2:3], a["L0_xattn_ln_ctx_g"].unsqueeze(1)), (col[:, 3:4], a["L0_xattn_ln_ctx_b"].unsqueeze(1)),
                (b_o[:], a["L0_xattn_bo"].partition_broadcast(P)),
            ):
                sp.dma_start(dst, src).then_inc(load.sem, 16)
            for r in range(4):
                for i, name in enumerate(("L0_xattn_cos", "L0_xattn_sin")):
                    sp.dma_start(turn[:, i, :, r, :], a[name].rearrange("(n p) d -> p n d", p=P)).then_inc(load.sem, 16)
            sp.dma_start(g.ctx[:], a["ctx_1024"].rearrange("b (n p) d -> p (b n) d", p=P)).then_inc(load.sem, 16)
            sp.wait_ge(load.sem, 16 * (N_LOADS))

        @block.gpsimd
        def _(pool):
            pool.wait_ge(load.sem, 16 * (N_LOADS))
            wk4 = wkv[:, 0:INNER].rearrange("p (h two d) -> p h two d", two=2, d=XD // 2)
            sw4 = wk_sw[:].rearrange("p (h two d) -> p h two d", two=2, d=XD // 2)
            for i in range(2):
                pool.tensor_copy(sw4[:, :, i, :], wk4[:, :, 1 - i, :]).then_inc(pre_g.sem, pre_g.tick(f"sw{i}"))
            minus = turn[:, 1, :, 0:4:2, :]
            pool.tensor_scalar(minus, minus, -1.0, None, ALU.mult).then_inc(pre_g.sem, pre_g.tick("sign"))
            pool.sem_inc(at_g.sem, at_g.at(f"k{NC - 1}", -1))
            pool.wait_ge(pre_a.sem, pre_a.at("ctx"))
            pool.wait_ge(pre_v.sem, pre_v.at("ctx"))
            with pool.Fori(0, B) as b:
                pool.wait_ge(at_p.sem, at_p.at(f"v{NK - 1}", b - 1))
                pool.tensor_copy(ctx_cur[:], ctxT[:, bass.ds(b * SC, SC)]).then_inc(at_g.sem, at_g.tick("ctx_cur"))
                for c in range(NC):
                    pool.wait_ge(at_v.sem, at_v.at(f"ks{c}", b))
                    if c == 0:
                        pool.wait_ge(at_p.sem, at_p.at("q", b))
                    pool.tensor_tensor(kh[:, c, :], kc[:, c % 2, :], ks[:, c % 2, :], ALU.add) \
                        .then_inc(at_g.sem, at_g.tick(f"k{c}"))

        @block.scalar
        def _(act):
            layernorm_root(act, ln1_v, ln1_a, stat)
            layernorm_root(act, ln2_v, ln2_a, stat2)
            layernorm_root(act, lnc_v, lnc_a, statc)
            act.wait_ge(pre_p.sem, pre_p.at("lat"))
            act.wait_ge(load.sem, 16 * (N_LOADS))
            act.activation(latT[:], banks(ps, 4, 8), ACT.Identity, scale=col[:, 0:1], bias=col[:, 1:2]) \
               .then_inc(pre_a.sem, pre_a.tick("lat"))
            act.wait_ge(pre_p.sem, pre_p.at("ctx0"))
            act.activation(ctxT[:, 0:T], banks(ps, 0, 4), ACT.Identity, scale=col[:, 2:3], bias=col[:, 3:4]) \
               .then_inc(pre_a.sem, pre_a.tick("ctx"))
            act.sem_inc(at_a.sem, at_a.at("oT0", -1))
            with act.Fori(0, B) as b:
                act.wait_ge(at_p.sem, at_p.at("q", b))
                act.activation(qh[:].rearrange("p c s -> p (c s)"), banks(ps, 0, 4), ACT.Copy) \
                   .then_inc(at_a.sem, at_a.tick("q"))
                for n in range(NK):
                    act.wait_ge(at_p.sem, at_p.at(f"v{n}", b))
                    b0 = 2 * (n % 2)
                    act.activation(va[:, n, :, 0:XD], rows(banks(ps, b0, b0 + 2), XH, XD), ACT.Copy) \
                       .then_inc(at_a.sem, at_a.tick(f"v{n}"))
                for h in range(XH):
                    b0 = 2 * (h % 2)
                    act.wait_ge(at_p.sem, at_p.at(f"S{h}", b))
                    act.wait_ge(at_p.sem, at_p.at(f"O{(h - 2) % XH}", b - (h < 2)))
                    act.activation(pt[:, h % 2].rearrange("p n s -> p (n s)"), banks(ps, b0, b0 + 2), ACT.Exp,
                                   scale=XD ** -0.5).then_inc(at_a.sem, at_a.tick(f"E{h}"))
                act.wait_ge(at_p.sem, at_p.at("oT0", b))
                act.activation(ohT[:, 0].rearrange("p c s -> p (c s)"), banks(ps, 6, 8), ACT.Copy) \
                   .then_inc(at_a.sem, at_a.tick("oT0"))

        @block.vector
        def _(dve):
            layernorm_vector(dve, ln1_v, ln1_a, x[:], nrm[:], sq[:, 0:NT, :], stat[:], NT)
            dve.wait_ge(ln1_v.sem, ln1_v.at("normal"))
            layernorm_vector(dve, ln2_v, ln2_a, nrm[:], nrm[:], sq[:, 0:NT, :], stat2[:], NT)
            dve.wait_ge(load.sem, 16 * (N_LOADS))
            layernorm_vector(dve, lnc_v, lnc_a, ctx[:], cn[:], rows(ctxT[:], NCT), statc[:], NCT)
            dve.tensor_tensor(x[:], x[:], b_o[:].unsqueeze(1).to_broadcast([P, NT, P]), ALU.add) \
               .then_inc(pre_v.sem, pre_v.tick("x_bias"))
            dve.memset(va[:, :, :, XD:XD + 1], 1.0).then_inc(pre_v.sem, pre_v.tick("ones"))
            dve.wait_ge(pre_p.sem, pre_p.at("turn"))
            dve.tensor_copy(turnT[:, 0, :], ps[:, 0, :]).then_inc(pre_v.sem, pre_v.tick("cos"))
            dve.tensor_copy(turnT[:, 1, :], ps[:, 1, :]).then_inc(pre_v.sem, pre_v.tick("sin"))
            dve.wait_ge(pre_p.sem, pre_p.at("ctx1"))
            dve.tensor_scalar(ctxT[:, T:2 * T], banks(ps, 4, 8), col[:, 2:3], col[:, 3:4], ALU.mult, ALU.add) \
               .then_inc(pre_v.sem, pre_v.tick("ctx"))
            dve.sem_inc(at_v.sem, at_v.at("x", -1))

            def normalise(h, b):
                dve.wait_ge(at_p.sem, at_p.at(f"O{h}", b))
                o = ps[:, 4 + h % 2, 0:2 * (XD + 1)].rearrange("p (t d) -> p t d", t=2)
                dve.reciprocal(rec[:, h % 2, :].unsqueeze(2), o[:, :, XD:XD + 1]).then_inc(at_v.sem, at_v.tick(f"R{h}"))
                dve.wait_ge(at_v.sem, at_v.at(f"R{h}", b))
                dve.tensor_tensor(oh[:, :, h // 2, bass.ts(h % 2, XD)], o[:, :, 0:XD],
                                  rec[:, h % 2, :].unsqueeze(2).to_broadcast([P, 2, XD]), ALU.mult) \
                   .then_inc(at_v.sem, at_v.tick(f"N{h}"))

            with dve.Fori(0, B) as b:
                for c in range(NC):
                    dve.wait_ge(at_p.sem, at_p.at(f"k{c}", b))
                    if c < 2:
                        dve.wait_ge(at_g.sem, at_g.at(f"k{NC - 2 + c}", b - 1))
                    else:
                        dve.wait_ge(at_g.sem, at_g.at(f"k{c - 2}", b))
                    b0 = 4 + 2 * (c % 2)
                    for i, (name, dst) in enumerate((("kc", kc), ("ks", ks))):
                        dve.tensor_tensor(dst[:, c % 2, :], ps[:, b0 + i, :], turnT[:, i, :], ALU.mult) \
                           .then_inc(at_v.sem, at_v.tick(f"{name}{c}"))
                for h in range(XH):
                    dve.wait_ge(at_a.sem, at_a.at(f"E{h}", b))
                    w = pt[:, h % 2].rearrange("p n s -> p (n s)")
                    dve.tensor_scalar(w, w, math.exp(-CLIP), math.exp(CLIP), ALU.max, ALU.min) \
                       .then_inc(at_v.sem, at_v.tick(f"C{h}"))
                    if h:
                        normalise(h - 1, b)
                normalise(XH - 1, b)
                dve.wait_ge(at_p.sem, at_p.at("oT1", b))
                dve.tensor_copy(ohT[:, 1].rearrange("p c s -> p (c s)"), banks(ps, 2, 4)) \
                   .then_inc(at_v.sem, at_v.tick("oT1"))
                dve.wait_ge(at_p.sem, at_p.at("out", b))
                xb = x[:, bass.ds(2 * b, 2), :]
                dve.tensor_tensor(xb, rows(ps[:, 4, 0:2 * P], 2), xb, ALU.add).then_inc(at_v.sem, at_v.tick("x"))

        @block.tensor
        def _(pe):
            pe.wait_ge(load.sem, 16 * (N_LOADS))
            pe.wait_ge(pre_g.sem, pre_g.at("sign"))
            for i in range(2):
                for n in range(NK):
                    mm = pe.transpose(ps[:, i, bass.ts(n, P)], turn[:, i, n].rearrange("p r d -> p (r d)"), ident)
            mm.then_inc(pre_p.sem, pre_p.tick("turn"))
            pe.wait_ge(ln2_v.sem, ln2_v.at("normal"))
            for t in range(NT):
                mm = pe.transpose(ps[:, 4 + t // 4, bass.ts(t % 4, P)], nrm[:, t, :], ident)
            mm.then_inc(pre_p.sem, pre_p.tick("lat"))
            pe.wait_ge(lnc_v.sem, lnc_v.at("normal"))
            pe.wait_ge(pre_v.sem, pre_v.at("sin"))
            for t in range(NT):
                mm = pe.transpose(ps[:, t // 4, bass.ts(t % 4, P)], cn[:, t, :], ident)
            mm.then_inc(pre_p.sem, pre_p.tick("ctx0"))
            pe.wait_ge(pre_a.sem, pre_a.at("lat"))
            for t in range(NT):
                mm = pe.transpose(ps[:, 4 + t // 4, bass.ts(t % 4, P)], cn[:, NT + t, :], ident)
            mm.then_inc(pre_p.sem, pre_p.tick("ctx1"))
            pe.sem_inc(at_p.sem, at_p.at("out", -1))
            pe.wait_ge(pre_a.sem, pre_a.at("ctx"))
            pe.wait_ge(pre_v.sem, pre_v.at("ctx"))

            def scores(h, b):
                pe.wait_ge(at_g.sem, at_g.at(f"k{h // 2}", b))
                if h < 2:
                    pe.wait_ge(at_a.sem, at_a.at(f"v{NK - 1}", b))
                else:
                    pe.wait_ge(at_a.sem, at_a.at(f"E{h - 2}", b))
                r = bass.ds(XD * (h % 2), XD)
                for n in range(NK):
                    mm = pe.matmul(ps[:, 2 * (h % 2) + n // 2, bass.ts(n % 2, S)], kh[r, h // 2, bass.ts(n, P)],
                                   qh[r, h // 2, :], start=True, stop=True)
                mm.then_inc(at_p.sem, at_p.tick(f"S{h}"))

            with pe.Fori(0, B) as b:
                pe.wait_ge(at_a.sem, at_a.at(f"E{XH - 1}", b - 1))
                pe.wait_ge(at_v.sem, at_v.at("oT1", b - 1))
                for c in range(NC):
                    mm = pe.matmul(ps[:, c // 2, bass.ts(c % 2, S)], wq[:, bass.ts(c, P)], latT[:, bass.ds(b * S, S)],
                                   start=True, stop=True)
                mm.then_inc(at_p.sem, at_p.tick("q"))
                for c in range(NC):
                    if c == 0:
                        pe.wait_ge(at_v.sem, at_v.at("x", b - 1))
                        pe.wait_ge(at_a.sem, at_a.at("oT0", b - 1))
                    if c >= 2:
                        pe.wait_ge(at_v.sem, at_v.at(f"ks{c - 2}", b))
                    for i, w in enumerate((wkv, wk_sw)):
                        mm = pe.matmul(ps[:, 4 + 2 * (c % 2) + i, :], w[:, bass.ts(c, P)], ctxT[:, bass.ds(b * SC, SC)],
                                       start=True, stop=True)
                    mm.then_inc(at_p.sem, at_p.tick(f"k{c}"))
                pe.wait_ge(at_g.sem, at_g.at("ctx_cur", b))
                for n in range(NK):
                    pe.wait_ge(at_a.sem, at_a.at("q", b) if n < 2 else at_a.at(f"v{n - 2}", b))
                    for i in range(2):
                        mm = pe.matmul(ps[:, 2 * (n % 2) + i, :], ctx_cur[:, bass.ts(n, P)],
                                       wkv[:, bass.ds(INNER + BLK * i, BLK)], start=True, stop=True)
                    mm.then_inc(at_p.sem, at_p.tick(f"v{n}"))
                scores(0, b)
                for h in range(XH):
                    if h + 1 < XH:
                        scores(h + 1, b)
                    pe.wait_ge(at_v.sem, at_v.at(f"C{h}", b))
                    pe.wait_ge(at_v.sem, at_v.at(f"N{h - 2}", b) if h >= 2 else at_v.at(f"ks{NC - 1}", b))
                    for i in range(2):
                        for n in range(NK):
                            mm = pe.matmul(ps[:, 4 + h % 2, bass.ds((XD + 1) * i, XD + 1)],
                                           pt[:, h % 2, n, bass.ts(i, P)], va[:, n, h, :],
                                           start=(n == 0), stop=(n == NK - 1))
                    mm.then_inc(at_p.sem, at_p.tick(f"O{h}"))
                pe.wait_ge(at_v.sem, at_v.at(f"N{XH - 1}", b))
                for i, b0 in enumerate((6, 2)):
                    for c in range(NC):
                        mm = pe.transpose(ps[:, b0 + c // 4, bass.ts(c % 4, P)], oh[:, i, c, :], ident)
                    mm.then_inc(at_p.sem, at_p.tick(f"oT{i}"))
                for i in range(2):
                    pe.wait_ge(at_v.sem, at_v.at("oT1", b)) if i else pe.wait_ge(at_a.sem, at_a.at("oT0", b))
                    for c in range(NC):
                        mm = pe.matmul(ps[:, 4, bass.ts(i, P)], ohT[:, i, c, :], wo[:, c, :],
                                       start=(c == 0), stop=(c == NC - 1))
                mm.then_inc(at_p.sem, at_p.tick("out"))



EH, ED = 16, 8
NE = 8
TOP = 2


def stage_experts(nc, g, a):
    with Stage(nc, "ex") as st:
        w_in = st.sb("w_in", [P, 3, P])
        w_inT = st.sb("w_inT", [P, 3 * P])
        w_out = st.sb("w_out", [P, P])
        w_outT = st.sb("w_outT", [P, P])
        gw = st.sb("gw", [NE, P])
        gwT = st.sb("gwT", [P, NE])
        b_in = st.sb("b_in", [P, 3 * P])
        b_out = st.sb("b_out", [P, P])
        b_gate = st.sb("b_gate", [P, NE])
        b1r = st.sb("b1r", [NE * NJ, P])
        b1T = st.sb("b1T", [P, NE * NJ])
        b2 = st.sb("b2", [NE, P])
        lng = st.sb("lng", [P, 4, P])
        lower = st.sb("lower", [P, NE, NE])
        nrm = st.sb("nrm", [P, NT, P])
        nT = st.sb("nT", [P, T])
        sq = st.sb("sq", [P, NT, P])
        stat = st.sb("stat", [P, 3, 4, NT])
        qkv = st.sb("qkv", [P, NT, 3 * P])
        prod = st.sb("prod", [P, 2, B, P])
        sc = st.sb("sc", [P, NT, B, EH])
        smx = st.sb("smx", [P, NT, EH])
        cx = st.sb("cx", [P, NT, P])
        tok = st.sb("tok", [P, NT, P])
        tokT = st.sb("tokT", [P, T])
        lg = st.sb("lg", [P, NT, NE])
        l1 = st.sb("l1", [P, NT])
        cmp = st.sb("cmp", [P, 2, NT, NE, NE])
        rank = st.sb("rank", [P, NT, NE])
        comb = st.sb("comb", [P, NT, NE])
        combT = st.sb("combT", [NE, T])
        comb_e = st.sb("comb_e", [P, NT])
        acc = st.sb("acc", [P, NT, P])
        w1r = st.sb("w1r", [P, NJ, P])
        w2r = st.sb("w2r", [P, HID])
        w1T = st.sb("w1T", [P, HID])
        w2T = st.sb("w2T", [P, NJ, P])
        fh = st.sb("fh", [P, NJ, BLK])
        ps, x = g.ps, g.x
        ident = g.ident

        load = st.steps("load", ["all"])
        N_LOADS = 13
        LOADED = 16 * N_LOADS
        w_load = st.steps("w_load", ["w1", "w2"])
        ln0_v, ln0_a = st.steps("ln0_v", LN_VECTOR), st.steps("ln0_a", ["root"])
        ln1_v, ln1_a = st.steps("ln1_v", LN_VECTOR), st.steps("ln1_a", ["root"])
        ln2_v, ln2_a = st.steps("ln2_v", LN_VECTOR), st.steps("ln2_a", ["root"])
        pre_p = st.steps("pre_p", ["w", "nT"])
        pre_v = st.steps("pre_v", ["w_inT", "w_outT", "gwT", "b1T", "nT1"] + [f"qkv{t}" for t in range(1, NT, 2)])
        pre_a = st.steps("pre_a", ["nT0"] + [f"raw{t}" for t in range(0, NT, 2)])
        qkv_p = st.steps("qkv_p", [f"t{t}" for t in range(NT)])
        pre_g = st.steps("pre_g", ["b_out"])
        s_g = st.steps("s_g", ["prod0", "prod1"], ahead=1)
        s_v = st.steps("s_v", ["sum0", "sum1"], ahead=1)
        c_g = st.steps("c_g", ["prod0", "prod1"], ahead=1)
        c_v = st.steps("c_v", ["sum0", "sum1"], ahead=1)
        sm_v = st.steps("sm_v", ["max", "shift", "sum", "inv", "p"])
        sm_a = st.steps("sm_a", ["exp"])
        mid_p = st.steps("mid_p", ["cT", "out", "tokT", "gate", "combT", "b2"])
        mid_a = st.steps("mid_a", ["cT", "tokT", "e", "combT"])
        mid_v = st.steps("mid_v", ["out", "scaled", "tok", "bias", "max", "shift", "gt", "eq", "lower", "beats", "rank",
                                   "top", "w", "sum", "inv", "comb", "acc"])
        e_p = st.steps("e_p", ["w1T", "w2T"], ahead=1)
        e_a = st.steps("e_a", ["w1T"], ahead=1)
        e_v = st.steps("e_v", ["w2T", "comb_e"], ahead=1)
        f_p = st.steps("f_p", ["h0", "h1", "h2", "h3", "o"], ahead=1)
        f_a = st.steps("f_a", ["h0", "h2"], ahead=1)
        f_v = st.steps("f_v", ["h1", "h3", "acc"], ahead=1)
        end_v = st.steps("end_v", ["scaled", "moved", "x"])

        block = st.block()

        @block.sync
        def _(sp):
            for dst, src in (
                (w_in[:], a["L0_ffn_in_proj_w"].rearrange("(i p) d -> p i d", p=P)), (w_out[:], a["L0_ffn_out_w"]),
                (gw[:], a["L0_ffn_gate_w"]), (b1r[:], a["L0_ffn_b1"].rearrange("e (j p) -> (e j) p", p=P)),
                (b_in[:], a["L0_ffn_in_proj_b"].partition_broadcast(P)), (b_out[:], a["L0_ffn_out_b"].partition_broadcast(P)),
                (b_gate[:], a["L0_ffn_gate_b"].partition_broadcast(P)), (b2[:], a["L0_ffn_b2"]),
                (lng[:, 0, :], a["L0_ffn_ln1_g"].partition_broadcast(P)), (lng[:, 1, :], a["L0_ffn_ln1_b"].partition_broadcast(P)),
                (lng[:, 2, :], a["L0_ffn_ln2_g"].partition_broadcast(P)), (lng[:, 3, :], a["L0_ffn_ln2_b"].partition_broadcast(P)),
                (lower[:].rearrange("p i j -> p (i j)"), a["lower"].partition_broadcast(P)),
            ):
                sp.dma_start(dst, src).then_inc(load.sem, 16)
            with sp.Fori(0, NE) as e:
                sp.wait_ge(e_p.sem, e_p.at("w1T", e - 1))
                sp.dma_start(w1r[:].unsqueeze(1), a["L0_ffn_w1"][bass.ds(e, 1)].rearrange("e (j p) d -> p e j d", p=P)) \
                  .then_inc(w_load.sem, 16)
                sp.wait_ge(e_p.sem, e_p.at("w2T", e - 1))
                sp.dma_start(w2r[:].unsqueeze(1), a["L0_ffn_w2"][bass.ds(e, 1)].rearrange("e d f -> d e f")) \
                  .then_inc(w_load.sem, 16)

        @block.gpsimd
        def _(pool):
            pool.sem_inc(s_g.sem, s_g.at("prod1", -1))
            pool.sem_inc(c_g.sem, c_g.at("prod1", -1))
            pool.wait_ge(load.sem, LOADED)
            pool.wait_ge(pre_p.sem, pre_p.at("nT"))
            pool.tensor_tensor(nrm[:], nrm[:], b_out[:].unsqueeze(1).to_broadcast([P, NT, P]), ALU.add) \
                .then_inc(pre_g.sem, pre_g.tick("b_out"))
            pool.wait_ge(pre_v.sem, pre_v.at(f"qkv{NT - 1}"))
            pool.wait_ge(pre_a.sem, pre_a.at(f"raw{NT - 2}"))
            with pool.Fori(0, B) as s:
                for f in range(2):
                    pool.wait_ge(s_v.sem, s_v.at(f"sum{f}", s - 1))
                    pool.tensor_tensor(prod[:, f], qkv[:, bass.ds(2 * s + f, 1), 0:P].to_broadcast([P, B, P]),
                                       qkv[:, f:NT:2, P:2 * P], ALU.mult).then_inc(s_g.sem, s_g.tick(f"prod{f}"))
            pool.wait_ge(sm_v.sem, sm_v.at("p"))
            with pool.Fori(0, B) as s:
                for f in range(2):
                    pool.wait_ge(c_v.sem, c_v.at(f"sum{f}", s - 1))
                    w = sc[:, bass.ds(2 * s + f, 1)].rearrange("p o t h -> p (o t) h").unsqueeze(3)
                    pool.tensor_tensor(prod[:, f].rearrange("p t (h d) -> p t h d", h=EH), w.to_broadcast([P, B, EH, ED]),
                                       qkv[:, f:NT:2, 2 * P:3 * P].rearrange("p t (h d) -> p t h d", h=EH), ALU.mult) \
                        .then_inc(c_g.sem, c_g.tick(f"prod{f}"))

        @block.scalar
        def _(act):
            layernorm_root(act, ln0_v, ln0_a, stat[:, 0])
            act.wait_ge(pre_p.sem, pre_p.at("nT"))
            act.activation(nT[:, 0:2 * BLK], banks(ps, 4, 6), ACT.Copy).then_inc(pre_a.sem, pre_a.tick("nT0"))
            for t in range(0, NT, 2):
                act.wait_ge(qkv_p.sem, qkv_p.at(f"t{t}"))
                act.activation(qkv[:, t, :], ps[:, t % 4, 0:3 * P], ACT.Copy).then_inc(pre_a.sem, pre_a.tick(f"raw{t}"))
            act.wait_ge(sm_v.sem, sm_v.at("shift"))
            act.activation(sc[:], sc[:], ACT.Exp, scale=ED ** -0.5).then_inc(sm_a.sem, sm_a.tick("exp"))
            act.wait_ge(mid_p.sem, mid_p.at("cT"))
            act.activation(nT[:], banks(ps, 0, 4), ACT.Copy).then_inc(mid_a.sem, mid_a.tick("cT"))
            layernorm_root(act, ln1_v, ln1_a, stat[:, 1])
            act.wait_ge(mid_p.sem, mid_p.at("tokT"))
            act.activation(tokT[:], banks(ps, 0, 4), ACT.Copy).then_inc(mid_a.sem, mid_a.tick("tokT"))
            act.wait_ge(mid_v.sem, mid_v.at("shift"))
            act.activation(lg[:], lg[:], ACT.Exp).then_inc(mid_a.sem, mid_a.tick("e"))
            act.wait_ge(mid_p.sem, mid_p.at("combT"))
            act.activation(combT[:], banks(ps, 0, 4)[0:NE, :], ACT.Copy).then_inc(mid_a.sem, mid_a.tick("combT"))
            act.sem_inc(e_a.sem, e_a.at("w1T", -1))
            act.sem_inc(f_a.sem, f_a.at("h2", -1))
            with act.Fori(0, NE) as e:
                act.wait_ge(e_p.sem, e_p.at("w1T", e))
                act.activation(w1T[:], ps[:, 6, :], ACT.Copy).then_inc(e_a.sem, e_a.tick("w1T"))
                with act.Fori(0, NB) as blk:
                    n = e * NB + blk
                    for j in (0, 2):
                        act.wait_ge(f_p.sem, f_p.at(f"h{j}", n))
                        act.activation(fh[:, j, :], ps[:, j, :], ACT.Relu, bias=b1T[:, bass.ds(e * NJ + j, 1)]) \
                           .then_inc(f_a.sem, f_a.tick(f"h{j}"))
            layernorm_root(act, ln2_v, ln2_a, stat[:, 2])

        @block.vector
        def _(dve):
            layernorm_vector(dve, ln0_v, ln0_a, x[:], nrm[:], sq[:], stat[:, 0], NT)
            dve.wait_ge(pre_p.sem, pre_p.at("w"))
            dve.tensor_copy(w_inT[:], ps[:, 0, 0:3 * P]).then_inc(pre_v.sem, pre_v.tick("w_inT"))
            dve.tensor_copy(w_outT[:], ps[:, 1, 0:P]).then_inc(pre_v.sem, pre_v.tick("w_outT"))
            dve.tensor_copy(gwT[:], ps[:, 1, P:P + NE]).then_inc(pre_v.sem, pre_v.tick("gwT"))
            dve.tensor_copy(b1T[:], ps[:, 1, 2 * P:2 * P + NE * NJ]).then_inc(pre_v.sem, pre_v.tick("b1T"))
            dve.wait_ge(pre_p.sem, pre_p.at("nT"))
            dve.tensor_copy(nT[:, 2 * BLK:T], banks(ps, 6, 8)).then_inc(pre_v.sem, pre_v.tick("nT1"))
            dve.wait_ge(load.sem, LOADED)
            for t in range(1, NT, 2):
                dve.wait_ge(qkv_p.sem, qkv_p.at(f"t{t}"))
                dve.tensor_copy(qkv[:, t, :], ps[:, t % 4, 0:3 * P]).then_inc(pre_v.sem, pre_v.tick(f"qkv{t}"))
            dve.sem_inc(s_v.sem, s_v.at("sum1", -1))
            dve.sem_inc(c_v.sem, c_v.at("sum1", -1))
            with dve.Fori(0, B) as s:
                for f in range(2):
                    dve.wait_ge(s_g.sem, s_g.at(f"prod{f}", s))
                    dve.tensor_reduce(sc[:, bass.ds(2 * s + f, 1)].rearrange("p o t h -> p (o t h)"),
                                      prod[:, f].rearrange("p t (h d) -> p (t h) d", h=EH), AX.X, ALU.add) \
                       .then_inc(s_v.sem, s_v.tick(f"sum{f}"))
            dve.wait_ge(s_v.sem, s_v.at("sum1", B - 1))
            by_t = sc[:].rearrange("p n t h -> p n h t")
            over = lambda v: v[:].unsqueeze(2).to_broadcast([P, NT, B, EH])
            dve.tensor_reduce(smx[:], by_t, AX.X, ALU.max).then_inc(sm_v.sem, sm_v.tick("max"))
            dve.wait_ge(sm_v.sem, sm_v.at("max"))
            dve.tensor_tensor(sc[:], sc[:], over(smx), ALU.subtract).then_inc(sm_v.sem, sm_v.tick("shift"))
            dve.wait_ge(sm_a.sem, sm_a.at("exp"))
            dve.tensor_reduce(smx[:], by_t, AX.X, ALU.add).then_inc(sm_v.sem, sm_v.tick("sum"))
            dve.wait_ge(sm_v.sem, sm_v.at("sum"))
            dve.reciprocal(smx[:], smx[:]).then_inc(sm_v.sem, sm_v.tick("inv"))
            dve.wait_ge(sm_v.sem, sm_v.at("inv"))
            dve.tensor_tensor(sc[:], sc[:], over(smx), ALU.mult).then_inc(sm_v.sem, sm_v.tick("p"))
            with dve.Fori(0, B) as s:
                for f in range(2):
                    dve.wait_ge(c_g.sem, c_g.at(f"prod{f}", s))
                    dve.tensor_reduce(cx[:, bass.ds(2 * s + f, 1), :].rearrange("p o d -> p (o d)"),
                                      prod[:, f].rearrange("p t d -> p d t"), AX.X, ALU.add) \
                       .then_inc(c_v.sem, c_v.tick(f"sum{f}"))
            dve.wait_ge(mid_p.sem, mid_p.at("out"))
            dve.wait_ge(pre_g.sem, pre_g.at("b_out"))
            dve.tensor_tensor(tok[:], rows(banks(ps, 4, 8), NT), nrm[:], ALU.add).then_inc(mid_v.sem, mid_v.tick("out"))
            dve.wait_ge(mid_v.sem, mid_v.at("out"))
            layernorm_vector(dve, ln1_v, ln1_a, tok[:], tok[:], sq[:], stat[:, 1], NT)
            row = lambda i: lng[:, i, :].unsqueeze(1).to_broadcast([P, NT, P])
            dve.wait_ge(ln1_v.sem, ln1_v.at("normal"))
            dve.tensor_tensor(tok[:], tok[:], row(0), ALU.mult).then_inc(mid_v.sem, mid_v.tick("scaled"))
            dve.wait_ge(mid_v.sem, mid_v.at("scaled"))
            dve.tensor_tensor(tok[:], tok[:], row(1), ALU.add).then_inc(mid_v.sem, mid_v.tick("tok"))
            per_tile = lambda v: v[:].unsqueeze(2).to_broadcast([P, NT, NE])
            dve.wait_ge(mid_p.sem, mid_p.at("gate"))
            dve.tensor_tensor(lg[:], ps[:, 4, 0:P].rearrange("p (t e) -> p t e", e=NE),
                              b_gate[:].unsqueeze(1).to_broadcast([P, NT, NE]), ALU.add).then_inc(mid_v.sem, mid_v.tick("bias"))
            dve.wait_ge(mid_v.sem, mid_v.at("bias"))
            dve.tensor_reduce(l1[:], lg[:], AX.X, ALU.max).then_inc(mid_v.sem, mid_v.tick("max"))
            dve.wait_ge(mid_v.sem, mid_v.at("max"))
            dve.tensor_tensor(lg[:], lg[:], per_tile(l1), ALU.subtract).then_inc(mid_v.sem, mid_v.tick("shift"))
            dve.wait_ge(mid_a.sem, mid_a.at("e"))
            mine = lg[:].unsqueeze(3).to_broadcast([P, NT, NE, NE])
            other = lg[:].unsqueeze(2).to_broadcast([P, NT, NE, NE])
            dve.tensor_tensor(cmp[:, 0], other, mine, ALU.is_gt).then_inc(mid_v.sem, mid_v.tick("gt"))
            dve.tensor_tensor(cmp[:, 1], other, mine, ALU.is_equal).then_inc(mid_v.sem, mid_v.tick("eq"))
            dve.wait_ge(mid_v.sem, mid_v.at("eq"))
            dve.tensor_tensor(cmp[:, 1], cmp[:, 1], lower[:].unsqueeze(1).to_broadcast([P, NT, NE, NE]), ALU.mult) \
               .then_inc(mid_v.sem, mid_v.tick("lower"))
            dve.wait_ge(mid_v.sem, mid_v.at("lower"))
            dve.tensor_tensor(cmp[:, 0], cmp[:, 0], cmp[:, 1], ALU.add).then_inc(mid_v.sem, mid_v.tick("beats"))
            dve.wait_ge(mid_v.sem, mid_v.at("beats"))
            dve.tensor_reduce(rank[:], cmp[:, 0], AX.X, ALU.add).then_inc(mid_v.sem, mid_v.tick("rank"))
            dve.wait_ge(mid_v.sem, mid_v.at("rank"))
            dve.tensor_scalar(rank[:], rank[:], TOP - 0.5, None, ALU.is_lt).then_inc(mid_v.sem, mid_v.tick("top"))
            dve.wait_ge(mid_v.sem, mid_v.at("top"))
            dve.tensor_tensor(comb[:], rank[:], lg[:], ALU.mult).then_inc(mid_v.sem, mid_v.tick("w"))
            dve.wait_ge(mid_v.sem, mid_v.at("w"))
            dve.tensor_reduce(l1[:], comb[:], AX.X, ALU.add).then_inc(mid_v.sem, mid_v.tick("sum"))
            dve.wait_ge(mid_v.sem, mid_v.at("sum"))
            dve.reciprocal(l1[:], l1[:]).then_inc(mid_v.sem, mid_v.tick("inv"))
            dve.wait_ge(mid_v.sem, mid_v.at("inv"))
            dve.tensor_tensor(comb[:], comb[:], per_tile(l1), ALU.mult).then_inc(mid_v.sem, mid_v.tick("comb"))
            dve.wait_ge(mid_p.sem, mid_p.at("b2"))
            dve.tensor_tensor(acc[:], rows(banks(ps, 4, 8), NT), tok[:], ALU.add).then_inc(mid_v.sem, mid_v.tick("acc"))
            dve.wait_ge(mid_v.sem, mid_v.at("acc"))
            dve.sem_inc(e_v.sem, e_v.at("comb_e", -1))
            dve.sem_inc(f_v.sem, f_v.at("acc", -1))
            with dve.Fori(0, NE) as e:
                dve.wait_ge(e_p.sem, e_p.at("w2T", e))
                dve.tensor_copy(w2T[:].rearrange("p j d -> p (j d)"), ps[:, 7, :]).then_inc(e_v.sem, e_v.tick("w2T"))
                dve.wait_ge(f_v.sem, f_v.at("acc", e * NB - 1))
                dve.tensor_copy(comb_e[:].unsqueeze(2), comb[:, :, bass.ds(e, 1)]).then_inc(e_v.sem, e_v.tick("comb_e"))
                with dve.Fori(0, NB) as blk:
                    n = e * NB + blk
                    for j in (1, 3):
                        dve.wait_ge(f_p.sem, f_p.at(f"h{j}", n))
                        dve.tensor_scalar(fh[:, j, :], ps[:, j, :], b1T[:, bass.ds(e * NJ + j, 1)], 0.0, ALU.add, ALU.max) \
                           .then_inc(f_v.sem, f_v.tick(f"h{j}"))
                    dve.wait_ge(e_v.sem, e_v.at("comb_e", e))
                    dve.wait_ge(f_p.sem, f_p.at("o", n))
                    for i in range(4):
                        at = acc[:, bass.ds(4 * blk + i, 1), :]
                        last = dve.scalar_tensor_tensor(at, ps[:, 4, bass.ts(i, P)].unsqueeze(1),
                                                        comb_e[:, bass.ds(4 * blk + i, 1)], at, ALU.mult, ALU.add)
                    last.then_inc(f_v.sem, f_v.tick("acc"))
            dve.wait_ge(f_v.sem, f_v.at("acc", NE * NB - 1))
            layernorm_vector(dve, ln2_v, ln2_a, acc[:], acc[:], sq[:], stat[:, 2], NT)
            dve.wait_ge(ln2_v.sem, ln2_v.at("normal"))
            dve.tensor_tensor(acc[:], acc[:], row(2), ALU.mult).then_inc(end_v.sem, end_v.tick("scaled"))
            dve.wait_ge(end_v.sem, end_v.at("scaled"))
            dve.tensor_tensor(acc[:], acc[:], row(3), ALU.add).then_inc(end_v.sem, end_v.tick("moved"))
            dve.wait_ge(end_v.sem, end_v.at("moved"))
            dve.tensor_tensor(x[:], acc[:], x[:], ALU.add).then_inc(end_v.sem, end_v.tick("x"))

        @block.tensor
        def _(pe):
            pe.wait_ge(load.sem, LOADED)
            for i in range(3):
                pe.transpose(ps[:, 0, bass.ts(i, P)], w_in[:, i, :], ident)
            pe.transpose(ps[:, 1, 0:P], w_out[:], ident)
            pe.transpose(ps[:, 1, P:P + NE], gw[:], ident[0:NE, 0:NE])
            pe.transpose(ps[:, 1, 2 * P:2 * P + NE * NJ], b1r[:], ident[0:NE * NJ, 0:NE * NJ]) \
              .then_inc(pre_p.sem, pre_p.tick("w"))
            pe.wait_ge(ln0_v.sem, ln0_v.at("normal"))
            for t in range(NT):
                mm = pe.transpose(ps[:, 4 + t // 4, bass.ts(t % 4, P)], nrm[:, t, :], ident)
            mm.then_inc(pre_p.sem, pre_p.tick("nT"))
            pe.wait_ge(pre_a.sem, pre_a.at("nT0"))
            pe.wait_ge(pre_v.sem, pre_v.at("nT1"))
            for t in range(NT):
                if t >= 4:
                    pe.wait_ge(pre_v.sem, pre_v.at(f"qkv{t - 4}")) if t % 2 else pe.wait_ge(pre_a.sem, pre_a.at(f"raw{t - 4}"))
                pe.matmul(ps[:, t % 4, 0:3 * P], nT[:, bass.ts(t, P)], w_inT[:], start=True, stop=False)
                pe.matmul(ps[:, t % 4, 0:3 * P], g.ones[0:1, :], b_in[0:1, :], start=False, stop=True) \
                  .then_inc(qkv_p.sem, qkv_p.tick(f"t{t}"))
            pe.wait_ge(pre_a.sem, pre_a.at(f"raw{NT - 2}"))
            pe.wait_ge(pre_v.sem, pre_v.at(f"qkv{NT - 1}"))
            pe.wait_ge(c_v.sem, c_v.at("sum1", B - 1))
            for t in range(NT):
                mm = pe.transpose(ps[:, t // 4, bass.ts(t % 4, P)], cx[:, t, :], ident)
            mm.then_inc(mid_p.sem, mid_p.tick("cT"))
            pe.wait_ge(mid_a.sem, mid_a.at("cT"))
            for t in range(NT):
                mm = pe.matmul(ps[:, 4 + t // 4, bass.ts(t % 4, P)], nT[:, bass.ts(t, P)], w_outT[:], start=True, stop=True)
            mm.then_inc(mid_p.sem, mid_p.tick("out"))
            pe.wait_ge(mid_v.sem, mid_v.at("tok"))
            for t in range(NT):
                mm = pe.transpose(ps[:, t // 4, bass.ts(t % 4, P)], tok[:, t, :], ident)
            mm.then_inc(mid_p.sem, mid_p.tick("tokT"))
            pe.wait_ge(mid_a.sem, mid_a.at("tokT"))
            for t in range(NT):
                mm = pe.matmul(ps[:, 4, bass.ts(t, NE)], tokT[:, bass.ts(t, P)], gwT[:], start=True, stop=True)
            mm.then_inc(mid_p.sem, mid_p.tick("gate"))
            pe.wait_ge(mid_v.sem, mid_v.at("comb"))
            for t in range(NT):
                mm = pe.transpose(ps[0:NE, t // 4, bass.ts(t % 4, P)], comb[:, t, :], ident)
            mm.then_inc(mid_p.sem, mid_p.tick("combT"))
            pe.wait_ge(mid_a.sem, mid_a.at("combT"))
            for t in range(NT):
                mm = pe.matmul(ps[:, 4 + t // 4, bass.ts(t % 4, P)], combT[:, bass.ts(t, P)], b2[:], start=True, stop=True)
            mm.then_inc(mid_p.sem, mid_p.tick("b2"))
            pe.sem_inc(e_p.sem, e_p.at("w2T", -1))
            pe.sem_inc(f_p.sem, f_p.at("o", -1))
            pe.wait_ge(mid_v.sem, mid_v.at("acc"))
            with pe.Fori(0, NE) as e:
                pe.wait_ge(w_load.sem, 32 * e + 32)
                pe.wait_ge(e_a.sem, e_a.at("w1T", e - 1))
                for j in range(NJ):
                    mm = pe.transpose(ps[:, 6, bass.ts(j, P)], w1r[:, j, :], ident)
                mm.then_inc(e_p.sem, e_p.tick("w1T"))
                pe.wait_ge(e_v.sem, e_v.at("w2T", e - 1))
                for j in range(NJ):
                    mm = pe.transpose(ps[:, 7, bass.ts(j, P)], w2r[:, bass.ts(j, P)], ident)
                mm.then_inc(e_p.sem, e_p.tick("w2T"))
                with pe.Fori(0, NB) as blk:
                    n = e * NB + blk
                    pe.wait_ge(e_a.sem, e_a.at("w1T", e))
                    for j in range(NJ):
                        free = f_v.at(f"h{j}", n - 1) if j % 2 else f_a.at(f"h{j}", n - 1)
                        pe.wait_ge(f_v.sem if j % 2 else f_a.sem, free)
                        pe.matmul(ps[:, j, :], w1T[:, bass.ts(j, P)], tokT[:, bass.ds(blk * BLK, BLK)],
                                  start=True, stop=True).then_inc(f_p.sem, f_p.tick(f"h{j}"))
                    pe.wait_ge(e_v.sem, e_v.at("w2T", e))
                    pe.wait_ge(f_v.sem, f_v.at("acc", n - 1))
                    pe.wait_ge(f_v.sem, f_v.at("h3", n))
                    pe.wait_ge(f_a.sem, f_a.at("h2", n))
                    for i in range(4):
                        for j in range(NJ):
                            mm = pe.matmul(ps[:, 4, bass.ts(i, P)], fh[:, j, bass.ts(i, P)], w2T[:, j, :],
                                           start=(j == 0), stop=(j == NJ - 1))
                    mm.then_inc(f_p.sem, f_p.tick("o"))



GK = 32


def stage_gated(nc, g, a):
    with Stage(nc, "ga") as st:
        w_lr = st.sb("w_lr", [P, 2, GK])
        thr = st.sb("thr", [P, 2])
        nrm = st.sb("nrm", [P, NT, P])
        nT = st.sb("nT", [P, T])
        sq = st.sb("sq", [P, NT, P])
        stat = st.sb("stat", [P, 4, NT])
        lr = st.sb("lr", [GK, 2, T])
        cm = st.sb("cm", [P, NT, S])
        ex = st.sb("ex", [P, NT, S])
        exT = st.sb("exT", [P, B, 2, S])
        mx = st.sb("mx", [P, NT])
        o = st.sb("o", [P, NT, P])
        ps, x = g.ps, g.x
        ident = g.ident

        load = st.steps("load", ["all"])
        LOADED = 16 * 4
        ln_v, ln_a = st.steps("ln_v", LN_VECTOR), st.steps("ln_a", ["root"])
        p = st.steps("p", ["nT", "lr", "cm", "T0", "T1", "o"])
        s_a = st.steps("s_a", ["nT", "left", "cm1", "exp", "T0"])
        s_v = st.steps("s_v", ["right", "cm0", "bias", "max", "shift", "pass", "sum", "inv", "gated", "T1", "o", "x"])

        block = st.block()

        @block.sync
        def _(sp):
            sp.dma_start(w_lr[:, 0, :], a["L1_attn_compare_left"]).then_inc(load.sem, 16)
            sp.dma_start(w_lr[:, 1, :], a["L1_attn_compare_right"]).then_inc(load.sem, 16)
            sp.dma_start(thr[:, 0:1], a["L1_attn_threshold"].partition_broadcast(P)).then_inc(load.sem, 16)
            sp.dma_start(thr[:, 1:2], a["L1_attn_gate_bias"].partition_broadcast(P)).then_inc(load.sem, 16)

        @block.scalar
        def _(act):
            layernorm_root(act, ln_v, ln_a, stat)
            act.wait_ge(p.sem, p.at("nT"))
            act.activation(nT[:], banks(ps, 0, 4), ACT.Copy).then_inc(s_a.sem, s_a.tick("nT"))
            act.wait_ge(p.sem, p.at("lr"))
            act.activation(lr[:, 0, :], banks(ps, 4, 8)[0:GK, :], ACT.Copy).then_inc(s_a.sem, s_a.tick("left"))
            act.wait_ge(p.sem, p.at("cm"))
            act.activation(cm[:, NT // 2:NT, :], rows(banks(ps, 4, 8), NT // 2, S), ACT.Copy, scale=P ** -0.5) \
               .then_inc(s_a.sem, s_a.tick("cm1"))
            act.wait_ge(s_v.sem, s_v.at("shift"))
            act.activation(ex[:], ex[:], ACT.Exp).then_inc(s_a.sem, s_a.tick("exp"))
            act.wait_ge(p.sem, p.at("T0"))
            act.activation(exT[:, 0:B // 2].rearrange("p b j i -> p (b j i)"), banks(ps, 0, 4), ACT.Copy) \
               .then_inc(s_a.sem, s_a.tick("T0"))

        @block.vector
        def _(dve):
            layernorm_vector(dve, ln_v, ln_a, x[:], nrm[:], sq[:], stat[:], NT)
            per_row = lambda v: v.unsqueeze(2).to_broadcast([P, NT, S])
            dve.wait_ge(p.sem, p.at("lr"))
            dve.tensor_copy(lr[:, 1, :], banks(ps, 0, 4)[0:GK, :]).then_inc(s_v.sem, s_v.tick("right"))
            dve.wait_ge(p.sem, p.at("cm"))
            dve.tensor_scalar(cm[:, 0:NT // 2, :], rows(banks(ps, 0, 4), NT // 2, S), P ** -0.5, None, ALU.mult) \
               .then_inc(s_v.sem, s_v.tick("cm0"))
            dve.wait_ge(s_v.sem, s_v.at("cm0"))
            dve.wait_ge(s_a.sem, s_a.at("cm1"))
            dve.wait_ge(load.sem, LOADED)
            dve.tensor_scalar(ex[:], cm[:], thr[:, 1:2], None, ALU.add).then_inc(s_v.sem, s_v.tick("bias"))
            dve.wait_ge(s_v.sem, s_v.at("bias"))
            dve.tensor_reduce(mx[:], ex[:], AX.X, ALU.max).then_inc(s_v.sem, s_v.tick("max"))
            dve.wait_ge(s_v.sem, s_v.at("max"))
            dve.tensor_tensor(ex[:], ex[:], per_row(mx[:]), ALU.subtract).then_inc(s_v.sem, s_v.tick("shift"))
            dve.tensor_scalar(cm[:], cm[:], thr[:, 0:1], None, ALU.is_gt).then_inc(s_v.sem, s_v.tick("pass"))
            dve.wait_ge(s_a.sem, s_a.at("exp"))
            dve.tensor_reduce(mx[:], ex[:], AX.X, ALU.add).then_inc(s_v.sem, s_v.tick("sum"))
            dve.wait_ge(s_v.sem, s_v.at("sum"))
            dve.reciprocal(mx[:], mx[:]).then_inc(s_v.sem, s_v.tick("inv"))
            dve.tensor_tensor(ex[:], ex[:], cm[:], ALU.mult).then_inc(s_v.sem, s_v.tick("gated"))
            dve.wait_ge(p.sem, p.at("T1"))
            dve.tensor_copy(exT[:, B // 2:B].rearrange("p b j i -> p (b j i)"), banks(ps, 4, 8)) \
               .then_inc(s_v.sem, s_v.tick("T1"))
            dve.wait_ge(p.sem, p.at("o"))
            dve.wait_ge(s_v.sem, s_v.at("inv"))
            dve.tensor_tensor(o[:], rows(banks(ps, 0, 4), NT), bcast(mx[:], NT), ALU.mult).then_inc(s_v.sem, s_v.tick("o"))
            dve.wait_ge(s_v.sem, s_v.at("o"))
            dve.tensor_tensor(x[:], x[:], o[:], ALU.add).then_inc(s_v.sem, s_v.tick("x"))

        @block.tensor
        def _(pe):
            pe.wait_ge(ln_v.sem, ln_v.at("normal"))
            for t in range(NT):
                mm = pe.transpose(ps[:, t // 4, bass.ts(t % 4, P)], nrm[:, t, :], ident)
            mm.then_inc(p.sem, p.tick("nT"))
            pe.wait_ge(s_a.sem, s_a.at("nT"))
            pe.wait_ge(load.sem, LOADED)
            for i, b0 in ((0, 4), (1, 0)):
                for b in range(NB):
                    mm = pe.matmul(ps[0:GK, b0 + b, :], w_lr[:, i, :], nT[:, bass.ts(b, BLK)], start=True, stop=True)
            mm.then_inc(p.sem, p.tick("lr"))
            pe.wait_ge(s_a.sem, s_a.at("left"))
            pe.wait_ge(s_v.sem, s_v.at("right"))
            for t in range(NT):
                mm = pe.matmul(ps[:, t // 2, bass.ts(t % 2, S)], lr[:, 0, bass.ts(t, P)], lr[:, 1, bass.ts(t // 2, S)],
                               start=True, stop=True)
            mm.then_inc(p.sem, p.tick("cm"))
            pe.wait_ge(s_a.sem, s_a.at("cm1"))
            pe.wait_ge(s_v.sem, s_v.at("gated"))
            for half in range(2):
                for b in range(B // 2 * half, B // 2 * (half + 1)):
                    for j in range(2):
                        for i in range(2):
                            mm = pe.transpose(ps[:, b, bass.ds(S * j + P * i, P)], ex[:, 2 * b + i, bass.ts(j, P)], ident)
                mm.then_inc(p.sem, p.tick(f"T{half}"))
            pe.wait_ge(s_a.sem, s_a.at("T0"))
            pe.wait_ge(s_v.sem, s_v.at("T1"))
            for t in range(NT):
                for j in range(2):
                    mm = pe.matmul(ps[:, t // 4, bass.ts(t % 4, P)], exT[:, t // 2, j, bass.ts(t % 2, P)],
                                   nrm[:, 2 * (t // 2) + j, :], start=(j == 0), stop=(j == 1))
            mm.then_inc(p.sem, p.tick("o"))



MH, MD = 16, 8
MG = 4
NBUCKET = 32
NREL = 768
NEVER = -1e9
NU = 2 * MH


def stage_masked_attention(nc, g, a):
    with Stage(nc, "ma") as st:
        w4 = st.sb("w4", [P, 4, P])
        w4T = st.sb("w4T", [P, 4, P])
        wqp = st.sb("wqp", [P, MG, 4, 32])
        wkp = st.sb("wkp", [P, MG, 4, 32])
        emb = st.sb("emb", [NBUCKET, MH])
        bucket = st.sb("bucket", [NBUCKET, NREL])
        rel = st.sb("rel", [MH, NREL])
        one8 = st.sb("one8", [P, 1])
        one8r = st.sb("one8r", [1, P])
        mask_u = st.sb("mask_u", [P, B * SC], U8)
        keep = st.sb("keep", [P, SC])
        off = st.sb("off", [1, SC])
        ctx_m = st.sb("ctx_m", [P, SC])
        tb = st.sb("tb", [P, 2, MH, SC])
        nrm = st.sb("nrm", [P, NT, P])
        nT = st.sb("nT", [P, T])
        stat = st.sb("stat", [P, 4, NT])
        ctxT = st.sb("ctxT", [P, B * SC])
        ctx_cur = st.sb("ctx_cur", [P, SC])
        qh = st.sb("qh", [P, MG, S])
        kh = st.sb("kh", [P, MG, SC])
        vh = st.sb("vh", [P, NK, P])
        sc = st.sb("sc", [P, 2, SC])
        pr = st.sb("pr", [P, 2, SC])
        prT = st.sb("prT", [P, 2, SC])
        low = st.sb("low", [P, NU])
        tot = st.sb("tot", [P, NU])
        rec = st.sb("rec", [P, NU])
        oh = st.sb("oh", [P, 2, P])
        ohT = st.sb("ohT", [P, 2, P])
        rel_dram = nc.dram_tensor("rel_by_distance", [MH, NREL], F32, kind="Internal").ap()
        ps, x, ctx = g.ps, g.x, g.ctx
        ident = g.ident
        sq = rows(tb[:, 0].rearrange("p h k -> p (h k)")[:, 0:T], NT)

        load = st.steps("load", ["all"])
        LOADED = 16 * 9
        rel_out = st.steps("rel_out", ["rel"])
        rel_in = st.steps("rel_in", ["tb"])
        ln_v, ln_a = st.steps("ln_v", LN_VECTOR), st.steps("ln_a", ["root"])
        pre_p = st.steps("pre_p", ["w4T", "rel", "nT", "ctx0", "ctx1"])
        pre_v = st.steps("pre_v", ["pad_q", "pad_k", "w4T", "wqp", "wkp", "rel", "ctx1"])
        pre_a = st.steps("pre_a", ["nT", "ctx0"])
        at_g = st.steps("at_g", ["keep", "off", "ctx_cur", "masked"], ahead=1)
        at_p = st.steps("at_p", ["q", "v", "k0", "k1", "S0", "S1"]
                        + [n for u in range(NU) for n in ([f"S{u + 2}"] if u + 2 < NU else []) + [f"T{u}"]
                           + ([f"O{u - 1}"] if u else [])] + [f"O{NU - 1}", "oT", "out"], ahead=1)
        at_a = st.steps("at_a", ["q", "v"]
                        + [n for u in range(NU) for n in [f"E{u}"] + ([f"T{u - 1}"] if u % 2 else [])] + ["oT"], ahead=1)
        at_v = st.steps("at_v", ["k0", "k1"]
                        + [n for u in range(NU) for n in [f"M{u}"] + ([f"T{u - 1}"] if u and u % 2 == 0 else [])]
                        + [f"T{NU - 1}", "rec", "o", "x"], ahead=1)

        passed_g, passed_v = st.steps("passed_g", ["keep"]).sem, st.steps("passed_v", ["score"]).sem

        block = st.block()

        @block.sync
        def _(sp):
            for dst, src in (
                (w4[:, 0, :], a["L1_xattn_Wq"]), (w4[:, 1, :], a["L1_xattn_Wk"]), (w4[:, 2, :], a["L1_xattn_Wv"]),
                (w4[:, 3, :], a["L1_xattn_Wo"]), (emb[:], a["L1_xattn_rel_emb"]), (bucket[:], a["bucket"]),
                (one8[:], a["one8"].unsqueeze(1)), (one8r[:], a["one8"].unsqueeze(0)),
                (mask_u[:], a["mask_Bx1x1xS2_bk0"].rearrange("b x y s -> (b x y s)").partition_broadcast(P)),
            ):
                sp.dma_start(dst, src).then_inc(load.sem, 16)
            sp.wait_ge(pre_v.sem, pre_v.at("rel"))
            sp.dma_start(rel_dram, rel[:]).then_inc(rel_out.sem, 16)
            sp.wait_ge(rel_out.sem, 16)
            sp.wait_ge(ln_v.sem, ln_v.at("squares"))
            for i in range(2):
                at = bass.AP(rel_dram.tensor, P * i, [[1, P], [NREL, MH], [1, SC]])
                sp.dma_start(tb[:, i], at).then_inc(rel_in.sem, 16)

        @block.gpsimd
        def _(pool):
            backwards = lambda v: bass.AP(v[:].tensor, SC - 1, [[SC, P], [-1, SC]])
            pool.sem_inc(at_g.sem, at_g.at("masked", -1))
            pool.wait_ge(load.sem, LOADED)
            pool.wait_ge(pre_a.sem, pre_a.at("ctx0"))
            pool.wait_ge(pre_v.sem, pre_v.at("ctx1"))
            with pool.Fori(0, B) as b:
                pool.wait_ge(at_p.sem, at_p.at("k1", b - 1))
                pool.tensor_copy(backwards(keep), mask_u[:, bass.ds(b * SC, SC)]).then_inc(at_g.sem, at_g.tick("keep"))
                pool.wait_ge(at_g.sem, at_g.at("keep", b))
                pool.sem_inc(passed_g, 1)
                pool.tensor_scalar(off[:], keep[0:1, :], NEVER, -NEVER, ALU.mult, ALU.add) \
                    .then_inc(at_g.sem, at_g.tick("off"))
                pool.tensor_copy(backwards(ctx_cur), ctxT[:, bass.ds(b * SC, SC)]).then_inc(at_g.sem, at_g.tick("ctx_cur"))
                pool.wait_ge(at_g.sem, at_g.at("ctx_cur", b))
                pool.tensor_tensor(ctx_m[:], ctx_cur[:], keep[:], ALU.mult).then_inc(at_g.sem, at_g.tick("masked"))

        @block.scalar
        def _(act):
            layernorm_root(act, ln_v, ln_a, stat)
            act.wait_ge(pre_p.sem, pre_p.at("nT"))
            act.activation(nT[:], banks(ps, 4, 8), ACT.Copy).then_inc(pre_a.sem, pre_a.tick("nT"))
            act.wait_ge(pre_p.sem, pre_p.at("ctx0"))
            act.activation(ctxT[:, 0:T], banks(ps, 0, 4), ACT.Copy).then_inc(pre_a.sem, pre_a.tick("ctx0"))
            act.sem_inc(at_a.sem, at_a.at("oT", -1))
            with act.Fori(0, B) as b:
                act.wait_ge(at_p.sem, at_p.at("q", b))
                act.activation(qh[:].rearrange("p g s -> p (g s)"), banks(ps, 0, 2), ACT.Identity, scale=-MD ** -0.5,
                               bias=one8[:, 0:1]).then_inc(at_a.sem, at_a.tick("q"))
                act.wait_ge(at_p.sem, at_p.at("v", b))
                act.activation(vh[:].rearrange("p n d -> p (n d)"), ps[:, 6, :], ACT.Copy).then_inc(at_a.sem, at_a.tick("v"))

                def move(u):
                    act.wait_ge(at_p.sem, at_p.at(f"T{u}", b))
                    act.activation(prT[:, u % 2, :], ps[:, 3 + u % 2, :], ACT.Copy).then_inc(at_a.sem, at_a.tick(f"T{u}"))

                for u in range(NU):
                    act.wait_ge(at_v.sem, at_v.at(f"M{u}", b))
                    if u >= 2:
                        act.wait_ge(at_p.sem, at_p.at(f"T{u - 2}", b))
                    act.activation(pr[:, u % 2, :], sc[:, u % 2, :], ACT.Exp, scale=-1.0, bias=low[:, u:u + 1],
                                   accum_out=tot[:, u:u + 1]).then_inc(at_a.sem, at_a.tick(f"E{u}"))
                    if u % 2:
                        if u >= 3:
                            act.wait_ge(at_p.sem, at_p.at(f"O{u - 3}", b))
                        move(u - 1)
                act.wait_ge(at_p.sem, at_p.at("oT", b))
                act.activation(ohT[:].rearrange("p i d -> p (i d)"), ps[:, 6, 0:2 * P], ACT.Copy) \
                   .then_inc(at_a.sem, at_a.tick("oT"))

        @block.vector
        def _(dve):
            dve.memset(wqp[:], 0.0).then_inc(pre_v.sem, pre_v.tick("pad_q"))
            dve.memset(wkp[:], 0.0).then_inc(pre_v.sem, pre_v.tick("pad_k"))
            dve.wait_ge(pre_p.sem, pre_p.at("w4T"))
            dve.tensor_copy(w4T[:].rearrange("p i d -> p (i d)"), ps[:, 0, :]).then_inc(pre_v.sem, pre_v.tick("w4T"))
            dve.wait_ge(pre_v.sem, pre_v.at("w4T"))
            for i, (name, w) in enumerate((("wqp", wqp), ("wkp", wkp))):
                dve.tensor_copy(w[:].rearrange("p g r c -> p (g r) c")[:, :, 0:MD],
                                w4T[:, i, :].rearrange("p (h d) -> p h d", h=MH)).then_inc(pre_v.sem, pre_v.tick(name))
            dve.wait_ge(pre_p.sem, pre_p.at("rel"))
            dve.tensor_scalar(rel[:], banks(ps, 1, 3)[0:MH, 0:NREL], -1.0, None, ALU.mult) \
               .then_inc(pre_v.sem, pre_v.tick("rel"))
            layernorm_vector(dve, ln_v, ln_a, x[:], nrm[:], sq, stat[:], NT)
            dve.wait_ge(pre_p.sem, pre_p.at("ctx1"))
            dve.tensor_copy(ctxT[:, T:2 * T], banks(ps, 4, 8)).then_inc(pre_v.sem, pre_v.tick("ctx1"))
            dve.sem_inc(at_v.sem, at_v.at("x", -1))
            dve.wait_ge(rel_in.sem, 32)
            with dve.Fori(0, B) as b:
                dve.wait_ge(at_p.sem, at_p.at("k0", b))
                dve.tensor_copy(kh[:, 0:3, :].rearrange("p g s -> p (g s)"), banks(ps, 2, 5)) \
                   .then_inc(at_v.sem, at_v.tick("k0"))
                dve.wait_ge(at_p.sem, at_p.at("k1", b))
                dve.tensor_copy(kh[:, 3, :], ps[:, 7, :]).then_inc(at_v.sem, at_v.tick("k1"))

                def move(u):
                    dve.wait_ge(at_p.sem, at_p.at(f"T{u}", b))
                    if u >= 2:
                        dve.wait_ge(at_p.sem, at_p.at(f"O{u - 2}", b))
                    dve.tensor_copy(prT[:, u % 2, :], ps[:, 3 + u % 2, :]).then_inc(at_v.sem, at_v.tick(f"T{u}"))

                for u in range(NU):
                    dve.wait_ge(at_p.sem, at_p.at(f"S{u}", b))
                    dve.wait_ge(at_a.sem, at_a.at(f"E{(u - 2) % NU}", b - (u < 2)))
                    dve.sem_inc(passed_v, 1)
                    dve.tensor_tensor_reduce(sc[:, u % 2, :], ps[:, u % 3, :], tb[:, u % 2, u // 2, :], 1.0, 3.0e38,
                                             ALU.add, ALU.min, low[:, u:u + 1]).then_inc(at_v.sem, at_v.tick(f"M{u}"))
                    if u and u % 2 == 0:
                        move(u - 1)
                move(NU - 1)
                dve.wait_ge(at_p.sem, at_p.at(f"O{NU - 1}", b))
                dve.reciprocal(rec[:], tot[:]).then_inc(at_v.sem, at_v.tick("rec"))
                dve.wait_ge(at_v.sem, at_v.at("rec", b))
                dve.tensor_tensor(oh[:].rearrange("p i (h d) -> p i h d", h=MH),
                                  ps[:, 5, 0:2 * P].rearrange("p (i h d) -> p i h d", i=2, h=MH),
                                  rec[:].rearrange("p (h i) -> p i h", i=2).unsqueeze(3).to_broadcast([P, 2, MH, MD]),
                                  ALU.mult).then_inc(at_v.sem, at_v.tick("o"))
                dve.wait_ge(at_p.sem, at_p.at("out", b))
                xb = x[:, bass.ds(2 * b, 2), :]
                dve.tensor_tensor(xb, rows(ps[:, 7, 0:2 * P], 2), xb, ALU.add).then_inc(at_v.sem, at_v.tick("x"))

        @block.tensor
        def _(pe):
            pe.wait_ge(load.sem, LOADED)
            for i in range(4):
                mm = pe.transpose(ps[:, 0, bass.ts(i, P)], w4[:, i, :], ident)
            mm.then_inc(pre_p.sem, pre_p.tick("w4T"))
            pe.matmul(ps[0:MH, 1, :], emb[:], bucket[:, 0:BLK], start=True, stop=True)
            pe.matmul(ps[0:MH, 2, 0:NREL - BLK], emb[:], bucket[:, BLK:NREL], start=True, stop=True) \
              .then_inc(pre_p.sem, pre_p.tick("rel"))
            pe.wait_ge(ln_v.sem, ln_v.at("normal"))
            for t in range(NT):
                mm = pe.transpose(ps[:, 4 + t // 4, bass.ts(t % 4, P)], nrm[:, t, :], ident)
            mm.then_inc(pre_p.sem, pre_p.tick("nT"))
            for t in range(NT):
                mm = pe.transpose(ps[:, t // 4, bass.ts(t % 4, P)], ctx[:, t, :], ident)
            mm.then_inc(pre_p.sem, pre_p.tick("ctx0"))
            pe.wait_ge(pre_a.sem, pre_a.at("nT"))
            for t in range(NT):
                mm = pe.transpose(ps[:, 4 + t // 4, bass.ts(t % 4, P)], ctx[:, NT + t, :], ident)
            mm.then_inc(pre_p.sem, pre_p.tick("ctx1"))
            pe.sem_inc(at_p.sem, at_p.at("out", -1))
            pe.wait_ge(pre_a.sem, pre_a.at("ctx0"))
            pe.wait_ge(pre_v.sem, pre_v.at("ctx1"))

            def scores(u, b):
                h, i = u // 2, u % 2
                if u >= 3:
                    pe.wait_ge(at_v.sem, at_v.at(f"M{u - 3}", b))
                r = bass.ds(32 * (h % 4), MD + 1)
                pe.matmul(ps[:, u % 3, :], qh[r, h // 4, bass.ts(i, P)], kh[r, h // 4, :], start=True, stop=True) \
                  .then_inc(at_p.sem, at_p.tick(f"S{u}"))

            def output(u, b):
                h, i = u // 2, u % 2
                pe.wait_ge(at_v.sem, at_v.at(f"T{u}", b)) if u % 2 else pe.wait_ge(at_a.sem, at_a.at(f"T{u}", b))
                for n in range(NK):
                    mm = pe.matmul(ps[:, 5, bass.ds(P * i + MD * h, MD)], prT[:, u % 2, bass.ts(n, P)],
                                   vh[:, n, bass.ts(h, MD)], start=(n == 0), stop=(n == NK - 1))
                mm.then_inc(at_p.sem, at_p.tick(f"O{u}"))

            with pe.Fori(0, B) as b:
                pe.wait_ge(at_v.sem, at_v.at("x", b - 1))
                for gr in range(MG):
                    mm = pe.matmul(ps[:, gr // 2, bass.ts(gr % 2, S)], wqp[:, gr].rearrange("p r c -> p (r c)"),
                                   nT[:, bass.ds(b * S, S)], start=True, stop=True)
                mm.then_inc(at_p.sem, at_p.tick("q"))
                pe.wait_ge(at_a.sem, at_a.at("oT", b - 1))
                pe.wait_ge(at_g.sem, at_g.at("ctx_cur", b))
                for n in range(NK):
                    mm = pe.matmul(ps[:, 6, bass.ts(n, P)], ctx_cur[:, bass.ts(n, P)], w4T[:, 2, :], start=True, stop=True)
                mm.then_inc(at_p.sem, at_p.tick("v"))
                pe.wait_ge(at_g.sem, at_g.at("masked", b))
                for gr, bank in enumerate((2, 3, 4, 7)):
                    pe.matmul(ps[:, bank, :], wkp[:, gr].rearrange("p r c -> p (r c)"), ctx_m[:], start=True, stop=False)
                    mm = pe.matmul(ps[:, bank, :], one8r[:], off[:], start=False, stop=True)
                    if gr == 2:
                        mm.then_inc(at_p.sem, at_p.tick("k0"))
                mm.then_inc(at_p.sem, at_p.tick("k1"))
                pe.wait_ge(at_a.sem, at_a.at("v", b))
                pe.wait_ge(at_v.sem, at_v.at("k1", b))
                scores(0, b)
                scores(1, b)
                for u in range(NU):
                    if u + 2 < NU:
                        scores(u + 2, b)
                    pe.wait_ge(at_a.sem, at_a.at(f"E{u}", b))
                    if u >= 2:
                        pe.wait_ge(at_v.sem, at_v.at(f"T{u - 2}", b)) if u % 2 else \
                            pe.wait_ge(at_a.sem, at_a.at(f"T{u - 2}", b))
                    for n in range(NK):
                        mm = pe.transpose(ps[:, 3 + u % 2, bass.ts(n, P)], pr[:, u % 2, bass.ts(n, P)], ident)
                    mm.then_inc(at_p.sem, at_p.tick(f"T{u}"))
                    if u:
                        output(u - 1, b)
                output(NU - 1, b)
                pe.wait_ge(at_v.sem, at_v.at("o", b))
                for i in range(2):
                    mm = pe.transpose(ps[:, 6, bass.ts(i, P)], oh[:, i, :], ident)
                mm.then_inc(at_p.sem, at_p.tick("oT"))
                pe.wait_ge(at_a.sem, at_a.at("oT", b))
                for i in range(2):
                    mm = pe.matmul(ps[:, 7, bass.ts(i, P)], ohT[:, i, :], w4T[:, 3, :], start=True, stop=True)
                mm.then_inc(at_p.sem, at_p.tick("out"))



ACT_ONE, W_ONE = 16.0, 64.0
MAGIC = 1.5 * 2.0 ** 23
QMIN, QMAX = -128.0, 127.0


def stage_quantized(nc, g, a):
    with Stage(nc, "qu") as st:
        w1 = st.sb("w1", [P, NJ, P])
        w2 = st.sb("w2", [P, HID])
        w1q = st.sb("w1q", [P, HID], BF16)
        w2q = st.sb("w2q", [P, NJ, P], BF16)
        b1 = st.sb("b1", [P, NJ])
        b2 = st.sb("b2", [P, P])
        nrm = st.sb("nrm", [P, NT, P])
        sq = st.sb("sq", [P, NT, P])
        stat = st.sb("stat", [P, 4, NT])
        xq = st.sb("xq", [P, T], BF16)
        hr = st.sb("hr", [P, 2, BLK])
        hq = st.sb("hq", [P, NB, NJ, BLK], BF16)
        ps, x = g.ps, g.x
        ident = g.ident

        load = st.steps("load", ["all"])
        LOADED = 16 * (3 + NJ)
        ln_v, ln_a = st.steps("ln_v", LN_VECTOR), st.steps("ln_a", ["root"])
        quant = [f"{n}_{s}" for n in ("w1", "w2", "b1", "b2") for s in ("up", "round", "clip")]
        q_v = st.steps("q_v", quant + ["b1", "b2", "w1T", "x_up", "x_round", "x_clip"])
        q_g = st.steps("q_g", ["x_bias"])
        q_a = st.steps("q_a", ["w2T", "xT"])
        q_p = st.steps("q_p", ["w1T", "w2T", "xT"])
        units = [(b, j) for b in range(NB) for j in range(NJ)]
        h_p = st.steps("h_p", [f"h{b}{j}" for b, j in units])
        h_a = st.steps("h_a", [f"r{b}{j}" for b, j in units])
        h_v = st.steps("h_v", [f"{n}{b}{j}" for b, j in units for n in ("m", "q")])
        o_p = st.steps("o_p", [f"o{b}" for b in range(NB)])
        o_v = st.steps("o_v", [f"x{b}" for b in range(NB)])

        block = st.block()

        @block.sync
        def _(sp):
            sp.dma_start(w1[:], a["L1_ffn_w1"].rearrange("(j p) d -> p j d", p=P)).then_inc(load.sem, 16)
            sp.dma_start(w2[:], a["L1_ffn_w2"]).then_inc(load.sem, 16)
            for j in range(NJ):
                sp.dma_start(b1[:, j:j + 1], a["L1_ffn_b1"][P * j:P * (j + 1)].unsqueeze(1)).then_inc(load.sem, 16)
            sp.dma_start(b2[:], a["L1_ffn_b2"].partition_broadcast(P)).then_inc(load.sem, 16)

        @block.gpsimd
        def _(pool):
            pool.wait_ge(q_v.sem, q_v.at("b2"))
            pool.wait_ge(ln_v.sem, ln_v.at("centred"))
            pool.tensor_tensor(x[:], x[:], b2[:].unsqueeze(1).to_broadcast([P, NT, P]), ALU.add) \
                .then_inc(q_g.sem, q_g.tick("x_bias"))

        @block.scalar
        def _(act):
            layernorm_root(act, ln_v, ln_a, stat)
            act.wait_ge(q_p.sem, q_p.at("w2T"))
            act.activation(w2q[:].rearrange("p j d -> p (j d)"), ps[:, 1, :], ACT.Copy).then_inc(q_a.sem, q_a.tick("w2T"))
            act.wait_ge(q_p.sem, q_p.at("xT"))
            act.activation(xq[:], banks(ps, 4, 8), ACT.Copy).then_inc(q_a.sem, q_a.tick("xT"))
            for u, (b, j) in enumerate(units):
                act.wait_ge(h_p.sem, h_p.at(f"h{b}{j}"))
                if u >= 2:
                    act.wait_ge(h_v.sem, h_v.at("q%d%d" % units[u - 2]))
                act.activation(hr[:, u % 2, :], ps[:, u % 4, :], ACT.Relu, bias=b1[:, j:j + 1], scale=1 / W_ONE) \
                   .then_inc(h_a.sem, h_a.tick(f"r{b}{j}"))

        @block.vector
        def _(dve):
            def quantize(name, v, one):
                dve.tensor_scalar(v, v, one, None, ALU.mult).then_inc(q_v.sem, q_v.tick(f"{name}_up"))
                dve.wait_ge(q_v.sem, q_v.at(f"{name}_up"))
                dve.tensor_scalar(v, v, MAGIC, MAGIC, ALU.add, ALU.subtract).then_inc(q_v.sem, q_v.tick(f"{name}_round"))
                dve.wait_ge(q_v.sem, q_v.at(f"{name}_round"))
                dve.tensor_scalar(v, v, QMIN, QMAX, ALU.max, ALU.min).then_inc(q_v.sem, q_v.tick(f"{name}_clip"))

            dve.wait_ge(load.sem, LOADED)
            quantize("w1", w1[:], W_ONE)
            quantize("w2", w2[:], W_ONE)
            quantize("b1", b1[:], W_ONE)
            quantize("b2", b2[:], W_ONE)
            dve.wait_ge(q_v.sem, q_v.at("b2_clip"))
            dve.tensor_scalar(b1[:], b1[:], ACT_ONE / W_ONE, None, ALU.mult).then_inc(q_v.sem, q_v.tick("b1"))
            dve.tensor_scalar(b2[:], b2[:], 1 / W_ONE, None, ALU.mult).then_inc(q_v.sem, q_v.tick("b2"))
            dve.wait_ge(q_p.sem, q_p.at("w1T"))
            dve.tensor_copy(w1q[:], ps[:, 0, :]).then_inc(q_v.sem, q_v.tick("w1T"))
            layernorm_vector(dve, ln_v, ln_a, x[:], nrm[:], sq[:], stat[:], NT)
            dve.wait_ge(ln_v.sem, ln_v.at("normal"))
            quantize("x", nrm[:], ACT_ONE)
            for u, (b, j) in enumerate(units):
                dve.wait_ge(h_a.sem, h_a.at(f"r{b}{j}"))
                dve.tensor_scalar(hr[:, u % 2, :], hr[:, u % 2, :], QMAX, MAGIC, ALU.min, ALU.add) \
                   .then_inc(h_v.sem, h_v.tick(f"m{b}{j}"))
                dve.wait_ge(h_v.sem, h_v.at(f"m{b}{j}"))
                dve.tensor_scalar(hq[:, b, j, :], hr[:, u % 2, :], MAGIC, None, ALU.subtract) \
                   .then_inc(h_v.sem, h_v.tick(f"q{b}{j}"))
            dve.wait_ge(q_g.sem, q_g.at("x_bias"))
            for b in range(NB):
                dve.wait_ge(o_p.sem, o_p.at(f"o{b}"))
                xb = x[:, 4 * b:4 * b + 4, :].rearrange("p t d -> p (t d)")
                dve.scalar_tensor_tensor(xb, ps[:, 4 + b, :], 1 / (ACT_ONE * W_ONE), xb, ALU.mult, ALU.add) \
                   .then_inc(o_v.sem, o_v.tick(f"x{b}"))

        @block.tensor
        def _(pe):
            pe.wait_ge(q_v.sem, q_v.at("w2_clip"))
            for j in range(NJ):
                mm = pe.transpose(ps[:, 0, bass.ts(j, P)], w1[:, j, :], ident)
            mm.then_inc(q_p.sem, q_p.tick("w1T"))
            for j in range(NJ):
                mm = pe.transpose(ps[:, 1, bass.ts(j, P)], w2[:, bass.ts(j, P)], ident)
            mm.then_inc(q_p.sem, q_p.tick("w2T"))
            pe.wait_ge(q_v.sem, q_v.at("x_clip"))
            for t in range(NT):
                mm = pe.transpose(ps[:, 4 + t // 4, bass.ts(t % 4, P)], nrm[:, t, :], ident)
            mm.then_inc(q_p.sem, q_p.tick("xT"))
            pe.wait_ge(q_a.sem, q_a.at("xT"))
            pe.wait_ge(q_v.sem, q_v.at("w1T"))

            def up(u):
                b, j = units[u]
                if u >= 4:
                    pe.wait_ge(h_a.sem, h_a.at("r%d%d" % units[u - 4]))
                pe.matmul(ps[:, u % 4, :], w1q[:, bass.ts(j, P)], xq[:, bass.ts(b, BLK)], start=True, stop=True) \
                  .then_inc(h_p.sem, h_p.tick(f"h{b}{j}"))

            def down(b):
                pe.wait_ge(h_v.sem, h_v.at(f"q{b}{NJ - 1}"))
                for i in range(4):
                    for j in range(NJ):
                        mm = pe.matmul(ps[:, 4 + b, bass.ts(i, P)], hq[:, b, j, bass.ts(i, P)], w2q[:, j, :],
                                       start=(j == 0), stop=(j == NJ - 1))
                mm.then_inc(o_p.sem, o_p.tick(f"o{b}"))

            for u in range(len(units)):
                up(u)
                if u % NJ == NJ - 1 and u > NJ:
                    down(u // NJ - 1)
            down(NB - 1)



class Shared:
    pass


def decoder(nc, a, out):
    g = Shared()
    with ExitStack() as stack:
        g.ps = stack.enter_context(nc.psum_tensor("ps", [P, 8, BLK], F32))
        g.x = stack.enter_context(nc.sbuf_tensor("x", [P, NT, P], F32))
        g.ctx = stack.enter_context(nc.sbuf_tensor("ctx", [P, B * SC // P, P], F32))
        const = stack.enter_context(nc.sbuf_tensor("const", [P, 2 * P], F32))
        rep8 = stack.enter_context(nc.sbuf_tensor("rep8", [8, P], F32))
        ones = stack.enter_context(nc.sbuf_tensor("ones", [P, P], F32))
        g.ident, g.bd8, g.rep8, g.ones = const[:, 0:P], const[:, P:2 * P], rep8[:], ones[:]
        x_dram = a["x"].rearrange("b (n p) d -> p (b n) d", p=P)
        with Stage(nc, "start") as st:
            loaded = st.steps("loaded", ["all"])
            made = st.steps("made", ["ones"])
            block = st.block()

            @block.sync
            def _(sp):
                sp.dma_start(g.x[:], x_dram).then_inc(loaded.sem, 16)
                sp.dma_start(const[:], a["const"]).then_inc(loaded.sem, 16)
                sp.dma_start(rep8[:], a["rep8"]).then_inc(loaded.sem, 16)
                sp.wait_ge(loaded.sem, 48)

            @block.vector
            def _(dve):
                dve.memset(ones[:], 1.0).then_inc(made.sem, made.tick("ones"))
                dve.wait_ge(made.sem, 1)

        stages = [stage_fast_weights, stage_cross_attention, stage_experts, stage_gated, stage_masked_attention, stage_quantized]
        for stage in stages[:LAST_STAGE]:
            stage(nc, g, a)
        with Stage(nc, "end") as st:
            stored = st.steps("stored", ["x"])
            block = st.block()

            @block.sync
            def _(sp):
                sp.dma_start(out.rearrange("b (n p) d -> p (b n) d", p=P), g.x[:]).then_inc(stored.sem, 16)
                sp.wait_ge(stored.sem, 16)


def constants():
    p = np.arange(P)
    const = np.concatenate([np.eye(P), p[:, None] // 8 == p[None, :] // 8], axis=1).astype(np.float32)
    rep8 = (np.arange(8)[:, None] == p[None, :] % 8).astype(np.float32)
    lower = np.tril(np.ones((8, 8), np.float32), -1).reshape(64)
    n = np.maximum(np.arange(NREL) - (SC - 1), 0)
    exact = NBUCKET // 2
    large = exact + (np.log(n.astype(np.float32) / exact + 1e-9) / math.log(128 / exact) * exact).astype(np.int32)
    of = np.where(n < exact, n, np.minimum(large, NBUCKET - 1))
    bucket = (np.arange(NBUCKET)[:, None] == of[None, :]).astype(np.float32)
    one8 = (p % 32 == MD).astype(np.float32)
    return {"const": const, "rep8": rep8, "lower": lower, "bucket": bucket, "one8": one8}


def kernel(**inputs):
    import numpy as _np
    import concourse.bacc as _bacc
    from concourse import mybir as _mybir
    from concourse.bass_utils import run_bass_kernel_spmd as _run

    nc = _bacc.Bacc("TRN2", target_bir_lowering=False, num_devices=1)
    arrays, args = {}, {}
    for name, value in list(inputs.items()) + list(constants().items()):
        v = _np.ascontiguousarray(value)
        arrays[f"in_{name}_dram"] = v
        args[name] = nc.dram_tensor(f"in_{name}_dram", v.shape, _mybir.dt.from_np(v.dtype), kind="ExternalInput").ap()
    out = nc.dram_tensor("out_0_dram", (B, S, P), F32, kind="ExternalOutput").ap()
    decoder(nc, args, out)
    r = _run(nc, [arrays], core_ids=[0])
    return r.results[0]["out_0_dram"]
```

```python
import math
from contextlib import ExitStack

import numpy as np

import concourse.bass as bass
from concourse import mybir

F32 = mybir.dt.float32
BF16 = mybir.dt.bfloat16
U8 = mybir.dt.uint8
ALU = mybir.AluOpType
ACT = mybir.ActivationFunctionType
AX = mybir.AxisListType

LAST_STAGE = 6

P = 128
B, S = 8, 256
T = B * S
NT = T // P
BLK = 512
NB = T // BLK
SC = 512
HID = 512
NJ = HID // P
LN_EPS = 1e-5


class Steps:

    def __init__(self, sem, names, ahead=0):
        self.sem, self.names, self.ahead = sem, list(names), ahead
        assert len(set(self.names)) == len(self.names)
        self.next = 0

    def at(self, name, t=0):
        return (t + self.ahead) * len(self.names) + self.names.index(name) + 1

    def tick(self, name):
        assert self.names[self.next % len(self.names)] == name, (name, self.names[self.next % len(self.names)])
        self.next += 1
        return 1


def bcast(stat, n, width=P):
    return stat.unsqueeze(2).to_broadcast([P, n, width])


def rows(flat, n, width=P):
    return flat.rearrange("p (n d) -> p n d", n=n)


def banks(ps, a, b):
    return ps[:, a:b, :].rearrange("p a b -> p (a b)")


LN_VECTOR = ["sum", "mean", "centred", "square", "squares", "variance", "rstd", "normal"]


def layernorm_vector(dve, vec, root, src, dst, sq, st, n):
    at = vec.at
    dve.tensor_reduce(st[:, 0, :], src, AX.X, ALU.add).then_inc(vec.sem, vec.tick("sum"))
    dve.wait_ge(vec.sem, at("sum"))
    dve.tensor_scalar(st[:, 1, :], st[:, 0, :], 1.0 / P, None, ALU.mult).then_inc(vec.sem, vec.tick("mean"))
    dve.wait_ge(vec.sem, at("mean"))
    dve.tensor_tensor(dst, src, bcast(st[:, 1, :], n), ALU.subtract).then_inc(vec.sem, vec.tick("centred"))
    dve.wait_ge(vec.sem, at("centred"))
    dve.tensor_tensor(sq, dst, dst, ALU.mult).then_inc(vec.sem, vec.tick("square"))
    dve.wait_ge(vec.sem, at("square"))
    dve.tensor_reduce(st[:, 2, :], sq, AX.X, ALU.add).then_inc(vec.sem, vec.tick("squares"))
    dve.wait_ge(vec.sem, at("squares"))
    dve.tensor_scalar(st[:, 2, :], st[:, 2, :], 1.0 / P, LN_EPS, ALU.mult, ALU.add) \
       .then_inc(vec.sem, vec.tick("variance"))
    dve.wait_ge(root.sem, root.at("root"))
    dve.reciprocal(st[:, 3, :], st[:, 3, :]).then_inc(vec.sem, vec.tick("rstd"))
    dve.wait_ge(vec.sem, at("rstd"))
    dve.tensor_tensor(dst, dst, bcast(st[:, 3, :], n), ALU.mult).then_inc(vec.sem, vec.tick("normal"))


def layernorm_root(act, vec, root, st):
    act.wait_ge(vec.sem, vec.at("variance"))
    act.activation(st[:, 3, :], st[:, 2, :], ACT.Sqrt).then_inc(root.sem, root.tick("root"))


class Stage:

    def __init__(self, nc, name):
        self.nc, self.name, self.stack = nc, name, ExitStack()

    def __enter__(self):
        return self

    def __exit__(self, *failed):
        return self.stack.__exit__(*failed)

    def sb(self, name, shape, dt=F32):
        return self.stack.enter_context(self.nc.sbuf_tensor(f"{self.name}_{name}", shape, dt))

    def steps(self, name, names, ahead=0):
        return Steps(self.stack.enter_context(self.nc.semaphore(f"{self.name}_{name}")), names, ahead)

    def block(self):
        return self.stack.enter_context(self.nc.Block())



NS_A, NS_B, NS_C = 3.4445, -4.775, 2.0315
NS_ITERS = 5
TTT_STEPS = 2
LR = 0.1
NS_GUARD = 1e-7 * T * P / 2


def stage_fast_weights(nc, g, a):
    with Stage(nc, "fw") as st:
        w_qkv = st.sb("w_qkv", [P, 3 * P])
        b_qk = st.sb("b_qk", [P, 2])
        b_v = st.sb("b_v", [P, P])
        b_o = st.sb("b_o", [P, P])
        w_o = st.sb("w_o", [P, P])
        head8 = st.sb("head8", [8, 4])
        hd = st.sb("hd", [P, 4])
        gate = st.sb("gate", [P, HID])
        val = st.sb("val", [P, HID])
        proj = st.sb("proj", [P, NJ, P])
        projT = st.sb("projT", [P, HID])
        nrm = st.sb("nrm", [P, NT, P])
        nT = st.sb("nT", [P, T])
        sq = st.sb("sq", [P, T])
        stat = st.sb("stat", [P, 4, NT])
        qT = st.sb("qT", [P, T])
        kk = st.sb("kk", [P, NT, 2, P])
        v = st.sb("v", [P, NT, P])
        qn = st.sb("qn", [P, T])
        kn = st.sb("kn", [P, T])
        kT_cur = st.sb("kT_cur", [P, P])
        k_cur = st.sb("k_cur", [P, P])
        sg = st.sb("sg", [P, 2, HID])
        sw = st.sb("sw", [P, 2, HID])
        h = st.sb("h", [P, 2, HID])
        vs = st.sb("vs", [P, 2, HID])
        u = st.sb("u", [P, 2, HID])
        e = st.sb("e", [P, 2, HID])
        dV = st.sb("dV", [P, 2, HID])
        dG = st.sb("dG", [P, 2, HID])
        hT = st.sb("hT", [P, 2, HID])
        dp = st.sb("dp", [P, 2, P])
        dpT = st.sb("dpT", [P, 2, P])
        X = st.sb("X", [P, 3, HID])
        XT = st.sb("XT", [P, 3, HID])
        Am = st.sb("Am", [P, 3, P])
        bA = st.sb("bA", [P, 3, P])
        Bm = st.sb("Bm", [P, 3, P])
        aI = st.sb("aI", [P, P])
        fro = st.sb("fro", [P, 3])
        frn = st.sb("frn", [P, 3])
        wo2 = st.sb("wo2", [P, NJ, P])
        fh = st.sb("fh", [P, NJ, BLK])
        fs = st.sb("fs", [P, 2, BLK])
        ps, x = g.ps, g.x
        ident, bd8, rep8, ones = g.ident, g.bd8, g.rep8, g.ones

        load = st.steps("load", [f"{i}" for i in range(256)])
        pre_v = st.steps("pre_v", LN_VECTOR + ["hd", "zeroed", "aI", "nT1", "nT3", "kT_raw", "k_sq", "k_guard", "k_inv", "k_unit",
                                               "kT", "v", "q_guard", "q_inv", "q_unit", "qT", "x_bias", "projT"])
        root = st.steps("root", ["root"])
        pre_a = st.steps("pre_a", ["nT0", "nT2", "qT_raw", "q_sq", "k_norm", "q_norm", "k_tok"])
        pre_p = st.steps("pre_p", ["hd", "nT0", "nT1", "nT2", "nT3", "k", "q", "k_sq", "q_sq", "v", "k_tok", "projT"])
        names = lambda *xs: [f"{n}{s}" for s in range(2) for n in xs]
        ttt_p = st.steps("ttt_p", names("gv", "grads", "hT", "pred", "dpT", "dh"), ahead=1)
        ttt_a = st.steps("ttt_a", names("sg", "vs", "hT", "dpT"), ahead=1)
        ttt_v = st.steps("ttt_v", names("sw", "h", "u", "ds", "dp", "dV", "dG"), ahead=1)
        ttt_g = st.steps("ttt_g", names("kT_cur", "k_cur", "e"), ahead=1)
        open_p = st.steps("open_p", ["opened", "last", "fro", "XT"])
        open_a = st.steps("open_a", ["fro0", "fro1", "fro2", "root", "XT0", "XT1", "XT2"])
        open_v = st.steps("open_v", ["guard", "inv", "X0", "X1", "X2"])
        ns_p = st.steps("ns_p", [f"{n}{m}" for n in ("A", "A2", "X") for m in range(3)], ahead=1)
        ns_a = st.steps("ns_a", [f"{n}{m}" for n in ("A", "X") for m in range(3)], ahead=1)
        ns_v = st.steps("ns_v", [f"{n}{m}" for n in ("bA", "B", "XT") for m in range(3)], ahead=1)
        upd_v = st.steps("upd_v", ["gate", "val", "projT", "proj"], ahead=1)
        fin_p = st.steps("fin_p", ["wo2"])
        fin_v = st.steps("fin_v", ["wo2"])
        ask_p = st.steps("ask_p", ["gv0", "gv1", "gv2", "gv3", "o"], ahead=1)
        ask_a = st.steps("ask_a", ["s0", "s1", "s2", "s3"], ahead=1)
        ask_v = st.steps("ask_v", [f"{n}{j}" for j in range(4) for n in ("sw", "h")] + ["x"], ahead=1)
        zero = st.sb("zero", [P, P])
        made_g = st.steps("made_g", ["zero"])
        zero_v = st.steps("zero_v", ["dp"])
        zero_g = st.steps("zero_g", ["k"])

        block = st.block()

        @block.sync
        def _(sp):
            for dst, src in (
                (w_qkv[:], a["L0_attn_qkv_w"]), (b_qk[:, 0:1], a["L0_attn_qkv_b"][0:P].unsqueeze(1)),
                (b_qk[:, 1:2], a["L0_attn_qkv_b"][P:2 * P].unsqueeze(1)),
                (b_v[:], a["L0_attn_qkv_b"][2 * P:3 * P].partition_broadcast(P)),
                (head8[:, 0:1], a["L0_attn_qn_scale"].unsqueeze(1)), (head8[:, 1:2], a["L0_attn_qn_bias"].unsqueeze(1)),
                (head8[:, 2:3], a["L0_attn_kn_scale"].unsqueeze(1)), (head8[:, 3:4], a["L0_attn_kn_bias"].unsqueeze(1)),
                (gate[:], a["L0_attn_ttt_gate"]), (val[:], a["L0_attn_ttt_val"]),
                (proj[:], a["L0_attn_ttt_proj"].rearrange("(j p) d -> p j d", p=P)),
                (w_o[:], a["L0_attn_proj_w"]), (b_o[:], a["L0_attn_proj_b"].partition_broadcast(P)),
            ):
                sp.dma_start(dst, src).then_inc(load.sem, 16)

        N_LOADS = 13

        @block.gpsimd
        def _(pool):
            pool.memset(zero[:], 0.0).then_inc(made_g.sem, made_g.tick("zero"))
            pool.wait_ge(made_g.sem, made_g.at("zero"))
            pool.sem_inc(ttt_g.sem, ttt_g.at("e1", -1))
            pool.wait_ge(pre_v.sem, pre_v.at("kT"))
            pool.wait_ge(pre_a.sem, pre_a.at("k_tok"))
            with pool.Fori(0, TTT_STEPS) as step:
                pool.wait_ge(upd_v.sem, upd_v.at("proj", step - 1))
                pool.tensor_tensor(k_cur[:], zero[:], zero[:], ALU.add).then_inc(zero_g.sem, zero_g.tick("k"))
                with pool.Fori(0, NT // 2) as i:
                    t = step * (NT // 2) + i
                    for s in range(2):
                        pool.wait_ge(ttt_p.sem, ttt_p.at("gv1", t - 1) if s == 0 else ttt_p.at("gv0", t))
                        pool.tensor_copy(kT_cur[:].unsqueeze(1), kk[:, bass.ds(2 * i + s, 1), 0, :]) \
                            .then_inc(ttt_g.sem, ttt_g.tick(f"kT_cur{s}"))
                        pool.wait_ge(ttt_p.sem, ttt_p.at(f"grads{s}", t))
                        pool.tensor_copy(k_cur[:].unsqueeze(1), kk[:, bass.ds(2 * i + s, 1), 1, :]) \
                            .then_inc(ttt_g.sem, ttt_g.tick(f"k_cur{s}"))
                        pool.wait_ge(ttt_v.sem, ttt_v.at(f"ds{s}", t))
                        pool.wait_ge(ttt_a.sem, ttt_a.at(f"vs{s}", t))
                        pool.tensor_tensor(e[:, s, :], u[:, s, :], vs[:, s, :], ALU.mult) \
                            .then_inc(ttt_g.sem, ttt_g.tick(f"e{s}"))

        @block.scalar
        def _(act):
            layernorm_root(act, pre_v, root, stat)
            for b in (0, 2):
                act.wait_ge(pre_p.sem, pre_p.at(f"nT{b}"))
                act.activation(nT[:, bass.ts(b, BLK)], ps[:, b, :], ACT.Copy).then_inc(pre_a.sem, pre_a.tick(f"nT{b}"))
            act.wait_ge(pre_p.sem, pre_p.at("q"))
            act.wait_ge(load.sem, 16 * N_LOADS)
            act.activation(qT[:], banks(ps, 4, 8), ACT.Identity, bias=b_qk[:, 0:1]) \
               .then_inc(pre_a.sem, pre_a.tick("qT_raw"))
            act.wait_ge(pre_a.sem, pre_a.at("qT_raw"))
            act.wait_ge(pre_v.sem, pre_v.at("normal"))
            act.activation(sq[:], qT[:], ACT.Square).then_inc(pre_a.sem, pre_a.tick("q_sq"))
            act.wait_ge(pre_p.sem, pre_p.at("k_sq"))
            act.activation(kn[:], banks(ps, 0, 4), ACT.Sqrt) \
               .then_inc(pre_a.sem, pre_a.tick("k_norm"))
            act.wait_ge(pre_p.sem, pre_p.at("q_sq"))
            act.activation(qn[:], banks(ps, 4, 8), ACT.Sqrt) \
               .then_inc(pre_a.sem, pre_a.tick("q_norm"))
            act.wait_ge(pre_p.sem, pre_p.at("k_tok"))
            act.activation(kk[:, :, 1, :], rows(banks(ps, 4, 8), NT), ACT.Copy) \
               .then_inc(pre_a.sem, pre_a.tick("k_tok"))
            act.sem_inc(ttt_a.sem, ttt_a.at("dpT1", -1))
            act.sem_inc(ns_a.sem, ns_a.at("X2", -1))
            act.sem_inc(ask_a.sem, ask_a.at("s3", -1))
            with act.Fori(0, TTT_STEPS) as step:
                with act.Fori(0, NT // 2) as i:
                    t = step * (NT // 2) + i
                    for s in range(2):
                        act.wait_ge(ttt_p.sem, ttt_p.at(f"gv{s}", t))
                        act.wait_ge(ttt_v.sem, ttt_v.at(f"u{s}", t - 1))
                        act.activation(sg[:, s, :], ps[:, 0, :], ACT.Sigmoid).then_inc(ttt_a.sem, ttt_a.tick(f"sg{s}"))
                        act.wait_ge(ttt_g.sem, ttt_g.at(f"e{s}", t - 1))
                        act.activation(vs[:, s, :], ps[:, 1, :], ACT.Copy).then_inc(ttt_a.sem, ttt_a.tick(f"vs{s}"))
                        act.wait_ge(ttt_p.sem, ttt_p.at(f"hT{s}", t))
                        act.activation(hT[:, s, :], ps[:, 2, :], ACT.Copy).then_inc(ttt_a.sem, ttt_a.tick(f"hT{s}"))
                        act.wait_ge(ttt_p.sem, ttt_p.at(f"dpT{s}", t))
                        act.activation(dpT[:, s, :], ps[:, 3, 0:P], ACT.Copy).then_inc(ttt_a.sem, ttt_a.tick(f"dpT{s}"))
                act.wait_ge(open_p.sem, open_p.at("last", step))
                for m in range(3):
                    act.activation(XT[:, m, :], ps[:, 5 + m, :], ACT.Square, accum_out=fro[:, m:m + 1]) \
                       .then_inc(open_a.sem, open_a.tick(f"fro{m}"))
                act.wait_ge(open_p.sem, open_p.at("fro", step))
                act.activation(frn[:], ps[:, 0, 0:3], ACT.Sqrt).then_inc(open_a.sem, open_a.tick("root"))
                act.wait_ge(open_p.sem, open_p.at("XT", step))
                for m in range(3):
                    act.activation(XT[:, m, :], ps[:, 1 + m, :], ACT.Copy).then_inc(open_a.sem, open_a.tick(f"XT{m}"))
                with act.Fori(0, NS_ITERS) as it:
                    n = step * NS_ITERS + it
                    for m in range(3):
                        act.wait_ge(ns_p.sem, ns_p.at(f"A{m}", n))
                        act.activation(Am[:, m, :], ps[:, m, 0:P], ACT.Copy).then_inc(ns_a.sem, ns_a.tick(f"A{m}"))
                    for m in range(3):
                        act.wait_ge(ns_p.sem, ns_p.at(f"X{m}", n))
                        act.activation(X[:, m, :], ps[:, m, :], ACT.Copy).then_inc(ns_a.sem, ns_a.tick(f"X{m}"))
            with act.Fori(0, NB) as blk:
                for j in range(NJ):
                    act.wait_ge(ask_p.sem, ask_p.at(f"gv{j}", blk))
                    act.wait_ge(ask_v.sem, ask_v.at(f"sw{(j - 2) % 4}", blk - (j < 2)))
                    act.activation(fs[:, j % 2, :], ps[:, 2 * (j % 2), :], ACT.Sigmoid) \
                       .then_inc(ask_a.sem, ask_a.tick(f"s{j}"))

        @block.vector
        def _(dve):
            layernorm_vector(dve, pre_v, root, x[:], nrm[:], rows(sq[:], NT), stat[:], NT)
            dve.wait_ge(pre_p.sem, pre_p.at("hd"))
            dve.tensor_copy(hd[:], ps[:, 7, 0:4]).then_inc(pre_v.sem, pre_v.tick("hd"))
            for buffer in (h, dV, dG):
                zeroed = dve.memset(buffer[:, 1, :], 0.0)
            zeroed.then_inc(pre_v.sem, pre_v.tick("zeroed"))
            dve.tensor_scalar(aI[:], ident, NS_A, None, ALU.mult).then_inc(pre_v.sem, pre_v.tick("aI"))
            for b in (1, 3):
                dve.wait_ge(pre_p.sem, pre_p.at(f"nT{b}"))
                dve.tensor_copy(nT[:, bass.ts(b, BLK)], ps[:, b, :]).then_inc(pre_v.sem, pre_v.tick(f"nT{b}"))
            kT = kk[:, :, 0, :]
            kn3 = rows(kn[:], NT)
            k_ps = rows(banks(ps, 0, 4), NT)
            dve.wait_ge(pre_p.sem, pre_p.at("k"))
            dve.wait_ge(load.sem, 16 * N_LOADS)
            dve.tensor_scalar(kT, k_ps, b_qk[:, 1:2], None, ALU.add).then_inc(pre_v.sem, pre_v.tick("kT_raw"))
            dve.wait_ge(pre_v.sem, pre_v.at("kT_raw"))
            dve.tensor_tensor(kn3, kT, kT, ALU.mult).then_inc(pre_v.sem, pre_v.tick("k_sq"))
            dve.wait_ge(pre_a.sem, pre_a.at("k_norm"))
            dve.tensor_scalar(kn[:], kn[:], 1e-6, None, ALU.add).then_inc(pre_v.sem, pre_v.tick("k_guard"))
            dve.wait_ge(pre_v.sem, pre_v.at("k_guard"))
            dve.reciprocal(kn[:], kn[:]).then_inc(pre_v.sem, pre_v.tick("k_inv"))
            dve.wait_ge(pre_v.sem, pre_v.at("k_inv"))
            dve.tensor_tensor(kT, kT, kn3, ALU.mult).then_inc(pre_v.sem, pre_v.tick("k_unit"))
            dve.wait_ge(pre_v.sem, pre_v.at("k_unit"))
            dve.tensor_scalar(kT, kT, hd[:, 2:3], hd[:, 3:4], ALU.mult, ALU.add) \
               .then_inc(pre_v.sem, pre_v.tick("kT"))
            dve.wait_ge(pre_p.sem, pre_p.at("v"))
            dve.tensor_tensor(v[:], k_ps, b_v[:].unsqueeze(1).to_broadcast([P, NT, P]), ALU.add) \
               .then_inc(pre_v.sem, pre_v.tick("v"))
            dve.wait_ge(pre_a.sem, pre_a.at("q_norm"))
            dve.tensor_scalar(qn[:], qn[:], 1e-6, None, ALU.add).then_inc(pre_v.sem, pre_v.tick("q_guard"))
            dve.wait_ge(pre_v.sem, pre_v.at("q_guard"))
            dve.reciprocal(qn[:], qn[:]).then_inc(pre_v.sem, pre_v.tick("q_inv"))
            dve.wait_ge(pre_v.sem, pre_v.at("q_inv"))
            dve.tensor_tensor(qT[:], qT[:], qn[:], ALU.mult).then_inc(pre_v.sem, pre_v.tick("q_unit"))
            dve.wait_ge(pre_v.sem, pre_v.at("q_unit"))
            dve.tensor_scalar(qT[:], qT[:], hd[:, 0:1], hd[:, 1:2], ALU.mult, ALU.add) \
               .then_inc(pre_v.sem, pre_v.tick("qT"))
            dve.tensor_tensor(x[:], x[:], b_o[:].unsqueeze(1).to_broadcast([P, NT, P]), ALU.add) \
               .then_inc(pre_v.sem, pre_v.tick("x_bias"))
            dve.wait_ge(pre_p.sem, pre_p.at("projT"))
            dve.tensor_copy(projT[:], ps[:, 0, :]).then_inc(pre_v.sem, pre_v.tick("projT"))
            dve.sem_inc(ttt_v.sem, ttt_v.at("dG1", -1))
            dve.sem_inc(ns_v.sem, ns_v.at("XT2", -1))
            dve.sem_inc(upd_v.sem, upd_v.at("proj", -1))
            dve.sem_inc(ask_v.sem, ask_v.at("x", -1))
            with dve.Fori(0, TTT_STEPS) as step:
                dve.memset(dp[:, 1, :], 0.0).then_inc(zero_v.sem, zero_v.tick("dp"))
                with dve.Fori(0, NT // 2) as i:
                    t = step * (NT // 2) + i
                    for s in range(2):
                        dve.wait_ge(ttt_a.sem, ttt_a.at(f"sg{s}", t))
                        dve.tensor_tensor(sw[:, s, :], ps[:, 0, :], sg[:, s, :], ALU.mult) \
                           .then_inc(ttt_v.sem, ttt_v.tick(f"sw{s}"))
                        dve.wait_ge(ttt_v.sem, ttt_v.at(f"sw{s}", t))
                        dve.wait_ge(ttt_a.sem, ttt_a.at(f"vs{s}", t))
                        dve.wait_ge(ttt_p.sem, ttt_p.at("grads1", t - 1) if s == 0 else ttt_p.at("grads0", t))
                        dve.tensor_tensor(h[:, s, :], sw[:, s, :], vs[:, s, :], ALU.mult) \
                           .then_inc(ttt_v.sem, ttt_v.tick(f"h{s}"))
                        dve.scalar_tensor_tensor(u[:, s, :], sw[:, s, :], 1.0, sg[:, s, :], ALU.subtract, ALU.mult) \
                           .then_inc(ttt_v.sem, ttt_v.tick(f"u{s}"))
                        dve.wait_ge(ttt_v.sem, ttt_v.at(f"u{s}", t))
                        dve.tensor_tensor(u[:, s, :], sw[:, s, :], u[:, s, :], ALU.subtract) \
                           .then_inc(ttt_v.sem, ttt_v.tick(f"ds{s}"))
                        dve.wait_ge(ttt_p.sem, ttt_p.at(f"pred{s}", t))
                        dve.tensor_tensor(dp[:, bass.ds(s, 1), :], ps[:, 3:4, 0:P], v[:, bass.ds(2 * i + s, 1), :],
                                          ALU.subtract).then_inc(ttt_v.sem, ttt_v.tick(f"dp{s}"))
                        dve.wait_ge(ttt_p.sem, ttt_p.at(f"dh{s}", t))
                        dve.tensor_tensor(dV[:, s, :], ps[:, 4, :], sw[:, s, :], ALU.mult) \
                           .then_inc(ttt_v.sem, ttt_v.tick(f"dV{s}"))
                        dve.wait_ge(ttt_g.sem, ttt_g.at(f"e{s}", t))
                        dve.tensor_tensor(dG[:, s, :], ps[:, 4, :], e[:, s, :], ALU.mult) \
                           .then_inc(ttt_v.sem, ttt_v.tick(f"dG{s}"))
                dve.wait_ge(open_a.sem, open_a.at("root", step))
                dve.tensor_scalar(frn[:], frn[:], NS_GUARD, None, ALU.add).then_inc(open_v.sem, open_v.tick("guard"))
                dve.wait_ge(open_v.sem, open_v.at("guard", step))
                dve.reciprocal(frn[:], frn[:]).then_inc(open_v.sem, open_v.tick("inv"))
                dve.wait_ge(open_v.sem, open_v.at("inv", step))
                for m in range(3):
                    dve.tensor_scalar(X[:, m, :], ps[:, 5 + m, :], frn[:, m:m + 1], None, ALU.mult) \
                       .then_inc(open_v.sem, open_v.tick(f"X{m}"))
                with dve.Fori(0, NS_ITERS) as it:
                    n = step * NS_ITERS + it
                    for m in range(3):
                        dve.wait_ge(ns_a.sem, ns_a.at(f"A{m}", n))
                        dve.scalar_tensor_tensor(bA[:, m, :], Am[:, m, :], NS_B, aI[:], ALU.mult, ALU.add) \
                           .then_inc(ns_v.sem, ns_v.tick(f"bA{m}"))
                    for m in range(3):
                        dve.wait_ge(ns_p.sem, ns_p.at(f"A2{m}", n))
                        dve.wait_ge(ns_v.sem, ns_v.at(f"bA{m}", n))
                        dve.scalar_tensor_tensor(Bm[:, m, :], ps[:, 3 + m, 0:P], NS_C, bA[:, m, :], ALU.mult, ALU.add) \
                           .then_inc(ns_v.sem, ns_v.tick(f"B{m}"))
                    for m in range(3):
                        dve.wait_ge(ns_p.sem, ns_p.at(f"X{m}", n))
                        dve.tensor_copy(XT[:, m, :], ps[:, 3 + m, :]).then_inc(ns_v.sem, ns_v.tick(f"XT{m}"))
                dve.wait_ge(ns_a.sem, ns_a.at("X2", step * NS_ITERS + NS_ITERS - 1))
                dve.wait_ge(ns_v.sem, ns_v.at("XT2", step * NS_ITERS + NS_ITERS - 1))
                for name, theta, d in (("gate", gate[:], X[:, 0, :]), ("val", val[:], X[:, 1, :]),
                                       ("projT", projT[:], X[:, 2, :]), ("proj", proj[:].rearrange("p j d -> p (j d)"), XT[:, 2, :])):
                    dve.scalar_tensor_tensor(theta, d, -LR, theta, ALU.mult, ALU.add) \
                       .then_inc(upd_v.sem, upd_v.tick(name))
            dve.wait_ge(fin_p.sem, fin_p.at("wo2"))
            dve.tensor_copy(wo2[:].rearrange("p j d -> p (j d)"), ps[:, 0, :]).then_inc(fin_v.sem, fin_v.tick("wo2"))
            with dve.Fori(0, NB) as blk:
                for j in range(NJ):
                    b = 2 * (j % 2)
                    dve.wait_ge(ask_a.sem, ask_a.at(f"s{j}", blk))
                    if j == 0:
                        dve.wait_ge(ask_p.sem, ask_p.at("o", blk - 1))
                    dve.tensor_tensor(fh[:, j, :], ps[:, b, :], fs[:, j % 2, :], ALU.mult) \
                       .then_inc(ask_v.sem, ask_v.tick(f"sw{j}"))
                    dve.wait_ge(ask_v.sem, ask_v.at(f"sw{j}", blk))
                    dve.tensor_tensor(fh[:, j, :], ps[:, b + 1, :], fh[:, j, :], ALU.mult) \
                       .then_inc(ask_v.sem, ask_v.tick(f"h{j}"))
                dve.wait_ge(ask_p.sem, ask_p.at("o", blk))
                xb = x[:, bass.ds(4 * blk, 4), :]
                dve.tensor_tensor(xb, rows(ps[:, 4, :], 4), xb, ALU.add).then_inc(ask_v.sem, ask_v.tick("x"))

        @block.tensor
        def _(pe):
            pe.wait_ge(load.sem, 16 * N_LOADS)
            pe.matmul(ps[:, 7, 0:4], rep8, head8[:], start=True, stop=True).then_inc(pre_p.sem, pre_p.tick("hd"))
            pe.wait_ge(pre_v.sem, pre_v.at("normal"))
            for b in range(NB):
                for i in range(4):
                    mm = pe.transpose(ps[:, b, bass.ts(i, P)], nrm[:, 4 * b + i, :], ident)
                mm.then_inc(pre_p.sem, pre_p.tick(f"nT{b}"))
            pe.wait_ge(pre_a.sem, pre_a.at("nT2"))
            pe.wait_ge(pre_v.sem, pre_v.at("nT3"))
            for name, part, b0 in (("k", 1, 0), ("q", 0, 4)):
                for b in range(NB):
                    mm = pe.matmul(ps[:, b0 + b, :], w_qkv[:, bass.ts(part, P)], nT[:, bass.ts(b, BLK)], start=True, stop=True)
                mm.then_inc(pre_p.sem, pre_p.tick(name))
            pe.wait_ge(pre_v.sem, pre_v.at("k_sq"))
            for b in range(NB):
                mm = pe.matmul(ps[:, b, :], bd8, kn[:, bass.ts(b, BLK)], start=True, stop=True)
            mm.then_inc(pre_p.sem, pre_p.tick("k_sq"))
            pe.wait_ge(pre_a.sem, pre_a.at("q_sq"))
            for b in range(NB):
                mm = pe.matmul(ps[:, 4 + b, :], bd8, sq[:, bass.ts(b, BLK)], start=True, stop=True)
            mm.then_inc(pre_p.sem, pre_p.tick("q_sq"))
            pe.wait_ge(pre_a.sem, pre_a.at("k_norm"))
            for t in range(NT):
                mm = pe.matmul(ps[:, t // 4, bass.ts(t % 4, P)], nT[:, bass.ts(t, P)], w_qkv[:, 2 * P:3 * P],
                               start=True, stop=True)
            mm.then_inc(pre_p.sem, pre_p.tick("v"))
            pe.wait_ge(pre_v.sem, pre_v.at("kT"))
            pe.wait_ge(pre_a.sem, pre_a.at("q_norm"))
            for t in range(NT):
                mm = pe.transpose(ps[:, 4 + t // 4, bass.ts(t % 4, P)], kk[:, t, 0, :], ident)
            mm.then_inc(pre_p.sem, pre_p.tick("k_tok"))
            pe.wait_ge(pre_v.sem, pre_v.at("v"))
            for j in range(NJ):
                mm = pe.transpose(ps[:, 0, bass.ts(j, P)], proj[:, j, :], ident)
            mm.then_inc(pre_p.sem, pre_p.tick("projT"))
            pe.wait_ge(pre_a.sem, pre_a.at("k_tok"))
            pe.sem_inc(ttt_p.sem, ttt_p.at("dh1", -1))
            pe.sem_inc(ns_p.sem, ns_p.at("X2", -1))
            pe.sem_inc(ask_p.sem, ask_p.at("o", -1))
            pe.wait_ge(pre_v.sem, pre_v.at("projT"))

            def gradients(s, start=False, stop=False):
                pe.matmul(ps[:, 7, :], dp[:, s, :], h[:, s, :], start=start, stop=stop, skip_group_check=True)
                pe.matmul(ps[:, 6, :], k_cur[:], dV[:, s, :], start=start, stop=stop, skip_group_check=True)
                return pe.matmul(ps[:, 5, :], k_cur[:], dG[:, s, :], start=start, stop=stop, skip_group_check=True)

            with pe.Fori(0, TTT_STEPS) as step:
                pe.wait_ge(upd_v.sem, upd_v.at("proj", step - 1))
                pe.wait_ge(zero_v.sem, zero_v.at("dp", step))
                pe.wait_ge(zero_g.sem, zero_g.at("k", step))
                gradients(1, start=True).then_inc(open_p.sem, open_p.tick("opened"))
                with pe.Fori(0, NT // 2) as i:
                    t = step * (NT // 2) + i
                    for s in range(2):
                        before = lambda name: f"{name}{1 - s}"
                        t_before = t - 1 if s == 0 else t
                        pe.wait_ge(ttt_g.sem, ttt_g.at(f"kT_cur{s}", t))
                        pe.wait_ge(ttt_v.sem, ttt_v.at(before("sw"), t_before))
                        pe.matmul(ps[:, 0, :], kT_cur[:], gate[:], start=True, stop=True)
                        pe.wait_ge(ttt_a.sem, ttt_a.at(before("vs"), t_before))
                        pe.matmul(ps[:, 1, :], kT_cur[:], val[:], start=True, stop=True) \
                          .then_inc(ttt_p.sem, ttt_p.tick(f"gv{s}"))
                        pe.wait_ge(ttt_v.sem, ttt_v.at(before("dG"), t_before))
                        pe.wait_ge(ttt_g.sem, ttt_g.at(before("k_cur"), t_before))
                        gradients(1 - s).then_inc(ttt_p.sem, ttt_p.tick(f"grads{s}"))
                        pe.wait_ge(ttt_v.sem, ttt_v.at(f"h{s}", t))
                        pe.wait_ge(ttt_a.sem, ttt_a.at(before("hT"), t_before))
                        for j in range(NJ):
                            mm = pe.transpose(ps[:, 2, bass.ts(j, P)], h[:, s, bass.ts(j, P)], ident)
                        mm.then_inc(ttt_p.sem, ttt_p.tick(f"hT{s}"))
                        pe.wait_ge(ttt_a.sem, ttt_a.at(f"hT{s}", t))
                        pe.wait_ge(ttt_a.sem, ttt_a.at(before("dpT"), t_before))
                        for j in range(NJ):
                            mm = pe.matmul(ps[:, 3, 0:P], hT[:, s, bass.ts(j, P)], proj[:, j, :],
                                           start=(j == 0), stop=(j == NJ - 1))
                        mm.then_inc(ttt_p.sem, ttt_p.tick(f"pred{s}"))
                        pe.wait_ge(ttt_v.sem, ttt_v.at(f"dp{s}", t))
                        pe.transpose(ps[:, 3, 0:P], dp[:, s, :], ident).then_inc(ttt_p.sem, ttt_p.tick(f"dpT{s}"))
                        pe.wait_ge(ttt_a.sem, ttt_a.at(f"dpT{s}", t))
                        pe.wait_ge(ttt_v.sem, ttt_v.at(before("dG"), t_before))
                        pe.matmul(ps[:, 4, :], dpT[:, s, :], projT[:], start=True, stop=True) \
                          .then_inc(ttt_p.sem, ttt_p.tick(f"dh{s}"))
                last = step * (NT // 2) + NT // 2 - 1
                pe.wait_ge(ttt_v.sem, ttt_v.at("dG1", last))
                pe.wait_ge(ttt_g.sem, ttt_g.at("k_cur1", last))
                gradients(1, stop=True).then_inc(open_p.sem, open_p.tick("last"))
                pe.wait_ge(open_a.sem, open_a.at("fro2", step))
                pe.matmul(ps[:, 0, 0:3], ones, fro[:], start=True, stop=True).then_inc(open_p.sem, open_p.tick("fro"))
                pe.wait_ge(open_v.sem, open_v.at("X2", step))
                for m in range(3):
                    for j in range(NJ):
                        mm = pe.transpose(ps[:, 1 + m, bass.ts(j, P)], X[:, m, bass.ts(j, P)], ident)
                mm.then_inc(open_p.sem, open_p.tick("XT"))
                with pe.Fori(0, NS_ITERS) as it:
                    n = step * NS_ITERS + it
                    pe.wait_ge(open_a.sem, open_a.at("XT2", step))
                    for m in range(3):
                        pe.wait_ge(ns_v.sem, ns_v.at(f"XT{m}", n - 1))
                        pe.wait_ge(ns_a.sem, ns_a.at(f"X{m}", n - 1))
                        for j in range(NJ):
                            mm = pe.matmul(ps[:, m, 0:P], XT[:, m, bass.ts(j, P)], XT[:, m, bass.ts(j, P)],
                                           start=(j == 0), stop=(j == NJ - 1))
                        mm.then_inc(ns_p.sem, ns_p.tick(f"A{m}"))
                    for m in range(3):
                        pe.wait_ge(ns_a.sem, ns_a.at(f"A{m}", n))
                        pe.matmul(ps[:, 3 + m, 0:P], Am[:, m, :], Am[:, m, :], start=True, stop=True) \
                          .then_inc(ns_p.sem, ns_p.tick(f"A2{m}"))
                    for m in range(3):
                        pe.wait_ge(ns_v.sem, ns_v.at(f"B{m}", n))
                        pe.matmul(ps[:, m, :], Bm[:, m, :], X[:, m, :], start=True, stop=True)
                        for j in range(NJ):
                            mm = pe.matmul(ps[:, 3 + m, bass.ts(j, P)], X[:, m, bass.ts(j, P)], Bm[:, m, :],
                                           start=True, stop=True)
                        mm.then_inc(ns_p.sem, ns_p.tick(f"X{m}"))
            pe.wait_ge(upd_v.sem, upd_v.at("proj", TTT_STEPS - 1))
            for j in range(NJ):
                mm = pe.matmul(ps[:, 0, bass.ts(j, P)], projT[:, bass.ts(j, P)], w_o[:], start=True, stop=True)
            mm.then_inc(fin_p.sem, fin_p.tick("wo2"))
            pe.wait_ge(fin_v.sem, fin_v.at("wo2"))
            pe.wait_ge(pre_v.sem, pre_v.at("qT"))
            with pe.Fori(0, NB) as blk:
                for j in range(NJ):
                    b = 2 * (j % 2)
                    pe.wait_ge(ask_v.sem, ask_v.at(f"h{(j - 2) % 4}", blk - (j < 2)))
                    for w, bank in ((gate, b), (val, b + 1)):
                        mm = pe.matmul(ps[:, bank, :], w[:, bass.ts(j, P)], qT[:, bass.ds(blk * BLK, BLK)],
                                       start=True, stop=True)
                    mm.then_inc(ask_p.sem, ask_p.tick(f"gv{j}"))
                pe.wait_ge(ask_v.sem, ask_v.at("h3", blk))
                pe.wait_ge(ask_v.sem, ask_v.at("x", blk - 1))
                for i in range(4):
                    for j in range(NJ):
                        mm = pe.matmul(ps[:, 4, bass.ts(i, P)], fh[:, j, bass.ts(i, P)], wo2[:, j, :],
                                       start=(j == 0), stop=(j == NJ - 1))
                mm.then_inc(ask_p.sem, ask_p.tick("o"))



XH, XD = 16, 64
INNER = XH * XD
NC = INNER // P
NK = SC // P
NCT = B * NK
CLIP = 11.0


def stage_cross_attention(nc, g, a):
    with Stage(nc, "xa") as st:
        wq = st.sb("wq", [P, INNER])
        wkv = st.sb("wkv", [P, 2 * INNER])
        wo = st.sb("wo", [P, NC, P])
        col = st.sb("col", [P, 4])
        b_o = st.sb("b_o", [P, P])
        turn = st.sb("turn", [P, 2, NK, 4, XD // 2])
        turnT = st.sb("turnT", [P, 2, SC])
        nrm = st.sb("nrm", [P, NT, P])
        cn = st.sb("cn", [P, NCT, P])
        latT = st.sb("latT", [P, T + S])
        ctxT = st.sb("ctxT", [P, B * SC + SC])
        stat = st.sb("stat", [P, 4, NT])
        stat2 = st.sb("stat2", [P, 4, NT])
        statc = st.sb("statc", [P, 4, NCT])
        ctx_cur = st.sb("ctx_cur", [P, SC])
        kz = st.sb("kz", [P, 2, 2, SC])
        qz = st.sb("qz", [P, 2, 2, S])
        va = st.sb("va", [P, 2, NK, 4, XD])
        pt = st.sb("pt", [P, 2, NK, S])
        rec = st.sb("rec", [P, S])
        oT = st.sb("oT", [P, NC, S])
        ps, x, ctx = g.ps, g.x, g.ctx
        ident = g.ident
        sq = cn

        load = st.steps("load", ["all"])
        N_LOADS = 17
        ln1_v, ln1_a = st.steps("ln1_v", LN_VECTOR), st.steps("ln1_a", ["root"])
        ln2_v, ln2_a = st.steps("ln2_v", LN_VECTOR), st.steps("ln2_a", ["root"])
        lnc_v, lnc_a = st.steps("lnc_v", LN_VECTOR), st.steps("lnc_a", ["root"])
        pre_v = st.steps("pre_v", ["x_bias", "lat_zeros", "ctx_zeros", "ones", "cos", "sin", "ctx"])
        pre_a = st.steps("pre_a", ["lat", "ctx"])
        pre_g = st.steps("pre_g", ["sign"])
        pre_p = st.steps("pre_p", ["turn", "lat", "ctx0", "ctx1"])
        pair = lambda *xs: [f"{n}{c}" for c in range(NC) for n in xs]
        pj_p = st.steps("pj_p", pair("q", "k", "v"), ahead=1)
        pj_a = st.steps("pj_a", pair("q", "v"), ahead=1)
        pj_v = st.steps("pj_v", pair("k"), ahead=1)
        pj_g = st.steps("pj_g", ["ctx_cur"], ahead=1)
        heads = lambda *xs: [f"{n}{h}" for h in range(XH) for n in xs]
        s_p = st.steps("s_p", heads("S"), ahead=1)
        e_a = st.steps("e_a", heads("E"), ahead=1)
        c_v = st.steps("c_v", heads("C"), ahead=1)
        o_p = st.steps("o_p", heads("O") + ["out"], ahead=1)
        n_v = st.steps("n_v", heads("R", "N") + ["x"], ahead=1)

        def free(eng, *steps):
            for each in steps:
                eng.sem_inc(each.sem, len(each.names))

        def of(i, n, b):
            return i % n, b + i // n

        block = st.block()

        @block.sync
        def _(sp):
            for dst, src in (
                (wq[:], a["L0_xattn_Wq"]), (wkv[:], a["L0_xattn_Wkv"]),
                (wo[:], a["L0_xattn_Wo"].rearrange("(c p) d -> p c d", p=P)),
                (col[:, 0:1], a["L0_xattn_ln_lat_g"].unsqueeze(1)), (col[:, 1:2], a["L0_xattn_ln_lat_b"].unsqueeze(1)),
                (col[:, 2:3], a["L0_xattn_ln_ctx_g"].unsqueeze(1)), (col[:, 3:4], a["L0_xattn_ln_ctx_b"].unsqueeze(1)),
                (b_o[:], a["L0_xattn_bo"].partition_broadcast(P)),
            ):
                sp.dma_start(dst, src).then_inc(load.sem, 16)
            for r in range(4):
                for i, name in enumerate(("L0_xattn_cos", "L0_xattn_sin")):
                    sp.dma_start(turn[:, i, :, r, :], a[name].rearrange("(n p) d -> p n d", p=P)).then_inc(load.sem, 16)
            sp.dma_start(g.ctx[:], a["ctx_1024"].rearrange("b (n p) d -> p (b n) d", p=P)).then_inc(load.sem, 16)
            sp.wait_ge(load.sem, 16 * (N_LOADS))

        @block.gpsimd
        def _(pool):
            pool.wait_ge(load.sem, 16 * (N_LOADS))
            minus = turn[:, 1, :, 1:4:2, :]
            pool.tensor_scalar(minus, minus, -1.0, None, ALU.mult).then_inc(pre_g.sem, pre_g.tick("sign"))
            free(pool, pj_g)
            pool.wait_ge(pre_g.sem, pre_g.at("sign"))
            pool.wait_ge(pre_a.sem, pre_a.at("ctx"))
            pool.wait_ge(pre_v.sem, pre_v.at("ctx"))
            pool.tensor_copy(ctx_cur[:], ctxT[:, 0:SC]).then_inc(pj_g.sem, pj_g.tick("ctx_cur"))
            with pool.Fori(0, B) as b:
                pool.wait_ge(pj_p.sem, pj_p.at(f"v{NC - 1}", b))
                pool.tensor_copy(ctx_cur[:], ctxT[:, bass.ds((b + 1) * SC, SC)]).then_inc(pj_g.sem, pj_g.tick("ctx_cur"))

        @block.scalar
        def _(act):
            layernorm_root(act, ln1_v, ln1_a, stat)
            layernorm_root(act, ln2_v, ln2_a, stat2)
            layernorm_root(act, lnc_v, lnc_a, statc)
            act.wait_ge(pre_p.sem, pre_p.at("lat"))
            act.wait_ge(load.sem, 16 * (N_LOADS))
            act.activation(latT[:, 0:T], banks(ps, 4, 8), ACT.Identity, scale=col[:, 0:1], bias=col[:, 1:2]) \
               .then_inc(pre_a.sem, pre_a.tick("lat"))
            act.wait_ge(pre_p.sem, pre_p.at("ctx0"))
            act.activation(ctxT[:, 0:T], banks(ps, 0, 4), ACT.Identity, scale=col[:, 2:3], bias=col[:, 3:4]) \
               .then_inc(pre_a.sem, pre_a.tick("ctx"))
            free(act, pj_a, e_a)

            def take_q(c, b, h):
                if h is not None:
                    act.wait_ge(s_p.sem, s_p.at(f"S{h}", b))
                c, b = of(c, NC, b)
                act.wait_ge(pj_p.sem, pj_p.at(f"q{c}", b))
                half = XD // 2
                for i in range(2):
                    for to, rows_in, n in ((0, XD * i, XD), (XD, XD * i + half, half), (XD + half, XD * i, half)):
                        mm = act.activation(qz[bass.ds(to, n), c % 2, i, :], ps[bass.ds(rows_in, n), 7, 0:S], ACT.Copy)
                mm.then_inc(pj_a.sem, pj_a.tick(f"q{c}"))

            def take_v(c, b):
                last, pass_ = of(2 * c - 3, XH, b)
                act.wait_ge(o_p.sem, o_p.at(f"O{last}", pass_))
                c, b = of(c, NC, b)
                act.wait_ge(pj_p.sem, pj_p.at(f"v{c}", b))
                act.activation(va[:, c % 2, :, 0:4:3, :], ps[:, 7, :].rearrange("p (n i d) -> p n i d", n=NK, i=2), ACT.Copy) \
                   .then_inc(pj_a.sem, pj_a.tick(f"v{c}"))

            def weights(h, b):
                last, pass_ = of(h - 2, XH, b)
                act.wait_ge(o_p.sem, o_p.at(f"O{last}", pass_))
                h, b = of(h, XH, b)
                act.wait_ge(s_p.sem, s_p.at(f"S{h}", b))
                b0 = 2 * (h % 2)
                act.activation(pt[:, h % 2].rearrange("p n s -> p (n s)"), banks(ps, b0, b0 + 2), ACT.Exp,
                               scale=XD ** -0.5).then_inc(e_a.sem, e_a.tick(f"E{h}"))

            take_q(0, 0, None)
            take_v(0, 0)
            weights(0, 0)
            take_q(1, 0, None)
            with act.Fori(0, B) as b:
                for h in range(XH):
                    weights(h + 1, b)
                    if h % 2 == 0:
                        take_v(h // 2 + 1, b)
                    else:
                        take_q((h + 1) // 2 + 1, b, h)

        @block.vector
        def _(dve):
            layernorm_vector(dve, ln1_v, ln1_a, x[:], nrm[:], sq[:, 0:NT, :], stat[:], NT)
            dve.wait_ge(ln1_v.sem, ln1_v.at("normal"))
            layernorm_vector(dve, ln2_v, ln2_a, nrm[:], nrm[:], sq[:, 0:NT, :], stat2[:], NT)
            dve.wait_ge(load.sem, 16 * (N_LOADS))
            layernorm_vector(dve, lnc_v, lnc_a, ctx[:], cn[:], rows(ctxT[:, 0:B * SC], NCT), statc[:], NCT)
            dve.tensor_tensor(x[:], x[:], b_o[:].unsqueeze(1).to_broadcast([P, NT, P]), ALU.add) \
               .then_inc(pre_v.sem, pre_v.tick("x_bias"))
            dve.memset(latT[:, T:T + S], 0.0).then_inc(pre_v.sem, pre_v.tick("lat_zeros"))
            dve.wait_ge(lnc_v.sem, lnc_v.at("normal"))
            dve.memset(ctxT[:, B * SC:B * SC + SC], 0.0).then_inc(pre_v.sem, pre_v.tick("ctx_zeros"))
            dve.memset(va[:, :, :, 1:3, :], 1.0).then_inc(pre_v.sem, pre_v.tick("ones"))
            dve.wait_ge(pre_p.sem, pre_p.at("turn"))
            dve.tensor_copy(turnT[:, 0, :], ps[:, 0, :]).then_inc(pre_v.sem, pre_v.tick("cos"))
            dve.tensor_copy(turnT[:, 1, :], ps[:, 1, :]).then_inc(pre_v.sem, pre_v.tick("sin"))
            dve.wait_ge(pre_p.sem, pre_p.at("ctx1"))
            dve.tensor_scalar(ctxT[:, T:2 * T], banks(ps, 4, 8), col[:, 2:3], col[:, 3:4], ALU.mult, ALU.add) \
               .then_inc(pre_v.sem, pre_v.tick("ctx"))
            free(dve, pj_v, c_v, n_v)

            def take_k(c, b, h):
                if h is not None:
                    dve.wait_ge(s_p.sem, s_p.at(f"S{h}", b))
                c, b = of(c, NC, b)
                dve.wait_ge(pj_p.sem, pj_p.at(f"k{c}", b))
                for i in range(2):
                    r = bass.ds(XD * i, XD)
                    for half in range(2):
                        op = dve.tensor_tensor(kz[bass.ds(XD * half, XD), c % 2, i, :], ps[r, 6, :], turnT[r, half, :], ALU.mult)
                op.then_inc(pj_v.sem, pj_v.tick(f"k{c}"))

            def clip(h, b):
                h, b = of(h, XH, b)
                dve.wait_ge(e_a.sem, e_a.at(f"E{h}", b))
                w = pt[:, h % 2].rearrange("p n s -> p (n s)")
                dve.tensor_scalar(w, w, math.exp(-CLIP), math.exp(CLIP), ALU.max, ALU.min) \
                   .then_inc(c_v.sem, c_v.tick(f"C{h}"))

            def normalise(h, b):
                out, sums = bass.ds(XD * (h % 2), XD), bass.ds(XD * (1 - h % 2), XD)
                dve.wait_ge(o_p.sem, o_p.at(f"O{h}", b))
                dve.reciprocal(rec[out], ps[sums, 4 + h % 2, 0:S]).then_inc(n_v.sem, n_v.tick(f"R{h}"))
                dve.wait_ge(n_v.sem, n_v.at(f"R{h}", b))
                dve.tensor_tensor(oT[out, h // 2, :], ps[out, 4 + h % 2, 0:S], rec[out], ALU.mult) \
                   .then_inc(n_v.sem, n_v.tick(f"N{h}"))

            take_k(0, 0, None)
            clip(0, 0)
            take_k(1, 0, None)
            with dve.Fori(0, B) as b:
                for h in range(XH):
                    clip(h + 1, b)
                    normalise(h, b)
                    if h % 2:
                        take_k((h + 1) // 2 + 1, b, h)
                dve.wait_ge(o_p.sem, o_p.at("out", b))
                xb = x[:, bass.ds(2 * b, 2), :]
                dve.tensor_tensor(xb, rows(ps[:, 4, 0:2 * P], 2), xb, ALU.add).then_inc(n_v.sem, n_v.tick("x"))

        @block.tensor
        def _(pe):
            pe.wait_ge(load.sem, 16 * (N_LOADS))
            pe.wait_ge(pre_g.sem, pre_g.at("sign"))
            for i in range(2):
                for n in range(NK):
                    mm = pe.transpose(ps[:, i, bass.ts(n, P)], turn[:, i, n].rearrange("p r d -> p (r d)"), ident)
            mm.then_inc(pre_p.sem, pre_p.tick("turn"))
            pe.wait_ge(ln2_v.sem, ln2_v.at("normal"))
            for t in range(NT):
                mm = pe.transpose(ps[:, 4 + t // 4, bass.ts(t % 4, P)], nrm[:, t, :], ident)
            mm.then_inc(pre_p.sem, pre_p.tick("lat"))
            pe.wait_ge(lnc_v.sem, lnc_v.at("normal"))
            pe.wait_ge(pre_v.sem, pre_v.at("sin"))
            for t in range(NT):
                mm = pe.transpose(ps[:, t // 4, bass.ts(t % 4, P)], cn[:, t, :], ident)
            mm.then_inc(pre_p.sem, pre_p.tick("ctx0"))
            pe.wait_ge(pre_a.sem, pre_a.at("lat"))
            for t in range(NT):
                mm = pe.transpose(ps[:, 4 + t // 4, bass.ts(t % 4, P)], cn[:, NT + t, :], ident)
            mm.then_inc(pre_p.sem, pre_p.tick("ctx1"))
            free(pe, pj_p, s_p, o_p)
            pe.wait_ge(pre_a.sem, pre_a.at("ctx"))
            pe.wait_ge(pre_v.sem, pre_v.at("ctx"))

            def project_qk(c, b):
                last, pass_ = of(c - 1, NC, b)
                pe.wait_ge(pj_a.sem, pj_a.at(f"v{last}", pass_))
                pe.wait_ge(pj_v.sem, pj_v.at(f"k{last}", pass_))
                c, b = of(c, NC, b)
                pe.matmul(ps[:, 7, 0:S], wq[:, bass.ts(c, P)], latT[:, bass.ds(b * S, S)], start=True, stop=True) \
                  .then_inc(pj_p.sem, pj_p.tick(f"q{c}"))
                pe.matmul(ps[:, 6, :], wkv[:, bass.ts(c, P)], ctxT[:, bass.ds(b * SC, SC)], start=True, stop=True) \
                  .then_inc(pj_p.sem, pj_p.tick(f"k{c}"))

            def project_v(c, b):
                c, b = of(c, NC, b)
                pe.wait_ge(pj_a.sem, pj_a.at(f"q{c}", b))
                if c == 0:
                    pe.wait_ge(pj_g.sem, pj_g.at("ctx_cur", b))
                for n in range(NK):
                    mm = pe.matmul(ps[:, 7, bass.ts(n, P)], ctx_cur[:, bass.ts(n, P)], wkv[:, bass.ds(INNER + P * c, P)],
                                   start=True, stop=True)
                mm.then_inc(pj_p.sem, pj_p.tick(f"v{c}"))

            def scores(h, b):
                last, pass_ = of(h - 2, XH, b)
                pe.wait_ge(e_a.sem, e_a.at(f"E{last}", pass_))
                h, b = of(h, XH, b)
                if h % 2 == 0:
                    pe.wait_ge(pj_v.sem, pj_v.at(f"k{h // 2}", b))
                    pe.wait_ge(pj_a.sem, pj_a.at(f"q{h // 2}", b))
                for n in range(NK):
                    mm = pe.matmul(ps[:, 2 * (h % 2) + n // 2, bass.ts(n % 2, S)], kz[:, h // 2 % 2, h % 2, bass.ts(n, P)],
                                   qz[:, h // 2 % 2, h % 2, :], start=True, stop=True)
                mm.then_inc(s_p.sem, s_p.tick(f"S{h}"))

            def output(h, b):
                last, pass_ = of(h - 2, XH, b)
                pe.wait_ge(n_v.sem, n_v.at(f"N{last}" if h else "x", pass_))
                if h % 2 == 0:
                    pe.wait_ge(pj_a.sem, pj_a.at(f"v{h // 2}", b))
                pe.wait_ge(c_v.sem, c_v.at(f"C{h}", b))
                for n in range(NK):
                    v_ones = va[:, h // 2 % 2, n, 2 * (h % 2):2 * (h % 2) + 2, :].rearrange("p f d -> p (f d)")
                    mm = pe.matmul(ps[:, 4 + h % 2, 0:S], v_ones, pt[:, h % 2, n, :], start=(n == 0), stop=(n == NK - 1))
                mm.then_inc(o_p.sem, o_p.tick(f"O{h}"))

            project_qk(0, 0)
            project_v(0, 0)
            scores(0, 0)
            project_qk(1, 0)
            with pe.Fori(0, B) as b:
                for h in range(XH):
                    scores(h + 1, b)
                    if h % 2 == 0:
                        project_v(h // 2 + 1, b)
                    output(h, b)
                    if h % 2:
                        project_qk((h + 1) // 2 + 1, b)
                pe.wait_ge(n_v.sem, n_v.at(f"N{XH - 1}", b))
                for i in range(2):
                    for c in range(NC):
                        mm = pe.matmul(ps[:, 4, bass.ts(i, P)], oT[:, c, bass.ts(i, P)], wo[:, c, :],
                                       start=(c == 0), stop=(c == NC - 1))
                mm.then_inc(o_p.sem, o_p.tick("out"))



EH, ED = 16, 8
NE = 8
TOP = 2


def stage_experts(nc, g, a):
    with Stage(nc, "ex") as st:
        w_in = st.sb("w_in", [P, 3, P])
        w_inT = st.sb("w_inT", [P, 3 * P])
        w_out = st.sb("w_out", [P, P])
        w_outT = st.sb("w_outT", [P, P])
        gw = st.sb("gw", [NE, P])
        gwT = st.sb("gwT", [P, NE])
        b_in = st.sb("b_in", [P, 3 * P])
        b_out = st.sb("b_out", [P, P])
        b_gate = st.sb("b_gate", [P, NE])
        b1r = st.sb("b1r", [NE * NJ, P])
        b1T = st.sb("b1T", [P, NE * NJ])
        b2 = st.sb("b2", [NE, P])
        lng = st.sb("lng", [P, 4, P])
        lower = st.sb("lower", [P, NE, NE])
        nrm = st.sb("nrm", [P, NT, P])
        nT = st.sb("nT", [P, T])
        sq = st.sb("sq", [P, NT, P])
        stat = st.sb("stat", [P, 3, 4, NT])
        qkv = st.sb("qkv", [P, NT, 3 * P])
        prod = st.sb("prod", [P, 2, B, P])
        sc = st.sb("sc", [P, NT, B, EH])
        smx = st.sb("smx", [P, NT, EH])
        cx = st.sb("cx", [P, NT, P])
        tok = st.sb("tok", [P, NT, P])
        tokT = st.sb("tokT", [P, T])
        lg = st.sb("lg", [P, NT, NE])
        l1 = st.sb("l1", [P, NT])
        cmp = st.sb("cmp", [P, 2, NT, NE, NE])
        rank = st.sb("rank", [P, NT, NE])
        comb = st.sb("comb", [P, NT, NE])
        combT = st.sb("combT", [NE, T])
        comb_e = st.sb("comb_e", [P, NT])
        acc = st.sb("acc", [P, NT, P])
        w1r = st.sb("w1r", [P, NJ, P])
        w2r = st.sb("w2r", [P, HID])
        w1T = st.sb("w1T", [P, HID])
        w2T = st.sb("w2T", [P, NJ, P])
        fh = st.sb("fh", [P, NJ, BLK])
        ps, x = g.ps, g.x
        ident = g.ident

        load = st.steps("load", ["all"])
        N_LOADS = 13
        LOADED = 16 * N_LOADS
        w_load = st.steps("w_load", ["w1", "w2"])
        ln0_v, ln0_a = st.steps("ln0_v", LN_VECTOR), st.steps("ln0_a", ["root"])
        ln1_v, ln1_a = st.steps("ln1_v", LN_VECTOR), st.steps("ln1_a", ["root"])
        ln2_v, ln2_a = st.steps("ln2_v", LN_VECTOR), st.steps("ln2_a", ["root"])
        pre_p = st.steps("pre_p", ["w", "nT"])
        pre_v = st.steps("pre_v", ["w_inT", "w_outT", "gwT", "b1T", "nT1"] + [f"qkv{t}" for t in range(1, NT, 2)])
        pre_a = st.steps("pre_a", ["nT0"] + [f"raw{t}" for t in range(0, NT, 2)])
        qkv_p = st.steps("qkv_p", [f"t{t}" for t in range(NT)])
        pre_g = st.steps("pre_g", ["b_out"])
        s_g = st.steps("s_g", ["prod0", "prod1"], ahead=1)
        s_v = st.steps("s_v", ["sum0", "sum1"], ahead=1)
        c_g = st.steps("c_g", ["prod0", "prod1"], ahead=1)
        c_v = st.steps("c_v", ["sum0", "sum1"], ahead=1)
        sm_v = st.steps("sm_v", ["max", "shift", "sum", "inv", "p"])
        sm_a = st.steps("sm_a", ["exp"])
        mid_p = st.steps("mid_p", ["cT", "out", "tokT", "gate", "combT", "b2"])
        mid_a = st.steps("mid_a", ["cT", "tokT", "e", "combT"])
        mid_v = st.steps("mid_v", ["out", "scaled", "tok", "bias", "max", "shift", "gt", "eq", "lower", "beats", "rank",
                                   "top", "w", "sum", "inv", "comb", "acc"])
        e_p = st.steps("e_p", ["w1T", "w2T"], ahead=1)
        e_a = st.steps("e_a", ["w1T"], ahead=1)
        e_v = st.steps("e_v", ["w2T", "comb_e"], ahead=1)
        f_p = st.steps("f_p", ["h0", "h1", "h2", "h3", "o"], ahead=1)
        f_a = st.steps("f_a", ["h0", "h2"], ahead=1)
        f_v = st.steps("f_v", ["h1", "h3", "acc"], ahead=1)
        end_v = st.steps("end_v", ["scaled", "moved", "x"])

        block = st.block()

        @block.sync
        def _(sp):
            for dst, src in (
                (w_in[:], a["L0_ffn_in_proj_w"].rearrange("(i p) d -> p i d", p=P)), (w_out[:], a["L0_ffn_out_w"]),
                (gw[:], a["L0_ffn_gate_w"]), (b1r[:], a["L0_ffn_b1"].rearrange("e (j p) -> (e j) p", p=P)),
                (b_in[:], a["L0_ffn_in_proj_b"].partition_broadcast(P)), (b_out[:], a["L0_ffn_out_b"].partition_broadcast(P)),
                (b_gate[:], a["L0_ffn_gate_b"].partition_broadcast(P)), (b2[:], a["L0_ffn_b2"]),
                (lng[:, 0, :], a["L0_ffn_ln1_g"].partition_broadcast(P)), (lng[:, 1, :], a["L0_ffn_ln1_b"].partition_broadcast(P)),
                (lng[:, 2, :], a["L0_ffn_ln2_g"].partition_broadcast(P)), (lng[:, 3, :], a["L0_ffn_ln2_b"].partition_broadcast(P)),
                (lower[:].rearrange("p i j -> p (i j)"), a["lower"].partition_broadcast(P)),
            ):
                sp.dma_start(dst, src).then_inc(load.sem, 16)
            with sp.Fori(0, NE) as e:
                sp.wait_ge(e_p.sem, e_p.at("w1T", e - 1))
                sp.dma_start(w1r[:].unsqueeze(1), a["L0_ffn_w1"][bass.ds(e, 1)].rearrange("e (j p) d -> p e j d", p=P)) \
                  .then_inc(w_load.sem, 16)
                sp.wait_ge(e_p.sem, e_p.at("w2T", e - 1))
                sp.dma_start(w2r[:].unsqueeze(1), a["L0_ffn_w2"][bass.ds(e, 1)].rearrange("e d f -> d e f")) \
                  .then_inc(w_load.sem, 16)

        @block.gpsimd
        def _(pool):
            pool.sem_inc(s_g.sem, s_g.at("prod1", -1))
            pool.sem_inc(c_g.sem, c_g.at("prod1", -1))
            pool.wait_ge(load.sem, LOADED)
            pool.wait_ge(pre_p.sem, pre_p.at("nT"))
            pool.tensor_tensor(nrm[:], nrm[:], b_out[:].unsqueeze(1).to_broadcast([P, NT, P]), ALU.add) \
                .then_inc(pre_g.sem, pre_g.tick("b_out"))
            pool.wait_ge(pre_v.sem, pre_v.at(f"qkv{NT - 1}"))
            pool.wait_ge(pre_a.sem, pre_a.at(f"raw{NT - 2}"))
            with pool.Fori(0, B) as s:
                for f in range(2):
                    pool.wait_ge(s_v.sem, s_v.at(f"sum{f}", s - 1))
                    pool.tensor_tensor(prod[:, f], qkv[:, bass.ds(2 * s + f, 1), 0:P].to_broadcast([P, B, P]),
                                       qkv[:, f:NT:2, P:2 * P], ALU.mult).then_inc(s_g.sem, s_g.tick(f"prod{f}"))
            pool.wait_ge(sm_v.sem, sm_v.at("p"))
            with pool.Fori(0, B) as s:
                for f in range(2):
                    pool.wait_ge(c_v.sem, c_v.at(f"sum{f}", s - 1))
                    w = sc[:, bass.ds(2 * s + f, 1)].rearrange("p o t h -> p (o t) h").unsqueeze(3)
                    pool.tensor_tensor(prod[:, f].rearrange("p t (h d) -> p t h d", h=EH), w.to_broadcast([P, B, EH, ED]),
                                       qkv[:, f:NT:2, 2 * P:3 * P].rearrange("p t (h d) -> p t h d", h=EH), ALU.mult) \
                        .then_inc(c_g.sem, c_g.tick(f"prod{f}"))

        @block.scalar
        def _(act):
            layernorm_root(act, ln0_v, ln0_a, stat[:, 0])
            act.wait_ge(pre_p.sem, pre_p.at("nT"))
            act.activation(nT[:, 0:2 * BLK], banks(ps, 4, 6), ACT.Copy).then_inc(pre_a.sem, pre_a.tick("nT0"))
            for t in range(0, NT, 2):
                act.wait_ge(qkv_p.sem, qkv_p.at(f"t{t}"))
                act.activation(qkv[:, t, :], ps[:, t % 4, 0:3 * P], ACT.Copy).then_inc(pre_a.sem, pre_a.tick(f"raw{t}"))
            act.wait_ge(sm_v.sem, sm_v.at("shift"))
            act.activation(sc[:], sc[:], ACT.Exp, scale=ED ** -0.5).then_inc(sm_a.sem, sm_a.tick("exp"))
            act.wait_ge(mid_p.sem, mid_p.at("cT"))
            act.activation(nT[:], banks(ps, 0, 4), ACT.Copy).then_inc(mid_a.sem, mid_a.tick("cT"))
            layernorm_root(act, ln1_v, ln1_a, stat[:, 1])
            act.wait_ge(mid_p.sem, mid_p.at("tokT"))
            act.activation(tokT[:], banks(ps, 0, 4), ACT.Copy).then_inc(mid_a.sem, mid_a.tick("tokT"))
            act.wait_ge(mid_v.sem, mid_v.at("shift"))
            act.activation(lg[:], lg[:], ACT.Exp).then_inc(mid_a.sem, mid_a.tick("e"))
            act.wait_ge(mid_p.sem, mid_p.at("combT"))
            act.activation(combT[:], banks(ps, 0, 4)[0:NE, :], ACT.Copy).then_inc(mid_a.sem, mid_a.tick("combT"))
            act.sem_inc(e_a.sem, e_a.at("w1T", -1))
            act.sem_inc(f_a.sem, f_a.at("h2", -1))
            with act.Fori(0, NE) as e:
                act.wait_ge(e_p.sem, e_p.at("w1T", e))
                act.activation(w1T[:], ps[:, 6, :], ACT.Copy).then_inc(e_a.sem, e_a.tick("w1T"))
                with act.Fori(0, NB) as blk:
                    n = e * NB + blk
                    for j in (0, 2):
                        act.wait_ge(f_p.sem, f_p.at(f"h{j}", n))
                        act.activation(fh[:, j, :], ps[:, j, :], ACT.Relu, bias=b1T[:, bass.ds(e * NJ + j, 1)]) \
                           .then_inc(f_a.sem, f_a.tick(f"h{j}"))
            layernorm_root(act, ln2_v, ln2_a, stat[:, 2])

        @block.vector
        def _(dve):
            layernorm_vector(dve, ln0_v, ln0_a, x[:], nrm[:], sq[:], stat[:, 0], NT)
            dve.wait_ge(pre_p.sem, pre_p.at("w"))
            dve.tensor_copy(w_inT[:], ps[:, 0, 0:3 * P]).then_inc(pre_v.sem, pre_v.tick("w_inT"))
            dve.tensor_copy(w_outT[:], ps[:, 1, 0:P]).then_inc(pre_v.sem, pre_v.tick("w_outT"))
            dve.tensor_copy(gwT[:], ps[:, 1, P:P + NE]).then_inc(pre_v.sem, pre_v.tick("gwT"))
            dve.tensor_copy(b1T[:], ps[:, 1, 2 * P:2 * P + NE * NJ]).then_inc(pre_v.sem, pre_v.tick("b1T"))
            dve.wait_ge(pre_p.sem, pre_p.at("nT"))
            dve.tensor_copy(nT[:, 2 * BLK:T], banks(ps, 6, 8)).then_inc(pre_v.sem, pre_v.tick("nT1"))
            dve.wait_ge(load.sem, LOADED)
            for t in range(1, NT, 2):
                dve.wait_ge(qkv_p.sem, qkv_p.at(f"t{t}"))
                dve.tensor_copy(qkv[:, t, :], ps[:, t % 4, 0:3 * P]).then_inc(pre_v.sem, pre_v.tick(f"qkv{t}"))
            dve.sem_inc(s_v.sem, s_v.at("sum1", -1))
            dve.sem_inc(c_v.sem, c_v.at("sum1", -1))
            with dve.Fori(0, B) as s:
                for f in range(2):
                    dve.wait_ge(s_g.sem, s_g.at(f"prod{f}", s))
                    dve.tensor_reduce(sc[:, bass.ds(2 * s + f, 1)].rearrange("p o t h -> p (o t h)"),
                                      prod[:, f].rearrange("p t (h d) -> p (t h) d", h=EH), AX.X, ALU.add) \
                       .then_inc(s_v.sem, s_v.tick(f"sum{f}"))
            dve.wait_ge(s_v.sem, s_v.at("sum1", B - 1))
            by_t = sc[:].rearrange("p n t h -> p n h t")
            over = lambda v: v[:].unsqueeze(2).to_broadcast([P, NT, B, EH])
            dve.tensor_reduce(smx[:], by_t, AX.X, ALU.max).then_inc(sm_v.sem, sm_v.tick("max"))
            dve.wait_ge(sm_v.sem, sm_v.at("max"))
            dve.tensor_tensor(sc[:], sc[:], over(smx), ALU.subtract).then_inc(sm_v.sem, sm_v.tick("shift"))
            dve.wait_ge(sm_a.sem, sm_a.at("exp"))
            dve.tensor_reduce(smx[:], by_t, AX.X, ALU.add).then_inc(sm_v.sem, sm_v.tick("sum"))
            dve.wait_ge(sm_v.sem, sm_v.at("sum"))
            dve.reciprocal(smx[:], smx[:]).then_inc(sm_v.sem, sm_v.tick("inv"))
            dve.wait_ge(sm_v.sem, sm_v.at("inv"))
            dve.tensor_tensor(sc[:], sc[:], over(smx), ALU.mult).then_inc(sm_v.sem, sm_v.tick("p"))
            with dve.Fori(0, B) as s:
                for f in range(2):
                    dve.wait_ge(c_g.sem, c_g.at(f"prod{f}", s))
                    dve.tensor_reduce(cx[:, bass.ds(2 * s + f, 1), :].rearrange("p o d -> p (o d)"),
                                      prod[:, f].rearrange("p t d -> p d t"), AX.X, ALU.add) \
                       .then_inc(c_v.sem, c_v.tick(f"sum{f}"))
            dve.wait_ge(mid_p.sem, mid_p.at("out"))
            dve.wait_ge(pre_g.sem, pre_g.at("b_out"))
            dve.tensor_tensor(tok[:], rows(banks(ps, 4, 8), NT), nrm[:], ALU.add).then_inc(mid_v.sem, mid_v.tick("out"))
            dve.wait_ge(mid_v.sem, mid_v.at("out"))
            layernorm_vector(dve, ln1_v, ln1_a, tok[:], tok[:], sq[:], stat[:, 1], NT)
            row = lambda i: lng[:, i, :].unsqueeze(1).to_broadcast([P, NT, P])
            dve.wait_ge(ln1_v.sem, ln1_v.at("normal"))
            dve.tensor_tensor(tok[:], tok[:], row(0), ALU.mult).then_inc(mid_v.sem, mid_v.tick("scaled"))
            dve.wait_ge(mid_v.sem, mid_v.at("scaled"))
            dve.tensor_tensor(tok[:], tok[:], row(1), ALU.add).then_inc(mid_v.sem, mid_v.tick("tok"))
            per_tile = lambda v: v[:].unsqueeze(2).to_broadcast([P, NT, NE])
            dve.wait_ge(mid_p.sem, mid_p.at("gate"))
            dve.tensor_tensor(lg[:], ps[:, 4, 0:P].rearrange("p (t e) -> p t e", e=NE),
                              b_gate[:].unsqueeze(1).to_broadcast([P, NT, NE]), ALU.add).then_inc(mid_v.sem, mid_v.tick("bias"))
            dve.wait_ge(mid_v.sem, mid_v.at("bias"))
            dve.tensor_reduce(l1[:], lg[:], AX.X, ALU.max).then_inc(mid_v.sem, mid_v.tick("max"))
            dve.wait_ge(mid_v.sem, mid_v.at("max"))
            dve.tensor_tensor(lg[:], lg[:], per_tile(l1), ALU.subtract).then_inc(mid_v.sem, mid_v.tick("shift"))
            dve.wait_ge(mid_a.sem, mid_a.at("e"))
            mine = lg[:].unsqueeze(3).to_broadcast([P, NT, NE, NE])
            other = lg[:].unsqueeze(2).to_broadcast([P, NT, NE, NE])
            dve.tensor_tensor(cmp[:, 0], other, mine, ALU.is_gt).then_inc(mid_v.sem, mid_v.tick("gt"))
            dve.tensor_tensor(cmp[:, 1], other, mine, ALU.is_equal).then_inc(mid_v.sem, mid_v.tick("eq"))
            dve.wait_ge(mid_v.sem, mid_v.at("eq"))
            dve.tensor_tensor(cmp[:, 1], cmp[:, 1], lower[:].unsqueeze(1).to_broadcast([P, NT, NE, NE]), ALU.mult) \
               .then_inc(mid_v.sem, mid_v.tick("lower"))
            dve.wait_ge(mid_v.sem, mid_v.at("lower"))
            dve.tensor_tensor(cmp[:, 0], cmp[:, 0], cmp[:, 1], ALU.add).then_inc(mid_v.sem, mid_v.tick("beats"))
            dve.wait_ge(mid_v.sem, mid_v.at("beats"))
            dve.tensor_reduce(rank[:], cmp[:, 0], AX.X, ALU.add).then_inc(mid_v.sem, mid_v.tick("rank"))
            dve.wait_ge(mid_v.sem, mid_v.at("rank"))
            dve.tensor_scalar(rank[:], rank[:], TOP - 0.5, None, ALU.is_lt).then_inc(mid_v.sem, mid_v.tick("top"))
            dve.wait_ge(mid_v.sem, mid_v.at("top"))
            dve.tensor_tensor(comb[:], rank[:], lg[:], ALU.mult).then_inc(mid_v.sem, mid_v.tick("w"))
            dve.wait_ge(mid_v.sem, mid_v.at("w"))
            dve.tensor_reduce(l1[:], comb[:], AX.X, ALU.add).then_inc(mid_v.sem, mid_v.tick("sum"))
            dve.wait_ge(mid_v.sem, mid_v.at("sum"))
            dve.reciprocal(l1[:], l1[:]).then_inc(mid_v.sem, mid_v.tick("inv"))
            dve.wait_ge(mid_v.sem, mid_v.at("inv"))
            dve.tensor_tensor(comb[:], comb[:], per_tile(l1), ALU.mult).then_inc(mid_v.sem, mid_v.tick("comb"))
            dve.wait_ge(mid_p.sem, mid_p.at("b2"))
            dve.tensor_tensor(acc[:], rows(banks(ps, 4, 8), NT), tok[:], ALU.add).then_inc(mid_v.sem, mid_v.tick("acc"))
            dve.wait_ge(mid_v.sem, mid_v.at("acc"))
            dve.sem_inc(e_v.sem, e_v.at("comb_e", -1))
            dve.sem_inc(f_v.sem, f_v.at("acc", -1))
            with dve.Fori(0, NE) as e:
                dve.wait_ge(e_p.sem, e_p.at("w2T", e))
                dve.tensor_copy(w2T[:].rearrange("p j d -> p (j d)"), ps[:, 7, :]).then_inc(e_v.sem, e_v.tick("w2T"))
                dve.wait_ge(f_v.sem, f_v.at("acc", e * NB - 1))
                dve.tensor_copy(comb_e[:].unsqueeze(2), comb[:, :, bass.ds(e, 1)]).then_inc(e_v.sem, e_v.tick("comb_e"))
                with dve.Fori(0, NB) as blk:
                    n = e * NB + blk
                    for j in (1, 3):
                        dve.wait_ge(f_p.sem, f_p.at(f"h{j}", n))
                        dve.tensor_scalar(fh[:, j, :], ps[:, j, :], b1T[:, bass.ds(e * NJ + j, 1)], 0.0, ALU.add, ALU.max) \
                           .then_inc(f_v.sem, f_v.tick(f"h{j}"))
                    dve.wait_ge(e_v.sem, e_v.at("comb_e", e))
                    dve.wait_ge(f_p.sem, f_p.at("o", n))
                    for i in range(4):
                        at = acc[:, bass.ds(4 * blk + i, 1), :]
                        last = dve.scalar_tensor_tensor(at, ps[:, 4, bass.ts(i, P)].unsqueeze(1),
                                                        comb_e[:, bass.ds(4 * blk + i, 1)], at, ALU.mult, ALU.add)
                    last.then_inc(f_v.sem, f_v.tick("acc"))
            dve.wait_ge(f_v.sem, f_v.at("acc", NE * NB - 1))
            layernorm_vector(dve, ln2_v, ln2_a, acc[:], acc[:], sq[:], stat[:, 2], NT)
            dve.wait_ge(ln2_v.sem, ln2_v.at("normal"))
            dve.tensor_tensor(acc[:], acc[:], row(2), ALU.mult).then_inc(end_v.sem, end_v.tick("scaled"))
            dve.wait_ge(end_v.sem, end_v.at("scaled"))
            dve.tensor_tensor(acc[:], acc[:], row(3), ALU.add).then_inc(end_v.sem, end_v.tick("moved"))
            dve.wait_ge(end_v.sem, end_v.at("moved"))
            dve.tensor_tensor(x[:], acc[:], x[:], ALU.add).then_inc(end_v.sem, end_v.tick("x"))

        @block.tensor
        def _(pe):
            pe.wait_ge(load.sem, LOADED)
            for i in range(3):
                pe.transpose(ps[:, 0, bass.ts(i, P)], w_in[:, i, :], ident)
            pe.transpose(ps[:, 1, 0:P], w_out[:], ident)
            pe.transpose(ps[:, 1, P:P + NE], gw[:], ident[0:NE, 0:NE])
            pe.transpose(ps[:, 1, 2 * P:2 * P + NE * NJ], b1r[:], ident[0:NE * NJ, 0:NE * NJ]) \
              .then_inc(pre_p.sem, pre_p.tick("w"))
            pe.wait_ge(ln0_v.sem, ln0_v.at("normal"))
            for t in range(NT):
                mm = pe.transpose(ps[:, 4 + t // 4, bass.ts(t % 4, P)], nrm[:, t, :], ident)
            mm.then_inc(pre_p.sem, pre_p.tick("nT"))
            pe.wait_ge(pre_a.sem, pre_a.at("nT0"))
            pe.wait_ge(pre_v.sem, pre_v.at("nT1"))
            for t in range(NT):
                if t >= 4:
                    pe.wait_ge(pre_v.sem, pre_v.at(f"qkv{t - 4}")) if t % 2 else pe.wait_ge(pre_a.sem, pre_a.at(f"raw{t - 4}"))
                pe.matmul(ps[:, t % 4, 0:3 * P], nT[:, bass.ts(t, P)], w_inT[:], start=True, stop=False)
                pe.matmul(ps[:, t % 4, 0:3 * P], g.ones[0:1, :], b_in[0:1, :], start=False, stop=True) \
                  .then_inc(qkv_p.sem, qkv_p.tick(f"t{t}"))
            pe.wait_ge(pre_a.sem, pre_a.at(f"raw{NT - 2}"))
            pe.wait_ge(pre_v.sem, pre_v.at(f"qkv{NT - 1}"))
            pe.wait_ge(c_v.sem, c_v.at("sum1", B - 1))
            for t in range(NT):
                mm = pe.transpose(ps[:, t // 4, bass.ts(t % 4, P)], cx[:, t, :], ident)
            mm.then_inc(mid_p.sem, mid_p.tick("cT"))
            pe.wait_ge(mid_a.sem, mid_a.at("cT"))
            for t in range(NT):
                mm = pe.matmul(ps[:, 4 + t // 4, bass.ts(t % 4, P)], nT[:, bass.ts(t, P)], w_outT[:], start=True, stop=True)
            mm.then_inc(mid_p.sem, mid_p.tick("out"))
            pe.wait_ge(mid_v.sem, mid_v.at("tok"))
            for t in range(NT):
                mm = pe.transpose(ps[:, t // 4, bass.ts(t % 4, P)], tok[:, t, :], ident)
            mm.then_inc(mid_p.sem, mid_p.tick("tokT"))
            pe.wait_ge(mid_a.sem, mid_a.at("tokT"))
            for t in range(NT):
                mm = pe.matmul(ps[:, 4, bass.ts(t, NE)], tokT[:, bass.ts(t, P)], gwT[:], start=True, stop=True)
            mm.then_inc(mid_p.sem, mid_p.tick("gate"))
            pe.wait_ge(mid_v.sem, mid_v.at("comb"))
            for t in range(NT):
                mm = pe.transpose(ps[0:NE, t // 4, bass.ts(t % 4, P)], comb[:, t, :], ident)
            mm.then_inc(mid_p.sem, mid_p.tick("combT"))
            pe.wait_ge(mid_a.sem, mid_a.at("combT"))
            for t in range(NT):
                mm = pe.matmul(ps[:, 4 + t // 4, bass.ts(t % 4, P)], combT[:, bass.ts(t, P)], b2[:], start=True, stop=True)
            mm.then_inc(mid_p.sem, mid_p.tick("b2"))
            pe.sem_inc(e_p.sem, e_p.at("w2T", -1))
            pe.sem_inc(f_p.sem, f_p.at("o", -1))
            pe.wait_ge(mid_v.sem, mid_v.at("acc"))
            with pe.Fori(0, NE) as e:
                pe.wait_ge(w_load.sem, 32 * e + 32)
                pe.wait_ge(e_a.sem, e_a.at("w1T", e - 1))
                for j in range(NJ):
                    mm = pe.transpose(ps[:, 6, bass.ts(j, P)], w1r[:, j, :], ident)
                mm.then_inc(e_p.sem, e_p.tick("w1T"))
                pe.wait_ge(e_v.sem, e_v.at("w2T", e - 1))
                for j in range(NJ):
                    mm = pe.transpose(ps[:, 7, bass.ts(j, P)], w2r[:, bass.ts(j, P)], ident)
                mm.then_inc(e_p.sem, e_p.tick("w2T"))
                with pe.Fori(0, NB) as blk:
                    n = e * NB + blk
                    pe.wait_ge(e_a.sem, e_a.at("w1T", e))
                    for j in range(NJ):
                        free = f_v.at(f"h{j}", n - 1) if j % 2 else f_a.at(f"h{j}", n - 1)
                        pe.wait_ge(f_v.sem if j % 2 else f_a.sem, free)
                        pe.matmul(ps[:, j, :], w1T[:, bass.ts(j, P)], tokT[:, bass.ds(blk * BLK, BLK)],
                                  start=True, stop=True).then_inc(f_p.sem, f_p.tick(f"h{j}"))
                    pe.wait_ge(e_v.sem, e_v.at("w2T", e))
                    pe.wait_ge(f_v.sem, f_v.at("acc", n - 1))
                    pe.wait_ge(f_v.sem, f_v.at("h3", n))
                    pe.wait_ge(f_a.sem, f_a.at("h2", n))
                    for i in range(4):
                        for j in range(NJ):
                            mm = pe.matmul(ps[:, 4, bass.ts(i, P)], fh[:, j, bass.ts(i, P)], w2T[:, j, :],
                                           start=(j == 0), stop=(j == NJ - 1))
                    mm.then_inc(f_p.sem, f_p.tick("o"))



GK = 32


def stage_gated(nc, g, a):
    with Stage(nc, "ga") as st:
        w_lr = st.sb("w_lr", [P, 2, GK])
        thr = st.sb("thr", [P, 2])
        nrm = st.sb("nrm", [P, NT, P])
        nT = st.sb("nT", [P, T])
        sq = st.sb("sq", [P, NT, P])
        stat = st.sb("stat", [P, 4, NT])
        lr = st.sb("lr", [GK, 2, T])
        cm = st.sb("cm", [P, NT, S])
        ex = st.sb("ex", [P, NT, S])
        exT = st.sb("exT", [P, B, 2, S])
        mx = st.sb("mx", [P, NT])
        o = st.sb("o", [P, NT, P])
        ps, x = g.ps, g.x
        ident = g.ident

        load = st.steps("load", ["all"])
        LOADED = 16 * 4
        ln_v, ln_a = st.steps("ln_v", LN_VECTOR), st.steps("ln_a", ["root"])
        p = st.steps("p", ["nT", "lr", "cm", "T0", "T1", "o"])
        s_a = st.steps("s_a", ["nT", "left", "cm1", "exp", "T0"])
        s_v = st.steps("s_v", ["right", "cm0", "bias", "max", "shift", "pass", "sum", "inv", "gated", "T1", "o", "x"])

        block = st.block()

        @block.sync
        def _(sp):
            sp.dma_start(w_lr[:, 0, :], a["L1_attn_compare_left"]).then_inc(load.sem, 16)
            sp.dma_start(w_lr[:, 1, :], a["L1_attn_compare_right"]).then_inc(load.sem, 16)
            sp.dma_start(thr[:, 0:1], a["L1_attn_threshold"].partition_broadcast(P)).then_inc(load.sem, 16)
            sp.dma_start(thr[:, 1:2], a["L1_attn_gate_bias"].partition_broadcast(P)).then_inc(load.sem, 16)

        @block.scalar
        def _(act):
            layernorm_root(act, ln_v, ln_a, stat)
            act.wait_ge(p.sem, p.at("nT"))
            act.activation(nT[:], banks(ps, 0, 4), ACT.Copy).then_inc(s_a.sem, s_a.tick("nT"))
            act.wait_ge(p.sem, p.at("lr"))
            act.activation(lr[:, 0, :], banks(ps, 4, 8)[0:GK, :], ACT.Copy).then_inc(s_a.sem, s_a.tick("left"))
            act.wait_ge(p.sem, p.at("cm"))
            act.activation(cm[:, NT // 2:NT, :], rows(banks(ps, 4, 8), NT // 2, S), ACT.Copy, scale=P ** -0.5) \
               .then_inc(s_a.sem, s_a.tick("cm1"))
            act.wait_ge(s_v.sem, s_v.at("shift"))
            act.activation(ex[:], ex[:], ACT.Exp).then_inc(s_a.sem, s_a.tick("exp"))
            act.wait_ge(p.sem, p.at("T0"))
            act.activation(exT[:, 0:B // 2].rearrange("p b j i -> p (b j i)"), banks(ps, 0, 4), ACT.Copy) \
               .then_inc(s_a.sem, s_a.tick("T0"))

        @block.vector
        def _(dve):
            layernorm_vector(dve, ln_v, ln_a, x[:], nrm[:], sq[:], stat[:], NT)
            per_row = lambda v: v.unsqueeze(2).to_broadcast([P, NT, S])
            dve.wait_ge(p.sem, p.at("lr"))
            dve.tensor_copy(lr[:, 1, :], banks(ps, 0, 4)[0:GK, :]).then_inc(s_v.sem, s_v.tick("right"))
            dve.wait_ge(p.sem, p.at("cm"))
            dve.tensor_scalar(cm[:, 0:NT // 2, :], rows(banks(ps, 0, 4), NT // 2, S), P ** -0.5, None, ALU.mult) \
               .then_inc(s_v.sem, s_v.tick("cm0"))
            dve.wait_ge(s_v.sem, s_v.at("cm0"))
            dve.wait_ge(s_a.sem, s_a.at("cm1"))
            dve.wait_ge(load.sem, LOADED)
            dve.tensor_scalar(ex[:], cm[:], thr[:, 1:2], None, ALU.add).then_inc(s_v.sem, s_v.tick("bias"))
            dve.wait_ge(s_v.sem, s_v.at("bias"))
            dve.tensor_reduce(mx[:], ex[:], AX.X, ALU.max).then_inc(s_v.sem, s_v.tick("max"))
            dve.wait_ge(s_v.sem, s_v.at("max"))
            dve.tensor_tensor(ex[:], ex[:], per_row(mx[:]), ALU.subtract).then_inc(s_v.sem, s_v.tick("shift"))
            dve.tensor_scalar(cm[:], cm[:], thr[:, 0:1], None, ALU.is_gt).then_inc(s_v.sem, s_v.tick("pass"))
            dve.wait_ge(s_a.sem, s_a.at("exp"))
            dve.tensor_reduce(mx[:], ex[:], AX.X, ALU.add).then_inc(s_v.sem, s_v.tick("sum"))
            dve.wait_ge(s_v.sem, s_v.at("sum"))
            dve.reciprocal(mx[:], mx[:]).then_inc(s_v.sem, s_v.tick("inv"))
            dve.tensor_tensor(ex[:], ex[:], cm[:], ALU.mult).then_inc(s_v.sem, s_v.tick("gated"))
            dve.wait_ge(p.sem, p.at("T1"))
            dve.tensor_copy(exT[:, B // 2:B].rearrange("p b j i -> p (b j i)"), banks(ps, 4, 8)) \
               .then_inc(s_v.sem, s_v.tick("T1"))
            dve.wait_ge(p.sem, p.at("o"))
            dve.wait_ge(s_v.sem, s_v.at("inv"))
            dve.tensor_tensor(o[:], rows(banks(ps, 0, 4), NT), bcast(mx[:], NT), ALU.mult).then_inc(s_v.sem, s_v.tick("o"))
            dve.wait_ge(s_v.sem, s_v.at("o"))
            dve.tensor_tensor(x[:], x[:], o[:], ALU.add).then_inc(s_v.sem, s_v.tick("x"))

        @block.tensor
        def _(pe):
            pe.wait_ge(ln_v.sem, ln_v.at("normal"))
            for t in range(NT):
                mm = pe.transpose(ps[:, t // 4, bass.ts(t % 4, P)], nrm[:, t, :], ident)
            mm.then_inc(p.sem, p.tick("nT"))
            pe.wait_ge(s_a.sem, s_a.at("nT"))
            pe.wait_ge(load.sem, LOADED)
            for i, b0 in ((0, 4), (1, 0)):
                for b in range(NB):
                    mm = pe.matmul(ps[0:GK, b0 + b, :], w_lr[:, i, :], nT[:, bass.ts(b, BLK)], start=True, stop=True)
            mm.then_inc(p.sem, p.tick("lr"))
            pe.wait_ge(s_a.sem, s_a.at("left"))
            pe.wait_ge(s_v.sem, s_v.at("right"))
            for t in range(NT):
                mm = pe.matmul(ps[:, t // 2, bass.ts(t % 2, S)], lr[:, 0, bass.ts(t, P)], lr[:, 1, bass.ts(t // 2, S)],
                               start=True, stop=True)
            mm.then_inc(p.sem, p.tick("cm"))
            pe.wait_ge(s_a.sem, s_a.at("cm1"))
            pe.wait_ge(s_v.sem, s_v.at("gated"))
            for half in range(2):
                for b in range(B // 2 * half, B // 2 * (half + 1)):
                    for j in range(2):
                        for i in range(2):
                            mm = pe.transpose(ps[:, b, bass.ds(S * j + P * i, P)], ex[:, 2 * b + i, bass.ts(j, P)], ident)
                mm.then_inc(p.sem, p.tick(f"T{half}"))
            pe.wait_ge(s_a.sem, s_a.at("T0"))
            pe.wait_ge(s_v.sem, s_v.at("T1"))
            for t in range(NT):
                for j in range(2):
                    mm = pe.matmul(ps[:, t // 4, bass.ts(t % 4, P)], exT[:, t // 2, j, bass.ts(t % 2, P)],
                                   nrm[:, 2 * (t // 2) + j, :], start=(j == 0), stop=(j == 1))
            mm.then_inc(p.sem, p.tick("o"))



MH, MD = 16, 8
NBUCKET = 32
NREL = 768
NEVER = 1e9
NU = 4 * MH
QK = S + SC
PRODUCTS = ((0, 0, 3), (1, 0, 2), (2, 0, 1))
HROWS = sum(n for _, _, n in PRODUCTS) * MD
MROW = 2 * HROWS
AHEAD = 4
HB = 32 // MD
N_STACK = 2 * (sum(n for _, _, n in PRODUCTS) + len(PRODUCTS)) + 1


def bf16_parts(value):
    parts = []
    for _ in range(3):
        unit = 2.0 ** (math.frexp(value)[1] - 8)
        parts.append(math.floor(value / unit) * unit)
        value -= parts[-1]
    assert value == 0
    return parts


def stage_masked_attention(nc, g, a):
    with Stage(nc, "ma") as st:
        w4 = st.sb("w4", [P, 4, P])
        w4T = st.sb("w4T", [P, 4, P])
        emb = st.sb("emb", [NBUCKET, MH])
        bucket = st.sb("bucket", [NBUCKET, NREL])
        rel = st.sb("rel", [MH, NREL])
        mask_u = st.sb("mask_u", [P, B * SC], U8)
        mask_b = st.sb("mask_b", [B, SC], U8)
        keep = st.sb("keep", [P, B * SC], BF16)
        keep_b = st.sb("keep_b", [B, SC])
        never = st.sb("never", [B, 3, SC], BF16)
        tb = st.sb("tb", [P, MH, P + SC])
        nrm = st.sb("nrm", [P, NT, P])
        nT = st.sb("nT", [P, T])
        stat = st.sb("stat", [P, 4, NT])
        ctxT = st.sb("ctxT", [P, B * SC])
        cur = st.sb("cur", [P, 2, SC])
        qk = st.sb("qk", [P, 2, QK])
        rest = st.sb("rest", [P, 2, QK])
        parts = st.sb("parts", [P, 2, 3, QK], BF16)
        q_stack = st.sb("q_stack", [P, 2, MH, S], BF16)
        k_stack = st.sb("k_stack", [P, 2, MH // 2, SC], BF16)
        v_cur = st.sb("v_cur", [P, 2, NK, P])
        sc = st.sb("sc", [P, 4, SC])
        pr = st.sb("pr", [P, 2, SC])
        prT = st.sb("prT", [P, 2, SC])
        low = st.sb("low", [P, NU])
        tot = st.sb("tot", [P, B, 2, MH])
        tot_cur = st.sb("tot_cur", [P, NU])
        rec = st.sb("rec", [P, B, 2, MH])
        which = st.sb("which", [P, HB])
        rel_dram = nc.dram_tensor("rel_by_distance", [MH, NREL], F32, kind="Internal").ap()
        q_dram = nc.dram_tensor("q_parts", [B, MH, 3, MD, S], BF16, kind="Internal").ap()
        k_dram = nc.dram_tensor("k_parts", [B, MH, 3, MD, SC], BF16, kind="Internal").ap()
        never_dram = nc.dram_tensor("never_parts", [B, 3, SC], BF16, kind="Internal").ap()
        ps, x, ctx = g.ps, g.x, g.ctx
        ident = g.ident
        sq = rows(nT[:], NT)
        rec_x = sq
        v = ctx
        oT = nrm[:].rearrange("p t d -> p (t d)")

        load = st.steps("load", ["all"])
        LOADED = 16 * 9
        rel_out = st.steps("rel_out", ["rel"])
        never_out = st.steps("never_out", ["never"])
        rel_in = st.steps("rel_in", ["tb"])
        ln_v, ln_a = st.steps("ln_v", LN_VECTOR), st.steps("ln_a", ["root"])
        pre_p = st.steps("pre_p", ["w4T", "rel", "nT", "ctx0", "ctx1"])
        pre_v = st.steps("pre_v", ["w4T", "rel", "ctx1", "q_zeros", "k_zeros"])
        pre_a = st.steps("pre_a", ["nT", "ctx0"])
        pre_g = st.steps("pre_g", ["keep", "keep_b", "never0", "never1", "never2", "q_ones"])
        two = lambda *xs: [f"{n}{j}" for j in range(2) for n in xs]
        cut_p = st.steps("cut_p", two("q", "k", "v"), ahead=1)
        cut_a = st.steps("cut_a", ["q0", "first0", "v0", "q1", "second0", "first1", "v1", "second1"], ahead=1)
        cut_v = st.steps("cut_v", ["k0", "rest0", "k1", "third0", "rest1", "third1"], ahead=1)
        cut_g = st.steps("cut_g", two("cur"), ahead=1)
        parts_out = [st.steps(f"parts_out{j}", ["parts"]) for j in range(2)]
        N_OUT = 6
        stack_in = [st.steps(f"stack_in{j}", ["stacks"]) for j in range(2)]
        at_p = st.steps("at_p", [f"S{u}" for u in range(AHEAD)]
                        + [n for u in range(NU) for n in ([f"S{u + AHEAD}"] if u + AHEAD < NU else []) + [f"T{u}"]
                           + ([f"O{u - 1}"] if u else [])] + [f"O{NU - 1}"], ahead=1)
        at_a = st.steps("at_a", [n for u in range(NU) for n in [f"E{u}"] + ([f"T{u - 1}"] if u % 2 else [])], ahead=1)
        TAKE = [[f"{n}{j}" for n in ["tot"] + [f"o{k}_" for k in range(HB)]] for j in range(2)]
        at_v = st.steps("at_v", [n for u in range(NU) for n in [f"M{u}"] + ([f"T{u - 3}"] if u > 2 and u % 2 == 0 else [])
                                 + (TAKE[0] if u == NU // 2 + 4 else [])] + [f"T{NU - 3}", f"T{NU - 1}"] + TAKE[1], ahead=1)
        at_g = st.steps("at_g", ["v0", "v1"], ahead=1)
        out_p = st.steps("out_p", ["rec", "out0", "out1", "out2", "out3"])
        out_v = st.steps("out_v", ["rec", "rec_x", "o"] + [f"x{i}" for i in range(NB)])
        passed_v = st.steps("passed_v", ["score"]).sem
        passed_s = st.steps("passed_s", ["stack"]).sem

        block = st.block()

        @block.sync
        def _(sp):
            mask = a["mask_Bx1x1xS2_bk0"]
            for dst, src in (
                (w4[:, 0, :], a["L1_xattn_Wq"]), (w4[:, 1, :], a["L1_xattn_Wk"]), (w4[:, 2, :], a["L1_xattn_Wv"]),
                (w4[:, 3, :], a["L1_xattn_Wo"]), (emb[:], a["L1_xattn_rel_emb"]), (bucket[:], a["bucket"]),
                (which[:], a["which"]),
                (mask_b[:], mask.rearrange("b x y s -> (b x y) s")),
                (mask_u[:], mask.rearrange("b x y s -> (b x y s)").partition_broadcast(P)),
            ):
                sp.dma_start(dst, src).then_inc(load.sem, 16)
            sp.wait_ge(pre_v.sem, pre_v.at("rel"))
            sp.dma_start(rel_dram, rel[:]).then_inc(rel_out.sem, 16)
            sp.wait_ge(rel_out.sem, 16)
            sp.dma_start(tb[:], bass.AP(rel_dram.tensor, 0, [[1, P], [NREL, MH], [1, P + SC]])).then_inc(rel_in.sem, 16)
            sp.wait_ge(pre_g.sem, pre_g.at("never2"))
            sp.dma_start(never_dram, never[:]).then_inc(never_out.sem, 16)
            with sp.Fori(0, B // 2) as i:
                for j in range(2):
                    sp.wait_ge(cut_v.sem, cut_v.at(f"third{j}", i))
                    sp.sem_inc(passed_s, 1)
                    for part in range(3):
                        for dram, cols in ((q_dram, slice(0, S)), (k_dram, slice(S, QK))):
                            dst = dram[bass.ds(2 * i + j, 1), :, part].rearrange("b h d s -> (b h) d s")
                            sp.dma_start(dst, parts[:, j, part, cols]).then_inc(parts_out[j].sem, 16)
            sp.wait_ge(never_out.sem, 16)
            for j in range(2):
                sp.wait_ge(parts_out[j].sem, 16 * N_OUT * (B // 2))
            sp.wait_ge(pre_v.sem, pre_v.at("k_zeros"))
            with sp.Fori(0, B // 2) as i:
                for j in range(2):
                    sp.wait_ge(at_p.sem, at_p.at(f"S{NU // 2 * (j + 1) - 1}", i - 1))
                    sp.sem_inc(passed_s, 1)
                    for side in range(2):
                        q_of = q_dram[bass.ds(2 * i + j, 1), side::2].rearrange("b c t d s -> (b t d) c s")
                        k_of = k_dram[bass.ds(2 * i + j, 1), side::2].rearrange("b c t d s -> (b t d) c s")
                        row = side * HROWS
                        for q_part, k_part, n in PRODUCTS:
                            sp.dma_start(k_stack[row:row + n * MD, j], k_of[k_part * MD:(k_part + n) * MD]) \
                              .then_inc(stack_in[j].sem, 16)
                            for _ in range(n):
                                sp.dma_start(q_stack[row:row + MD, j, side::2, :], q_of[q_part * MD:(q_part + 1) * MD]) \
                                  .then_inc(stack_in[j].sem, 16)
                                row += MD
                    nv = never_dram[bass.ds(2 * i + j, 1)].rearrange("b t s -> (b t) s")
                    sp.dma_start(k_stack[MROW:MROW + 3, j], nv.unsqueeze(1).to_broadcast([3, MH // 2, SC])) \
                      .then_inc(stack_in[j].sem, 16)

        @block.gpsimd
        def _(pool):
            pool.wait_ge(load.sem, LOADED)
            back = lambda buf, n, w: bass.AP(buf[:].tensor, SC - 1, [[w, n], [SC, w // SC], [-1, SC]])
            pool.tensor_copy(back(keep, P, B * SC), mask_u[:].rearrange("p (b s) -> p b s", b=B)) \
                .then_inc(pre_g.sem, pre_g.tick("keep"))
            pool.tensor_copy(back(keep_b, B, SC), mask_b[:].unsqueeze(1)).then_inc(pre_g.sem, pre_g.tick("keep_b"))
            pool.wait_ge(pre_g.sem, pre_g.at("keep_b"))
            for i, c in enumerate(bf16_parts(NEVER)):
                pool.tensor_scalar(never[:, i, :], keep_b[:], -c, c, ALU.mult, ALU.add) \
                    .then_inc(pre_g.sem, pre_g.tick(f"never{i}"))
            pool.wait_ge(pre_v.sem, pre_v.at("q_zeros"))
            pool.memset(q_stack[MROW:MROW + 3], 1.0).then_inc(pre_g.sem, pre_g.tick("q_ones"))
            pool.sem_inc(cut_g.sem, cut_g.at("cur1", -1))
            pool.sem_inc(at_g.sem, at_g.at("v1", -1))
            pool.wait_ge(pre_g.sem, pre_g.at("q_ones"))
            pool.wait_ge(pre_a.sem, pre_a.at("ctx0"))
            pool.wait_ge(pre_v.sem, pre_v.at("ctx1"))
            with pool.Fori(0, B // 2) as i:
                for j in range(2):
                    pool.wait_ge(cut_p.sem, cut_p.at(f"v{j}", i - 1))
                    pool.tensor_copy(cur[:, j, :], ctxT[:, bass.ds(2 * SC * i + SC * j, SC)]) \
                        .then_inc(cut_g.sem, cut_g.tick(f"cur{j}"))
            pool.wait_ge(cut_a.sem, cut_a.at("second1", B // 2 - 1))
            with pool.Fori(0, B // 2) as i:
                for j in range(2):
                    pool.wait_ge(at_p.sem, at_p.at(f"O{NU // 2 * (j + 1) - 1}", i - 1))
                    pool.tensor_copy(v_cur[:, j], v[:, bass.ds(2 * NK * i + NK * j, NK), :]) \
                        .then_inc(at_g.sem, at_g.tick(f"v{j}"))

        backwards = lambda b: bass.AP(ctxT[:].tensor, b * SC + SC - 1, [[B * SC, P], [SC, NB], [-1, SC]])

        @block.scalar
        def _(act):
            layernorm_root(act, ln_v, ln_a, stat)
            act.wait_ge(pre_p.sem, pre_p.at("nT"))
            act.activation(nT[:], banks(ps, 4, 8), ACT.Copy).then_inc(pre_a.sem, pre_a.tick("nT"))
            act.wait_ge(pre_p.sem, pre_p.at("ctx0"))
            act.activation(backwards(0), ps[:, 0:4, :], ACT.Copy).then_inc(pre_a.sem, pre_a.tick("ctx0"))
            act.sem_inc(cut_a.sem, cut_a.at("second1", -1))
            with act.Fori(0, B // 2) as i:
                def take_q(j):
                    act.wait_ge(cut_p.sem, cut_p.at(f"q{j}", i))
                    act.wait_ge(cut_v.sem, cut_v.at(f"rest{j}", i - 1))
                    act.activation(qk[:, j, 0:S], ps[:, 3 * j, 0:S], ACT.Copy, scale=-MD ** -0.5) \
                       .then_inc(cut_a.sem, cut_a.tick(f"q{j}"))

                def first_v(j):
                    act.wait_ge(cut_a.sem, cut_a.at(f"q{j}", i))
                    act.wait_ge(cut_v.sem, cut_v.at(f"k{j}", i))
                    act.wait_ge(parts_out[j].sem, parts_before(i))
                    act.activation(parts[:, j, 0, :], qk[:, j, :], ACT.Copy).then_inc(cut_a.sem, cut_a.tick(f"first{j}"))
                    act.wait_ge(cut_p.sem, cut_p.at(f"v{j}", i))
                    act.activation(v[:, bass.ds(2 * NK * i + NK * j, NK), :], rows(ps[:, 3 * j + 2, :], NK), ACT.Copy) \
                       .then_inc(cut_a.sem, cut_a.tick(f"v{j}"))

                def second(j):
                    act.wait_ge(cut_v.sem, cut_v.at(f"rest{j}", i))
                    act.activation(parts[:, j, 1, :], rest[:, j, :], ACT.Copy).then_inc(cut_a.sem, cut_a.tick(f"second{j}"))

                parts_before = lambda i: 16 * N_OUT * i
                take_q(0)
                first_v(0)
                take_q(1)
                second(0)
                first_v(1)
                second(1)
            act.sem_inc(at_a.sem, at_a.at(f"T{NU - 2}", -1))
            with act.Fori(0, B // 2) as i:
                def move(u):
                    act.wait_ge(at_p.sem, at_p.at(f"T{u}", i))
                    act.activation(prT[:, u % 2, :], ps[:, 2 + u % 2, :], ACT.Copy).then_inc(at_a.sem, at_a.tick(f"T{u}"))

                for u in range(NU):
                    act.wait_ge(at_v.sem, at_v.at(f"M{u}", i))
                    if u >= 2:
                        act.wait_ge(at_p.sem, at_p.at(f"T{u - 2}", i))
                    act.activation(pr[:, u % 2, :], sc[:, u % 4, :], ACT.Exp, scale=-1.0, bias=low[:, u:u + 1],
                                   accum_out=tot_cur[:, u:u + 1]).then_inc(at_a.sem, at_a.tick(f"E{u}"))
                    if u % 2:
                        if u >= 3:
                            act.wait_ge(at_p.sem, at_p.at(f"O{u - 3}", i))
                        move(u - 1)

        @block.vector
        def _(dve):
            dve.wait_ge(pre_p.sem, pre_p.at("w4T"))
            dve.tensor_copy(w4T[:].rearrange("p i d -> p (i d)"), ps[:, 0, :]).then_inc(pre_v.sem, pre_v.tick("w4T"))
            dve.wait_ge(pre_p.sem, pre_p.at("rel"))
            dve.tensor_scalar(rel[:], banks(ps, 1, 3)[0:MH, 0:NREL], -1.0, None, ALU.mult) \
               .then_inc(pre_v.sem, pre_v.tick("rel"))
            layernorm_vector(dve, ln_v, ln_a, x[:], nrm[:], sq, stat[:], NT)
            dve.wait_ge(pre_p.sem, pre_p.at("ctx1"))
            dve.tensor_copy(backwards(NB), ps[:, 4:8, :]).then_inc(pre_v.sem, pre_v.tick("ctx1"))
            dve.memset(q_stack[:], 0.0).then_inc(pre_v.sem, pre_v.tick("q_zeros"))
            dve.memset(k_stack[:], 0.0).then_inc(pre_v.sem, pre_v.tick("k_zeros"))
            dve.sem_inc(cut_v.sem, cut_v.at("third1", -1))
            dve.wait_ge(pre_g.sem, pre_g.at("keep"))
            with dve.Fori(0, B // 2) as i:
                def take_k(j):
                    dve.wait_ge(cut_p.sem, cut_p.at(f"k{j}", i))
                    dve.wait_ge(cut_v.sem, cut_v.at(f"rest{j}", i - 1))
                    dve.tensor_tensor(qk[:, j, S:QK], ps[:, 3 * j + 1, :], keep[:, bass.ds(2 * SC * i + SC * j, SC)],
                                      ALU.mult).then_inc(cut_v.sem, cut_v.tick(f"k{j}"))

                def take_rest(j):
                    dve.wait_ge(cut_a.sem, cut_a.at(f"first{j}", i))
                    dve.wait_ge(cut_v.sem, cut_v.at(f"third{j}", i - 1))
                    dve.tensor_tensor(rest[:, j, :], qk[:, j, :], parts[:, j, 0, :], ALU.subtract) \
                       .then_inc(cut_v.sem, cut_v.tick(f"rest{j}"))

                def third(j):
                    dve.wait_ge(cut_a.sem, cut_a.at(f"second{j}", i))
                    dve.tensor_tensor(parts[:, j, 2, :], rest[:, j, :], parts[:, j, 1, :], ALU.subtract) \
                       .then_inc(cut_v.sem, cut_v.tick(f"third{j}"))

                take_k(0)
                take_rest(0)
                take_k(1)
                third(0)
                take_rest(1)
                third(1)
            dve.sem_inc(at_v.sem, at_v.at(TAKE[1][-1], -1))
            dve.wait_ge(rel_in.sem, 16)
            with dve.Fori(0, B // 2) as i:
                def move(u):
                    dve.wait_ge(at_p.sem, at_p.at(f"T{u}", i))
                    if u >= 2:
                        dve.wait_ge(at_p.sem, at_p.at(f"O{u - 2}", i))
                    dve.tensor_copy(prT[:, u % 2, :], ps[:, 2 + u % 2, :]).then_inc(at_v.sem, at_v.tick(f"T{u}"))

                def take(j):
                    half = NU // 2
                    dve.wait_ge(at_p.sem, at_p.at(f"O{half * (j + 1) - 1}", i))
                    dve.tensor_copy(tot[:, bass.ds(2 * i + j, 1)].rearrange("p o t h -> p (o t) h"),
                                    tot_cur[:, bass.ts(j, half)].rearrange("p (h t) -> p t h", t=2)) \
                       .then_inc(at_v.sem, at_v.tick(f"tot{j}"))
                    o = oT[:, bass.ds((2 * i + j) * S, S)].rearrange("p (t q) -> p t q", t=2)
                    for k in range(HB):
                        mine = ps[:, 4 + 2 * j:6 + 2 * j, bass.ts(k, P)]
                        if k == 0:
                            take_k = dve.tensor_scalar(o, mine, which[:, 0:1], None, ALU.mult)
                        else:
                            dve.wait_ge(at_v.sem, at_v.at(f"o{k - 1}_{j}", i))
                            dve.sem_inc(passed_v, 1)
                            take_k = dve.scalar_tensor_tensor(o, mine, which[:, k:k + 1], o, ALU.mult, ALU.add)
                        take_k.then_inc(at_v.sem, at_v.tick(f"o{k}_{j}"))

                for u in range(NU):
                    dve.wait_ge(at_p.sem, at_p.at(f"S{u}", i))
                    dve.wait_ge(at_a.sem, at_a.at(f"E{(u - 4) % NU}", i - (u < 4)))
                    dve.sem_inc(passed_v, 1)
                    dve.tensor_tensor_reduce(sc[:, u % 4, :], ps[:, u % 2, :],
                                             tb[:, u // 2 % MH, bass.ds(P * (u % 2), SC)], 1.0, 3.0e38,
                                             ALU.add, ALU.min, low[:, u:u + 1]).then_inc(at_v.sem, at_v.tick(f"M{u}"))
                    if u > 2 and u % 2 == 0:
                        move(u - 3)
                    if u == NU // 2 + 4:
                        take(0)
                move(NU - 3)
                move(NU - 1)
                take(1)
            dve.wait_ge(at_v.sem, at_v.at(TAKE[1][0], B // 2 - 1))
            dve.reciprocal(rec[:], tot[:]).then_inc(out_v.sem, out_v.tick("rec"))
            dve.wait_ge(out_v.sem, out_v.at("rec"))
            dve.tensor_copy(rec_x.rearrange("p t (h d) -> p (t h) d", h=MH),
                            rec[:].rearrange("p b t h -> p (b t h)").unsqueeze(2).to_broadcast([P, NT * MH, MD])) \
               .then_inc(out_v.sem, out_v.tick("rec_x"))
            dve.wait_ge(out_p.sem, out_p.at("rec"))
            dve.wait_ge(at_v.sem, at_v.at(TAKE[1][-1], B // 2 - 1))
            dve.tensor_tensor(oT, oT, banks(ps, 0, 4), ALU.mult).then_inc(out_v.sem, out_v.tick("o"))
            for i in range(NB):
                dve.wait_ge(out_p.sem, out_p.at(f"out{i}"))
                xb = x[:, bass.ts(i, 4), :]
                dve.tensor_tensor(xb, rows(ps[:, 4 + i, :], 4), xb, ALU.add).then_inc(out_v.sem, out_v.tick(f"x{i}"))

        @block.tensor
        def _(pe):
            pe.wait_ge(load.sem, LOADED)
            for i in range(4):
                mm = pe.transpose(ps[:, 0, bass.ts(i, P)], w4[:, i, :], ident)
            mm.then_inc(pre_p.sem, pre_p.tick("w4T"))
            pe.matmul(ps[0:MH, 1, :], emb[:], bucket[:, 0:BLK], start=True, stop=True)
            pe.matmul(ps[0:MH, 2, 0:NREL - BLK], emb[:], bucket[:, BLK:NREL], start=True, stop=True) \
              .then_inc(pre_p.sem, pre_p.tick("rel"))
            pe.wait_ge(ln_v.sem, ln_v.at("normal"))
            for t in range(NT):
                mm = pe.transpose(ps[:, 4 + t // 4, bass.ts(t % 4, P)], nrm[:, t, :], ident)
            mm.then_inc(pre_p.sem, pre_p.tick("nT"))
            for t in range(NT):
                mm = pe.transpose(ps[:, t // 4, bass.ts(t % 4, P)], ctx[:, t, :], ident)
            mm.then_inc(pre_p.sem, pre_p.tick("ctx0"))
            pe.wait_ge(pre_a.sem, pre_a.at("nT"))
            for t in range(NT):
                mm = pe.transpose(ps[:, 4 + t // 4, bass.ts(t % 4, P)], ctx[:, NT + t, :], ident)
            mm.then_inc(pre_p.sem, pre_p.tick("ctx1"))
            pe.sem_inc(cut_p.sem, cut_p.at("v1", -1))
            pe.wait_ge(pre_a.sem, pre_a.at("ctx0"))
            pe.wait_ge(pre_v.sem, pre_v.at("ctx1"))
            with pe.Fori(0, B // 2) as i:
                for j in range(2):
                    pe.wait_ge(cut_a.sem, cut_a.at(f"q{j}", i - 1))
                    pe.matmul(ps[:, 3 * j, 0:S], w4T[:, 0, :], nT[:, bass.ds(2 * S * i + S * j, S)], start=True, stop=True) \
                      .then_inc(cut_p.sem, cut_p.tick(f"q{j}"))
                    pe.wait_ge(cut_v.sem, cut_v.at(f"k{j}", i - 1))
                    pe.matmul(ps[:, 3 * j + 1, :], w4T[:, 1, :], ctxT[:, bass.ds(2 * SC * i + SC * j, SC)],
                              start=True, stop=True).then_inc(cut_p.sem, cut_p.tick(f"k{j}"))
                    pe.wait_ge(cut_a.sem, cut_a.at(f"v{j}", i - 1))
                    pe.wait_ge(cut_g.sem, cut_g.at(f"cur{j}", i))
                    for n in range(NK):
                        mm = pe.matmul(ps[:, 3 * j + 2, bass.ts(n, P)], cur[:, j, bass.ts(n, P)], w4T[:, 2, :],
                                       start=True, stop=True)
                    mm.then_inc(cut_p.sem, cut_p.tick(f"v{j}"))
            pe.sem_inc(at_p.sem, at_p.at(f"O{NU - 1}", -1))
            pe.wait_ge(cut_a.sem, cut_a.at("second1", B // 2 - 1))
            pe.wait_ge(cut_v.sem, cut_v.at("third1", B // 2 - 1))
            pe.wait_ge(pre_g.sem, pre_g.at("q_ones"))

            def scores(u, i):
                j, h = u // (NU // 2), u // 2 % MH
                if u % (NU // 2) == 0:
                    pe.wait_ge(stack_in[j].sem, 16 * N_STACK * (i + 1))
                pe.wait_ge(at_v.sem, at_v.at(f"M{(u - 2) % NU}", i - (u < 2)))
                pe.matmul(ps[:, u % 2, :], q_stack[:, j, h, bass.ts(u % 2, P)], k_stack[:, j, h // 2, :],
                          start=True, stop=True).then_inc(at_p.sem, at_p.tick(f"S{u}"))

            def output(u, i):
                j, h = u // (NU // 2), u // 2 % MH
                pe.wait_ge(at_v.sem, at_v.at(f"T{u}", i)) if u % 2 else pe.wait_ge(at_a.sem, at_a.at(f"T{u}", i))
                if u % (NU // 2) == 0:
                    pe.wait_ge(at_g.sem, at_g.at(f"v{j}", i))
                r = bass.ts(h // HB, 32)
                for n in range(NK):
                    mm = pe.matmul(ps[r, 4 + 2 * j + u % 2, bass.ts(h % HB, P)], v_cur[:, j, n, r],
                                   prT[:, u % 2, bass.ts(n, P)], start=(n == 0), stop=(n == NK - 1))
                mm.then_inc(at_p.sem, at_p.tick(f"O{u}"))

            with pe.Fori(0, B // 2) as i:
                for u in range(AHEAD):
                    scores(u, i)
                for u in range(NU):
                    if u + AHEAD < NU:
                        scores(u + AHEAD, i)
                    pe.wait_ge(at_a.sem, at_a.at(f"E{u}", i))
                    if u >= 2:
                        pe.wait_ge(at_v.sem, at_v.at(f"T{u - 2}", i)) if u % 2 else \
                            pe.wait_ge(at_a.sem, at_a.at(f"T{u - 2}", i))
                    for n in range(NK):
                        mm = pe.transpose(ps[:, 2 + u % 2, bass.ts(n, P)], pr[:, u % 2, bass.ts(n, P)], ident)
                    mm.then_inc(at_p.sem, at_p.tick(f"T{u}"))
                    if u:
                        output(u - 1, i)
                output(NU - 1, i)
            pe.wait_ge(out_v.sem, out_v.at("rec_x"))
            for t in range(NT):
                mm = pe.transpose(ps[:, t // 4, bass.ts(t % 4, P)], rec_x[:, t, :], ident)
            mm.then_inc(out_p.sem, out_p.tick("rec"))
            pe.wait_ge(out_v.sem, out_v.at("o"))
            for i in range(NB):
                for t in range(4):
                    mm = pe.matmul(ps[:, 4 + i, bass.ts(t, P)], oT[:, bass.ts(4 * i + t, P)], w4T[:, 3, :],
                                   start=True, stop=True)
                mm.then_inc(out_p.sem, out_p.tick(f"out{i}"))



ACT_ONE, W_ONE = 16.0, 64.0
MAGIC = 1.5 * 2.0 ** 23
QMIN, QMAX = -128.0, 127.0


def stage_quantized(nc, g, a):
    with Stage(nc, "qu") as st:
        w1 = st.sb("w1", [P, NJ, P])
        w2 = st.sb("w2", [P, HID])
        w1q = st.sb("w1q", [P, HID], BF16)
        w2q = st.sb("w2q", [P, NJ, P], BF16)
        b1 = st.sb("b1", [P, NJ])
        b2 = st.sb("b2", [P, P])
        nrm = st.sb("nrm", [P, NT, P])
        sq = st.sb("sq", [P, NT, P])
        stat = st.sb("stat", [P, 4, NT])
        xq = st.sb("xq", [P, T], BF16)
        hr = st.sb("hr", [P, 2, BLK])
        hq = st.sb("hq", [P, NB, NJ, BLK], BF16)
        ps, x = g.ps, g.x
        ident = g.ident

        load = st.steps("load", ["all"])
        LOADED = 16 * (3 + NJ)
        ln_v, ln_a = st.steps("ln_v", LN_VECTOR), st.steps("ln_a", ["root"])
        quant = [f"{n}_{s}" for n in ("w1", "w2", "b1", "b2") for s in ("up", "round", "clip")]
        q_v = st.steps("q_v", quant + ["b1", "b2", "w1T", "x_up", "x_round", "x_clip"])
        q_g = st.steps("q_g", ["x_bias"])
        q_a = st.steps("q_a", ["w2T", "xT"])
        q_p = st.steps("q_p", ["w1T", "w2T", "xT"])
        units = [(b, j) for b in range(NB) for j in range(NJ)]
        h_p = st.steps("h_p", [f"h{b}{j}" for b, j in units])
        h_a = st.steps("h_a", [f"r{b}{j}" for b, j in units])
        h_v = st.steps("h_v", [f"{n}{b}{j}" for b, j in units for n in ("m", "q")])
        o_p = st.steps("o_p", [f"o{b}" for b in range(NB)])
        o_v = st.steps("o_v", [f"x{b}" for b in range(NB)])

        block = st.block()

        @block.sync
        def _(sp):
            sp.dma_start(w1[:], a["L1_ffn_w1"].rearrange("(j p) d -> p j d", p=P)).then_inc(load.sem, 16)
            sp.dma_start(w2[:], a["L1_ffn_w2"]).then_inc(load.sem, 16)
            for j in range(NJ):
                sp.dma_start(b1[:, j:j + 1], a["L1_ffn_b1"][P * j:P * (j + 1)].unsqueeze(1)).then_inc(load.sem, 16)
            sp.dma_start(b2[:], a["L1_ffn_b2"].partition_broadcast(P)).then_inc(load.sem, 16)

        @block.gpsimd
        def _(pool):
            pool.wait_ge(q_v.sem, q_v.at("b2"))
            pool.wait_ge(ln_v.sem, ln_v.at("centred"))
            pool.tensor_tensor(x[:], x[:], b2[:].unsqueeze(1).to_broadcast([P, NT, P]), ALU.add) \
                .then_inc(q_g.sem, q_g.tick("x_bias"))

        @block.scalar
        def _(act):
            layernorm_root(act, ln_v, ln_a, stat)
            act.wait_ge(q_p.sem, q_p.at("w2T"))
            act.activation(w2q[:].rearrange("p j d -> p (j d)"), ps[:, 1, :], ACT.Copy).then_inc(q_a.sem, q_a.tick("w2T"))
            act.wait_ge(q_p.sem, q_p.at("xT"))
            act.activation(xq[:], banks(ps, 4, 8), ACT.Copy).then_inc(q_a.sem, q_a.tick("xT"))
            for u, (b, j) in enumerate(units):
                act.wait_ge(h_p.sem, h_p.at(f"h{b}{j}"))
                if u >= 2:
                    act.wait_ge(h_v.sem, h_v.at("q%d%d" % units[u - 2]))
                act.activation(hr[:, u % 2, :], ps[:, u % 4, :], ACT.Relu, bias=b1[:, j:j + 1], scale=1 / W_ONE) \
                   .then_inc(h_a.sem, h_a.tick(f"r{b}{j}"))

        @block.vector
        def _(dve):
            def quantize(name, v, one):
                dve.tensor_scalar(v, v, one, None, ALU.mult).then_inc(q_v.sem, q_v.tick(f"{name}_up"))
                dve.wait_ge(q_v.sem, q_v.at(f"{name}_up"))
                dve.tensor_scalar(v, v, MAGIC, MAGIC, ALU.add, ALU.subtract).then_inc(q_v.sem, q_v.tick(f"{name}_round"))
                dve.wait_ge(q_v.sem, q_v.at(f"{name}_round"))
                dve.tensor_scalar(v, v, QMIN, QMAX, ALU.max, ALU.min).then_inc(q_v.sem, q_v.tick(f"{name}_clip"))

            dve.wait_ge(load.sem, LOADED)
            quantize("w1", w1[:], W_ONE)
            quantize("w2", w2[:], W_ONE)
            quantize("b1", b1[:], W_ONE)
            quantize("b2", b2[:], W_ONE)
            dve.wait_ge(q_v.sem, q_v.at("b2_clip"))
            dve.tensor_scalar(b1[:], b1[:], ACT_ONE / W_ONE, None, ALU.mult).then_inc(q_v.sem, q_v.tick("b1"))
            dve.tensor_scalar(b2[:], b2[:], 1 / W_ONE, None, ALU.mult).then_inc(q_v.sem, q_v.tick("b2"))
            dve.wait_ge(q_p.sem, q_p.at("w1T"))
            dve.tensor_copy(w1q[:], ps[:, 0, :]).then_inc(q_v.sem, q_v.tick("w1T"))
            layernorm_vector(dve, ln_v, ln_a, x[:], nrm[:], sq[:], stat[:], NT)
            dve.wait_ge(ln_v.sem, ln_v.at("normal"))
            quantize("x", nrm[:], ACT_ONE)
            for u, (b, j) in enumerate(units):
                dve.wait_ge(h_a.sem, h_a.at(f"r{b}{j}"))
                dve.tensor_scalar(hr[:, u % 2, :], hr[:, u % 2, :], QMAX, MAGIC, ALU.min, ALU.add) \
                   .then_inc(h_v.sem, h_v.tick(f"m{b}{j}"))
                dve.wait_ge(h_v.sem, h_v.at(f"m{b}{j}"))
                dve.tensor_scalar(hq[:, b, j, :], hr[:, u % 2, :], MAGIC, None, ALU.subtract) \
                   .then_inc(h_v.sem, h_v.tick(f"q{b}{j}"))
            dve.wait_ge(q_g.sem, q_g.at("x_bias"))
            for b in range(NB):
                dve.wait_ge(o_p.sem, o_p.at(f"o{b}"))
                xb = x[:, 4 * b:4 * b + 4, :].rearrange("p t d -> p (t d)")
                dve.scalar_tensor_tensor(xb, ps[:, 4 + b, :], 1 / (ACT_ONE * W_ONE), xb, ALU.mult, ALU.add) \
                   .then_inc(o_v.sem, o_v.tick(f"x{b}"))

        @block.tensor
        def _(pe):
            pe.wait_ge(q_v.sem, q_v.at("w2_clip"))
            for j in range(NJ):
                mm = pe.transpose(ps[:, 0, bass.ts(j, P)], w1[:, j, :], ident)
            mm.then_inc(q_p.sem, q_p.tick("w1T"))
            for j in range(NJ):
                mm = pe.transpose(ps[:, 1, bass.ts(j, P)], w2[:, bass.ts(j, P)], ident)
            mm.then_inc(q_p.sem, q_p.tick("w2T"))
            pe.wait_ge(q_v.sem, q_v.at("x_clip"))
            for t in range(NT):
                mm = pe.transpose(ps[:, 4 + t // 4, bass.ts(t % 4, P)], nrm[:, t, :], ident)
            mm.then_inc(q_p.sem, q_p.tick("xT"))
            pe.wait_ge(q_a.sem, q_a.at("xT"))
            pe.wait_ge(q_v.sem, q_v.at("w1T"))

            def up(u):
                b, j = units[u]
                if u >= 4:
                    pe.wait_ge(h_a.sem, h_a.at("r%d%d" % units[u - 4]))
                pe.matmul(ps[:, u % 4, :], w1q[:, bass.ts(j, P)], xq[:, bass.ts(b, BLK)], start=True, stop=True) \
                  .then_inc(h_p.sem, h_p.tick(f"h{b}{j}"))

            def down(b):
                pe.wait_ge(h_v.sem, h_v.at(f"q{b}{NJ - 1}"))
                for i in range(4):
                    for j in range(NJ):
                        mm = pe.matmul(ps[:, 4 + b, bass.ts(i, P)], hq[:, b, j, bass.ts(i, P)], w2q[:, j, :],
                                       start=(j == 0), stop=(j == NJ - 1))
                mm.then_inc(o_p.sem, o_p.tick(f"o{b}"))

            for u in range(len(units)):
                up(u)
                if u % NJ == NJ - 1 and u > NJ:
                    down(u // NJ - 1)
            down(NB - 1)



class Shared:
    pass


def decoder(nc, a, out):
    g = Shared()
    with ExitStack() as stack:
        g.ps = stack.enter_context(nc.psum_tensor("ps", [P, 8, BLK], F32))
        g.x = stack.enter_context(nc.sbuf_tensor("x", [P, NT, P], F32))
        g.ctx = stack.enter_context(nc.sbuf_tensor("ctx", [P, B * SC // P, P], F32))
        const = stack.enter_context(nc.sbuf_tensor("const", [P, 2 * P], F32))
        rep8 = stack.enter_context(nc.sbuf_tensor("rep8", [8, P], F32))
        ones = stack.enter_context(nc.sbuf_tensor("ones", [P, P], F32))
        g.ident, g.bd8, g.rep8, g.ones = const[:, 0:P], const[:, P:2 * P], rep8[:], ones[:]
        x_dram = a["x"].rearrange("b (n p) d -> p (b n) d", p=P)
        with Stage(nc, "start") as st:
            loaded = st.steps("loaded", ["all"])
            made = st.steps("made", ["ones"])
            block = st.block()

            @block.sync
            def _(sp):
                sp.dma_start(g.x[:], x_dram).then_inc(loaded.sem, 16)
                sp.dma_start(const[:], a["const"]).then_inc(loaded.sem, 16)
                sp.dma_start(rep8[:], a["rep8"]).then_inc(loaded.sem, 16)
                sp.wait_ge(loaded.sem, 48)

            @block.vector
            def _(dve):
                dve.memset(ones[:], 1.0).then_inc(made.sem, made.tick("ones"))
                dve.wait_ge(made.sem, 1)

        stages = [stage_fast_weights, stage_cross_attention, stage_experts, stage_gated, stage_masked_attention, stage_quantized]
        for stage in stages[:LAST_STAGE]:
            stage(nc, g, a)
        with Stage(nc, "end") as st:
            stored = st.steps("stored", ["x"])
            block = st.block()

            @block.sync
            def _(sp):
                sp.dma_start(out.rearrange("b (n p) d -> p (b n) d", p=P), g.x[:]).then_inc(stored.sem, 16)
                sp.wait_ge(stored.sem, 16)


def constants():
    p = np.arange(P)
    const = np.concatenate([np.eye(P), p[:, None] // 8 == p[None, :] // 8], axis=1).astype(np.float32)
    rep8 = (np.arange(8)[:, None] == p[None, :] % 8).astype(np.float32)
    lower = np.tril(np.ones((8, 8), np.float32), -1).reshape(64)
    n = np.maximum(np.arange(NREL) - (SC - 1), 0)
    exact = NBUCKET // 2
    large = exact + (np.log(n.astype(np.float32) / exact + 1e-9) / math.log(128 / exact) * exact).astype(np.int32)
    of = np.where(n < exact, n, np.minimum(large, NBUCKET - 1))
    bucket = (np.arange(NBUCKET)[:, None] == of[None, :]).astype(np.float32)
    which = (p[:, None] // MD % HB == np.arange(HB)[None, :]).astype(np.float32)
    return {"const": const, "rep8": rep8, "lower": lower, "bucket": bucket, "which": which}


def kernel(**inputs):
    import numpy as _np
    import concourse.bacc as _bacc
    from concourse import mybir as _mybir
    from concourse.bass_utils import run_bass_kernel_spmd as _run

    nc = _bacc.Bacc("TRN2", target_bir_lowering=False, num_devices=1)
    arrays, args = {}, {}
    for name, value in list(inputs.items()) + list(constants().items()):
        v = _np.ascontiguousarray(value)
        arrays[f"in_{name}_dram"] = v
        args[name] = nc.dram_tensor(f"in_{name}_dram", v.shape, _mybir.dt.from_np(v.dtype), kind="ExternalInput").ap()
    out = nc.dram_tensor("out_0_dram", (B, S, P), F32, kind="ExternalOutput").ap()
    decoder(nc, args, out)
    r = _run(nc, [arrays], core_ids=[0])
    return r.results[0]["out_0_dram"]
```

```python
import math
from contextlib import ExitStack

import numpy as np

import concourse.bass as bass
from concourse import mybir

F32 = mybir.dt.float32
BF16 = mybir.dt.bfloat16
U8 = mybir.dt.uint8
ALU = mybir.AluOpType
ACT = mybir.ActivationFunctionType
AX = mybir.AxisListType

LAST_STAGE = 6

P = 128
B, S = 8, 256
T = B * S
NT = T // P
BLK = 512
NB = T // BLK
SC = 512
HID = 512
NJ = HID // P
LN_EPS = 1e-5


class Steps:

    def __init__(self, sem, names, ahead=0):
        self.sem, self.names, self.ahead = sem, list(names), ahead
        assert len(set(self.names)) == len(self.names)
        self.next = 0

    def at(self, name, t=0):
        return (t + self.ahead) * len(self.names) + self.names.index(name) + 1

    def tick(self, name):
        assert self.names[self.next % len(self.names)] == name, (name, self.names[self.next % len(self.names)])
        self.next += 1
        return 1


def bcast(stat, n, width=P):
    return stat.unsqueeze(2).to_broadcast([P, n, width])


def rows(flat, n, width=P):
    return flat.rearrange("p (n d) -> p n d", n=n)


def banks(ps, a, b):
    return ps[:, a:b, :].rearrange("p a b -> p (a b)")


LN_VECTOR = ["stats", "moments", "variance", "rstd", "normal0", "normal1", "normal2", "normal"]


def normal_of(t, n=NT):
    quarter = t // (n // 4)
    return "normal" if quarter == 3 else f"normal{quarter}"


def layernorm_vector(dve, vec, root, src, dst, scratch, st, n):
    at = vec.at
    for t in range(n):
        stats = dve.bn_stats(scratch[:, t, 0:6], src[:, t, :])
    stats.then_inc(vec.sem, vec.tick("stats"))
    dve.wait_ge(vec.sem, at("stats"))
    for t in range(n):
        moments = dve.bn_aggr(scratch[:, t, 8:10], scratch[:, t, 0:6])
    moments.then_inc(vec.sem, vec.tick("moments"))
    dve.wait_ge(vec.sem, at("moments"))
    dve.tensor_scalar(st[:, 2, :].unsqueeze(2), scratch[:, 0:n, 9:10], LN_EPS, None, ALU.add) \
       .then_inc(vec.sem, vec.tick("variance"))
    dve.wait_ge(root.sem, root.at("root"))
    dve.reciprocal(st[:, 3, :], st[:, 3, :]).then_inc(vec.sem, vec.tick("rstd"))
    dve.wait_ge(vec.sem, at("rstd"))
    for t in range(n):
        normal = dve.tensor_scalar(dst[:, t, :], src[:, t, :], scratch[:, t, 8:9], st[:, 3, t:t + 1],
                                   ALU.subtract, ALU.mult)
        if (t + 1) % (n // 4) == 0:
            normal.then_inc(vec.sem, vec.tick(normal_of(t, n)))


def layernorm_root(act, vec, root, st):
    act.wait_ge(vec.sem, vec.at("variance"))
    act.activation(st[:, 3, :], st[:, 2, :], ACT.Sqrt).then_inc(root.sem, root.tick("root"))


class Stage:

    def __init__(self, nc, name):
        self.nc, self.name, self.stack = nc, name, ExitStack()

    def __enter__(self):
        return self

    def __exit__(self, *failed):
        return self.stack.__exit__(*failed)

    def sb(self, name, shape, dt=F32):
        return self.stack.enter_context(self.nc.sbuf_tensor(f"{self.name}_{name}", shape, dt))

    def steps(self, name, names, ahead=0):
        return Steps(self.stack.enter_context(self.nc.semaphore(f"{self.name}_{name}")), names, ahead)

    def block(self):
        return self.stack.enter_context(self.nc.Block())



NS_A, NS_B, NS_C = 3.4445, -4.775, 2.0315
NS_ITERS = 5
TTT_STEPS = 2
LR = 0.1
NS_GUARD = 1e-7 * T * P / 2


def stage_fast_weights(nc, g, a):
    with Stage(nc, "fw") as st:
        w_qkv = st.sb("w_qkv", [P, 3 * P])
        b_qk = st.sb("b_qk", [P, 2])
        b_v = st.sb("b_v", [P, P])
        b_o = st.sb("b_o", [P, P])
        w_o = st.sb("w_o", [P, P])
        head8 = st.sb("head8", [8, 4])
        hd = st.sb("hd", [P, 4])
        gate = st.sb("gate", [P, HID])
        val = st.sb("val", [P, HID])
        proj = st.sb("proj", [P, NJ, P])
        projT = st.sb("projT", [P, HID])
        nrm = st.sb("nrm", [P, NT, P])
        nT = st.sb("nT", [P, T])
        sq = st.sb("sq", [P, T])
        stat = st.sb("stat", [P, 4, NT])
        qT = st.sb("qT", [P, T])
        kk = st.sb("kk", [P, NT + 2, 2, P])
        v = st.sb("v", [P, NT, P])
        qn = st.sb("qn", [P, T])
        kn = st.sb("kn", [P, T])
        kT_cur = st.sb("kT_cur", [P, P])
        k_cur = st.sb("k_cur", [P, P])
        sg = st.sb("sg", [P, 2, HID])
        sw = st.sb("sw", [P, 2, HID])
        h = st.sb("h", [P, 2, HID])
        vs = st.sb("vs", [P, 2, HID])
        u = st.sb("u", [P, 2, HID])
        e = st.sb("e", [P, 2, HID])
        dV = st.sb("dV", [P, 2, HID])
        dG = st.sb("dG", [P, 2, HID])
        hT = st.sb("hT", [P, 2, HID])
        dp = st.sb("dp", [P, 2, P])
        dpT = st.sb("dpT", [P, 2, P])
        X = st.sb("X", [P, 3, HID])
        XT = st.sb("XT", [P, 3, HID])
        Am = st.sb("Am", [P, 3, P])
        bA = st.sb("bA", [P, 3, P])
        Bm = st.sb("Bm", [P, 3, P])
        aI = st.sb("aI", [P, P])
        fro = st.sb("fro", [P, 3])
        frn = st.sb("frn", [P, 3])
        wo2 = st.sb("wo2", [P, NJ, P])
        fh = st.sb("fh", [P, NJ, BLK])
        fs = st.sb("fs", [P, 2, BLK])
        ps, x = g.ps, g.x
        ident, bd8, rep8, ones = g.ident, g.bd8, g.rep8, g.ones

        load = st.steps("load", [f"{i}" for i in range(256)])
        pre_v = st.steps("pre_v", LN_VECTOR + ["hd", "zeroed", "kk_zeros", "aI", "nT1", "nT3", "kT_raw", "k_sq", "k_guard", "k_inv", "k_unit",
                                               "kT", "v", "x_bias", "projT"])
        root = st.steps("root", ["root"])
        pre_a = st.steps("pre_a", ["nT0", "nT2", "qT_raw", "q_sq", "k_norm", "q_norm", "k_tok"])
        pre_p = st.steps("pre_p", ["hd", "nT0", "nT1", "nT2", "nT3", "k", "q", "k_sq", "q_sq", "k_spread", "v", "k_tok", "projT"])
        fw_p = st.steps("fw_p", ["g", "v"], ahead=1)
        fw_a = st.steps("fw_a", ["sg", "vs"], ahead=1)
        fw_v = st.steps("fw_v", ["sw", "h", "u", "ds"], ahead=1)
        fw_g = st.steps("fw_g", ["e"], ahead=1)
        kT_g = st.steps("kT_g", ["kT_cur"])
        q_v = st.steps("q_v", ["inv", "unit", "q"])
        q_g = st.steps("q_g", ["guard"])
        QCOLS = T // (TTT_STEPS * NT)
        norm_load = st.steps("norm_load", ["all"])
        gather = st.sb("gather", [P, B, P])
        spread = st.sb("spread", [P, B, P])
        k_norm = st.sb("k_norm", [P, S])
        passed_g = st.steps("passed_g", ["wait"]).sem
        bw_p = st.steps("bw_p", ["hT", "dproj", "pred", "dpT", "dh", "grads"], ahead=1)
        bw_a = st.steps("bw_a", ["hT", "dpT"], ahead=1)
        bw_v = st.steps("bw_v", ["dp", "dV", "dG"], ahead=1)
        bw_g = st.steps("bw_g", ["k_cur"], ahead=1)
        UNROLL = 4
        A_STEP, KT_STEP = NT + 1, NT + 2
        open_p = st.steps("open_p", ["opened", "last", "fro", "XT"])
        open_a = st.steps("open_a", ["fro0", "fro1", "fro2", "root", "XT0", "XT1", "XT2"])
        open_v = st.steps("open_v", ["guard", "inv", "X0", "X1", "X2"])
        ns_p = st.steps("ns_p", [f"{n}{m}" for n in ("A", "A2", "X") for m in range(3)], ahead=1)
        ns_a = st.steps("ns_a", [f"{n}{m}" for n in ("A", "X") for m in range(3)], ahead=1)
        ns_v = st.steps("ns_v", [f"{n}{m}" for n in ("bA", "B", "XT") for m in range(3)], ahead=1)
        upd_v = st.steps("upd_v", ["gate", "val", "projT", "proj"], ahead=1)
        fin_p = st.steps("fin_p", ["wo2"])
        fin_v = st.steps("fin_v", ["wo2"])
        ask_p = st.steps("ask_p", ["gv0", "gv1", "gv2", "gv3", "o"], ahead=1)
        ask_a = st.steps("ask_a", ["s0", "s1", "s2", "s3"], ahead=1)
        ask_v = st.steps("ask_v", [f"{n}{j}" for j in range(4) for n in ("sw", "h")] + ["x"], ahead=1)
        zero = st.sb("zero", [P, P])
        made_g = st.steps("made_g", ["zero"])
        zero_v = st.steps("zero_v", ["dp"])
        zero_g = st.steps("zero_g", ["k"])

        block = st.block()

        @block.sync
        def _(sp):
            for dst, src in (
                (w_qkv[:], a["L0_attn_qkv_w"]), (b_qk[:, 0:1], a["L0_attn_qkv_b"][0:P].unsqueeze(1)),
                (b_qk[:, 1:2], a["L0_attn_qkv_b"][P:2 * P].unsqueeze(1)),
                (b_v[:], a["L0_attn_qkv_b"][2 * P:3 * P].partition_broadcast(P)),
                (head8[:, 0:1], a["L0_attn_qn_scale"].unsqueeze(1)), (head8[:, 1:2], a["L0_attn_qn_bias"].unsqueeze(1)),
                (head8[:, 2:3], a["L0_attn_kn_scale"].unsqueeze(1)), (head8[:, 3:4], a["L0_attn_kn_bias"].unsqueeze(1)),
                (gate[:], a["L0_attn_ttt_gate"]), (val[:], a["L0_attn_ttt_val"]),
                (proj[:], a["L0_attn_ttt_proj"].rearrange("(j p) d -> p j d", p=P)),
                (w_o[:], a["L0_attn_proj_w"]), (b_o[:], a["L0_attn_proj_b"].partition_broadcast(P)),
            ):
                sp.dma_start(dst, src).then_inc(load.sem, 16)

            sp.dma_start(gather[:], a["gather"]).then_inc(norm_load.sem, 16)
            sp.dma_start(spread[:], a["spread"]).then_inc(norm_load.sem, 16)

        N_LOADS = 13

        @block.gpsimd
        def _(pool):
            pool.memset(zero[:], 0.0).then_inc(made_g.sem, made_g.tick("zero"))
            pool.wait_ge(made_g.sem, made_g.at("zero"))
            pool.wait_ge(pre_a.sem, pre_a.at("q_norm"))
            pool.tensor_scalar(qn[:], qn[:], 1e-6, None, ALU.add).then_inc(q_g.sem, q_g.tick("guard"))
            pool.wait_ge(q_g.sem, q_g.at("guard"))
            pool.sem_inc(fw_g.sem, fw_g.at("e", -1))
            pool.sem_inc(bw_g.sem, bw_g.at("k_cur", -1))
            pool.wait_ge(pre_v.sem, pre_v.at("kT"))
            pool.wait_ge(pre_a.sem, pre_a.at("k_tok"))

            def take_kT(step, tile, n):
                pool.wait_ge(fw_p.sem, fw_p.at("v", step * A_STEP + n - 1))
                pool.sem_inc(passed_g, 1)
                pool.tensor_copy(kT_cur[:].unsqueeze(1), kk[:, tile, 0, :]).then_inc(kT_g.sem, kT_g.tick("kT_cur"))

            def take_e(n, s):
                pool.wait_ge(fw_a.sem, fw_a.at("vs", n))
                pool.wait_ge(fw_v.sem, fw_v.at("ds", n))
                pool.tensor_tensor(e[:, s, :], u[:, s, :], vs[:, s, :], ALU.mult).then_inc(fw_g.sem, fw_g.tick("e"))

            with pool.Fori(0, TTT_STEPS) as step:
                pool.wait_ge(upd_v.sem, upd_v.at("proj", step - 1))
                pool.tensor_tensor(k_cur[:], zero[:], zero[:], ALU.add).then_inc(zero_g.sem, zero_g.tick("k"))
                take_kT(step, slice(0, 1), 0)
                take_kT(step, slice(1, 2), 1)
                take_e(step * A_STEP, 0)
                with pool.Fori(0, NT // UNROLL) as i:
                    for r in range(UNROLL):
                        t = UNROLL * i + r
                        take_kT(step, bass.ds(t + 2, 1), t + 2)
                        pool.wait_ge(bw_p.sem, bw_p.at("grads", step * NT + t))
                        pool.tensor_copy(k_cur[:].unsqueeze(1), kk[:, bass.ds(t, 1), 1, :]) \
                            .then_inc(bw_g.sem, bw_g.tick("k_cur"))
                        take_e(step * A_STEP + t + 1, (r + 1) % 2)

        @block.scalar
        def _(act):
            layernorm_root(act, pre_v, root, stat)
            for b in (0, 2):
                act.wait_ge(pre_p.sem, pre_p.at(f"nT{b}"))
                act.activation(nT[:, bass.ts(b, BLK)], ps[:, b, :], ACT.Copy).then_inc(pre_a.sem, pre_a.tick(f"nT{b}"))
            act.wait_ge(pre_p.sem, pre_p.at("q"))
            act.wait_ge(load.sem, 16 * N_LOADS)
            act.activation(qT[:], banks(ps, 4, 8), ACT.Identity, bias=b_qk[:, 0:1]) \
               .then_inc(pre_a.sem, pre_a.tick("qT_raw"))
            act.wait_ge(pre_a.sem, pre_a.at("qT_raw"))
            act.wait_ge(pre_v.sem, pre_v.at("normal"))
            act.activation(sq[:], qT[:], ACT.Square).then_inc(pre_a.sem, pre_a.tick("q_sq"))
            act.wait_ge(pre_p.sem, pre_p.at("k_sq"))
            act.activation(k_norm[:], ps[:, 0, 0:S], ACT.Sqrt) \
               .then_inc(pre_a.sem, pre_a.tick("k_norm"))
            act.wait_ge(pre_p.sem, pre_p.at("q_sq"))
            act.activation(qn[:], banks(ps, 4, 8), ACT.Sqrt) \
               .then_inc(pre_a.sem, pre_a.tick("q_norm"))
            act.wait_ge(pre_p.sem, pre_p.at("k_tok"))
            act.activation(kk[:, 0:NT, 1, :], rows(banks(ps, 4, 8), NT), ACT.Copy) \
               .then_inc(pre_a.sem, pre_a.tick("k_tok"))
            for each in (fw_a, bw_a):
                act.sem_inc(each.sem, len(each.names))
            act.sem_inc(ns_a.sem, ns_a.at("X2", -1))
            act.sem_inc(ask_a.sem, ask_a.at("s3", -1))
            with act.Fori(0, TTT_STEPS) as step:
                def forward(n, s, before, between=lambda: None):
                    act.wait_ge(fw_p.sem, fw_p.at("g", n))
                    act.wait_ge(fw_v.sem, fw_v.at("ds", before))
                    act.activation(sg[:, s, :], ps[:, 0, :], ACT.Sigmoid).then_inc(fw_a.sem, fw_a.tick("sg"))
                    between()
                    act.wait_ge(fw_p.sem, fw_p.at("v", n))
                    act.wait_ge(fw_g.sem, fw_g.at("e", before))
                    act.activation(vs[:, s, :], ps[:, 1, :], ACT.Copy).then_inc(fw_a.sem, fw_a.tick("vs"))

                forward(step * A_STEP, 0, step * A_STEP - 1)
                with act.Fori(0, NT // UNROLL) as i:
                    for r in range(UNROLL):
                        t, s = UNROLL * i + r, r % 2
                        n, n_fw = step * NT + t, step * A_STEP + t
                        act.wait_ge(bw_p.sem, bw_p.at("hT", n))
                        act.activation(hT[:, s, :], ps[:, 2, :], ACT.Copy).then_inc(bw_a.sem, bw_a.tick("hT"))

                        def take_dpT():
                            act.wait_ge(bw_p.sem, bw_p.at("dpT", n))
                            act.activation(dpT[:, s, :], ps[:, 3, 0:P], ACT.Copy).then_inc(bw_a.sem, bw_a.tick("dpT"))

                        forward(n_fw + 1, 1 - s, n_fw - 1, take_dpT)
                act.wait_ge(open_p.sem, open_p.at("last", step))
                for m in range(3):
                    act.activation(XT[:, m, :], ps[:, 5 + m, :], ACT.Square, accum_out=fro[:, m:m + 1]) \
                       .then_inc(open_a.sem, open_a.tick(f"fro{m}"))
                act.wait_ge(open_p.sem, open_p.at("fro", step))
                act.activation(frn[:], ps[:, 0, 0:3], ACT.Sqrt).then_inc(open_a.sem, open_a.tick("root"))
                act.wait_ge(open_p.sem, open_p.at("XT", step))
                for m in range(3):
                    act.activation(XT[:, m, :], ps[:, 1 + m, :], ACT.Copy).then_inc(open_a.sem, open_a.tick(f"XT{m}"))
                with act.Fori(0, NS_ITERS) as it:
                    n = step * NS_ITERS + it
                    for m in range(3):
                        act.wait_ge(ns_p.sem, ns_p.at(f"A{m}", n))
                        act.activation(Am[:, m, :], ps[:, m, 0:P], ACT.Copy).then_inc(ns_a.sem, ns_a.tick(f"A{m}"))
                    for m in range(3):
                        act.wait_ge(ns_p.sem, ns_p.at(f"X{m}", n))
                        act.activation(X[:, m, :], ps[:, m, :], ACT.Copy).then_inc(ns_a.sem, ns_a.tick(f"X{m}"))
            with act.Fori(0, NB) as blk:
                for j in range(NJ):
                    act.wait_ge(ask_p.sem, ask_p.at(f"gv{j}", blk))
                    act.wait_ge(ask_v.sem, ask_v.at(f"sw{(j - 2) % 4}", blk - (j < 2)))
                    act.activation(fs[:, j % 2, :], ps[:, 2 * (j % 2), :], ACT.Sigmoid) \
                       .then_inc(ask_a.sem, ask_a.tick(f"s{j}"))

        @block.vector
        def _(dve):
            layernorm_vector(dve, pre_v, root, x[:], nrm[:], rows(sq[:], NT), stat[:], NT)
            dve.wait_ge(pre_p.sem, pre_p.at("hd"))
            dve.tensor_copy(hd[:], ps[:, 7, 0:4]).then_inc(pre_v.sem, pre_v.tick("hd"))
            for buffer in (h, dV, dG):
                zeroed = dve.memset(buffer[:, 1, :], 0.0)
            zeroed.then_inc(pre_v.sem, pre_v.tick("zeroed"))
            dve.memset(kk[:, NT:NT + 2], 0.0).then_inc(pre_v.sem, pre_v.tick("kk_zeros"))
            dve.tensor_scalar(aI[:], ident, NS_A, None, ALU.mult).then_inc(pre_v.sem, pre_v.tick("aI"))
            for b in (1, 3):
                dve.wait_ge(pre_p.sem, pre_p.at(f"nT{b}"))
                dve.tensor_copy(nT[:, bass.ts(b, BLK)], ps[:, b, :]).then_inc(pre_v.sem, pre_v.tick(f"nT{b}"))
            kT = kk[:, 0:NT, 0, :]
            kn3 = rows(kn[:], NT)
            k_ps = rows(banks(ps, 0, 4), NT)
            dve.wait_ge(pre_p.sem, pre_p.at("k"))
            dve.wait_ge(load.sem, 16 * N_LOADS)
            dve.tensor_scalar(kT, k_ps, b_qk[:, 1:2], None, ALU.add).then_inc(pre_v.sem, pre_v.tick("kT_raw"))
            dve.wait_ge(pre_v.sem, pre_v.at("kT_raw"))
            dve.tensor_tensor(kn3, kT, kT, ALU.mult).then_inc(pre_v.sem, pre_v.tick("k_sq"))
            dve.wait_ge(pre_a.sem, pre_a.at("k_norm"))
            dve.tensor_scalar(k_norm[:], k_norm[:], 1e-6, None, ALU.add).then_inc(pre_v.sem, pre_v.tick("k_guard"))
            dve.wait_ge(pre_v.sem, pre_v.at("k_guard"))
            dve.reciprocal(k_norm[:], k_norm[:]).then_inc(pre_v.sem, pre_v.tick("k_inv"))
            dve.wait_ge(pre_p.sem, pre_p.at("k_spread"))
            dve.tensor_tensor(kT, kT, k_ps, ALU.mult).then_inc(pre_v.sem, pre_v.tick("k_unit"))
            dve.wait_ge(pre_v.sem, pre_v.at("k_unit"))
            dve.tensor_scalar(kT, kT, hd[:, 2:3], hd[:, 3:4], ALU.mult, ALU.add) \
               .then_inc(pre_v.sem, pre_v.tick("kT"))
            dve.wait_ge(pre_p.sem, pre_p.at("v"))
            dve.tensor_tensor(v[:], k_ps, b_v[:].unsqueeze(1).to_broadcast([P, NT, P]), ALU.add) \
               .then_inc(pre_v.sem, pre_v.tick("v"))
            dve.tensor_tensor(x[:], x[:], b_o[:].unsqueeze(1).to_broadcast([P, NT, P]), ALU.add) \
               .then_inc(pre_v.sem, pre_v.tick("x_bias"))
            dve.wait_ge(pre_p.sem, pre_p.at("projT"))
            dve.tensor_copy(projT[:], ps[:, 0, :]).then_inc(pre_v.sem, pre_v.tick("projT"))
            for each in (fw_v, bw_v):
                dve.sem_inc(each.sem, len(each.names))
            dve.sem_inc(ns_v.sem, ns_v.at("XT2", -1))
            dve.sem_inc(upd_v.sem, upd_v.at("proj", -1))
            dve.sem_inc(ask_v.sem, ask_v.at("x", -1))
            dve.wait_ge(q_g.sem, q_g.at("guard"))
            with dve.Fori(0, TTT_STEPS) as step:
                dve.memset(dp[:, 1, :], 0.0).then_inc(zero_v.sem, zero_v.tick("dp"))

                def forward(n, s, dproj, between=lambda: None):
                    dve.wait_ge(fw_a.sem, fw_a.at("sg", n))
                    dve.tensor_tensor(sw[:, s, :], ps[:, 0, :], sg[:, s, :], ALU.mult).then_inc(fw_v.sem, fw_v.tick("sw"))
                    dve.wait_ge(fw_v.sem, fw_v.at("sw", n))
                    dve.wait_ge(fw_a.sem, fw_a.at("vs", n))
                    dve.wait_ge(bw_p.sem, bw_p.at("dproj", dproj))
                    dve.tensor_tensor(h[:, s, :], sw[:, s, :], vs[:, s, :], ALU.mult).then_inc(fw_v.sem, fw_v.tick("h"))
                    between()
                    dve.scalar_tensor_tensor(u[:, s, :], sw[:, s, :], 1.0, sg[:, s, :], ALU.subtract, ALU.mult) \
                       .then_inc(fw_v.sem, fw_v.tick("u"))
                    dve.wait_ge(fw_v.sem, fw_v.at("u", n))
                    dve.tensor_tensor(u[:, s, :], sw[:, s, :], u[:, s, :], ALU.subtract) \
                       .then_inc(fw_v.sem, fw_v.tick("ds"))

                forward(step * A_STEP, 0, step * NT - 1)
                with dve.Fori(0, NT // UNROLL) as i:
                    for r in range(UNROLL):
                        t, s = UNROLL * i + r, r % 2
                        n, n_fw = step * NT + t, step * A_STEP + t
                        dve.wait_ge(bw_p.sem, bw_p.at("pred", n))
                        dve.tensor_tensor(dp[:, bass.ds(s, 1), :], ps[:, 3:4, 0:P], v[:, bass.ds(t, 1), :],
                                          ALU.subtract).then_inc(bw_v.sem, bw_v.tick("dp"))
                        dve.wait_ge(bw_v.sem, bw_v.at("dG", n - 1))

                        def hidden():
                            dve.wait_ge(bw_p.sem, bw_p.at("dh", n))
                            dve.tensor_tensor(dV[:, s, :], ps[:, 4, :], sw[:, s, :], ALU.mult) \
                               .then_inc(bw_v.sem, bw_v.tick("dV"))
                            dve.wait_ge(fw_g.sem, fw_g.at("e", n_fw))
                            dve.tensor_tensor(dG[:, s, :], ps[:, 4, :], e[:, s, :], ALU.mult) \
                               .then_inc(bw_v.sem, bw_v.tick("dG"))

                        forward(n_fw + 1, 1 - s, n, hidden)
                        cols = bass.ds(n * QCOLS, QCOLS)
                        dve.reciprocal(qn[:, cols], qn[:, cols]).then_inc(q_v.sem, q_v.tick("inv"))
                        dve.wait_ge(q_v.sem, q_v.at("inv", n))
                        dve.tensor_tensor(qT[:, cols], qT[:, cols], qn[:, cols], ALU.mult).then_inc(q_v.sem, q_v.tick("unit"))
                        dve.wait_ge(q_v.sem, q_v.at("unit", n))
                        dve.tensor_scalar(qT[:, cols], qT[:, cols], hd[:, 0:1], hd[:, 1:2], ALU.mult, ALU.add) \
                           .then_inc(q_v.sem, q_v.tick("q"))
                dve.wait_ge(open_a.sem, open_a.at("root", step))
                dve.tensor_scalar(frn[:], frn[:], NS_GUARD, None, ALU.add).then_inc(open_v.sem, open_v.tick("guard"))
                dve.wait_ge(open_v.sem, open_v.at("guard", step))
                dve.reciprocal(frn[:], frn[:]).then_inc(open_v.sem, open_v.tick("inv"))
                dve.wait_ge(open_v.sem, open_v.at("inv", step))
                for m in range(3):
                    dve.tensor_scalar(X[:, m, :], ps[:, 5 + m, :], frn[:, m:m + 1], None, ALU.mult) \
                       .then_inc(open_v.sem, open_v.tick(f"X{m}"))
                with dve.Fori(0, NS_ITERS) as it:
                    n = step * NS_ITERS + it
                    for m in range(3):
                        dve.wait_ge(ns_a.sem, ns_a.at(f"A{m}", n))
                        dve.scalar_tensor_tensor(bA[:, m, :], Am[:, m, :], NS_B, aI[:], ALU.mult, ALU.add) \
                           .then_inc(ns_v.sem, ns_v.tick(f"bA{m}"))
                    for m in range(3):
                        dve.wait_ge(ns_p.sem, ns_p.at(f"A2{m}", n))
                        dve.wait_ge(ns_v.sem, ns_v.at(f"bA{m}", n))
                        dve.scalar_tensor_tensor(Bm[:, m, :], ps[:, 3 + m, 0:P], NS_C, bA[:, m, :], ALU.mult, ALU.add) \
                           .then_inc(ns_v.sem, ns_v.tick(f"B{m}"))
                    for m in range(3):
                        dve.wait_ge(ns_p.sem, ns_p.at(f"X{m}", n))
                        dve.tensor_copy(XT[:, m, :], ps[:, 3 + m, :]).then_inc(ns_v.sem, ns_v.tick(f"XT{m}"))
                dve.wait_ge(ns_a.sem, ns_a.at("X2", step * NS_ITERS + NS_ITERS - 1))
                dve.wait_ge(ns_v.sem, ns_v.at("XT2", step * NS_ITERS + NS_ITERS - 1))
                for name, theta, d in (("gate", gate[:], X[:, 0, :]), ("val", val[:], X[:, 1, :]),
                                       ("projT", projT[:], X[:, 2, :]), ("proj", proj[:].rearrange("p j d -> p (j d)"), XT[:, 2, :])):
                    dve.scalar_tensor_tensor(theta, d, -LR, theta, ALU.mult, ALU.add) \
                       .then_inc(upd_v.sem, upd_v.tick(name))
            dve.wait_ge(fin_p.sem, fin_p.at("wo2"))
            dve.tensor_copy(wo2[:].rearrange("p j d -> p (j d)"), ps[:, 0, :]).then_inc(fin_v.sem, fin_v.tick("wo2"))
            with dve.Fori(0, NB) as blk:
                for j in range(NJ):
                    b = 2 * (j % 2)
                    dve.wait_ge(ask_a.sem, ask_a.at(f"s{j}", blk))
                    if j == 0:
                        dve.wait_ge(ask_p.sem, ask_p.at("o", blk - 1))
                    dve.tensor_tensor(fh[:, j, :], ps[:, b, :], fs[:, j % 2, :], ALU.mult) \
                       .then_inc(ask_v.sem, ask_v.tick(f"sw{j}"))
                    dve.wait_ge(ask_v.sem, ask_v.at(f"sw{j}", blk))
                    dve.tensor_tensor(fh[:, j, :], ps[:, b + 1, :], fh[:, j, :], ALU.mult) \
                       .then_inc(ask_v.sem, ask_v.tick(f"h{j}"))
                dve.wait_ge(ask_p.sem, ask_p.at("o", blk))
                xb = x[:, bass.ds(4 * blk, 4), :]
                dve.tensor_tensor(xb, rows(ps[:, 4, :], 4), xb, ALU.add).then_inc(ask_v.sem, ask_v.tick("x"))

        @block.tensor
        def _(pe):
            pe.wait_ge(load.sem, 16 * N_LOADS)
            pe.matmul(ps[:, 7, 0:4], rep8, head8[:], start=True, stop=True).then_inc(pre_p.sem, pre_p.tick("hd"))
            for b in range(NB):
                pe.wait_ge(pre_v.sem, pre_v.at(normal_of(4 * b)))
                for i in range(4):
                    mm = pe.transpose(ps[:, b, bass.ts(i, P)], nrm[:, 4 * b + i, :], ident)
                mm.then_inc(pre_p.sem, pre_p.tick(f"nT{b}"))
            pe.wait_ge(pre_a.sem, pre_a.at("nT2"))
            pe.wait_ge(pre_v.sem, pre_v.at("nT3"))
            for name, part, b0 in (("k", 1, 0), ("q", 0, 4)):
                for b in range(NB):
                    mm = pe.matmul(ps[:, b0 + b, :], w_qkv[:, bass.ts(part, P)], nT[:, bass.ts(b, BLK)], start=True, stop=True)
                mm.then_inc(pre_p.sem, pre_p.tick(name))
            pe.wait_ge(pre_v.sem, pre_v.at("k_sq"))
            pe.wait_ge(norm_load.sem, 32)
            for b in range(B):
                mm = pe.matmul(ps[:, 0, 0:S], gather[:, b, :], kn[:, bass.ts(b, S)], start=(b == 0), stop=(b == B - 1))
            mm.then_inc(pre_p.sem, pre_p.tick("k_sq"))
            pe.wait_ge(pre_a.sem, pre_a.at("q_sq"))
            for b in range(NB):
                mm = pe.matmul(ps[:, 4 + b, :], bd8, sq[:, bass.ts(b, BLK)], start=True, stop=True)
            mm.then_inc(pre_p.sem, pre_p.tick("q_sq"))
            pe.wait_ge(pre_v.sem, pre_v.at("k_inv"))
            for b in range(B):
                mm = pe.matmul(ps[:, b // 2, bass.ts(b % 2, S)], spread[:, b, :], k_norm[:], start=True, stop=True)
            mm.then_inc(pre_p.sem, pre_p.tick("k_spread"))
            pe.wait_ge(pre_v.sem, pre_v.at("k_unit"))
            for t in range(NT):
                mm = pe.matmul(ps[:, t // 4, bass.ts(t % 4, P)], nT[:, bass.ts(t, P)], w_qkv[:, 2 * P:3 * P],
                               start=True, stop=True)
            mm.then_inc(pre_p.sem, pre_p.tick("v"))
            pe.wait_ge(pre_v.sem, pre_v.at("kT"))
            pe.wait_ge(pre_a.sem, pre_a.at("q_norm"))
            for t in range(NT):
                mm = pe.transpose(ps[:, 4 + t // 4, bass.ts(t % 4, P)], kk[:, t, 0, :], ident)
            mm.then_inc(pre_p.sem, pre_p.tick("k_tok"))
            pe.wait_ge(pre_v.sem, pre_v.at("v"))
            for j in range(NJ):
                mm = pe.transpose(ps[:, 0, bass.ts(j, P)], proj[:, j, :], ident)
            mm.then_inc(pre_p.sem, pre_p.tick("projT"))
            pe.wait_ge(pre_a.sem, pre_a.at("k_tok"))
            for each in (fw_p, bw_p):
                pe.sem_inc(each.sem, len(each.names))
            pe.sem_inc(ns_p.sem, ns_p.at("X2", -1))
            pe.sem_inc(ask_p.sem, ask_p.at("o", -1))
            pe.wait_ge(pre_v.sem, pre_v.at("projT"))

            def d_proj(s, start=False, stop=False):
                return pe.matmul(ps[:, 7, :], dp[:, s, :], h[:, s, :], start=start, stop=stop, skip_group_check=True)

            def d_gate_val(s, start=False, stop=False):
                pe.matmul(ps[:, 6, :], k_cur[:], dV[:, s, :], start=start, stop=stop, skip_group_check=True)
                return pe.matmul(ps[:, 5, :], k_cur[:], dG[:, s, :], start=start, stop=stop, skip_group_check=True)

            def take_g(step, t, n):
                pe.wait_ge(kT_g.sem, kT_g.at("kT_cur", step * KT_STEP + t))
                pe.wait_ge(fw_v.sem, fw_v.at("sw", n - 1))
                pe.matmul(ps[:, 0, :], kT_cur[:], gate[:], start=True, stop=True).then_inc(fw_p.sem, fw_p.tick("g"))

            def take_v(n):
                pe.wait_ge(fw_a.sem, fw_a.at("vs", n - 1))
                pe.matmul(ps[:, 1, :], kT_cur[:], val[:], start=True, stop=True).then_inc(fw_p.sem, fw_p.tick("v"))

            with pe.Fori(0, TTT_STEPS) as step:
                pe.wait_ge(upd_v.sem, upd_v.at("proj", step - 1))
                take_g(step, 0, step * A_STEP)
                take_v(step * A_STEP)
                pe.wait_ge(zero_v.sem, zero_v.at("dp", step))
                pe.wait_ge(zero_g.sem, zero_g.at("k", step))
                d_proj(1, start=True)
                d_gate_val(1, start=True).then_inc(open_p.sem, open_p.tick("opened"))
                with pe.Fori(0, NT // UNROLL) as i:
                    for r in range(UNROLL):
                        t, s = UNROLL * i + r, r % 2
                        n, n_fw = step * NT + t, step * A_STEP + t
                        pe.wait_ge(fw_v.sem, fw_v.at("h", n_fw))
                        pe.wait_ge(bw_a.sem, bw_a.at("hT", n - 1))
                        for j in range(NJ):
                            mm = pe.transpose(ps[:, 2, bass.ts(j, P)], h[:, s, bass.ts(j, P)], ident)
                        mm.then_inc(bw_p.sem, bw_p.tick("hT"))
                        d_proj(1 - s).then_inc(bw_p.sem, bw_p.tick("dproj"))
                        pe.wait_ge(bw_a.sem, bw_a.at("hT", n))
                        pe.wait_ge(bw_a.sem, bw_a.at("dpT", n - 1))
                        for j in range(NJ):
                            mm = pe.matmul(ps[:, 3, 0:P], hT[:, s, bass.ts(j, P)], proj[:, j, :],
                                           start=(j == 0), stop=(j == NJ - 1))
                        mm.then_inc(bw_p.sem, bw_p.tick("pred"))
                        take_g(step, t + 1, n_fw + 1)
                        pe.wait_ge(bw_v.sem, bw_v.at("dp", n))
                        pe.transpose(ps[:, 3, 0:P], dp[:, s, :], ident).then_inc(bw_p.sem, bw_p.tick("dpT"))
                        take_v(n_fw + 1)
                        pe.wait_ge(bw_a.sem, bw_a.at("dpT", n))
                        pe.wait_ge(bw_v.sem, bw_v.at("dG", n - 1))
                        pe.matmul(ps[:, 4, :], dpT[:, s, :], projT[:], start=True, stop=True) \
                          .then_inc(bw_p.sem, bw_p.tick("dh"))
                        pe.wait_ge(bw_g.sem, bw_g.at("k_cur", n - 1))
                        d_gate_val(1 - s).then_inc(bw_p.sem, bw_p.tick("grads"))
                last = step * NT + NT - 1
                pe.wait_ge(bw_v.sem, bw_v.at("dG", last))
                pe.wait_ge(bw_g.sem, bw_g.at("k_cur", last))
                d_proj(1, stop=True)
                d_gate_val(1, stop=True).then_inc(open_p.sem, open_p.tick("last"))
                pe.wait_ge(open_a.sem, open_a.at("fro2", step))
                pe.matmul(ps[:, 0, 0:3], ones, fro[:], start=True, stop=True).then_inc(open_p.sem, open_p.tick("fro"))
                pe.wait_ge(open_v.sem, open_v.at("X2", step))
                for m in range(3):
                    for j in range(NJ):
                        mm = pe.transpose(ps[:, 1 + m, bass.ts(j, P)], X[:, m, bass.ts(j, P)], ident)
                mm.then_inc(open_p.sem, open_p.tick("XT"))
                with pe.Fori(0, NS_ITERS) as it:
                    n = step * NS_ITERS + it
                    pe.wait_ge(open_a.sem, open_a.at("XT2", step))
                    for m in range(3):
                        pe.wait_ge(ns_v.sem, ns_v.at(f"XT{m}", n - 1))
                        pe.wait_ge(ns_a.sem, ns_a.at(f"X{m}", n - 1))
                        for j in range(NJ):
                            mm = pe.matmul(ps[:, m, 0:P], XT[:, m, bass.ts(j, P)], XT[:, m, bass.ts(j, P)],
                                           start=(j == 0), stop=(j == NJ - 1))
                        mm.then_inc(ns_p.sem, ns_p.tick(f"A{m}"))
                    for m in range(3):
                        pe.wait_ge(ns_a.sem, ns_a.at(f"A{m}", n))
                        pe.matmul(ps[:, 3 + m, 0:P], Am[:, m, :], Am[:, m, :], start=True, stop=True) \
                          .then_inc(ns_p.sem, ns_p.tick(f"A2{m}"))
                    for m in range(3):
                        pe.wait_ge(ns_v.sem, ns_v.at(f"B{m}", n))
                        pe.matmul(ps[:, m, :], Bm[:, m, :], X[:, m, :], start=True, stop=True)
                        for j in range(NJ):
                            mm = pe.matmul(ps[:, 3 + m, bass.ts(j, P)], X[:, m, bass.ts(j, P)], Bm[:, m, :],
                                           start=True, stop=True)
                        mm.then_inc(ns_p.sem, ns_p.tick(f"X{m}"))
            pe.wait_ge(upd_v.sem, upd_v.at("proj", TTT_STEPS - 1))
            for j in range(NJ):
                mm = pe.matmul(ps[:, 0, bass.ts(j, P)], projT[:, bass.ts(j, P)], w_o[:], start=True, stop=True)
            mm.then_inc(fin_p.sem, fin_p.tick("wo2"))
            pe.wait_ge(fin_v.sem, fin_v.at("wo2"))
            pe.wait_ge(q_v.sem, q_v.at("q", TTT_STEPS * NT - 1))
            with pe.Fori(0, NB) as blk:
                for j in range(NJ):
                    b = 2 * (j % 2)
                    pe.wait_ge(ask_v.sem, ask_v.at(f"h{(j - 2) % 4}", blk - (j < 2)))
                    for w, bank in ((gate, b), (val, b + 1)):
                        mm = pe.matmul(ps[:, bank, :], w[:, bass.ts(j, P)], qT[:, bass.ds(blk * BLK, BLK)],
                                       start=True, stop=True)
                    mm.then_inc(ask_p.sem, ask_p.tick(f"gv{j}"))
                pe.wait_ge(ask_v.sem, ask_v.at("h3", blk))
                pe.wait_ge(ask_v.sem, ask_v.at("x", blk - 1))
                for i in range(4):
                    for j in range(NJ):
                        mm = pe.matmul(ps[:, 4, bass.ts(i, P)], fh[:, j, bass.ts(i, P)], wo2[:, j, :],
                                       start=(j == 0), stop=(j == NJ - 1))
                mm.then_inc(ask_p.sem, ask_p.tick("o"))



XH, XD = 16, 64
INNER = XH * XD
NC = INNER // P
NK = SC // P
NCT = B * NK
CLIP = 11.0


def stage_cross_attention(nc, g, a):
    with Stage(nc, "xa") as st:
        wq = st.sb("wq", [P, INNER])
        wkv = st.sb("wkv", [P, 2 * INNER])
        wo = st.sb("wo", [P, NC, P])
        col = st.sb("col", [P, 4])
        b_o = st.sb("b_o", [P, P])
        turn = st.sb("turn", [P, 2, NK, 4, XD // 2])
        turnT = st.sb("turnT", [P, 2, SC])
        nrm = st.sb("nrm", [P, NT, P])
        cn = st.sb("cn", [P, NCT, P])
        latT = st.sb("latT", [P, T + S])
        ctxT = st.sb("ctxT", [P, B * SC + SC])
        stat = st.sb("stat", [P, 4, NT])
        stat2 = st.sb("stat2", [P, 4, NT])
        statc = st.sb("statc", [P, 4, NCT])
        ctx_cur = st.sb("ctx_cur", [P, SC])
        kz = st.sb("kz", [P, 2, 2, SC])
        qz = st.sb("qz", [P, 2, 2, S])
        va = st.sb("va", [P, 2, NK, 4, XD])
        pt = st.sb("pt", [P, 2, NK, S])
        rec = st.sb("rec", [P, S])
        oT = st.sb("oT", [P, NC, S])
        ps, x, ctx = g.ps, g.x, g.ctx
        ident = g.ident
        sq = cn

        load = st.steps("load", ["all"])
        N_LOADS = 17
        ln1_v, ln1_a = st.steps("ln1_v", LN_VECTOR), st.steps("ln1_a", ["root"])
        ln2_v, ln2_a = st.steps("ln2_v", LN_VECTOR), st.steps("ln2_a", ["root"])
        lnc_v, lnc_a = st.steps("lnc_v", LN_VECTOR), st.steps("lnc_a", ["root"])
        pre_v = st.steps("pre_v", ["ctx"])
        pre_a = st.steps("pre_a", ["cos", "sin", "lat", "ctx"])
        pre_g = st.steps("pre_g", ["sign", "lat_zeros", "ones", "x_bias", "ctx_zeros"])
        pre_p = st.steps("pre_p", ["turn", "lat", "ctx0", "ctx1"])
        pair = lambda *xs: [f"{n}{c}" for c in range(NC) for n in xs]
        pj_p = st.steps("pj_p", pair("q", "k", "v"), ahead=1)
        pj_a = st.steps("pj_a", pair("q", "v"), ahead=1)
        pj_v = st.steps("pj_v", pair("k"), ahead=1)
        pj_g = st.steps("pj_g", ["ctx_cur"], ahead=1)
        heads = lambda *xs: [f"{n}{h}" for h in range(XH) for n in xs]
        s_p = st.steps("s_p", heads("S"), ahead=1)
        e_a = st.steps("e_a", heads("E"), ahead=1)
        c_v = st.steps("c_v", heads("C"), ahead=1)
        o_p = st.steps("o_p", heads("O") + ["out"], ahead=1)
        n_v = st.steps("n_v", heads("R", "N") + ["x"], ahead=1)

        def free(eng, *steps):
            for each in steps:
                eng.sem_inc(each.sem, len(each.names))

        def of(i, n, b):
            return i % n, b + i // n

        block = st.block()

        @block.sync
        def _(sp):
            for dst, src in (
                (wq[:], a["L0_xattn_Wq"]), (wkv[:], a["L0_xattn_Wkv"]),
                (wo[:], a["L0_xattn_Wo"].rearrange("(c p) d -> p c d", p=P)),
                (col[:, 0:1], a["L0_xattn_ln_lat_g"].unsqueeze(1)), (col[:, 1:2], a["L0_xattn_ln_lat_b"].unsqueeze(1)),
                (col[:, 2:3], a["L0_xattn_ln_ctx_g"].unsqueeze(1)), (col[:, 3:4], a["L0_xattn_ln_ctx_b"].unsqueeze(1)),
                (b_o[:], a["L0_xattn_bo"].partition_broadcast(P)),
            ):
                sp.dma_start(dst, src).then_inc(load.sem, 16)
            for r in range(4):
                for i, name in enumerate(("L0_xattn_cos", "L0_xattn_sin")):
                    sp.dma_start(turn[:, i, :, r, :], a[name].rearrange("(n p) d -> p n d", p=P)).then_inc(load.sem, 16)
            sp.dma_start(g.ctx[:], a["ctx_1024"].rearrange("b (n p) d -> p (b n) d", p=P)).then_inc(load.sem, 16)
            sp.wait_ge(load.sem, 16 * (N_LOADS))

        @block.gpsimd
        def _(pool):
            pool.wait_ge(load.sem, 16 * (N_LOADS))
            minus = turn[:, 1, :, 1:4:2, :]
            pool.tensor_scalar(minus, minus, -1.0, None, ALU.mult).then_inc(pre_g.sem, pre_g.tick("sign"))
            pool.memset(latT[:, T:T + S], 0.0).then_inc(pre_g.sem, pre_g.tick("lat_zeros"))
            pool.memset(va[:, :, :, 1:3, :], 1.0).then_inc(pre_g.sem, pre_g.tick("ones"))
            pool.wait_ge(ln1_v.sem, ln1_v.at("normal"))
            pool.wait_ge(pre_g.sem, pre_g.at("ones"))
            pool.tensor_tensor(x[:], x[:], b_o[:].unsqueeze(1).to_broadcast([P, NT, P]), ALU.add) \
                .then_inc(pre_g.sem, pre_g.tick("x_bias"))
            pool.wait_ge(lnc_v.sem, lnc_v.at("normal"))
            pool.wait_ge(pre_g.sem, pre_g.at("x_bias"))
            pool.memset(ctxT[:, B * SC:B * SC + SC], 0.0).then_inc(pre_g.sem, pre_g.tick("ctx_zeros"))
            pool.wait_ge(pre_g.sem, pre_g.at("ctx_zeros"))
            free(pool, pj_g)
            pool.wait_ge(pre_a.sem, pre_a.at("ctx"))
            pool.wait_ge(pre_v.sem, pre_v.at("ctx"))
            pool.tensor_copy(ctx_cur[:], ctxT[:, 0:SC]).then_inc(pj_g.sem, pj_g.tick("ctx_cur"))
            with pool.Fori(0, B) as b:
                pool.wait_ge(pj_p.sem, pj_p.at(f"v{NC - 1}", b))
                pool.tensor_copy(ctx_cur[:], ctxT[:, bass.ds((b + 1) * SC, SC)]).then_inc(pj_g.sem, pj_g.tick("ctx_cur"))

        @block.scalar
        def _(act):
            layernorm_root(act, ln1_v, ln1_a, stat)
            layernorm_root(act, ln2_v, ln2_a, stat2)
            act.wait_ge(pre_p.sem, pre_p.at("turn"))
            for i, name in enumerate(("cos", "sin")):
                act.activation(turnT[:, i, :], ps[:, i, :], ACT.Copy).then_inc(pre_a.sem, pre_a.tick(name))
            act.wait_ge(pre_p.sem, pre_p.at("lat"))
            act.wait_ge(load.sem, 16 * (N_LOADS))
            act.activation(latT[:, 0:T], banks(ps, 4, 8), ACT.Identity, scale=col[:, 0:1], bias=col[:, 1:2]) \
               .then_inc(pre_a.sem, pre_a.tick("lat"))
            layernorm_root(act, lnc_v, lnc_a, statc)
            act.wait_ge(pre_p.sem, pre_p.at("ctx0"))
            act.activation(ctxT[:, 0:T], banks(ps, 0, 4), ACT.Identity, scale=col[:, 2:3], bias=col[:, 3:4]) \
               .then_inc(pre_a.sem, pre_a.tick("ctx"))
            free(act, pj_a, e_a)

            def take_q(c, b, h):
                if h is not None:
                    act.wait_ge(s_p.sem, s_p.at(f"S{h}", b))
                c, b = of(c, NC, b)
                act.wait_ge(pj_p.sem, pj_p.at(f"q{c}", b))
                half = XD // 2
                for i in range(2):
                    for to, rows_in, n in ((0, XD * i, XD), (XD, XD * i + half, half), (XD + half, XD * i, half)):
                        mm = act.activation(qz[bass.ds(to, n), c % 2, i, :], ps[bass.ds(rows_in, n), 7, 0:S], ACT.Copy)
                mm.then_inc(pj_a.sem, pj_a.tick(f"q{c}"))

            def take_v(c, b):
                last, pass_ = of(2 * c - 3, XH, b)
                act.wait_ge(o_p.sem, o_p.at(f"O{last}", pass_))
                c, b = of(c, NC, b)
                act.wait_ge(pj_p.sem, pj_p.at(f"v{c}", b))
                act.activation(va[:, c % 2, :, 0:4:3, :], ps[:, 7, :].rearrange("p (n i d) -> p n i d", n=NK, i=2), ACT.Copy) \
                   .then_inc(pj_a.sem, pj_a.tick(f"v{c}"))

            def weights(h, b):
                last, pass_ = of(h - 2, XH, b)
                act.wait_ge(o_p.sem, o_p.at(f"O{last}", pass_))
                h, b = of(h, XH, b)
                act.wait_ge(s_p.sem, s_p.at(f"S{h}", b))
                b0 = 2 * (h % 2)
                act.activation(pt[:, h % 2].rearrange("p n s -> p (n s)"), banks(ps, b0, b0 + 2), ACT.Exp,
                               scale=XD ** -0.5).then_inc(e_a.sem, e_a.tick(f"E{h}"))

            take_q(0, 0, None)
            take_v(0, 0)
            weights(0, 0)
            take_q(1, 0, None)
            with act.Fori(0, B) as b:
                for h in range(XH):
                    weights(h + 1, b)
                    if h % 2 == 0:
                        take_v(h // 2 + 1, b)
                    else:
                        take_q((h + 1) // 2 + 1, b, h)

        @block.vector
        def _(dve):
            layernorm_vector(dve, ln1_v, ln1_a, x[:], nrm[:], sq[:, 0:NT, :], stat[:], NT)
            dve.wait_ge(ln1_v.sem, ln1_v.at("normal"))
            layernorm_vector(dve, ln2_v, ln2_a, nrm[:], nrm[:], sq[:, 0:NT, :], stat2[:], NT)
            dve.wait_ge(load.sem, 16 * (N_LOADS))
            layernorm_vector(dve, lnc_v, lnc_a, ctx[:], cn[:], rows(ctxT[:, 0:B * SC], NCT), statc[:], NCT)
            dve.wait_ge(pre_p.sem, pre_p.at("ctx1"))
            dve.tensor_scalar(ctxT[:, T:2 * T], banks(ps, 4, 8), col[:, 2:3], col[:, 3:4], ALU.mult, ALU.add) \
               .then_inc(pre_v.sem, pre_v.tick("ctx"))
            free(dve, pj_v, c_v, n_v)
            dve.wait_ge(pre_a.sem, pre_a.at("sin"))
            dve.wait_ge(pre_g.sem, pre_g.at("x_bias"))

            def take_k(c, b, h):
                if h is not None:
                    dve.wait_ge(s_p.sem, s_p.at(f"S{h}", b))
                c, b = of(c, NC, b)
                dve.wait_ge(pj_p.sem, pj_p.at(f"k{c}", b))
                for i in range(2):
                    r = bass.ds(XD * i, XD)
                    for half in range(2):
                        op = dve.tensor_tensor(kz[bass.ds(XD * half, XD), c % 2, i, :], ps[r, 6, :], turnT[r, half, :], ALU.mult)
                op.then_inc(pj_v.sem, pj_v.tick(f"k{c}"))

            def clip(h, b):
                h, b = of(h, XH, b)
                dve.wait_ge(e_a.sem, e_a.at(f"E{h}", b))
                w = pt[:, h % 2].rearrange("p n s -> p (n s)")
                dve.tensor_scalar(w, w, math.exp(-CLIP), math.exp(CLIP), ALU.max, ALU.min) \
                   .then_inc(c_v.sem, c_v.tick(f"C{h}"))

            def normalise(h, b):
                out, sums = bass.ds(XD * (h % 2), XD), bass.ds(XD * (1 - h % 2), XD)
                dve.wait_ge(o_p.sem, o_p.at(f"O{h}", b))
                dve.reciprocal(rec[out], ps[sums, 4 + h % 2, 0:S]).then_inc(n_v.sem, n_v.tick(f"R{h}"))
                dve.wait_ge(n_v.sem, n_v.at(f"R{h}", b))
                dve.tensor_tensor(oT[out, h // 2, :], ps[out, 4 + h % 2, 0:S], rec[out], ALU.mult) \
                   .then_inc(n_v.sem, n_v.tick(f"N{h}"))

            take_k(0, 0, None)
            clip(0, 0)
            take_k(1, 0, None)
            with dve.Fori(0, B) as b:
                for h in range(XH):
                    clip(h + 1, b)
                    normalise(h, b)
                    if h % 2:
                        take_k((h + 1) // 2 + 1, b, h)
                dve.wait_ge(o_p.sem, o_p.at("out", b))
                xb = x[:, bass.ds(2 * b, 2), :]
                dve.tensor_tensor(xb, rows(ps[:, 4, 0:2 * P], 2), xb, ALU.add).then_inc(n_v.sem, n_v.tick("x"))

        @block.tensor
        def _(pe):
            pe.wait_ge(load.sem, 16 * (N_LOADS))
            pe.wait_ge(pre_g.sem, pre_g.at("sign"))
            for i in range(2):
                for n in range(NK):
                    mm = pe.transpose(ps[:, i, bass.ts(n, P)], turn[:, i, n].rearrange("p r d -> p (r d)"), ident)
            mm.then_inc(pre_p.sem, pre_p.tick("turn"))
            for t in range(NT):
                if t % 4 == 0:
                    pe.wait_ge(ln2_v.sem, ln2_v.at(normal_of(t)))
                mm = pe.transpose(ps[:, 4 + t // 4, bass.ts(t % 4, P)], nrm[:, t, :], ident)
            mm.then_inc(pre_p.sem, pre_p.tick("lat"))
            pe.wait_ge(pre_a.sem, pre_a.at("sin"))
            for t in range(NT):
                if t % 8 == 0:
                    pe.wait_ge(lnc_v.sem, lnc_v.at(normal_of(t, NCT)))
                mm = pe.transpose(ps[:, t // 4, bass.ts(t % 4, P)], cn[:, t, :], ident)
            mm.then_inc(pre_p.sem, pre_p.tick("ctx0"))
            pe.wait_ge(pre_a.sem, pre_a.at("lat"))
            for t in range(NT):
                if t % 8 == 0:
                    pe.wait_ge(lnc_v.sem, lnc_v.at(normal_of(NT + t, NCT)))
                mm = pe.transpose(ps[:, 4 + t // 4, bass.ts(t % 4, P)], cn[:, NT + t, :], ident)
            mm.then_inc(pre_p.sem, pre_p.tick("ctx1"))
            free(pe, pj_p, s_p, o_p)
            pe.wait_ge(pre_a.sem, pre_a.at("ctx"))
            pe.wait_ge(pre_v.sem, pre_v.at("ctx"))
            pe.wait_ge(pre_g.sem, pre_g.at("ctx_zeros"))

            def project_qk(c, b):
                last, pass_ = of(c - 1, NC, b)
                pe.wait_ge(pj_a.sem, pj_a.at(f"v{last}", pass_))
                pe.wait_ge(pj_v.sem, pj_v.at(f"k{last}", pass_))
                c, b = of(c, NC, b)
                pe.matmul(ps[:, 7, 0:S], wq[:, bass.ts(c, P)], latT[:, bass.ds(b * S, S)], start=True, stop=True) \
                  .then_inc(pj_p.sem, pj_p.tick(f"q{c}"))
                pe.matmul(ps[:, 6, :], wkv[:, bass.ts(c, P)], ctxT[:, bass.ds(b * SC, SC)], start=True, stop=True) \
                  .then_inc(pj_p.sem, pj_p.tick(f"k{c}"))

            def project_v(c, b):
                c, b = of(c, NC, b)
                pe.wait_ge(pj_a.sem, pj_a.at(f"q{c}", b))
                if c == 0:
                    pe.wait_ge(pj_g.sem, pj_g.at("ctx_cur", b))
                for n in range(NK):
                    mm = pe.matmul(ps[:, 7, bass.ts(n, P)], ctx_cur[:, bass.ts(n, P)], wkv[:, bass.ds(INNER + P * c, P)],
                                   start=True, stop=True)
                mm.then_inc(pj_p.sem, pj_p.tick(f"v{c}"))

            def scores(h, b):
                last, pass_ = of(h - 2, XH, b)
                pe.wait_ge(e_a.sem, e_a.at(f"E{last}", pass_))
                h, b = of(h, XH, b)
                if h % 2 == 0:
                    pe.wait_ge(pj_v.sem, pj_v.at(f"k{h // 2}", b))
                    pe.wait_ge(pj_a.sem, pj_a.at(f"q{h // 2}", b))
                for n in range(NK):
                    mm = pe.matmul(ps[:, 2 * (h % 2) + n // 2, bass.ts(n % 2, S)], kz[:, h // 2 % 2, h % 2, bass.ts(n, P)],
                                   qz[:, h // 2 % 2, h % 2, :], start=True, stop=True)
                mm.then_inc(s_p.sem, s_p.tick(f"S{h}"))

            def output(h, b):
                last, pass_ = of(h - 2, XH, b)
                pe.wait_ge(n_v.sem, n_v.at(f"N{last}" if h else "x", pass_))
                if h % 2 == 0:
                    pe.wait_ge(pj_a.sem, pj_a.at(f"v{h // 2}", b))
                pe.wait_ge(c_v.sem, c_v.at(f"C{h}", b))
                for n in range(NK):
                    v_ones = va[:, h // 2 % 2, n, 2 * (h % 2):2 * (h % 2) + 2, :].rearrange("p f d -> p (f d)")
                    mm = pe.matmul(ps[:, 4 + h % 2, 0:S], v_ones, pt[:, h % 2, n, :], start=(n == 0), stop=(n == NK - 1))
                mm.then_inc(o_p.sem, o_p.tick(f"O{h}"))

            project_qk(0, 0)
            project_v(0, 0)
            scores(0, 0)
            project_qk(1, 0)
            with pe.Fori(0, B) as b:
                for h in range(XH):
                    scores(h + 1, b)
                    if h % 2 == 0:
                        project_v(h // 2 + 1, b)
                    output(h, b)
                    if h % 2:
                        project_qk((h + 1) // 2 + 1, b)
                pe.wait_ge(n_v.sem, n_v.at(f"N{XH - 1}", b))
                for i in range(2):
                    for c in range(NC):
                        mm = pe.matmul(ps[:, 4, bass.ts(i, P)], oT[:, c, bass.ts(i, P)], wo[:, c, :],
                                       start=(c == 0), stop=(c == NC - 1))
                mm.then_inc(o_p.sem, o_p.tick("out"))



EH, ED = 16, 8
NE = 8
TOP = 2


def stage_experts(nc, g, a):
    with Stage(nc, "ex") as st:
        w_in = st.sb("w_in", [P, 3, P])
        w_inT = st.sb("w_inT", [P, 3 * P])
        w_out = st.sb("w_out", [P, P])
        w_outT = st.sb("w_outT", [P, P])
        gw = st.sb("gw", [NE, P])
        gwT = st.sb("gwT", [P, NE])
        b_in = st.sb("b_in", [P, 3 * P])
        b_out = st.sb("b_out", [P, P])
        b_gate = st.sb("b_gate", [P, NE])
        b1r = st.sb("b1r", [NE * NJ, P])
        b1T = st.sb("b1T", [P, NE * NJ + NJ])
        b1_cur = st.sb("b1_cur", [P, NJ])
        b2 = st.sb("b2", [NE, P])
        lng = st.sb("lng", [P, 4, P])
        lower = st.sb("lower", [P, NE, NE])
        nrm = st.sb("nrm", [P, NT, P])
        nT = st.sb("nT", [P, T])
        sq = st.sb("sq", [P, NT, P])
        stat = st.sb("stat", [P, 3, 4, NT])
        qkv = st.sb("qkv", [P, NT, 3 * P])
        prod = st.sb("prod", [P, 3, B, P])
        sc = st.sb("sc", [P, NT, B, EH])
        smx = st.sb("smx", [P, NT, EH])
        cx = st.sb("cx", [P, NT, P])
        tok = st.sb("tok", [P, NT, P])
        tokT = st.sb("tokT", [P, T])
        lg = st.sb("lg", [P, NT, NE])
        l1 = st.sb("l1", [P, NT])
        cmp = st.sb("cmp", [P, 2, NT, NE, NE])
        rank = st.sb("rank", [P, NT, NE])
        comb_pad = st.sb("comb", [P, NT, NE + 1])
        combT = st.sb("combT", [NE, T])
        comb_e = st.sb("comb_e", [P, NT])
        acc = st.sb("acc", [P, NT, P])
        w1r = st.sb("w1r", [P, NJ, P])
        w2r = st.sb("w2r", [P, HID])
        w1T = st.sb("w1T", [P, HID])
        w2T = st.sb("w2T", [P, NJ, P])
        fh = st.sb("fh", [P, 2, NJ, BLK])
        comb = comb_pad[:, :, 0:NE]
        ps, x = g.ps, g.x
        ident = g.ident

        load = st.steps("load", ["all"])
        N_LOADS = 13
        LOADED = 16 * N_LOADS
        w_load = st.steps("w_load", ["w1", "w2"])
        ln0_v, ln0_a = st.steps("ln0_v", LN_VECTOR), st.steps("ln0_a", ["root"])
        ln1_v, ln1_a = st.steps("ln1_v", LN_VECTOR), st.steps("ln1_a", ["root"])
        ln2_v, ln2_a = st.steps("ln2_v", LN_VECTOR), st.steps("ln2_a", ["root"])
        pre_p = st.steps("pre_p", ["w", "nT"])
        pre_v = st.steps("pre_v", ["w_inT", "w_outT", "gwT", "b1T", "nT1"] + [f"qkv{t}" for t in range(NT)])
        pre_a = st.steps("pre_a", ["nT0"])
        qkv_p = st.steps("qkv_p", [f"t{t}" for t in range(NT)])
        pre_g = st.steps("pre_g", ["b_out"])
        s_g, c_g = (st.steps(name, ["prod0", "prod1"], ahead=1) for name in ("s_g", "c_g"))
        s_v, c_v = (st.steps(name, [f"{n}{r}" for r in range(2) for n in ("own", "own_sum", "sum")], ahead=1)
                    for name in ("s_v", "c_v"))

        def score_products(eng, s, f, to):
            return eng.tensor_tensor(prod[:, to], qkv[:, bass.ds(2 * s + f, 1), 0:P].to_broadcast([P, B, P]),
                                     qkv[:, f:NT:2, P:2 * P], ALU.mult)

        def context_products(eng, s, f, to):
            w = sc[:, bass.ds(2 * s + f, 1)].rearrange("p o t h -> p (o t) h").unsqueeze(3)
            return eng.tensor_tensor(prod[:, to].rearrange("p t (h d) -> p t h d", h=EH), w.to_broadcast([P, B, EH, ED]),
                                     qkv[:, f:NT:2, 2 * P:3 * P].rearrange("p t (h d) -> p t h d", h=EH), ALU.mult)

        sm_v = st.steps("sm_v", ["max", "shift", "sum", "inv", "p"])
        sm_a = st.steps("sm_a", ["exp"])
        mid_p = st.steps("mid_p", ["cT", "out", "tokT", "gate", "combT", "b2"])
        mid_a = st.steps("mid_a", ["cT", "tokT", "e", "combT"])
        mid_v = st.steps("mid_v", ["out", "scaled", "tok", "bias", "max", "shift", "gt", "eq", "lower", "beats", "rank",
                                   "top", "w", "sum", "inv", "comb", "b1_pad", "comb_pad", "acc"])
        e_p = st.steps("e_p", ["w1T", "w2T"], ahead=1)
        e_a = st.steps("e_a", ["w1T"])
        e_v = st.steps("e_v", ["b1", "w2T", "comb_e"])
        blocks = lambda up, down: [n for k in range(NB + 1) for n in ([f"h{k}{j}" for j in up] if k < NB else [])
                                   + ([f"{down}{k - 1}"] if down and k else [])]
        f_p = st.steps("f_p", blocks(range(NJ), "o"), ahead=1)
        f_a = st.steps("f_a", blocks((0, 2), ""), ahead=1)
        f_v = st.steps("f_v", blocks((1, 3), "acc"), ahead=1)
        before = lambda k, n, e: ((k - n) % NB, e - (k < n))
        end_v = st.steps("end_v", ["scaled", "moved", "x"])

        block = st.block()

        @block.sync
        def _(sp):
            for dst, src in (
                (w_in[:], a["L0_ffn_in_proj_w"].rearrange("(i p) d -> p i d", p=P)), (w_out[:], a["L0_ffn_out_w"]),
                (gw[:], a["L0_ffn_gate_w"]), (b1r[:], a["L0_ffn_b1"].rearrange("e (j p) -> (e j) p", p=P)),
                (b_in[:], a["L0_ffn_in_proj_b"].partition_broadcast(P)), (b_out[:], a["L0_ffn_out_b"].partition_broadcast(P)),
                (b_gate[:], a["L0_ffn_gate_b"].partition_broadcast(P)), (b2[:], a["L0_ffn_b2"]),
                (lng[:, 0, :], a["L0_ffn_ln1_g"].partition_broadcast(P)), (lng[:, 1, :], a["L0_ffn_ln1_b"].partition_broadcast(P)),
                (lng[:, 2, :], a["L0_ffn_ln2_g"].partition_broadcast(P)), (lng[:, 3, :], a["L0_ffn_ln2_b"].partition_broadcast(P)),
                (lower[:].rearrange("p i j -> p (i j)"), a["lower"].partition_broadcast(P)),
            ):
                sp.dma_start(dst, src).then_inc(load.sem, 16)
            with sp.Fori(0, NE) as e:
                sp.wait_ge(e_p.sem, e_p.at("w1T", e - 1))
                sp.dma_start(w1r[:].unsqueeze(1), a["L0_ffn_w1"][bass.ds(e, 1)].rearrange("e (j p) d -> p e j d", p=P)) \
                  .then_inc(w_load.sem, 16)
                sp.wait_ge(e_p.sem, e_p.at("w2T", e - 1))
                sp.dma_start(w2r[:].unsqueeze(1), a["L0_ffn_w2"][bass.ds(e, 1)].rearrange("e d f -> d e f")) \
                  .then_inc(w_load.sem, 16)
            sp.wait_ge(w_load.sem, 32 * NE)
            sp.sem_inc(w_load.sem, 32)

        @block.gpsimd
        def _(pool):
            for each in (s_g, c_g):
                pool.sem_inc(each.sem, len(each.names))
            pool.wait_ge(load.sem, LOADED)
            pool.wait_ge(pre_p.sem, pre_p.at("nT"))
            pool.tensor_tensor(nrm[:], nrm[:], b_out[:].unsqueeze(1).to_broadcast([P, NT, P]), ALU.add) \
                .then_inc(pre_g.sem, pre_g.tick("b_out"))
            pool.wait_ge(pre_v.sem, pre_v.at(f"qkv{NT - 1}"))
            def multiply(products, mine, theirs):
                with pool.Fori(0, B // 2) as i:
                    for r in range(2):
                        pool.wait_ge(theirs.sem, theirs.at(f"sum{r}", i - 1))
                        products(pool, 2 * i + r, 0, r).then_inc(mine.sem, mine.tick(f"prod{r}"))

            multiply(score_products, s_g, s_v)
            pool.wait_ge(sm_v.sem, sm_v.at("p"))
            multiply(context_products, c_g, c_v)

        @block.scalar
        def _(act):
            layernorm_root(act, ln0_v, ln0_a, stat[:, 0])
            act.wait_ge(pre_p.sem, pre_p.at("nT"))
            act.activation(nT[:, 0:2 * BLK], banks(ps, 4, 6), ACT.Copy).then_inc(pre_a.sem, pre_a.tick("nT0"))
            act.wait_ge(sm_v.sem, sm_v.at("shift"))
            act.activation(sc[:], sc[:], ACT.Exp, scale=ED ** -0.5).then_inc(sm_a.sem, sm_a.tick("exp"))
            act.wait_ge(mid_p.sem, mid_p.at("cT"))
            act.activation(nT[:], banks(ps, 0, 4), ACT.Copy).then_inc(mid_a.sem, mid_a.tick("cT"))
            layernorm_root(act, ln1_v, ln1_a, stat[:, 1])
            act.wait_ge(mid_p.sem, mid_p.at("tokT"))
            act.activation(tokT[:], banks(ps, 0, 4), ACT.Copy).then_inc(mid_a.sem, mid_a.tick("tokT"))
            act.wait_ge(mid_v.sem, mid_v.at("shift"))
            act.activation(lg[:], lg[:], ACT.Exp).then_inc(mid_a.sem, mid_a.tick("e"))
            act.wait_ge(mid_p.sem, mid_p.at("combT"))
            act.activation(combT[:], banks(ps, 0, 4)[0:NE, :], ACT.Copy).then_inc(mid_a.sem, mid_a.tick("combT"))
            act.sem_inc(f_a.sem, len(f_a.names))

            def take_w1T(e):
                act.wait_ge(e_p.sem, e_p.at("w1T", e))
                act.activation(w1T[:], ps[:, 6, :], ACT.Copy).then_inc(e_a.sem, e_a.tick("w1T"))

            take_w1T(0)
            with act.Fori(0, NE) as e:
                act.wait_ge(e_v.sem, e_v.at("b1", e))
                for k in range(NB):
                    for j in (0, 2):
                        last, pass_ = before(k, 2, e)
                        act.wait_ge(f_p.sem, f_p.at(f"o{last}", pass_))
                        act.wait_ge(f_p.sem, f_p.at(f"h{k}{j}", e))
                        act.activation(fh[:, k % 2, j, :], ps[:, j, :], ACT.Relu, bias=b1_cur[:, j:j + 1]) \
                           .then_inc(f_a.sem, f_a.tick(f"h{k}{j}"))
                take_w1T(e + 1)
            layernorm_root(act, ln2_v, ln2_a, stat[:, 2])

        @block.vector
        def _(dve):
            layernorm_vector(dve, ln0_v, ln0_a, x[:], nrm[:], sq[:], stat[:, 0], NT)
            dve.wait_ge(pre_p.sem, pre_p.at("w"))
            dve.tensor_copy(w_inT[:], ps[:, 0, 0:3 * P]).then_inc(pre_v.sem, pre_v.tick("w_inT"))
            dve.tensor_copy(w_outT[:], ps[:, 1, 0:P]).then_inc(pre_v.sem, pre_v.tick("w_outT"))
            dve.tensor_copy(gwT[:], ps[:, 1, P:P + NE]).then_inc(pre_v.sem, pre_v.tick("gwT"))
            dve.tensor_copy(b1T[:, 0:NE * NJ], ps[:, 1, 2 * P:2 * P + NE * NJ]).then_inc(pre_v.sem, pre_v.tick("b1T"))
            dve.wait_ge(pre_p.sem, pre_p.at("nT"))
            dve.tensor_copy(nT[:, 2 * BLK:T], banks(ps, 6, 8)).then_inc(pre_v.sem, pre_v.tick("nT1"))
            dve.wait_ge(load.sem, LOADED)
            for t in range(NT):
                dve.wait_ge(qkv_p.sem, qkv_p.at(f"t{t}"))
                dve.tensor_tensor(qkv[:, t, :], ps[:, t % 4, 0:3 * P], b_in[:], ALU.add).then_inc(pre_v.sem, pre_v.tick(f"qkv{t}"))
            for each in (s_v, c_v):
                dve.sem_inc(each.sem, len(each.names))

            def multiply_and_sum(products, total, mine, theirs):
                with dve.Fori(0, B // 2) as i:
                    for r in range(2):
                        last, pass_ = (0, i) if r else (1, i - 1)
                        dve.wait_ge(mine.sem, mine.at(f"own_sum{last}", pass_))
                        products(dve, 2 * i + r, 1, 2).then_inc(mine.sem, mine.tick(f"own{r}"))
                        dve.wait_ge(mine.sem, mine.at(f"own{r}", i))
                        total(2 * i + r, 1, 2).then_inc(mine.sem, mine.tick(f"own_sum{r}"))
                        dve.wait_ge(theirs.sem, theirs.at(f"prod{r}", i))
                        total(2 * i + r, 0, r).then_inc(mine.sem, mine.tick(f"sum{r}"))

            def score_sums(s, f, of):
                return dve.tensor_reduce(sc[:, bass.ds(2 * s + f, 1)].rearrange("p o t h -> p (o t h)"),
                                         prod[:, of].rearrange("p t (h d) -> p (t h) d", h=EH), AX.X, ALU.add)

            def context_sums(s, f, of):
                return dve.tensor_reduce(cx[:, bass.ds(2 * s + f, 1), :].rearrange("p o d -> p (o d)"),
                                         prod[:, of].rearrange("p t d -> p d t"), AX.X, ALU.add)

            dve.wait_ge(pre_v.sem, pre_v.at(f"qkv{NT - 1}"))
            multiply_and_sum(score_products, score_sums, s_v, s_g)
            dve.wait_ge(s_v.sem, s_v.at("sum1", B // 2 - 1))
            by_t = sc[:].rearrange("p n t h -> p n h t")
            over = lambda v: v[:].unsqueeze(2).to_broadcast([P, NT, B, EH])
            dve.tensor_reduce(smx[:], by_t, AX.X, ALU.max).then_inc(sm_v.sem, sm_v.tick("max"))
            dve.wait_ge(sm_v.sem, sm_v.at("max"))
            dve.tensor_tensor(sc[:], sc[:], over(smx), ALU.subtract).then_inc(sm_v.sem, sm_v.tick("shift"))
            dve.wait_ge(sm_a.sem, sm_a.at("exp"))
            dve.tensor_reduce(smx[:], by_t, AX.X, ALU.add).then_inc(sm_v.sem, sm_v.tick("sum"))
            dve.wait_ge(sm_v.sem, sm_v.at("sum"))
            dve.reciprocal(smx[:], smx[:]).then_inc(sm_v.sem, sm_v.tick("inv"))
            dve.wait_ge(sm_v.sem, sm_v.at("inv"))
            dve.tensor_tensor(sc[:], sc[:], over(smx), ALU.mult).then_inc(sm_v.sem, sm_v.tick("p"))
            dve.wait_ge(sm_v.sem, sm_v.at("p"))
            multiply_and_sum(context_products, context_sums, c_v, c_g)
            dve.wait_ge(mid_p.sem, mid_p.at("out"))
            dve.wait_ge(pre_g.sem, pre_g.at("b_out"))
            dve.tensor_tensor(tok[:], rows(banks(ps, 4, 8), NT), nrm[:], ALU.add).then_inc(mid_v.sem, mid_v.tick("out"))
            dve.wait_ge(mid_v.sem, mid_v.at("out"))
            layernorm_vector(dve, ln1_v, ln1_a, tok[:], tok[:], sq[:], stat[:, 1], NT)
            row = lambda i: lng[:, i, :].unsqueeze(1).to_broadcast([P, NT, P])
            dve.wait_ge(ln1_v.sem, ln1_v.at("normal"))
            dve.tensor_tensor(tok[:], tok[:], row(0), ALU.mult).then_inc(mid_v.sem, mid_v.tick("scaled"))
            dve.wait_ge(mid_v.sem, mid_v.at("scaled"))
            dve.tensor_tensor(tok[:], tok[:], row(1), ALU.add).then_inc(mid_v.sem, mid_v.tick("tok"))
            per_tile = lambda v: v[:].unsqueeze(2).to_broadcast([P, NT, NE])
            dve.wait_ge(mid_p.sem, mid_p.at("gate"))
            dve.tensor_tensor(lg[:], ps[:, 4, 0:P].rearrange("p (t e) -> p t e", e=NE),
                              b_gate[:].unsqueeze(1).to_broadcast([P, NT, NE]), ALU.add).then_inc(mid_v.sem, mid_v.tick("bias"))
            dve.wait_ge(mid_v.sem, mid_v.at("bias"))
            dve.tensor_reduce(l1[:], lg[:], AX.X, ALU.max).then_inc(mid_v.sem, mid_v.tick("max"))
            dve.wait_ge(mid_v.sem, mid_v.at("max"))
            dve.tensor_tensor(lg[:], lg[:], per_tile(l1), ALU.subtract).then_inc(mid_v.sem, mid_v.tick("shift"))
            dve.wait_ge(mid_a.sem, mid_a.at("e"))
            mine = lg[:].unsqueeze(3).to_broadcast([P, NT, NE, NE])
            other = lg[:].unsqueeze(2).to_broadcast([P, NT, NE, NE])
            dve.tensor_tensor(cmp[:, 0], other, mine, ALU.is_gt).then_inc(mid_v.sem, mid_v.tick("gt"))
            dve.tensor_tensor(cmp[:, 1], other, mine, ALU.is_equal).then_inc(mid_v.sem, mid_v.tick("eq"))
            dve.wait_ge(mid_v.sem, mid_v.at("eq"))
            dve.tensor_tensor(cmp[:, 1], cmp[:, 1], lower[:].unsqueeze(1).to_broadcast([P, NT, NE, NE]), ALU.mult) \
               .then_inc(mid_v.sem, mid_v.tick("lower"))
            dve.wait_ge(mid_v.sem, mid_v.at("lower"))
            dve.tensor_tensor(cmp[:, 0], cmp[:, 0], cmp[:, 1], ALU.add).then_inc(mid_v.sem, mid_v.tick("beats"))
            dve.wait_ge(mid_v.sem, mid_v.at("beats"))
            dve.tensor_reduce(rank[:], cmp[:, 0], AX.X, ALU.add).then_inc(mid_v.sem, mid_v.tick("rank"))
            dve.wait_ge(mid_v.sem, mid_v.at("rank"))
            dve.tensor_scalar(rank[:], rank[:], TOP - 0.5, None, ALU.is_lt).then_inc(mid_v.sem, mid_v.tick("top"))
            dve.wait_ge(mid_v.sem, mid_v.at("top"))
            dve.tensor_tensor(comb, rank[:], lg[:], ALU.mult).then_inc(mid_v.sem, mid_v.tick("w"))
            dve.wait_ge(mid_v.sem, mid_v.at("w"))
            dve.tensor_reduce(l1[:], comb, AX.X, ALU.add).then_inc(mid_v.sem, mid_v.tick("sum"))
            dve.wait_ge(mid_v.sem, mid_v.at("sum"))
            dve.reciprocal(l1[:], l1[:]).then_inc(mid_v.sem, mid_v.tick("inv"))
            dve.wait_ge(mid_v.sem, mid_v.at("inv"))
            dve.tensor_tensor(comb, comb, per_tile(l1), ALU.mult).then_inc(mid_v.sem, mid_v.tick("comb"))
            dve.memset(b1T[:, NE * NJ:], 0.0).then_inc(mid_v.sem, mid_v.tick("b1_pad"))
            dve.memset(comb_pad[:, :, NE:NE + 1], 0.0).then_inc(mid_v.sem, mid_v.tick("comb_pad"))
            dve.wait_ge(mid_p.sem, mid_p.at("b2"))
            dve.tensor_tensor(acc[:], rows(banks(ps, 4, 8), NT), tok[:], ALU.add).then_inc(mid_v.sem, mid_v.tick("acc"))
            dve.wait_ge(mid_v.sem, mid_v.at("acc"))
            dve.sem_inc(f_v.sem, len(f_v.names))

            def take_b1(columns):
                dve.tensor_copy(b1_cur[:], b1T[:, columns]).then_inc(e_v.sem, e_v.tick("b1"))

            def take_w2T(e):
                dve.wait_ge(e_p.sem, e_p.at("w2T", e))
                dve.tensor_copy(w2T[:].rearrange("p j d -> p (j d)"), ps[:, 7, :]).then_inc(e_v.sem, e_v.tick("w2T"))

            def take_comb(column):
                dve.tensor_copy(comb_e[:].unsqueeze(2), comb_pad[:, :, column]).then_inc(e_v.sem, e_v.tick("comb_e"))

            def add_block(k, e):
                dve.wait_ge(f_p.sem, f_p.at(f"o{k}", e))
                for i in range(4):
                    at = acc[:, 4 * k + i, :]
                    last = dve.scalar_tensor_tensor(at, ps[:, 4 + k % 2, bass.ts(i, P)], comb_e[:, 4 * k + i:4 * k + i + 1],
                                                    at, ALU.mult, ALU.add)
                last.then_inc(f_v.sem, f_v.tick(f"acc{k}"))

            dve.wait_ge(pre_v.sem, pre_v.at("b1T"))
            take_b1(slice(0, NJ))
            take_w2T(0)
            take_comb(slice(0, 1))
            with dve.Fori(0, NE) as e:
                dve.wait_ge(e_v.sem, e_v.at("comb_e", e))
                for k in range(NB):
                    for j in (1, 3):
                        last, pass_ = before(k, 2, e)
                        dve.wait_ge(f_p.sem, f_p.at(f"o{last}", pass_))
                        dve.wait_ge(f_p.sem, f_p.at(f"h{k}{j}", e))
                        dve.tensor_scalar(fh[:, k % 2, j, :], ps[:, j, :], b1_cur[:, j:j + 1], 0.0,
                                          ALU.add, ALU.max).then_inc(f_v.sem, f_v.tick(f"h{k}{j}"))
                    if k:
                        add_block(k - 1, e)
                dve.wait_ge(f_a.sem, f_a.at(f"h{NB - 1}2", e))
                dve.wait_ge(f_v.sem, f_v.at(f"h{NB - 1}3", e))
                take_b1(bass.ds(e * NJ + NJ, NJ))
                add_block(NB - 1, e)
                take_w2T(e + 1)
                dve.wait_ge(f_v.sem, f_v.at(f"acc{NB - 1}", e))
                take_comb(bass.ds(e + 1, 1))
            dve.wait_ge(f_v.sem, f_v.at(f"acc{NB - 1}", NE - 1))
            layernorm_vector(dve, ln2_v, ln2_a, acc[:], acc[:], sq[:], stat[:, 2], NT)
            dve.wait_ge(ln2_v.sem, ln2_v.at("normal"))
            dve.tensor_tensor(acc[:], acc[:], row(2), ALU.mult).then_inc(end_v.sem, end_v.tick("scaled"))
            dve.wait_ge(end_v.sem, end_v.at("scaled"))
            dve.tensor_tensor(acc[:], acc[:], row(3), ALU.add).then_inc(end_v.sem, end_v.tick("moved"))
            dve.wait_ge(end_v.sem, end_v.at("moved"))
            dve.tensor_tensor(x[:], acc[:], x[:], ALU.add).then_inc(end_v.sem, end_v.tick("x"))

        @block.tensor
        def _(pe):
            pe.wait_ge(load.sem, LOADED)
            for i in range(3):
                pe.transpose(ps[:, 0, bass.ts(i, P)], w_in[:, i, :], ident)
            pe.transpose(ps[:, 1, 0:P], w_out[:], ident)
            pe.transpose(ps[:, 1, P:P + NE], gw[:], ident[0:NE, 0:NE])
            pe.transpose(ps[:, 1, 2 * P:2 * P + NE * NJ], b1r[:], ident[0:NE * NJ, 0:NE * NJ]) \
              .then_inc(pre_p.sem, pre_p.tick("w"))
            for t in range(NT):
                if t % 4 == 0:
                    pe.wait_ge(ln0_v.sem, ln0_v.at(normal_of(t)))
                mm = pe.transpose(ps[:, 4 + t // 4, bass.ts(t % 4, P)], nrm[:, t, :], ident)
            mm.then_inc(pre_p.sem, pre_p.tick("nT"))
            pe.wait_ge(pre_a.sem, pre_a.at("nT0"))
            pe.wait_ge(pre_v.sem, pre_v.at("nT1"))
            for t in range(NT):
                if t >= 4:
                    pe.wait_ge(pre_v.sem, pre_v.at(f"qkv{t - 4}"))
                pe.matmul(ps[:, t % 4, 0:3 * P], nT[:, bass.ts(t, P)], w_inT[:], start=True, stop=True) \
                  .then_inc(qkv_p.sem, qkv_p.tick(f"t{t}"))
            pe.wait_ge(pre_v.sem, pre_v.at(f"qkv{NT - 1}"))
            pe.wait_ge(c_v.sem, c_v.at("sum1", B // 2 - 1))
            for t in range(NT):
                mm = pe.transpose(ps[:, t // 4, bass.ts(t % 4, P)], cx[:, t, :], ident)
            mm.then_inc(mid_p.sem, mid_p.tick("cT"))
            pe.wait_ge(mid_a.sem, mid_a.at("cT"))
            for t in range(NT):
                mm = pe.matmul(ps[:, 4 + t // 4, bass.ts(t % 4, P)], nT[:, bass.ts(t, P)], w_outT[:], start=True, stop=True)
            mm.then_inc(mid_p.sem, mid_p.tick("out"))
            pe.wait_ge(mid_v.sem, mid_v.at("tok"))
            for t in range(NT):
                mm = pe.transpose(ps[:, t // 4, bass.ts(t % 4, P)], tok[:, t, :], ident)
            mm.then_inc(mid_p.sem, mid_p.tick("tokT"))
            pe.wait_ge(mid_a.sem, mid_a.at("tokT"))
            for t in range(NT):
                mm = pe.matmul(ps[:, 4, bass.ts(t, NE)], tokT[:, bass.ts(t, P)], gwT[:], start=True, stop=True)
            mm.then_inc(mid_p.sem, mid_p.tick("gate"))
            pe.wait_ge(mid_v.sem, mid_v.at("comb"))
            for t in range(NT):
                mm = pe.transpose(ps[0:NE, t // 4, bass.ts(t % 4, P)], comb[:, t, :], ident)
            mm.then_inc(mid_p.sem, mid_p.tick("combT"))
            pe.wait_ge(mid_a.sem, mid_a.at("combT"))
            for t in range(NT):
                mm = pe.matmul(ps[:, 4 + t // 4, bass.ts(t % 4, P)], combT[:, bass.ts(t, P)], b2[:], start=True, stop=True)
            mm.then_inc(mid_p.sem, mid_p.tick("b2"))
            pe.sem_inc(e_p.sem, len(e_p.names))
            pe.sem_inc(f_p.sem, len(f_p.names))
            pe.wait_ge(mid_v.sem, mid_v.at("acc"))

            def transposes(e):
                pe.wait_ge(w_load.sem, 32 * e + 32)
                for j in range(NJ):
                    mm = pe.transpose(ps[:, 6, bass.ts(j, P)], w1r[:, j, :], ident)
                mm.then_inc(e_p.sem, e_p.tick("w1T"))
                for j in range(NJ):
                    mm = pe.transpose(ps[:, 7, bass.ts(j, P)], w2r[:, bass.ts(j, P)], ident)
                mm.then_inc(e_p.sem, e_p.tick("w2T"))

            def up(k, e):
                if k == 0:
                    pe.wait_ge(e_a.sem, e_a.at("w1T", e))
                last, pass_ = before(k, 1, e)
                for j in range(NJ):
                    pe.wait_ge(f_v.sem, f_v.at(f"h{last}{j}", pass_)) if j % 2 else \
                        pe.wait_ge(f_a.sem, f_a.at(f"h{last}{j}", pass_))
                    pe.matmul(ps[:, j, :], w1T[:, bass.ts(j, P)], tokT[:, bass.ts(k, BLK)], start=True, stop=True) \
                      .then_inc(f_p.sem, f_p.tick(f"h{k}{j}"))

            def down(k, e):
                if k == 0:
                    pe.wait_ge(e_v.sem, e_v.at("w2T", e))
                last, pass_ = before(k, 2, e)
                pe.wait_ge(f_v.sem, f_v.at(f"acc{last}", pass_))
                pe.wait_ge(f_v.sem, f_v.at(f"h{k}3", e))
                pe.wait_ge(f_a.sem, f_a.at(f"h{k}2", e))
                for i in range(4):
                    for j in range(NJ):
                        mm = pe.matmul(ps[:, 4 + k % 2, bass.ts(i, P)], fh[:, k % 2, j, bass.ts(i, P)], w2T[:, j, :],
                                       start=(j == 0), stop=(j == NJ - 1))
                mm.then_inc(f_p.sem, f_p.tick(f"o{k}"))

            transposes(0)
            with pe.Fori(0, NE) as e:
                for k in range(NB):
                    up(k, e)
                    if k:
                        down(k - 1, e)
                transposes(e + 1)
                down(NB - 1, e)



GK = 32


def stage_gated(nc, g, a):
    with Stage(nc, "ga") as st:
        w_lr = st.sb("w_lr", [P, 2, GK])
        thr = st.sb("thr", [P, 2])
        nrm = st.sb("nrm", [P, NT, P])
        nT = st.sb("nT", [P, T])
        sq = st.sb("sq", [P, NT, P])
        stat = st.sb("stat", [P, 4, NT])
        lr = st.sb("lr", [GK, 2, T])
        cm = st.sb("cm", [P, NT, S])
        ex = st.sb("ex", [P, NT, S])
        exT = st.sb("exT", [P, B, 2, S])
        mx = st.sb("mx", [P, NT])
        low = st.sb("low", [P, NT])
        tot = st.sb("tot", [P, NT])
        o = st.sb("o", [P, NT, P])
        ps, x = g.ps, g.x
        ident = g.ident

        load = st.steps("load", ["all"])
        LOADED = 16 * 4
        ln_v, ln_a = st.steps("ln_v", LN_VECTOR), st.steps("ln_a", ["root"])
        H = NT // 2
        p = st.steps("p", ["nT", "left", "right", "cm0", "cm1", "T0", "T1", "o0", "o1"])
        s_a = st.steps("s_a", ["nT", "left"] + [f"exp{t}" for t in range(NT)] + ["T0"])
        s_v = st.steps("s_v", ["right"] + [f"{n}{k}" for k in range(2) for n in ("cm", "max", "bias", "low")]
                       + ["inv0", "gated0", "inv1", "gated1", "T1", "o0", "x0", "o1", "x1"])

        block = st.block()

        @block.sync
        def _(sp):
            sp.dma_start(w_lr[:, 0, :], a["L1_attn_compare_left"]).then_inc(load.sem, 16)
            sp.dma_start(w_lr[:, 1, :], a["L1_attn_compare_right"]).then_inc(load.sem, 16)
            sp.dma_start(thr[:, 0:1], a["L1_attn_threshold"].partition_broadcast(P)).then_inc(load.sem, 16)
            sp.dma_start(thr[:, 1:2], a["L1_attn_gate_bias"].partition_broadcast(P)).then_inc(load.sem, 16)

        @block.scalar
        def _(act):
            layernorm_root(act, ln_v, ln_a, stat)
            act.wait_ge(p.sem, p.at("nT"))
            act.activation(nT[:], banks(ps, 0, 4), ACT.Copy).then_inc(s_a.sem, s_a.tick("nT"))
            act.wait_ge(p.sem, p.at("left"))
            act.activation(lr[:, 0, :], banks(ps, 4, 8)[0:GK, :], ACT.Copy).then_inc(s_a.sem, s_a.tick("left"))
            for t in range(NT):
                if t % H == 0:
                    act.wait_ge(s_v.sem, s_v.at(f"low{t // H}"))
                act.activation(ex[:, t, :], cm[:, t, :], ACT.Exp, bias=low[:, t:t + 1], accum_out=tot[:, t:t + 1]) \
                   .then_inc(s_a.sem, s_a.tick(f"exp{t}"))
            act.wait_ge(p.sem, p.at("T0"))
            act.activation(exT[:, 0:B // 2].rearrange("p b j i -> p (b j i)"), banks(ps, 0, 4), ACT.Copy) \
               .then_inc(s_a.sem, s_a.tick("T0"))

        @block.vector
        def _(dve):
            layernorm_vector(dve, ln_v, ln_a, x[:], nrm[:], sq[:], stat[:], NT)
            dve.wait_ge(p.sem, p.at("right"))
            dve.tensor_copy(lr[:, 1, :], banks(ps, 0, 4)[0:GK, :]).then_inc(s_v.sem, s_v.tick("right"))
            dve.wait_ge(load.sem, LOADED)
            half = lambda k: slice(H * k, H * k + H)
            for k in range(2):
                n = half(k)
                dve.wait_ge(p.sem, p.at(f"cm{k}"))
                dve.tensor_scalar(cm[:, n, :], rows(banks(ps, 4 * k, 4 * k + 4), H, S), P ** -0.5, None, ALU.mult) \
                   .then_inc(s_v.sem, s_v.tick(f"cm{k}"))
                dve.wait_ge(s_v.sem, s_v.at(f"cm{k}"))
                dve.tensor_reduce(mx[:, n], cm[:, n], AX.X, ALU.max).then_inc(s_v.sem, s_v.tick(f"max{k}"))
                dve.wait_ge(s_v.sem, s_v.at(f"max{k}"))
                dve.tensor_scalar(mx[:, n], mx[:, n], thr[:, 1:2], None, ALU.add).then_inc(s_v.sem, s_v.tick(f"bias{k}"))
                dve.wait_ge(s_v.sem, s_v.at(f"bias{k}"))
                dve.tensor_scalar(low[:, n], mx[:, n], -1.0, thr[:, 1:2], ALU.mult, ALU.add) \
                   .then_inc(s_v.sem, s_v.tick(f"low{k}"))
            for k in range(2):
                n = half(k)
                dve.wait_ge(s_a.sem, s_a.at(f"exp{H * k + H - 1}"))
                dve.reciprocal(mx[:, n], tot[:, n]).then_inc(s_v.sem, s_v.tick(f"inv{k}"))
                dve.scalar_tensor_tensor(ex[:, n], cm[:, n], thr[:, 0:1], ex[:, n], ALU.is_gt, ALU.mult) \
                   .then_inc(s_v.sem, s_v.tick(f"gated{k}"))
            dve.wait_ge(p.sem, p.at("T1"))
            dve.tensor_copy(exT[:, B // 2:B].rearrange("p b j i -> p (b j i)"), banks(ps, 4, 8)) \
               .then_inc(s_v.sem, s_v.tick("T1"))
            dve.wait_ge(s_v.sem, s_v.at("inv1"))
            for k in range(2):
                n = half(k)
                dve.wait_ge(p.sem, p.at(f"o{k}"))
                dve.tensor_tensor(o[:, n], rows(banks(ps, 2 * k, 2 * k + 2), H), bcast(mx[:, n], H), ALU.mult) \
                   .then_inc(s_v.sem, s_v.tick(f"o{k}"))
                dve.wait_ge(s_v.sem, s_v.at(f"o{k}"))
                dve.tensor_tensor(x[:, n], x[:, n], o[:, n], ALU.add).then_inc(s_v.sem, s_v.tick(f"x{k}"))

        @block.tensor
        def _(pe):
            for t in range(NT):
                if t % 4 == 0:
                    pe.wait_ge(ln_v.sem, ln_v.at(normal_of(t)))
                mm = pe.transpose(ps[:, t // 4, bass.ts(t % 4, P)], nrm[:, t, :], ident)
            mm.then_inc(p.sem, p.tick("nT"))
            pe.wait_ge(s_a.sem, s_a.at("nT"))
            pe.wait_ge(load.sem, LOADED)
            for i, b0, name in ((0, 4, "left"), (1, 0, "right")):
                for b in range(NB):
                    mm = pe.matmul(ps[0:GK, b0 + b, :], w_lr[:, i, :], nT[:, bass.ts(b, BLK)], start=True, stop=True)
                mm.then_inc(p.sem, p.tick(name))
            pe.wait_ge(s_a.sem, s_a.at("left"))
            pe.wait_ge(s_v.sem, s_v.at("right"))
            for t in range(NT):
                mm = pe.matmul(ps[:, t // 2, bass.ts(t % 2, S)], lr[:, 0, bass.ts(t, P)], lr[:, 1, bass.ts(t // 2, S)],
                               start=True, stop=True)
                if t % H == H - 1:
                    mm.then_inc(p.sem, p.tick(f"cm{t // H}"))
            for k in range(2):
                pe.wait_ge(s_v.sem, s_v.at(f"gated{k}"))
                for b in range(B // 2 * k, B // 2 * (k + 1)):
                    for j in range(2):
                        for i in range(2):
                            mm = pe.transpose(ps[:, b, bass.ds(S * j + P * i, P)], ex[:, 2 * b + i, bass.ts(j, P)], ident)
                mm.then_inc(p.sem, p.tick(f"T{k}"))
            pe.wait_ge(s_a.sem, s_a.at("T0"))
            for t in range(NT):
                if t == H:
                    pe.wait_ge(s_v.sem, s_v.at("T1"))
                for j in range(2):
                    mm = pe.matmul(ps[:, t // 4, bass.ts(t % 4, P)], exT[:, t // 2, j, bass.ts(t % 2, P)],
                                   nrm[:, 2 * (t // 2) + j, :], start=(j == 0), stop=(j == 1))
                if t % H == H - 1:
                    mm.then_inc(p.sem, p.tick(f"o{t // H}"))



MH, MD = 16, 8
NBUCKET = 32
NREL = 768
NEVER = 1e9
NU = 4 * MH
QK = S + SC
PRODUCTS = ((0, 0, 3), (1, 0, 2), (2, 0, 1))
HROWS = sum(n for _, _, n in PRODUCTS) * MD
MROW = 2 * HROWS
AHEAD = 4
HB = 32 // MD
N_STACK = 2 * (sum(n for _, _, n in PRODUCTS) + len(PRODUCTS)) + 1


def bf16_parts(value):
    parts = []
    for _ in range(3):
        unit = 2.0 ** (math.frexp(value)[1] - 8)
        parts.append(math.floor(value / unit) * unit)
        value -= parts[-1]
    assert value == 0
    return parts


def stage_masked_attention(nc, g, a):
    with Stage(nc, "ma") as st:
        w4 = st.sb("w4", [P, 4, P])
        w4T = st.sb("w4T", [P, 4, P])
        emb = st.sb("emb", [NBUCKET, MH])
        bucket = st.sb("bucket", [NBUCKET, NREL])
        rel = st.sb("rel", [MH, NREL])
        mask_u = st.sb("mask_u", [P, B * SC], U8)
        mask_b = st.sb("mask_b", [B, SC], U8)
        keep = st.sb("keep", [P, B * SC], BF16)
        keep_b = st.sb("keep_b", [B, SC])
        never = st.sb("never", [B, 3, SC], BF16)
        tb = st.sb("tb", [P, MH, P + SC])
        nrm_pad = st.sb("nrm", [P, NT + 2, P])
        nT = st.sb("nT", [P, T])
        stat = st.sb("stat", [P, 4, NT])
        ctxT = st.sb("ctxT", [P, B * SC])
        cur = st.sb("cur", [P, 2, SC])
        qk = st.sb("qk", [P, 2, QK])
        rest = st.sb("rest", [P, 2, QK])
        parts = st.sb("parts", [P, 2, 3, QK], BF16)
        q_stack = st.sb("q_stack", [P, 2, MH, S], BF16)
        k_stack = st.sb("k_stack", [P, 2, MH // 2, SC], BF16)
        v_cur = st.sb("v_cur", [P, 2, NK, P])
        sc = st.sb("sc", [P, 4, SC])
        pr = st.sb("pr", [P, 2, SC])
        prT = st.sb("prT", [P, 2, SC])
        low = st.sb("low", [P, NU])
        tot = st.sb("tot", [P, B + 1, 2, MH])
        tot_cur = st.sb("tot_cur", [P, NU])
        rec = st.sb("rec", [P, B, 2, MH])
        which = st.sb("which", [P, HB])
        rel_dram = nc.dram_tensor("rel_by_distance", [MH, NREL], F32, kind="Internal").ap()
        q_dram = nc.dram_tensor("q_parts", [B, MH, 3, MD, S], BF16, kind="Internal").ap()
        k_dram = nc.dram_tensor("k_parts", [B, MH, 3, MD, SC], BF16, kind="Internal").ap()
        never_dram = nc.dram_tensor("never_parts", [B, 3, SC], BF16, kind="Internal").ap()
        ps, x, ctx = g.ps, g.x, g.ctx
        ident = g.ident
        sq = rows(nT[:], NT)
        rec_x = sq
        v = ctx
        nrm = nrm_pad[:, 0:NT, :]
        oT_pad = nrm_pad[:].rearrange("p t d -> p (t d)")
        oT = oT_pad[:, S:S + T]

        load = st.steps("load", ["all"])
        LOADED = 16 * 9
        rel_out = st.steps("rel_out", ["rel"])
        never_out = st.steps("never_out", ["never"])
        rel_in = st.steps("rel_in", ["tb"])
        ln_v, ln_a = st.steps("ln_v", LN_VECTOR), st.steps("ln_a", ["root"])
        pre_p = st.steps("pre_p", ["ctx0", "w4T", "rel", "nT", "ctx1"])
        pre_v = st.steps("pre_v", ["q_zeros", "k_zeros", "q_ones", "tot_ones"])
        pre_a = st.steps("pre_a", ["ctx0", "w4T", "rel", "nT", "ctx1"])
        pre_g = st.steps("pre_g", ["keep", "keep_b", "never0", "never1", "never2"])
        two = lambda *xs: [f"{n}{j}" for j in range(2) for n in xs]
        cut_p = st.steps("cut_p", two("q", "k", "v"), ahead=1)
        cut_a = st.steps("cut_a", ["q0", "first0", "v0", "q1", "second0", "first1", "v1", "second1"], ahead=1)
        cut_v = st.steps("cut_v", ["k0", "rest0", "k1", "third0", "rest1", "third1"], ahead=1)
        cut_g = st.steps("cut_g", two("cur"), ahead=1)
        parts_out = [st.steps(f"parts_out{j}", ["parts"]) for j in range(2)]
        N_OUT = 6
        stack_in = [st.steps(f"stack_in{j}", ["stacks"]) for j in range(2)]
        at_p = st.steps("at_p", [f"S{u}" for u in range(AHEAD)]
                        + [n for u in range(NU) for n in ([f"S{u + AHEAD}"] if u + AHEAD < NU else []) + [f"T{u}"]
                           + ([f"O{u - 1}"] if u else [])] + [f"O{NU - 1}"], ahead=1)
        at_a = st.steps("at_a", [n for u in range(NU) for n in [f"E{u}"] + ([f"T{u - 1}"] if u % 2 else [])], ahead=1)
        TAKE = [[f"{n}{j}" for n in ["tot"] + [f"o{k}_" for k in range(HB)]] for j in range(2)]
        at_v = st.steps("at_v", [n for u in range(NU) for n in [f"M{u}"] + ([f"T{u - 3}"] if u > 2 and u % 2 == 0 else [])
                                 + (TAKE[1] if u == 4 else TAKE[0] if u == NU // 2 + 4 else [])]
                        + [f"T{NU - 3}", f"T{NU - 1}"], ahead=1)
        last_v = st.steps("last_v", TAKE[1])
        at_g = st.steps("at_g", ["v0", "v1"], ahead=1)
        out_p = st.steps("out_p", ["rec", "out0", "out1", "out2", "out3"])
        out_v = st.steps("out_v", ["rec", "rec_x", "o"] + [f"x{i}" for i in range(NB)])
        passed_v = st.steps("passed_v", ["score"]).sem
        passed_s = st.steps("passed_s", ["stack"]).sem

        block = st.block()

        @block.sync
        def _(sp):
            mask = a["mask_Bx1x1xS2_bk0"]
            for dst, src in (
                (w4[:, 0, :], a["L1_xattn_Wq"]), (w4[:, 1, :], a["L1_xattn_Wk"]), (w4[:, 2, :], a["L1_xattn_Wv"]),
                (w4[:, 3, :], a["L1_xattn_Wo"]), (emb[:], a["L1_xattn_rel_emb"]), (bucket[:], a["bucket"]),
                (which[:], a["which"]),
                (mask_b[:], mask.rearrange("b x y s -> (b x y) s")),
                (mask_u[:], mask.rearrange("b x y s -> (b x y s)").partition_broadcast(P)),
            ):
                sp.dma_start(dst, src).then_inc(load.sem, 16)
            sp.wait_ge(pre_a.sem, pre_a.at("rel"))
            sp.dma_start(rel_dram, rel[:]).then_inc(rel_out.sem, 16)
            sp.wait_ge(rel_out.sem, 16)
            sp.dma_start(tb[:], bass.AP(rel_dram.tensor, 0, [[1, P], [NREL, MH], [1, P + SC]])).then_inc(rel_in.sem, 16)
            sp.wait_ge(pre_g.sem, pre_g.at("never2"))
            sp.dma_start(never_dram, never[:]).then_inc(never_out.sem, 16)

            def store(i):
                for j in range(2):
                    sp.wait_ge(cut_v.sem, cut_v.at(f"third{j}", i))
                    sp.sem_inc(passed_s, 1)
                    for part in range(3):
                        for dram, cols in ((q_dram, slice(0, S)), (k_dram, slice(S, QK))):
                            dst = dram[batch(i, j), :, part].rearrange("b h d s -> (b h) d s")
                            sp.dma_start(dst, parts[:, j, part, cols]).then_inc(parts_out[j].sem, 16)

            def stack(i, of_pass=(0, 1), first=False):
                for j in of_pass:
                    if not first:
                        sp.wait_ge(at_p.sem, at_p.at(f"S{NU // 2 * (j + 1) - 1}", i - 1))
                        sp.sem_inc(passed_s, 1)
                    for side in range(2):
                        q_of = q_dram[batch(i, j), side::2].rearrange("b c t d s -> (b t d) c s")
                        k_of = k_dram[batch(i, j), side::2].rearrange("b c t d s -> (b t d) c s")
                        row = side * HROWS
                        for q_part, k_part, n in PRODUCTS:
                            sp.dma_start(k_stack[row:row + n * MD, j], k_of[k_part * MD:(k_part + n) * MD]) \
                              .then_inc(stack_in[j].sem, 16)
                            for _ in range(n):
                                sp.dma_start(q_stack[row:row + MD, j, side::2, :], q_of[q_part * MD:(q_part + 1) * MD]) \
                                  .then_inc(stack_in[j].sem, 16)
                                row += MD
                    nv = never_dram[batch(i, j)].rearrange("b t s -> (b t) s")
                    sp.dma_start(k_stack[MROW:MROW + 3, j], nv.unsqueeze(1).to_broadcast([3, MH // 2, SC])) \
                      .then_inc(stack_in[j].sem, 16)

            batch = lambda i, j: bass.ds(2 * i + j, 1)
            last = B // 2 - 1
            with sp.Fori(0, last) as i:
                store(i)
            for j in range(2):
                sp.wait_ge(parts_out[j].sem, 16 * N_OUT * last)
            sp.wait_ge(never_out.sem, 16)
            sp.wait_ge(pre_v.sem, pre_v.at("k_zeros"))
            stack(0, (0,), first=True)
            store(last)
            stack(0, (1,), first=True)
            for j in range(2):
                sp.wait_ge(parts_out[j].sem, 16 * N_OUT * (B // 2))
            with sp.Fori(1, B // 2) as i:
                stack(i)

        @block.gpsimd
        def _(pool):
            pool.wait_ge(load.sem, LOADED)
            back = lambda buf, n, w: bass.AP(buf[:].tensor, SC - 1, [[w, n], [SC, w // SC], [-1, SC]])
            pool.tensor_copy(back(keep, P, B * SC), mask_u[:].rearrange("p (b s) -> p b s", b=B)) \
                .then_inc(pre_g.sem, pre_g.tick("keep"))
            pool.tensor_copy(back(keep_b, B, SC), mask_b[:].unsqueeze(1)).then_inc(pre_g.sem, pre_g.tick("keep_b"))
            pool.wait_ge(pre_g.sem, pre_g.at("keep_b"))
            for i, c in enumerate(bf16_parts(NEVER)):
                pool.tensor_scalar(never[:, i, :], keep_b[:], -c, c, ALU.mult, ALU.add) \
                    .then_inc(pre_g.sem, pre_g.tick(f"never{i}"))
            pool.sem_inc(cut_g.sem, cut_g.at("cur1", -1))
            pool.sem_inc(at_g.sem, at_g.at("v1", -1))
            pool.wait_ge(pre_g.sem, pre_g.at("never2"))
            pool.wait_ge(pre_a.sem, pre_a.at("ctx1"))
            with pool.Fori(0, B // 2) as i:
                for j in range(2):
                    pool.wait_ge(cut_p.sem, cut_p.at(f"v{j}", i - 1))
                    pool.tensor_copy(cur[:, j, :], ctxT[:, bass.ds(2 * SC * i + SC * j, SC)]) \
                        .then_inc(cut_g.sem, cut_g.tick(f"cur{j}"))
            pool.wait_ge(cut_a.sem, cut_a.at("second1", B // 2 - 1))
            with pool.Fori(0, B // 2) as i:
                for j in range(2):
                    pool.wait_ge(at_p.sem, at_p.at(f"O{NU // 2 * (j + 1) - 1}", i - 1))
                    pool.tensor_copy(v_cur[:, j], v[:, bass.ds(2 * NK * i + NK * j, NK), :]) \
                        .then_inc(at_g.sem, at_g.tick(f"v{j}"))

        backwards = lambda b: bass.AP(ctxT[:].tensor, b * SC + SC - 1, [[B * SC, P], [SC, NB], [-1, SC]])

        @block.scalar
        def _(act):
            act.wait_ge(pre_p.sem, pre_p.at("ctx0"))
            act.activation(backwards(0), ps[:, 4:8, :], ACT.Copy).then_inc(pre_a.sem, pre_a.tick("ctx0"))
            layernorm_root(act, ln_v, ln_a, stat)
            act.wait_ge(pre_p.sem, pre_p.at("w4T"))
            act.activation(w4T[:].rearrange("p i d -> p (i d)"), ps[:, 0, :], ACT.Copy).then_inc(pre_a.sem, pre_a.tick("w4T"))
            act.wait_ge(pre_p.sem, pre_p.at("rel"))
            act.activation(rel[:], banks(ps, 1, 3)[0:MH, 0:NREL], ACT.Copy, scale=-1.0).then_inc(pre_a.sem, pre_a.tick("rel"))
            act.wait_ge(pre_p.sem, pre_p.at("nT"))
            act.activation(nT[:], banks(ps, 4, 8), ACT.Copy).then_inc(pre_a.sem, pre_a.tick("nT"))
            act.wait_ge(pre_p.sem, pre_p.at("ctx1"))
            act.activation(backwards(NB), ps[:, 0:4, :], ACT.Copy).then_inc(pre_a.sem, pre_a.tick("ctx1"))
            act.sem_inc(cut_a.sem, cut_a.at("second1", -1))
            with act.Fori(0, B // 2) as i:
                def take_q(j):
                    act.wait_ge(cut_p.sem, cut_p.at(f"q{j}", i))
                    act.wait_ge(cut_v.sem, cut_v.at(f"rest{j}", i - 1))
                    act.activation(qk[:, j, 0:S], ps[:, 3 * j, 0:S], ACT.Copy, scale=-MD ** -0.5) \
                       .then_inc(cut_a.sem, cut_a.tick(f"q{j}"))

                def first_v(j):
                    act.wait_ge(cut_a.sem, cut_a.at(f"q{j}", i))
                    act.wait_ge(cut_v.sem, cut_v.at(f"k{j}", i))
                    act.wait_ge(parts_out[j].sem, parts_before(i))
                    act.activation(parts[:, j, 0, :], qk[:, j, :], ACT.Copy).then_inc(cut_a.sem, cut_a.tick(f"first{j}"))
                    act.wait_ge(cut_p.sem, cut_p.at(f"v{j}", i))
                    act.activation(v[:, bass.ds(2 * NK * i + NK * j, NK), :], rows(ps[:, 3 * j + 2, :], NK), ACT.Copy) \
                       .then_inc(cut_a.sem, cut_a.tick(f"v{j}"))

                def second(j):
                    act.wait_ge(cut_v.sem, cut_v.at(f"rest{j}", i))
                    act.activation(parts[:, j, 1, :], rest[:, j, :], ACT.Copy).then_inc(cut_a.sem, cut_a.tick(f"second{j}"))

                parts_before = lambda i: 16 * N_OUT * i
                take_q(0)
                first_v(0)
                take_q(1)
                second(0)
                first_v(1)
                second(1)
            act.sem_inc(at_a.sem, at_a.at(f"T{NU - 2}", -1))
            with act.Fori(0, B // 2) as i:
                def move(u):
                    act.wait_ge(at_p.sem, at_p.at(f"T{u}", i))
                    act.activation(prT[:, u % 2, :], ps[:, 2 + u % 2, :], ACT.Copy).then_inc(at_a.sem, at_a.tick(f"T{u}"))

                for u in range(NU):
                    act.wait_ge(at_v.sem, at_v.at(f"M{u}", i))
                    if u >= 2:
                        act.wait_ge(at_p.sem, at_p.at(f"T{u - 2}", i))
                    act.activation(pr[:, u % 2, :], sc[:, u % 4, :], ACT.Exp, scale=-1.0, bias=low[:, u:u + 1],
                                   accum_out=tot_cur[:, u:u + 1]).then_inc(at_a.sem, at_a.tick(f"E{u}"))
                    if u % 2:
                        if u >= 3:
                            act.wait_ge(at_p.sem, at_p.at(f"O{u - 3}", i))
                        move(u - 1)

        @block.vector
        def _(dve):
            layernorm_vector(dve, ln_v, ln_a, x[:], nrm, sq, stat[:], NT)
            dve.memset(q_stack[:], 0.0).then_inc(pre_v.sem, pre_v.tick("q_zeros"))
            dve.memset(k_stack[:], 0.0).then_inc(pre_v.sem, pre_v.tick("k_zeros"))
            dve.wait_ge(pre_v.sem, pre_v.at("q_zeros"))
            dve.memset(q_stack[MROW:MROW + 3], 1.0).then_inc(pre_v.sem, pre_v.tick("q_ones"))
            dve.sem_inc(cut_v.sem, cut_v.at("third1", -1))
            dve.wait_ge(pre_g.sem, pre_g.at("keep"))
            with dve.Fori(0, B // 2) as i:
                def take_k(j):
                    dve.wait_ge(cut_p.sem, cut_p.at(f"k{j}", i))
                    dve.wait_ge(cut_v.sem, cut_v.at(f"rest{j}", i - 1))
                    dve.tensor_tensor(qk[:, j, S:QK], ps[:, 3 * j + 1, :], keep[:, bass.ds(2 * SC * i + SC * j, SC)],
                                      ALU.mult).then_inc(cut_v.sem, cut_v.tick(f"k{j}"))

                def take_rest(j):
                    dve.wait_ge(cut_a.sem, cut_a.at(f"first{j}", i))
                    dve.wait_ge(cut_v.sem, cut_v.at(f"third{j}", i - 1))
                    dve.tensor_tensor(rest[:, j, :], qk[:, j, :], parts[:, j, 0, :], ALU.subtract) \
                       .then_inc(cut_v.sem, cut_v.tick(f"rest{j}"))

                def third(j):
                    dve.wait_ge(cut_a.sem, cut_a.at(f"second{j}", i))
                    dve.tensor_tensor(parts[:, j, 2, :], rest[:, j, :], parts[:, j, 1, :], ALU.subtract) \
                       .then_inc(cut_v.sem, cut_v.tick(f"third{j}"))

                take_k(0)
                take_rest(0)
                take_k(1)
                third(0)
                take_rest(1)
                third(1)
            dve.memset(tot_cur[:], 1.0).then_inc(pre_v.sem, pre_v.tick("tot_ones"))
            dve.sem_inc(at_v.sem, len(at_v.names))

            def take(j, i, place, steps, n):
                half = NU // 2
                dve.wait_ge(at_p.sem, at_p.at(f"O{half * (j + 1) - 1}", i))
                dve.tensor_copy(tot[:, place].rearrange("p o t h -> p (o t) h"),
                                tot_cur[:, bass.ts(j, half)].rearrange("p (h t) -> p t h", t=2)) \
                   .then_inc(steps.sem, steps.tick(f"tot{j}"))
                o = oT_pad.rearrange("p (b t q) -> p b t q", t=2, q=P)[:, place].rearrange("p o t q -> p (o t) q")
                for k in range(HB):
                    mine = ps[:, 4 + 2 * j:6 + 2 * j, bass.ts(k, P)]
                    if k == 0:
                        take_k = dve.tensor_scalar(o, mine, which[:, 0:1], None, ALU.mult)
                    else:
                        dve.wait_ge(steps.sem, steps.at(f"o{k - 1}_{j}", n))
                        dve.sem_inc(passed_v, 1)
                        take_k = dve.scalar_tensor_tensor(o, mine, which[:, k:k + 1], o, ALU.mult, ALU.add)
                    take_k.then_inc(steps.sem, steps.tick(f"o{k}_{j}"))

            dve.wait_ge(rel_in.sem, 16)
            with dve.Fori(0, B // 2) as i:
                def move(u):
                    dve.wait_ge(at_p.sem, at_p.at(f"T{u}", i))
                    if u >= 2:
                        dve.wait_ge(at_p.sem, at_p.at(f"O{u - 2}", i))
                    dve.tensor_copy(prT[:, u % 2, :], ps[:, 2 + u % 2, :]).then_inc(at_v.sem, at_v.tick(f"T{u}"))

                for u in range(NU):
                    dve.wait_ge(at_p.sem, at_p.at(f"S{u}", i))
                    dve.wait_ge(at_a.sem, at_a.at(f"E{(u - 4) % NU}", i - (u < 4)))
                    dve.sem_inc(passed_v, 1)
                    dve.tensor_tensor_reduce(sc[:, u % 4, :], ps[:, u % 2, :],
                                             tb[:, u // 2 % MH, bass.ds(P * (u % 2), SC)], 1.0, 3.0e38,
                                             ALU.add, ALU.min, low[:, u:u + 1]).then_inc(at_v.sem, at_v.tick(f"M{u}"))
                    if u > 2 and u % 2 == 0:
                        move(u - 3)
                    if u == 4:
                        take(1, i - 1, bass.ds(2 * i, 1), at_v, i)
                    if u == NU // 2 + 4:
                        take(0, i, bass.ds(2 * i + 1, 1), at_v, i)
                move(NU - 3)
                move(NU - 1)
            take(1, B // 2 - 1, slice(B, B + 1), last_v, 0)
            dve.wait_ge(last_v.sem, last_v.at(TAKE[1][0]))
            dve.reciprocal(rec[:], tot[:, 1:]).then_inc(out_v.sem, out_v.tick("rec"))
            dve.wait_ge(out_v.sem, out_v.at("rec"))
            dve.tensor_copy(rec_x.rearrange("p t (h d) -> p (t h) d", h=MH),
                            rec[:].rearrange("p b t h -> p (b t h)").unsqueeze(2).to_broadcast([P, NT * MH, MD])) \
               .then_inc(out_v.sem, out_v.tick("rec_x"))
            dve.wait_ge(out_p.sem, out_p.at("rec"))
            dve.wait_ge(last_v.sem, last_v.at(TAKE[1][-1]))
            dve.tensor_tensor(oT, oT, banks(ps, 0, 4), ALU.mult).then_inc(out_v.sem, out_v.tick("o"))
            for i in range(NB):
                dve.wait_ge(out_p.sem, out_p.at(f"out{i}"))
                xb = x[:, bass.ts(i, 4), :]
                dve.tensor_tensor(xb, rows(ps[:, 4 + i, :], 4), xb, ALU.add).then_inc(out_v.sem, out_v.tick(f"x{i}"))

        @block.tensor
        def _(pe):
            for t in range(NT):
                mm = pe.transpose(ps[:, 4 + t // 4, bass.ts(t % 4, P)], ctx[:, t, :], ident)
            mm.then_inc(pre_p.sem, pre_p.tick("ctx0"))
            pe.wait_ge(load.sem, LOADED)
            for i in range(4):
                mm = pe.transpose(ps[:, 0, bass.ts(i, P)], w4[:, i, :], ident)
            mm.then_inc(pre_p.sem, pre_p.tick("w4T"))
            pe.matmul(ps[0:MH, 1, :], emb[:], bucket[:, 0:BLK], start=True, stop=True)
            pe.matmul(ps[0:MH, 2, 0:NREL - BLK], emb[:], bucket[:, BLK:NREL], start=True, stop=True) \
              .then_inc(pre_p.sem, pre_p.tick("rel"))
            pe.wait_ge(pre_a.sem, pre_a.at("ctx0"))
            for t in range(NT):
                if t % 4 == 0:
                    pe.wait_ge(ln_v.sem, ln_v.at(normal_of(t)))
                mm = pe.transpose(ps[:, 4 + t // 4, bass.ts(t % 4, P)], nrm[:, t, :], ident)
            mm.then_inc(pre_p.sem, pre_p.tick("nT"))
            pe.wait_ge(pre_a.sem, pre_a.at("rel"))
            for t in range(NT):
                mm = pe.transpose(ps[:, t // 4, bass.ts(t % 4, P)], ctx[:, NT + t, :], ident)
            mm.then_inc(pre_p.sem, pre_p.tick("ctx1"))
            pe.sem_inc(cut_p.sem, cut_p.at("v1", -1))
            pe.wait_ge(pre_a.sem, pre_a.at("ctx1"))
            with pe.Fori(0, B // 2) as i:
                for j in range(2):
                    pe.wait_ge(cut_a.sem, cut_a.at(f"q{j}", i - 1))
                    pe.matmul(ps[:, 3 * j, 0:S], w4T[:, 0, :], nT[:, bass.ds(2 * S * i + S * j, S)], start=True, stop=True) \
                      .then_inc(cut_p.sem, cut_p.tick(f"q{j}"))
                    pe.wait_ge(cut_v.sem, cut_v.at(f"k{j}", i - 1))
                    pe.matmul(ps[:, 3 * j + 1, :], w4T[:, 1, :], ctxT[:, bass.ds(2 * SC * i + SC * j, SC)],
                              start=True, stop=True).then_inc(cut_p.sem, cut_p.tick(f"k{j}"))
                    pe.wait_ge(cut_a.sem, cut_a.at(f"v{j}", i - 1))
                    pe.wait_ge(cut_g.sem, cut_g.at(f"cur{j}", i))
                    for n in range(NK):
                        mm = pe.matmul(ps[:, 3 * j + 2, bass.ts(n, P)], cur[:, j, bass.ts(n, P)], w4T[:, 2, :],
                                       start=True, stop=True)
                    mm.then_inc(cut_p.sem, cut_p.tick(f"v{j}"))
            pe.sem_inc(at_p.sem, at_p.at(f"O{NU - 1}", -1))
            pe.wait_ge(cut_a.sem, cut_a.at("second1", B // 2 - 1))
            pe.wait_ge(cut_v.sem, cut_v.at("third1", B // 2 - 1))
            pe.wait_ge(pre_v.sem, pre_v.at("q_ones"))

            def scores(u, i):
                j, h = u // (NU // 2), u // 2 % MH
                if u % (NU // 2) == 0:
                    pe.wait_ge(stack_in[j].sem, 16 * N_STACK * (i + 1))
                pe.wait_ge(at_v.sem, at_v.at(f"M{(u - 2) % NU}", i - (u < 2)))
                pe.matmul(ps[:, u % 2, :], q_stack[:, j, h, bass.ts(u % 2, P)], k_stack[:, j, h // 2, :],
                          start=True, stop=True).then_inc(at_p.sem, at_p.tick(f"S{u}"))

            def output(u, i):
                j, h = u // (NU // 2), u // 2 % MH
                pe.wait_ge(at_v.sem, at_v.at(f"T{u}", i)) if u % 2 else pe.wait_ge(at_a.sem, at_a.at(f"T{u}", i))
                if u % (NU // 2) == 0:
                    pe.wait_ge(at_g.sem, at_g.at(f"v{j}", i))
                r = bass.ts(h // HB, 32)
                for n in range(NK):
                    mm = pe.matmul(ps[r, 4 + 2 * j + u % 2, bass.ts(h % HB, P)], v_cur[:, j, n, r],
                                   prT[:, u % 2, bass.ts(n, P)], start=(n == 0), stop=(n == NK - 1))
                mm.then_inc(at_p.sem, at_p.tick(f"O{u}"))

            with pe.Fori(0, B // 2) as i:
                for u in range(AHEAD):
                    scores(u, i)
                for u in range(NU):
                    if u + AHEAD < NU:
                        scores(u + AHEAD, i)
                    pe.wait_ge(at_a.sem, at_a.at(f"E{u}", i))
                    if u >= 2:
                        pe.wait_ge(at_v.sem, at_v.at(f"T{u - 2}", i)) if u % 2 else \
                            pe.wait_ge(at_a.sem, at_a.at(f"T{u - 2}", i))
                    for n in range(NK):
                        mm = pe.transpose(ps[:, 2 + u % 2, bass.ts(n, P)], pr[:, u % 2, bass.ts(n, P)], ident)
                    mm.then_inc(at_p.sem, at_p.tick(f"T{u}"))
                    if u:
                        output(u - 1, i)
                output(NU - 1, i)
            pe.wait_ge(out_v.sem, out_v.at("rec_x"))
            for t in range(NT):
                mm = pe.transpose(ps[:, t // 4, bass.ts(t % 4, P)], rec_x[:, t, :], ident)
            mm.then_inc(out_p.sem, out_p.tick("rec"))
            pe.wait_ge(out_v.sem, out_v.at("o"))
            for i in range(NB):
                for t in range(4):
                    mm = pe.matmul(ps[:, 4 + i, bass.ts(t, P)], oT[:, bass.ts(4 * i + t, P)], w4T[:, 3, :],
                                   start=True, stop=True)
                mm.then_inc(out_p.sem, out_p.tick(f"out{i}"))



ACT_ONE, W_ONE = 16.0, 64.0
MAGIC = 1.5 * 2.0 ** 23
QMIN, QMAX = -128.0, 127.0


def stage_quantized(nc, g, a):
    with Stage(nc, "qu") as st:
        w1 = st.sb("w1", [P, NJ, P])
        w2 = st.sb("w2", [P, HID])
        w1q = st.sb("w1q", [P, HID], BF16)
        w2q = st.sb("w2q", [P, NJ, P], BF16)
        b1 = st.sb("b1", [P, NJ])
        b2 = st.sb("b2", [P, P])
        nrm = st.sb("nrm", [P, NT, P])
        sq = st.sb("sq", [P, NT, P])
        stat = st.sb("stat", [P, 4, NT])
        xq = st.sb("xq", [P, T], BF16)
        hr = st.sb("hr", [P, 2, BLK])
        hq = st.sb("hq", [P, NB, NJ, BLK], BF16)
        ps, x = g.ps, g.x
        ident = g.ident

        load = st.steps("load", ["all"])
        LOADED = 16 * (3 + NJ)
        ln_v, ln_a = st.steps("ln_v", LN_VECTOR), st.steps("ln_a", ["root"])
        quant = [f"{n}_{s}" for n in ("w1", "w2", "b1", "b2") for s in ("up", "round", "clip")]
        q_v = st.steps("q_v", quant + ["b1", "b2", "w1T", "x_up", "x_round", "x_clip"])
        q_g = st.steps("q_g", ["x_bias"])
        q_a = st.steps("q_a", ["w2T", "xT"])
        q_p = st.steps("q_p", ["w1T", "w2T", "xT"])
        units = [(b, j) for b in range(NB) for j in range(NJ)]
        h_p = st.steps("h_p", [f"h{b}{j}" for b, j in units])
        h_a = st.steps("h_a", [f"r{b}{j}" for b, j in units])
        h_v = st.steps("h_v", [f"{n}{b}{j}" for b, j in units for n in ("m", "q")])
        o_p = st.steps("o_p", [f"o{b}" for b in range(NB)])
        o_v = st.steps("o_v", [f"x{b}" for b in range(NB)])

        block = st.block()

        @block.sync
        def _(sp):
            sp.dma_start(w1[:], a["L1_ffn_w1"].rearrange("(j p) d -> p j d", p=P)).then_inc(load.sem, 16)
            sp.dma_start(w2[:], a["L1_ffn_w2"]).then_inc(load.sem, 16)
            for j in range(NJ):
                sp.dma_start(b1[:, j:j + 1], a["L1_ffn_b1"][P * j:P * (j + 1)].unsqueeze(1)).then_inc(load.sem, 16)
            sp.dma_start(b2[:], a["L1_ffn_b2"].partition_broadcast(P)).then_inc(load.sem, 16)

        @block.gpsimd
        def _(pool):
            pool.wait_ge(q_v.sem, q_v.at("b2"))
            pool.wait_ge(ln_v.sem, ln_v.at("normal"))
            pool.tensor_tensor(x[:], x[:], b2[:].unsqueeze(1).to_broadcast([P, NT, P]), ALU.add) \
                .then_inc(q_g.sem, q_g.tick("x_bias"))

        @block.scalar
        def _(act):
            layernorm_root(act, ln_v, ln_a, stat)
            act.wait_ge(q_p.sem, q_p.at("w2T"))
            act.activation(w2q[:].rearrange("p j d -> p (j d)"), ps[:, 1, :], ACT.Copy).then_inc(q_a.sem, q_a.tick("w2T"))
            act.wait_ge(q_p.sem, q_p.at("xT"))
            act.activation(xq[:], banks(ps, 4, 8), ACT.Copy).then_inc(q_a.sem, q_a.tick("xT"))
            for u, (b, j) in enumerate(units):
                act.wait_ge(h_p.sem, h_p.at(f"h{b}{j}"))
                if u >= 2:
                    act.wait_ge(h_v.sem, h_v.at("q%d%d" % units[u - 2]))
                act.activation(hr[:, u % 2, :], ps[:, u % 4, :], ACT.Relu, bias=b1[:, j:j + 1], scale=1 / W_ONE) \
                   .then_inc(h_a.sem, h_a.tick(f"r{b}{j}"))

        @block.vector
        def _(dve):
            def quantize(name, v, one):
                dve.tensor_scalar(v, v, one, None, ALU.mult).then_inc(q_v.sem, q_v.tick(f"{name}_up"))
                dve.wait_ge(q_v.sem, q_v.at(f"{name}_up"))
                dve.tensor_scalar(v, v, MAGIC, MAGIC, ALU.add, ALU.subtract).then_inc(q_v.sem, q_v.tick(f"{name}_round"))
                dve.wait_ge(q_v.sem, q_v.at(f"{name}_round"))
                dve.tensor_scalar(v, v, QMIN, QMAX, ALU.max, ALU.min).then_inc(q_v.sem, q_v.tick(f"{name}_clip"))

            layernorm_vector(dve, ln_v, ln_a, x[:], nrm[:], sq[:], stat[:], NT)
            dve.wait_ge(load.sem, LOADED)
            quantize("w1", w1[:], W_ONE)
            quantize("w2", w2[:], W_ONE)
            quantize("b1", b1[:], W_ONE)
            quantize("b2", b2[:], W_ONE)
            dve.wait_ge(q_v.sem, q_v.at("b2_clip"))
            dve.tensor_scalar(b1[:], b1[:], ACT_ONE / W_ONE, None, ALU.mult).then_inc(q_v.sem, q_v.tick("b1"))
            dve.tensor_scalar(b2[:], b2[:], 1 / W_ONE, None, ALU.mult).then_inc(q_v.sem, q_v.tick("b2"))
            dve.wait_ge(q_p.sem, q_p.at("w1T"))
            dve.tensor_copy(w1q[:], ps[:, 0, :]).then_inc(q_v.sem, q_v.tick("w1T"))
            dve.wait_ge(ln_v.sem, ln_v.at("normal"))
            quantize("x", nrm[:], ACT_ONE)
            for u, (b, j) in enumerate(units):
                dve.wait_ge(h_a.sem, h_a.at(f"r{b}{j}"))
                dve.tensor_scalar(hr[:, u % 2, :], hr[:, u % 2, :], QMAX, MAGIC, ALU.min, ALU.add) \
                   .then_inc(h_v.sem, h_v.tick(f"m{b}{j}"))
                dve.wait_ge(h_v.sem, h_v.at(f"m{b}{j}"))
                dve.tensor_scalar(hq[:, b, j, :], hr[:, u % 2, :], MAGIC, None, ALU.subtract) \
                   .then_inc(h_v.sem, h_v.tick(f"q{b}{j}"))
            dve.wait_ge(q_g.sem, q_g.at("x_bias"))
            for b in range(NB):
                dve.wait_ge(o_p.sem, o_p.at(f"o{b}"))
                xb = x[:, 4 * b:4 * b + 4, :].rearrange("p t d -> p (t d)")
                dve.scalar_tensor_tensor(xb, ps[:, 4 + b, :], 1 / (ACT_ONE * W_ONE), xb, ALU.mult, ALU.add) \
                   .then_inc(o_v.sem, o_v.tick(f"x{b}"))

        @block.tensor
        def _(pe):
            pe.wait_ge(q_v.sem, q_v.at("w2_clip"))
            for j in range(NJ):
                mm = pe.transpose(ps[:, 0, bass.ts(j, P)], w1[:, j, :], ident)
            mm.then_inc(q_p.sem, q_p.tick("w1T"))
            for j in range(NJ):
                mm = pe.transpose(ps[:, 1, bass.ts(j, P)], w2[:, bass.ts(j, P)], ident)
            mm.then_inc(q_p.sem, q_p.tick("w2T"))
            pe.wait_ge(q_v.sem, q_v.at("x_clip"))
            for t in range(NT):
                mm = pe.transpose(ps[:, 4 + t // 4, bass.ts(t % 4, P)], nrm[:, t, :], ident)
            mm.then_inc(q_p.sem, q_p.tick("xT"))
            pe.wait_ge(q_a.sem, q_a.at("xT"))
            pe.wait_ge(q_v.sem, q_v.at("w1T"))

            def up(u):
                b, j = units[u]
                if u >= 4:
                    pe.wait_ge(h_a.sem, h_a.at("r%d%d" % units[u - 4]))
                pe.matmul(ps[:, u % 4, :], w1q[:, bass.ts(j, P)], xq[:, bass.ts(b, BLK)], start=True, stop=True) \
                  .then_inc(h_p.sem, h_p.tick(f"h{b}{j}"))

            def down(b):
                pe.wait_ge(h_v.sem, h_v.at(f"q{b}{NJ - 1}"))
                for i in range(4):
                    for j in range(NJ):
                        mm = pe.matmul(ps[:, 4 + b, bass.ts(i, P)], hq[:, b, j, bass.ts(i, P)], w2q[:, j, :],
                                       start=(j == 0), stop=(j == NJ - 1))
                mm.then_inc(o_p.sem, o_p.tick(f"o{b}"))

            for u in range(len(units)):
                up(u)
                if u % NJ == NJ - 1 and u > NJ:
                    down(u // NJ - 1)
            down(NB - 1)



class Shared:
    pass


def decoder(nc, a, out):
    g = Shared()
    with ExitStack() as stack:
        g.ps = stack.enter_context(nc.psum_tensor("ps", [P, 8, BLK], F32))
        g.x = stack.enter_context(nc.sbuf_tensor("x", [P, NT, P], F32))
        g.ctx = stack.enter_context(nc.sbuf_tensor("ctx", [P, B * SC // P, P], F32))
        const = stack.enter_context(nc.sbuf_tensor("const", [P, 2 * P], F32))
        rep8 = stack.enter_context(nc.sbuf_tensor("rep8", [8, P], F32))
        ones = stack.enter_context(nc.sbuf_tensor("ones", [P, P], F32))
        g.ident, g.bd8, g.rep8, g.ones = const[:, 0:P], const[:, P:2 * P], rep8[:], ones[:]
        x_dram = a["x"].rearrange("b (n p) d -> p (b n) d", p=P)
        with Stage(nc, "start") as st:
            loaded = st.steps("loaded", ["all"])
            made = st.steps("made", ["ones"])
            block = st.block()

            @block.sync
            def _(sp):
                sp.dma_start(g.x[:], x_dram).then_inc(loaded.sem, 16)
                sp.dma_start(const[:], a["const"]).then_inc(loaded.sem, 16)
                sp.dma_start(rep8[:], a["rep8"]).then_inc(loaded.sem, 16)
                sp.wait_ge(loaded.sem, 48)

            @block.vector
            def _(dve):
                dve.memset(ones[:], 1.0).then_inc(made.sem, made.tick("ones"))
                dve.wait_ge(made.sem, 1)

        stages = [stage_fast_weights, stage_cross_attention, stage_experts, stage_gated, stage_masked_attention, stage_quantized]
        for stage in stages[:LAST_STAGE]:
            stage(nc, g, a)
        with Stage(nc, "end") as st:
            stored = st.steps("stored", ["x"])
            block = st.block()

            @block.sync
            def _(sp):
                sp.dma_start(out.rearrange("b (n p) d -> p (b n) d", p=P), g.x[:]).then_inc(stored.sem, 16)
                sp.wait_ge(stored.sem, 16)


def constants():
    p = np.arange(P)
    const = np.concatenate([np.eye(P), p[:, None] // 8 == p[None, :] // 8], axis=1).astype(np.float32)
    rep8 = (np.arange(8)[:, None] == p[None, :] % 8).astype(np.float32)
    lower = np.tril(np.ones((8, 8), np.float32), -1).reshape(64)
    n = np.maximum(np.arange(NREL) - (SC - 1), 0)
    exact = NBUCKET // 2
    large = exact + (np.log(n.astype(np.float32) / exact + 1e-9) / math.log(128 / exact) * exact).astype(np.int32)
    of = np.where(n < exact, n, np.minimum(large, NBUCKET - 1))
    bucket = (np.arange(NBUCKET)[:, None] == of[None, :]).astype(np.float32)
    which = (p[:, None] // MD % HB == np.arange(HB)[None, :]).astype(np.float32)
    gather = (np.arange(B)[None, :, None] * (P // 8) + p[:, None, None] // 8 == p[None, None, :]).astype(np.float32)
    spread = np.ascontiguousarray(gather.transpose(2, 1, 0))
    return {"gather": gather, "spread": spread, "const": const, "rep8": rep8, "lower": lower, "bucket": bucket, "which": which}


def kernel(**inputs):
    import numpy as _np
    import concourse.bacc as _bacc
    from concourse import mybir as _mybir
    from concourse.bass_utils import run_bass_kernel_spmd as _run

    nc = _bacc.Bacc("TRN2", target_bir_lowering=False, num_devices=1)
    arrays, args = {}, {}
    for name, value in list(inputs.items()) + list(constants().items()):
        v = _np.ascontiguousarray(value)
        arrays[f"in_{name}_dram"] = v
        args[name] = nc.dram_tensor(f"in_{name}_dram", v.shape, _mybir.dt.from_np(v.dtype), kind="ExternalInput").ap()
    out = nc.dram_tensor("out_0_dram", (B, S, P), F32, kind="ExternalOutput").ap()
    decoder(nc, args, out)
    r = _run(nc, [arrays], core_ids=[0])
    return r.results[0]["out_0_dram"]
```
